# Optimizing a Trainium2 kernel written in Bass

```python
import numpy as np
import jax
import jax.numpy as jnp

def _softmax(x, axis=-1):
    return jax.nn.softmax(x, axis=axis)

def _gelu(x):
    return jax.nn.gelu(x, approximate=True)

def _silu(x):
    return jax.nn.silu(x)

def _sigmoid(x):
    return jax.nn.sigmoid(x)

def _layernorm(x, axis=-1, eps=1e-05):
    m = jnp.mean(x, axis=axis, keepdims=True)
    v = jnp.var(x, axis=axis, keepdims=True)
    return (x - m) / jnp.sqrt(v + eps)

def _scatter_add(tgt, idx, src, axis=0):
    return tgt.at[idx].add(src)

def _segment_sum(src, seg, n):
    return jax.ops.segment_sum(src, seg, n)
kernel_name = 'mk_decoder_postln_d2_seqx_r8_4f80f4'

def setup_inputs(seed: int=0):
    np.random.seed(seed)
    _w = jnp.asarray

    def _rec_inputs():
        import jax
        import jax.numpy as jnp
        _rk = jax.random.key(seed)
        x = -0.0002928 + 1 * jax.random.normal(jax.random.fold_in(_rk, 1), (4, 256, 128), jnp.float32)
        _lenS = 256 - jax.random.randint(jax.random.fold_in(_rk, 7), (4,), 0, max(1, 256 // 4) + 1, jnp.int32)
        _lenS2 = 256 - jax.random.randint(jax.random.fold_in(_rk, 8), (4,), 0, max(1, 256 // 4) + 1, jnp.int32)
        _ctx_1024P = jax.random.normal(jax.random.fold_in(_rk, 11), (4, 16, 128), jnp.float32)
        _ctx_1024c = jax.random.dirichlet(jax.random.fold_in(_rk, 511), 0.3 * jnp.ones((16,), jnp.float32), (4, 256))
        _ctx_1024t = jnp.einsum('bsk,bkd->bsd', _ctx_1024c, _ctx_1024P)
        _ctx_1024t = _ctx_1024t * jax.lax.rsqrt(jnp.mean(jnp.square(_ctx_1024t)) + 1e-12) * 0.953939
        ctx_1024 = -1.39393e-06 + 0.999914 * (_ctx_1024t + 0.3 * jax.random.normal(jax.random.fold_in(_rk, 611), (4, 256, 128), jnp.float32))
        return (x, ctx_1024)
    x, ctx_1024 = _rec_inputs()

    def _L0_attn_setup():
        import jax, jax.numpy as jnp
        import numpy as np
        D_MODEL = 128
        D_STATE = 16
        DT_RANK = 64
        DT_MIN = 0.001
        DT_MAX = 0.1
        key = jax.random.key(seed)
        ks = jax.random.split(key, 7)
        B, S = (2, 256)
        return {'x': jax.random.normal(ks[0], (B, S, D_MODEL), jnp.float32), 'w_in': jax.random.normal(ks[1], (D_MODEL, D_MODEL), jnp.float32) / np.sqrt(D_MODEL).astype(np.float32), 'w_x': jax.random.normal(ks[2], (D_MODEL, DT_RANK + 2 * D_STATE), jnp.float32) / np.sqrt(D_MODEL).astype(np.float32), 'w_dt': jax.random.normal(ks[3], (DT_RANK, D_MODEL), jnp.float32) / np.sqrt(DT_RANK).astype(np.float32), 'b_dt': jnp.zeros((D_MODEL,), jnp.float32), 'A_log': jax.random.normal(ks[5], (D_MODEL, D_STATE), jnp.float32) * 0.5, 'Dp': jax.random.normal(ks[6], (D_MODEL,), jnp.float32)}
    _L0_attn_all = _L0_attn_setup()
    _L0_attn_in = {k: v for k, v in _L0_attn_all.items() if k in ('w_in', 'w_x', 'w_dt', 'b_dt', 'A_log', 'Dp')}
    del _L0_attn_all

    def _L0_xattn_setup():
        import jax, jax.numpy as jnp
        import numpy as np
        H, DK, DV = (16, 64, 64)
        MEM = 128
        D_MODEL = 128
        OUT_DIM = 128
        key = jax.random.key(seed)
        ks = jax.random.split(key, 12)
        B, S = (2, 256)
        scale = 1.0 / np.sqrt(D_MODEL)
        inp = {'queries': jax.random.normal(ks[0], (B, S, D_MODEL), jnp.float32), 'keys': jax.random.normal(ks[1], (B, S, D_MODEL), jnp.float32), 'values': jax.random.normal(ks[2], (B, S, D_MODEL), jnp.float32), 'wq_w': jax.random.normal(ks[3], (D_MODEL, H * DK), jnp.float32) * scale, 'wq_b': jnp.zeros((H * DK,), jnp.float32), 'wk_w': jax.random.normal(ks[4], (D_MODEL, H * DK), jnp.float32) * scale, 'wk_b': jnp.zeros((H * DK,), jnp.float32), 'wv_w': jax.random.normal(ks[5], (D_MODEL, H * DV), jnp.float32) * scale, 'wv_b': jnp.zeros((H * DV,), jnp.float32), 'mk': jax.random.normal(ks[6], (1, MEM, H * DK), jnp.float32) * (0.1 / DK), 'mv': jax.random.normal(ks[7], (1, MEM, H * DV), jnp.float32) * (0.1 / MEM), 'wo_w': jax.random.normal(ks[8], (H * DV, OUT_DIM), jnp.float32) * (1.0 / np.sqrt(H * DV)), 'wo_b': jnp.zeros((OUT_DIM,), jnp.float32)}
        return inp
    _L0_xattn_all = _L0_xattn_setup()
    _L0_xattn_in = {k: v for k, v in _L0_xattn_all.items() if k in ('wq_w', 'wq_b', 'wk_w', 'wk_b', 'wv_w', 'wv_b', 'mk', 'mv', 'wo_w', 'wo_b')}
    del _L0_xattn_all

    def _L0_ffn_setup():
        import jax, jax.numpy as jnp
        import numpy as np
        H = 16
        E = 8
        EPS = 1e-05

        def _layernorm(x, g, b):
            mu = jnp.mean(x, axis=-1, keepdims=True)
            var = jnp.mean(jnp.square(x - mu), axis=-1, keepdims=True)
            return (x - mu) * jax.lax.rsqrt(var + EPS) * g + b
        key = jax.random.key(seed)
        T, B, C = (128, 8, 128)
        ks = jax.random.split(key, 12)
        s = 0.02
        return {'x': jax.random.normal(ks[0], (T, B, C), jnp.float32), 'in_proj_w': jax.random.normal(ks[1], (3 * C, C), jnp.float32) * s, 'in_proj_b': jnp.zeros((3 * C,), jnp.float32), 'out_w': jax.random.normal(ks[2], (C, C), jnp.float32) * s, 'out_b': jnp.zeros((C,), jnp.float32), 'ln1_g': jnp.ones((C,), jnp.float32), 'ln1_b': jnp.zeros((C,), jnp.float32), 'router_w': jax.random.normal(ks[3], (E, C), jnp.float32) * s, 'router_b': jnp.zeros((E,), jnp.float32), 'w1': jax.random.normal(ks[4], (E, C, C), jnp.float32) * s, 'b1': jnp.zeros((E, C), jnp.float32), 'w2': jax.random.normal(ks[5], (E, C, C), jnp.float32) * s, 'b2': jnp.zeros((E, C), jnp.float32), 'ln2_g': jnp.ones((C,), jnp.float32), 'ln2_b': jnp.zeros((C,), jnp.float32)}
    _L0_ffn_all = _L0_ffn_setup()
    _L0_ffn_in = {k: v for k, v in _L0_ffn_all.items() if k in ('in_proj_w', 'in_proj_b', 'out_w', 'out_b', 'ln1_g', 'ln1_b', 'router_w', 'router_b', 'w1', 'b1', 'w2', 'b2', 'ln2_g', 'ln2_b')}
    del _L0_ffn_all

    def _L1_attn_setup():
        import jax, jax.numpy as jnp
        import numpy as np
        B, N, DIM = (2, 256, 128)
        HEADS, DHEAD = (16, 64)
        GNN_DEPTH = 2
        EPS = 1e-05

        def layer_norm(x, gamma):
            mu = jnp.mean(x, axis=-1, keepdims=True)
            var = jnp.var(x, axis=-1, keepdims=True)
            return (x - mu) / jnp.sqrt(var + EPS) * gamma
        key = jax.random.key(seed)
        ks = jax.random.split(key, 12)
        hd = HEADS * DHEAD
        s = lambda fan: 1.0 / np.sqrt(fan)
        return {'x': jax.random.normal(ks[0], (B, N, DIM), dtype=jnp.float32), 'gamma_in': jnp.ones((DIM,), dtype=jnp.float32), 'Wq': jax.random.normal(ks[1], (DIM, hd), dtype=jnp.float32) * s(DIM), 'Wk': jax.random.normal(ks[2], (DIM, hd), dtype=jnp.float32) * s(DIM), 'Wv': jax.random.normal(ks[3], (DIM, hd), dtype=jnp.float32) * s(DIM), 'gnn_w': jax.random.normal(ks[4], (GNN_DEPTH, DHEAD, DHEAD), dtype=jnp.float32) * s(DHEAD), 'gnn_b': jnp.zeros((GNN_DEPTH, DHEAD), dtype=jnp.float32), 'lin_w': jax.random.normal(ks[5], (DHEAD, DHEAD), dtype=jnp.float32) * s(DHEAD), 'lin_b': jnp.zeros((DHEAD,), dtype=jnp.float32), 'Wo': jax.random.normal(ks[6], (hd, DIM), dtype=jnp.float32) * s(hd), 'gamma_out': jnp.ones((DIM,), dtype=jnp.float32)}
    _L1_attn_all = _L1_attn_setup()
    _L1_attn_in = {k: v for k, v in _L1_attn_all.items() if k in ('gamma_in', 'Wq', 'Wk', 'Wv', 'gnn_w', 'gnn_b', 'lin_w', 'lin_b', 'Wo', 'gamma_out')}
    del _L1_attn_all

    def _L1_xattn_setup():
        import jax, jax.numpy as jnp
        import numpy as np
        EMBED_DIM = 128
        NUM_HEADS = 16
        DEPTH = EMBED_DIM // NUM_HEADS

        def _split_heads(x):
            B, S, _ = x.shape
            return x.reshape(B, S, NUM_HEADS, DEPTH).transpose(0, 2, 1, 3)
        key = jax.random.key(seed)
        ks = jax.random.split(key, 11)
        B, S, D = (2, 256, EMBED_DIM)
        scale = 1.0 / np.sqrt(D)
        inp = {'q': jax.random.normal(ks[0], (B, S, D), jnp.float32), 'k': jax.random.normal(ks[1], (B, S, D), jnp.float32), 'v': jax.random.normal(ks[2], (B, S, D), jnp.float32), 'Wq': jax.random.normal(ks[3], (D, D), jnp.float32) * scale, 'bq': jnp.zeros((D,), jnp.float32), 'Wk': jax.random.normal(ks[4], (D, D), jnp.float32) * scale, 'bk': jnp.zeros((D,), jnp.float32), 'Wv': jax.random.normal(ks[5], (D, D), jnp.float32) * scale, 'bv': jnp.zeros((D,), jnp.float32), 'Wo': jax.random.normal(ks[6], (D, D), jnp.float32) * scale, 'bo': jnp.zeros((D,), jnp.float32)}
        return inp
    _L1_xattn_all = _L1_xattn_setup()
    _L1_xattn_in = {k: v for k, v in _L1_xattn_all.items() if k in ('Wq', 'bq', 'Wk', 'bk', 'Wv', 'bv', 'Wo', 'bo')}
    del _L1_xattn_all

    def _L1_ffn_setup():
        import jax, jax.numpy as jnp
        import numpy as np
        B, S, D_MODEL, D_HIDDEN = (4, 256, 128, 512)

        def act_quant(x):
            scale = 127.0 / jnp.clip(jnp.max(jnp.abs(x), axis=-1, keepdims=True), 1e-05)
            return jnp.clip(jnp.round(x * scale), -128, 127) / scale

        def weight_quant(w):
            scale = 1.0 / jnp.clip(jnp.mean(jnp.abs(w)), 1e-05)
            return jnp.clip(jnp.round(w * scale), -1, 1) / scale

        def bit_linear(x, w):
            xq = x + jax.lax.stop_gradient(act_quant(x) - x)
            wq = w + jax.lax.stop_gradient(weight_quant(w) - w)
            return jnp.einsum('bsd,hd->bsh', xq, wq)

        def depthwise_conv1d(x_bcl, w, b):
            y = jax.lax.conv_general_dilated(x_bcl, w, window_strides=(1,), padding=[(1, 1)], dimension_numbers=('NCH', 'OIH', 'NCH'), feature_group_count=x_bcl.shape[1])
            return y + b[None, :, None]
        key = jax.random.key(seed)
        ks = jax.random.split(key, 5)
        lim1 = 1.0 / np.sqrt(D_MODEL)
        lim2 = 1.0 / np.sqrt(D_HIDDEN)
        limc = 1.0 / np.sqrt(3.0)
        return {'x': jax.random.normal(ks[0], (B, S, D_MODEL), dtype=jnp.float32), 'w1': jax.random.uniform(ks[1], (D_HIDDEN, D_MODEL), jnp.float32, -lim1, lim1), 'conv_w': jax.random.uniform(ks[2], (D_HIDDEN, 1, 3), jnp.float32, -limc, limc), 'conv_b': jax.random.uniform(ks[3], (D_HIDDEN,), jnp.float32, -limc, limc), 'w2': jax.random.uniform(ks[4], (D_MODEL, D_HIDDEN), jnp.float32, -lim2, lim2)}
    _L1_ffn_all = _L1_ffn_setup()
    _L1_ffn_in = {k: v for k, v in _L1_ffn_all.items() if k in ('w1', 'conv_w', 'conv_b', 'w2')}
    del _L1_ffn_all
    return {'x': x, 'ctx_1024': ctx_1024, 'L0_attn_w_in': _L0_attn_in['w_in'], 'L0_attn_w_x': _L0_attn_in['w_x'], 'L0_attn_w_dt': _L0_attn_in['w_dt'], 'L0_attn_b_dt': _L0_attn_in['b_dt'], 'L0_attn_A_log': _L0_attn_in['A_log'], 'L0_attn_Dp': _L0_attn_in['Dp'], 'L0_xattn_wq_w': _L0_xattn_in['wq_w'], 'L0_xattn_wq_b': _L0_xattn_in['wq_b'], 'L0_xattn_wk_w': _L0_xattn_in['wk_w'], 'L0_xattn_wk_b': _L0_xattn_in['wk_b'], 'L0_xattn_wv_w': _L0_xattn_in['wv_w'], 'L0_xattn_wv_b': _L0_xattn_in['wv_b'], 'L0_xattn_mk': _L0_xattn_in['mk'], 'L0_xattn_mv': _L0_xattn_in['mv'], 'L0_xattn_wo_w': _L0_xattn_in['wo_w'], 'L0_xattn_wo_b': _L0_xattn_in['wo_b'], 'L0_ffn_in_proj_w': _L0_ffn_in['in_proj_w'], 'L0_ffn_in_proj_b': _L0_ffn_in['in_proj_b'], 'L0_ffn_out_w': _L0_ffn_in['out_w'], 'L0_ffn_out_b': _L0_ffn_in['out_b'], 'L0_ffn_ln1_g': _L0_ffn_in['ln1_g'], 'L0_ffn_ln1_b': _L0_ffn_in['ln1_b'], 'L0_ffn_router_w': _L0_ffn_in['router_w'], 'L0_ffn_router_b': _L0_ffn_in['router_b'], 'L0_ffn_w1': _L0_ffn_in['w1'], 'L0_ffn_b1': _L0_ffn_in['b1'], 'L0_ffn_w2': _L0_ffn_in['w2'], 'L0_ffn_b2': _L0_ffn_in['b2'], 'L0_ffn_ln2_g': _L0_ffn_in['ln2_g'], 'L0_ffn_ln2_b': _L0_ffn_in['ln2_b'], 'L1_attn_gamma_in': _L1_attn_in['gamma_in'], 'L1_attn_Wq': _L1_attn_in['Wq'], 'L1_attn_Wk': _L1_attn_in['Wk'], 'L1_attn_Wv': _L1_attn_in['Wv'], 'L1_attn_gnn_w': _L1_attn_in['gnn_w'], 'L1_attn_gnn_b': _L1_attn_in['gnn_b'], 'L1_attn_lin_w': _L1_attn_in['lin_w'], 'L1_attn_lin_b': _L1_attn_in['lin_b'], 'L1_attn_Wo': _L1_attn_in['Wo'], 'L1_attn_gamma_out': _L1_attn_in['gamma_out'], 'L1_xattn_Wq': _L1_xattn_in['Wq'], 'L1_xattn_bq': _L1_xattn_in['bq'], 'L1_xattn_Wk': _L1_xattn_in['Wk'], 'L1_xattn_bk': _L1_xattn_in['bk'], 'L1_xattn_Wv': _L1_xattn_in['Wv'], 'L1_xattn_bv': _L1_xattn_in['bv'], 'L1_xattn_Wo': _L1_xattn_in['Wo'], 'L1_xattn_bo': _L1_xattn_in['bo'], 'L1_ffn_w1': _L1_ffn_in['w1'], 'L1_ffn_conv_w': _L1_ffn_in['conv_w'], 'L1_ffn_conv_b': _L1_ffn_in['conv_b'], 'L1_ffn_w2': _L1_ffn_in['w2']}

def reference(x, ctx_1024, L0_attn_w_in, L0_attn_w_x, L0_attn_w_dt, L0_attn_b_dt, L0_attn_A_log, L0_attn_Dp, L0_xattn_wq_w, L0_xattn_wq_b, L0_xattn_wk_w, L0_xattn_wk_b, L0_xattn_wv_w, L0_xattn_wv_b, L0_xattn_mk, L0_xattn_mv, L0_xattn_wo_w, L0_xattn_wo_b, L0_ffn_in_proj_w, L0_ffn_in_proj_b, L0_ffn_out_w, L0_ffn_out_b, L0_ffn_ln1_g, L0_ffn_ln1_b, L0_ffn_router_w, L0_ffn_router_b, L0_ffn_w1, L0_ffn_b1, L0_ffn_w2, L0_ffn_b2, L0_ffn_ln2_g, L0_ffn_ln2_b, L1_attn_gamma_in, L1_attn_Wq, L1_attn_Wk, L1_attn_Wv, L1_attn_gnn_w, L1_attn_gnn_b, L1_attn_lin_w, L1_attn_lin_b, L1_attn_Wo, L1_attn_gamma_out, L1_xattn_Wq, L1_xattn_bq, L1_xattn_Wk, L1_xattn_bk, L1_xattn_Wv, L1_xattn_bv, L1_xattn_Wo, L1_xattn_bo, L1_ffn_w1, L1_ffn_conv_w, L1_ffn_conv_b, L1_ffn_w2):
    import jax
    import jax.numpy as jnp

    def _L0_attn_ref(x, w_in, w_x, w_dt, b_dt, A_log, Dp):
        import jax, jax.numpy as jnp
        import numpy as np
        D_MODEL = 128
        D_STATE = 16
        DT_RANK = 64
        DT_MIN = 0.001
        DT_MAX = 0.1
        x_in = jnp.einsum('bsd,de->bse', x, w_in)
        proj = jnp.einsum('bsd,dp->bsp', x_in, w_x)
        dt_low, Bm, Cm = jnp.split(proj, [DT_RANK, DT_RANK + D_STATE], axis=-1)
        dt = jax.nn.softplus(jnp.einsum('bsr,rd->bsd', dt_low, w_dt) + b_dt) * (DT_MAX - DT_MIN) + DT_MIN
        A = -jnp.exp(A_log)
        b, s, d = x.shape
        h0 = jnp.zeros((b, d, D_STATE), x.dtype)
        dt_tm = jnp.swapaxes(dt, 0, 1)
        u_tm = jnp.swapaxes(x_in, 0, 1)
        B_tm = jnp.swapaxes(Bm, 0, 1)
        C_tm = jnp.swapaxes(Cm, 0, 1)

        def step(h, inp):
            dtt, ut, bt, ct = inp
            dA = dtt[:, :, None] * A
            barA = jnp.exp(dA)
            inp_term = jnp.einsum('bdn,bn,bd->bn', dA, bt, ut)
            h = barA * h + inp_term[:, None, :]
            y = jnp.einsum('bdn,bn->bd', h, ct) + Dp * ut
            return (h, y)
        _, ys = jax.lax.scan(step, h0, (dt_tm, u_tm, B_tm, C_tm))
        return jnp.swapaxes(ys, 0, 1)

    def _L0_xattn_ref(queries, keys, values, wq_w, wq_b, wk_w, wk_b, wv_w, wv_b, mk, mv, wo_w, wo_b):
        import jax, jax.numpy as jnp
        import numpy as np
        H, DK, DV = (16, 64, 64)
        MEM = 128
        D_MODEL = 128
        OUT_DIM = 128
        B, S, _ = queries.shape
        q = (queries @ wq_w + wq_b).reshape(B, S, H, DK).transpose(0, 2, 1, 3)
        k_proj = keys @ wk_w + wk_b
        v_proj = values @ wv_w + wv_b
        k_ext = jnp.concatenate([k_proj, jnp.broadcast_to(mk, (B, MEM, H * DK))], axis=1)
        v_ext = jnp.concatenate([v_proj, jnp.broadcast_to(mv, (B, MEM, H * DV))], axis=1)
        T = S + MEM
        k = k_ext.reshape(B, T, H, DK).transpose(0, 2, 1, 3)
        v = v_ext.reshape(B, T, H, DV).transpose(0, 2, 1, 3)
        scores = jnp.einsum('bhsd,bhtd->bhst', q, k) / jnp.sqrt(jnp.float32(DK))
        attn = jax.nn.softmax(scores, axis=-1)
        out = jnp.einsum('bhst,bhtd->bhsd', attn, v)
        out = out.transpose(0, 2, 1, 3).reshape(B, S, H * DV)
        return out @ wo_w + wo_b

    def _L0_ffn_ref(x, in_proj_w, in_proj_b, out_w, out_b, ln1_g, ln1_b, router_w, router_b, w1, b1, w2, b2, ln2_g, ln2_b):
        import jax, jax.numpy as jnp
        import numpy as np
        H = 16
        E = 8
        EPS = 1e-05

        def _layernorm(x, g, b):
            mu = jnp.mean(x, axis=-1, keepdims=True)
            var = jnp.mean(jnp.square(x - mu), axis=-1, keepdims=True)
            return (x - mu) * jax.lax.rsqrt(var + EPS) * g + b
        T, B, C = x.shape
        D = C // H
        qkv = x @ in_proj_w.T + in_proj_b
        q, k, v = jnp.split(qkv, 3, axis=-1)
        q = q.reshape(T, B, H, D)
        k = k.reshape(T, B, H, D)
        v = v.reshape(T, B, H, D)
        scale = 1.0 / np.sqrt(D).astype(np.float32)
        scores = jnp.einsum('tbhd,sbhd->bhts', q, k) * scale
        attn = jax.nn.softmax(scores, axis=-1)
        ctx = jnp.einsum('bhts,sbhd->tbhd', attn, v).reshape(T, B, C)
        attn_out = ctx @ out_w.T + out_b
        h = _layernorm(x + attn_out, ln1_g, ln1_b)
        flat = h.reshape(-1, C)
        logits = flat @ router_w.T + router_b
        probs = jax.nn.softmax(logits, axis=-1)
        _, top_i = jax.lax.top_k(probs, 2)
        assign = jnp.max(top_i, axis=-1)
        out = jnp.zeros_like(flat)
        for e in range(E):
            he = jax.nn.gelu(flat @ w1[e].T + b1[e], approximate=False)
            oe = he @ w2[e].T + b2[e]
            out = jnp.where((assign == e)[:, None], oe, out)
        moe_out = out.reshape(T, B, C)
        return _layernorm(h + moe_out, ln2_g, ln2_b)

    def _L1_attn_ref(x, gamma_in, Wq, Wk, Wv, gnn_w, gnn_b, lin_w, lin_b, Wo, gamma_out):
        import jax, jax.numpy as jnp
        import numpy as np
        B, N, DIM = (2, 256, 128)
        HEADS, DHEAD = (16, 64)
        GNN_DEPTH = 2
        EPS = 1e-05

        def layer_norm(x, gamma):
            mu = jnp.mean(x, axis=-1, keepdims=True)
            var = jnp.var(x, axis=-1, keepdims=True)
            return (x - mu) / jnp.sqrt(var + EPS) * gamma
        b, n, _ = x.shape
        scale = DHEAD ** (-0.5)
        xn = layer_norm(x, gamma_in)
        q = (xn @ Wq).reshape(b, n, HEADS, DHEAD).transpose(0, 2, 1, 3) * scale
        k = (xn @ Wk).reshape(b, n, HEADS, DHEAD).transpose(0, 2, 1, 3)
        v = (xn @ Wv).reshape(b, n, HEADS, DHEAD).transpose(0, 2, 1, 3)
        sim = jnp.einsum('bhid,bhjd->bhij', q, k)
        mask_value = -jnp.finfo(sim.dtype).max
        causal_mask = jnp.triu(jnp.ones((n, n), dtype=bool), k=1)
        sim = jnp.where(causal_mask, mask_value, sim)
        attn = jax.nn.softmax(sim.astype(jnp.float32), axis=-1)
        out = jnp.einsum('bhij,bhjd->bhid', attn, v)
        adj = attn.reshape(b * HEADS, n, n)
        adj = jnp.clip(adj + jnp.eye(n, dtype=adj.dtype), 0.0, 1.0)
        deg = jnp.sum(adj, axis=-1, keepdims=True)
        feats = v.reshape(b * HEADS, n, DHEAD)
        for l in range(GNN_DEPTH):
            h = feats @ gnn_w[l] + gnn_b[l]
            h = jnp.einsum('bij,bjd->bid', adj, h) / deg
            feats = jax.nn.gelu(h + feats, approximate=False)
        gnn_out = feats @ lin_w + lin_b
        out = out + gnn_out.reshape(b, HEADS, n, DHEAD)
        out = out.transpose(0, 2, 1, 3).reshape(b, n, HEADS * DHEAD)
        return layer_norm(out @ Wo, gamma_out)

    def _L1_xattn_ref(q, k, v, Wq, bq, Wk, bk, Wv, bv, Wo, bo):
        import jax, jax.numpy as jnp
        import numpy as np
        EMBED_DIM = 128
        NUM_HEADS = 16
        DEPTH = EMBED_DIM // NUM_HEADS

        def _split_heads(x):
            B, S, _ = x.shape
            return x.reshape(B, S, NUM_HEADS, DEPTH).transpose(0, 2, 1, 3)
        query = _split_heads(q @ Wq + bq)
        key_ = _split_heads(k @ Wk + bk)
        value = _split_heads(v @ Wv + bv)
        logits = jnp.einsum('bhqd,bhkd->bhqk', query, key_) / jnp.sqrt(jnp.asarray(DEPTH, query.dtype))
        attn = jax.nn.softmax(logits, axis=-1)
        out = jnp.einsum('bhqk,bhkd->bhqd', attn, value)
        B, H, S, d = out.shape
        concat = out.transpose(0, 2, 1, 3).reshape(B, S, H * d)
        return concat @ Wo + bo

    def _L1_ffn_ref(x, w1, conv_w, conv_b, w2):
        import jax, jax.numpy as jnp
        import numpy as np
        B, S, D_MODEL, D_HIDDEN = (4, 256, 128, 512)

        def act_quant(x):
            scale = 127.0 / jnp.clip(jnp.max(jnp.abs(x), axis=-1, keepdims=True), 1e-05)
            return jnp.clip(jnp.round(x * scale), -128, 127) / scale

        def weight_quant(w):
            scale = 1.0 / jnp.clip(jnp.mean(jnp.abs(w)), 1e-05)
            return jnp.clip(jnp.round(w * scale), -1, 1) / scale

        def bit_linear(x, w):
            xq = x + jax.lax.stop_gradient(act_quant(x) - x)
            wq = w + jax.lax.stop_gradient(weight_quant(w) - w)
            return jnp.einsum('bsd,hd->bsh', xq, wq)

        def depthwise_conv1d(x_bcl, w, b):
            y = jax.lax.conv_general_dilated(x_bcl, w, window_strides=(1,), padding=[(1, 1)], dimension_numbers=('NCH', 'OIH', 'NCH'), feature_group_count=x_bcl.shape[1])
            return y + b[None, :, None]
        h = bit_linear(x, w1)
        h = depthwise_conv1d(h.transpose(0, 2, 1), conv_w, conv_b)
        h = h.transpose(0, 2, 1)
        h = jax.nn.silu(h)
        return bit_linear(h, w2)
    x = _layernorm(x + _L0_attn_ref(x, L0_attn_w_in, L0_attn_w_x, L0_attn_w_dt, L0_attn_b_dt, L0_attn_A_log, L0_attn_Dp), axis=-1)
    x = _layernorm(x + _L0_xattn_ref(x, ctx_1024, ctx_1024, L0_xattn_wq_w, L0_xattn_wq_b, L0_xattn_wk_w, L0_xattn_wk_b, L0_xattn_wv_w, L0_xattn_wv_b, L0_xattn_mk, L0_xattn_mv, L0_xattn_wo_w, L0_xattn_wo_b), axis=-1)
    x = _layernorm(x + _L0_ffn_ref(x, L0_ffn_in_proj_w, L0_ffn_in_proj_b, L0_ffn_out_w, L0_ffn_out_b, L0_ffn_ln1_g, L0_ffn_ln1_b, L0_ffn_router_w, L0_ffn_router_b, L0_ffn_w1, L0_ffn_b1, L0_ffn_w2, L0_ffn_b2, L0_ffn_ln2_g, L0_ffn_ln2_b), axis=-1)
    x = _layernorm(x + _L1_attn_ref(x, L1_attn_gamma_in, L1_attn_Wq, L1_attn_Wk, L1_attn_Wv, L1_attn_gnn_w, L1_attn_gnn_b, L1_attn_lin_w, L1_attn_lin_b, L1_attn_Wo, L1_attn_gamma_out), axis=-1)
    x = _layernorm(x + _L1_xattn_ref(x, ctx_1024, ctx_1024, L1_xattn_Wq, L1_xattn_bq, L1_xattn_Wk, L1_xattn_bk, L1_xattn_Wv, L1_xattn_bv, L1_xattn_Wo, L1_xattn_bo), axis=-1)
    x = _layernorm(x + _L1_ffn_ref(x, L1_ffn_w1, L1_ffn_conv_w, L1_ffn_conv_b, L1_ffn_w2), axis=-1)
    return x

_drawn_inputs = setup_inputs


def setup_inputs(seed=0):
    import zlib

    import numpy as np

    out = dict(_drawn_inputs(seed))
    spreads = {'L0_attn_b_dt': (0.0, 0.1),
     'L0_xattn_wq_b': (0.0, 0.449),
     'L0_xattn_wk_b': (0.0, 0.8),
     'L0_xattn_wv_b': (0.0, 0.1),
     'L0_xattn_wo_b': (0.0, 0.1),
     'L0_ffn_in_proj_b': (0.0, 0.522),
     'L0_ffn_out_b': (0.0, 0.1),
     'L0_ffn_ln1_g': (1.0, 0.2),
     'L0_ffn_ln1_b': (0.0, 0.1),
     'L0_ffn_router_b': (0.0, 0.1),
     'L0_ffn_b1': (0.0, 0.8),
     'L0_ffn_b2': (0.0, 0.1),
     'L0_ffn_ln2_g': (1.0, 0.2),
     'L0_ffn_ln2_b': (0.0, 0.1),
     'L1_attn_gamma_in': (1.0, 0.2),
     'L1_attn_gnn_b': (0.0, 0.1),
     'L1_attn_lin_b': (0.0, 0.1),
     'L1_attn_gamma_out': (1.0, 0.2),
     'L1_xattn_bq': (0.0, 0.418),
     'L1_xattn_bk': (0.0, 0.8),
     'L1_xattn_bv': (0.0, 0.1),
     'L1_xattn_bo': (0.0, 0.1)}
    factors = {'L0_xattn_mk': 8.0,
     'L0_xattn_mv': 8.0,
     'L0_ffn_in_proj_w': 4.139,
     'L0_ffn_out_w': 2.734,
     'L0_ffn_w1': 4.769,
     'L0_ffn_w2': 4.376}
    for name, (base, spread) in spreads.items():
        noise = np.random.default_rng([zlib.crc32(name.encode()), seed]).standard_normal(out[name].shape)
        drawn = base * np.exp(spread * noise) if base else spread * noise
        out[name] = jnp.asarray(drawn.astype(out[name].dtype))
    for name, factor in factors.items():
        out[name] = (out[name] * factor).astype(out[name].dtype)
    return out
```

```python
from contextlib import ExitStack

import concourse.bass as bass
from concourse import mybir

F32 = mybir.dt.float32
BF16 = mybir.dt.bfloat16
F16 = mybir.dt.float16
U32 = mybir.dt.uint32
ALU = mybir.AluOpType
ACT = mybir.ActivationFunctionType
AX = mybir.AxisListType
ds = bass.ds

P = 128
BATCH, SEQ, D = 4, 256, 128
TOK = BATCH * SEQ
TILES = TOK // P
BANK = 512
EPS = 1e-5


class Tally:

    def __init__(self, engine, sem, before=0):
        self.engine, self.sem, self.n, self.before = engine, sem, 0, before

    def add(self, instruction):
        instruction.then_inc(self.sem, 1)
        self.n += 1

    def settle(self):
        self.engine.wait_ge(self.sem, self.before + self.n)

    def step(self, instruction):
        self.add(instruction)
        self.settle()


class Resources:

    def __init__(self, nc, ctx, sems, tag):
        self.nc, self.ctx, self.sems, self.tag = nc, ctx, sems, tag

    def sb(self, name, shape, dt=F32):
        return self.ctx.enter_context(self.nc.sbuf_tensor(name, shape, dt))

    def sem(self, name):
        self.sems.append(self.nc.alloc_semaphore(name=f"{self.tag}_{name}"))
        return self.sems[-1]


class Shared:

    def __init__(self, nc, ctx):
        r = Resources(nc, ctx, [], "kernel")
        self.sems = []
        self.x, self.xt = r.sb("x_rows", [P, TILES, D]), r.sb("x_cols", [P, TOK])
        self.ctx, self.ct = r.sb("ctx_rows", [P, TILES, D]), r.sb("ctx_cols", [P, TOK])
        self.ident, self.ones_row = r.sb("identity", [P, P]), r.sb("ones_row", [1, P])
        self.ones_row_b = r.sb("ones_row_b", [1, P], BF16)
        self.psum = ctx.enter_context(nc.psum_tensor("banks", [P, 8, BANK], F32))


def halves(ap):
    return ap.rearrange("p (h n) -> p h n", h=2)


def transpose_rows(nc, pe, src, src_ready, ident, banks, done):
    for t in range(TILES):
        if src_ready is not None:
            pe.wait_ge(src_ready[0], src_ready[1](t))
        ins = nc.tensor.transpose(banks[t // 4][:, (t % 4) * P:(t % 4 + 1) * P], src[:, t, :], ident)
        if t % 4 == 3:
            ins.then_inc(done, 1)


class NormBuffers:
    def __init__(self, r, tag):
        self.stats, self.mv = r.sb(f"{tag}_stats", [P, TILES, 6]), r.sb(f"{tag}_mean_var", [P, TILES, 2])
        self.ve, self.sd = r.sb(f"{tag}_var_eps", [P, TILES]), r.sb(f"{tag}_std", [P, TILES])
        self.rstd, self.shift = r.sb(f"{tag}_rstd", [P, TILES]), r.sb(f"{tag}_shift", [P, TILES])
        self.var_ready, self.sd_ready = r.sem(f"{tag}_var_ready"), r.sem(f"{tag}_sd_ready")


def norm_stats(nc, tally, b, rows):
    for t in range(TILES):
        tally.add(nc.vector.bn_stats(b.stats[:, t, :], rows[:, t, :]))
    tally.settle()
    for t in range(TILES):
        tally.add(nc.vector.bn_aggr(b.mv[:, t, :], b.stats[:, t, :]))
    tally.settle()
    nc.vector.tensor_scalar(b.ve[:], b.mv[:, :, 1], EPS, None, ALU.add).then_inc(b.var_ready, 1)


def norm_root(nc, act, b, k):
    act.wait_ge(b.var_ready, k)
    nc.scalar.activation(b.sd[:], b.ve[:], ACT.Sqrt).then_inc(b.sd_ready, 1)


def norm_scale(nc, dve, tally, b, k):
    dve.wait_ge(b.sd_ready, k)
    tally.step(nc.vector.reciprocal(b.rstd[:], b.sd[:]))
    tally.step(nc.vector.scalar_tensor_tensor(b.shift[:], b.mv[:, :, 0], -1.0, b.rstd[:], ALU.mult, ALU.mult))


def norm_apply(nc, tally, b, rows, out):
    for t in range(TILES):
        tally.add(nc.vector.tensor_scalar(out[:, t, :], rows[:, t, :], b.rstd[:, t:t + 1],
                                          b.shift[:, t:t + 1], ALU.mult, ALU.add))
    tally.settle()


DT_RANK, STATES = 64, 16
DT_MIN, DT_MAX = 0.001, 0.1


def selective_scan(nc, g, a):
    with ExitStack() as ctx:
        r = Resources(nc, ctx, g.sems, "ssm")
        w_in = r.sb("w_in", [P, D])
        w_x = r.sb("w_x", [P, DT_RANK + 2 * STATES])
        w_dt = r.sb("w_dt", [DT_RANK, D])
        vecs = r.sb("ssm_vecs", [P, 2])
        a_log = r.sb("a_log", [P, STATES])
        neg_a = r.sb("neg_a", [P, STATES])
        pick = r.sb("pick_state", [96, STATES, P], BF16)
        pick_rows = pick[:].rearrange("k n p -> k (n p)")
        parts = r.sb("row_parts", [96, 2, TOK], BF16)
        u = r.sb("u_cols", [P, TOK])
        low = r.sb("dt_low_cols", [DT_RANK, TOK])
        bm = r.sb("b_cols", [STATES, TOK])
        rows2 = r.sb("inp_c_cols", [STATES, 2, TOK])
        part = r.sb("rounded_part", [STATES, 2, TOK], BF16)
        absz = r.sb("abs_z", [P, TOK])
        soft = r.sb("soft_tail", [P, TOK])
        dt = r.sb("dt_cols", [P, TOK])
        dtu = r.sb("dtu_cols", [P, TOK])
        decay = [r.sb(f"decay{i}", [P, TOK]) for i in range(2)]
        zeros = r.sb("zeros", [P, BATCH])
        state = r.sb("state", [P, TOK])
        hc = [r.sb(f"state_c{i}", [P, TOK]) for i in range(2)]
        y = r.sb("ssm_y_cols", [P, TOK])
        rsd = r.sb("ssm_rows", [P, TILES, D])
        nb = NormBuffers(r, "ssm_norm")

        loaded = {k: r.sem(f"loaded_{k}") for k in ("x", "ctx", "w", "small")}
        const_done, xt_psum, xt_ready, ct_psum, ct_ready = (r.sem(n) for n in (
            "const_done", "xt_psum", "xt_ready", "ct_psum", "ct_ready"))
        u_psum, u_ready, low_psum, low_ready, bc_psum, z_psum = (r.sem(n) for n in (
            "u_psum", "u_ready", "low_psum", "low_ready", "bc_psum", "z_psum"))
        abs_ready, soft_ready, nega_exp, nega_ready, dt_ready, dtu_ready = (r.sem(n) for n in (
            "abs_ready", "soft_ready", "nega_exp", "nega_ready", "dt_ready", "dtu_ready"))
        s_psum, parts_ready, inp_bc, c_bc, decay_exp, decay_ready = (r.sem(n) for n in (
            "s_psum", "parts_ready", "inp_bc", "c_bc", "decay_exp", "decay_ready"))
        scanned, hc_ready, summed, y_ready, yt_psum = (r.sem(n) for n in (
            "scanned", "hc_ready", "summed", "y_ready", "yt_psum"))
        dve_steps, act_steps, pool_steps = r.sem("dve_steps"), r.sem("act_steps"), r.sem("pool_steps")
        bank = [g.psum[:, i, :] for i in range(8)]
        pair = [g.psum[:, 2 * i:2 * i + 2, :] for i in range(4)]
        block = ctx.enter_context(nc.Block())

        @block.sync
        def _(sp):
            sp.dma_start(g.x[:], a["x"].rearrange("b (h p) c -> p (b h) c", p=P)).then_inc(loaded["x"], 16)
            sp.dma_start(w_in[:], a["L0_attn_w_in"]).then_inc(loaded["w"], 16)
            sp.dma_start(w_x[:], a["L0_attn_w_x"]).then_inc(loaded["w"], 16)
            sp.dma_start(w_dt[:], a["L0_attn_w_dt"]).then_inc(loaded["w"], 16)
            sp.dma_start(g.ctx[:], a["ctx_1024"].rearrange("b (h p) c -> p (b h) c", p=P)).then_inc(loaded["ctx"], 16)

        @block.gpsimd
        def _(pool):
            steps = Tally(pool, pool_steps)
            steps.add(nc.gpsimd.memset(zeros[:], 0.0))
            steps.add(nc.gpsimd.memset(g.ident[:], 0.0))
            steps.add(nc.gpsimd.memset(g.ones_row[:], 1.0))
            steps.add(nc.gpsimd.memset(pick[:], 0.0))
            steps.settle()
            nc.gpsimd.affine_select(out=g.ident[:], in_=g.ident[:], compare_op=ALU.not_equal, fill=1.0,
                                    base=0, pattern=[[-1, P]], channel_multiplier=1).then_inc(const_done, 1)
            for j in range(3):
                steps.step(nc.gpsimd.affine_select(out=pick[:], in_=pick[:], compare_op=ALU.not_equal, fill=1.0,
                                                   base=-32 * j, pattern=[[-1, STATES], [0, P]],
                                                   channel_multiplier=1))
            steps.step(nc.gpsimd.memset(parts[:], 0.0))
            nc.gpsimd.memset(g.ones_row_b[:], 1.0).then_inc(const_done, 1)

            def clear_starts(n, k):
                pool.wait_ge(decay_exp, n + 1)
                nc.gpsimd.tensor_tensor(decay[k][:].rearrange("p (b s) -> p b s", b=BATCH)[:, :, 0],
                                        zeros[:], zeros[:], ALU.add)\
                    .then_inc(decay_ready, 1)

            with pool.Fori(0, STATES // 2) as i:
                for k in range(2):
                    clear_starts(2 * i + k, k)

        @block.scalar
        def _(act):
            act.dma_start(vecs[:, 0:1], a["L0_attn_b_dt"]).then_inc(loaded["small"], 16)
            act.dma_start(vecs[:, 1:2], a["L0_attn_Dp"]).then_inc(loaded["small"], 16)
            act.dma_start(a_log[:], a["L0_attn_A_log"]).then_inc(loaded["small"], 16)
            act.wait_ge(loaded["small"], 48)
            nc.scalar.activation(neg_a[:], a_log[:], ACT.Exp).then_inc(nega_exp, 1)
            act.wait_ge(xt_psum, 1)
            nc.scalar.copy(g.xt[:, 0:BANK], bank[0]).then_inc(xt_ready, 1)
            for h in range(2):
                act.wait_ge(u_psum, h + 1)
                nc.scalar.copy(u[:, h * BANK:(h + 1) * BANK], bank[2 + h]).then_inc(u_ready, 1)
            for h in range(2):
                act.wait_ge(low_psum, h + 1)
                nc.scalar.copy(low[:, h * BANK:(h + 1) * BANK], bank[4 + h][0:DT_RANK, :]).then_inc(low_ready, 1)
            act.wait_ge(z_psum, 2)
            steps = Tally(act, act_steps)
            steps.step(nc.scalar.activation(absz[:], g.psum[:, 6:8, :], ACT.Abs, bias=vecs[:, 0:1]))
            abs_sem = steps
            steps.step(nc.scalar.activation(absz[:], absz[:], ACT.Exp, scale=-1.0))
            nc.scalar.activation(soft[:], absz[:], ACT.Ln, bias=1.0).then_inc(soft_ready, 1)
            act.wait_ge(dt_ready, 1)
            act.wait_ge(nega_ready, 1)

            def decays(n, k, first):
                if not first:
                    act.wait_ge(scanned, n - 1)
                nc.scalar.activation(decay[k][:], dt[:], ACT.Exp, scale=neg_a[:, ds(n, 1)]).then_inc(decay_exp, 1)

            for k in range(2):
                decays(k, k, True)
            with act.Fori(1, STATES // 2) as i:
                for k in range(2):
                    decays(2 * i + k, k, False)
            norm_root(nc, act, nb, 1)

        @block.tensor
        def _(pe):
            pe.wait_ge(const_done, 1)
            pe.wait_ge(loaded["x"], 16)
            transpose_rows(nc, pe, g.x, None, g.ident[:], bank, xt_psum)
            pe.wait_ge(loaded["w"], 48)
            for h in range(2):
                pe.wait_ge(xt_ready, 2)
                nc.tensor.matmul(bank[2 + h], w_in[:], g.xt[:, h * BANK:(h + 1) * BANK], start=True, stop=True)\
                    .then_inc(u_psum, 1)
            for h in range(2):
                pe.wait_ge(u_ready, h + 1)
                nc.tensor.matmul(bank[4 + h][0:DT_RANK, :], w_x[:, 0:DT_RANK], u[:, h * BANK:(h + 1) * BANK],
                                 start=True, stop=True).then_inc(low_psum, 1)
            for h in range(2):
                pe.wait_ge(low_ready, h + 1)
                nc.tensor.matmul(bank[6 + h], w_dt[:], low[:, h * BANK:(h + 1) * BANK], start=True, stop=True)\
                    .then_inc(z_psum, 1)
            for h in range(2):
                for m in range(2):
                    lo = DT_RANK + m * STATES
                    ins = nc.tensor.matmul(bank[2 * m + h][0:STATES, :], w_x[:, lo:lo + STATES],
                                           u[:, h * BANK:(h + 1) * BANK], start=True, stop=True)
            ins.then_inc(bc_psum, 1)
            pe.wait_ge(loaded["ctx"], 16)
            pe.wait_ge(low_ready, 2)
            transpose_rows(nc, pe, g.ctx, None, g.ident[:], bank[4:6], ct_psum)
            pe.wait_ge(dtu_ready, 1)
            pe.wait_ge(nega_ready, 1)
            for h in range(2):
                nc.tensor.matmul(bank[6 + h][0:STATES, :], neg_a[:], dtu[:, h * BANK:(h + 1) * BANK],
                                 start=True, stop=True).then_inc(s_psum, 1)
            pe.wait_ge(parts_ready, 1)
            pe.wait_ge(const_done, 2)
            pe.wait_ge(ct_ready, 2)

            def broadcasts(n, k, first):
                if not first:
                    pe.wait_ge(scanned, n - 1)
                for h in range(2):
                    ins = nc.tensor.matmul(bank[2 * k + h], pick_rows[:, ds(n * P, P)],
                                           parts[:, 0, h * BANK:(h + 1) * BANK], start=True, stop=True)
                ins.then_inc(inp_bc, 1)

            def outputs(n, k, zero, first, last):
                if not zero:
                    pe.wait_ge(hc_ready, n)
                for h in range(2):
                    ins = nc.tensor.matmul(bank[4 + h], pick_rows[:, ds(n * P, P)],
                                           parts[:, 1, h * BANK:(h + 1) * BANK], start=True, stop=True)
                ins.then_inc(c_bc, 1)
                if not zero:
                    gather(n - 1, 1 - k, last == "first", False)

            def gather(n, k, start, stop):
                pe.wait_ge(hc_ready, n + 1)
                for h in range(2):
                    ins = nc.tensor.matmul(bank[6 + h], g.ident[:], hc[k][:, h * BANK:(h + 1) * BANK],
                                           start=start, stop=stop)
                ins.then_inc(summed, 1)

            broadcasts(0, 0, True)
            broadcasts(1, 1, True)
            outputs(0, 0, True, True, "")
            outputs(1, 1, False, True, "first")
            with pe.Fori(1, STATES // 2) as i:
                for k in range(2):
                    broadcasts(2 * i + k, k, False)
                    outputs(2 * i + k, k, False, False, "")
            gather(STATES - 1, 1, False, True)
            pe.wait_ge(y_ready, 1)
            pe.wait_ge(scanned, STATES)
            for t in range(TILES):
                ins = nc.tensor.transpose(bank[t // 4][:, (t % 4) * P:(t % 4 + 1) * P],
                                          y[:, t * P:(t + 1) * P], g.ident[:])
            ins.then_inc(yt_psum, 1)

        @block.vector
        def _(dve):
            steps = Tally(dve, dve_steps)
            dve.wait_ge(xt_psum, 2)
            nc.vector.tensor_copy(g.xt[:, BANK:], bank[1]).then_inc(xt_ready, 1)
            dve.wait_ge(nega_exp, 1)
            steps.step(nc.vector.tensor_scalar(neg_a[:], neg_a[:], -1.0, None, ALU.mult))
            nc.vector.tensor_scalar(neg_a[:], neg_a[:], 1.0, None, ALU.mult).then_inc(nega_ready, 1)
            dve.wait_ge(bc_psum, 1)
            steps.add(nc.vector.tensor_copy(halves(bm[:]), pair[0][0:STATES]))
            steps.step(nc.vector.tensor_copy(halves(rows2[:, 1, :]), pair[1][0:STATES]))
            dve.wait_ge(ct_psum, 2)
            for h in range(2):
                nc.vector.tensor_copy(g.ct[:, h * BANK:(h + 1) * BANK], bank[4 + h]).then_inc(ct_ready, 1)
            dve.wait_ge(soft_ready, 1)
            dve.wait_ge(z_psum, 2)
            steps.step(nc.vector.tensor_scalar(halves(dt[:]), pair[3], vecs[:, 0:1], 0.0, ALU.add, ALU.max))
            steps.step(nc.vector.tensor_tensor(dt[:], dt[:], soft[:], ALU.add))
            steps.step(nc.vector.tensor_scalar(dtu[:], dt[:], DT_MAX - DT_MIN, DT_MIN, ALU.mult, ALU.add))
            nc.vector.tensor_copy(dt[:], dtu[:]).then_inc(dt_ready, 1)
            dve.wait_ge(dt_ready, 1)
            dve.wait_ge(u_ready, 2)
            nc.vector.tensor_tensor(dtu[:], dt[:], u[:], ALU.mult).then_inc(dtu_ready, 1)
            dve.wait_ge(s_psum, 2)
            steps.step(nc.vector.tensor_tensor(halves(rows2[:, 0, :]), halves(bm[:]), pair[3][0:STATES], ALU.mult))
            dve.wait_ge(const_done, 2)
            steps.step(nc.vector.tensor_copy(part[:], rows2[:]))
            steps.add(nc.vector.tensor_copy(parts[0:STATES], part[:]))
            steps.step(nc.vector.tensor_tensor(rows2[:], rows2[:], part[:], ALU.subtract))
            steps.step(nc.vector.tensor_copy(part[:], rows2[:]))
            steps.add(nc.vector.tensor_copy(parts[32:32 + STATES], part[:]))
            steps.step(nc.vector.tensor_tensor(rows2[:], rows2[:], part[:], ALU.subtract))
            nc.vector.tensor_copy(parts[64:64 + STATES], rows2[:]).then_inc(parts_ready, 1)

            def scan(n, k, first):
                dve.wait_ge(inp_bc, n + 1)
                dve.wait_ge(decay_ready, n + 1)
                nc.vector.tensor_tensor_scan(state[:], decay[k][:], g.psum[:, 2 * k:2 * k + 2, :]
                                             .rearrange("p h n -> p (h n)"), 0.0, ALU.mult, ALU.add)\
                    .then_inc(scanned, 1)
                dve.wait_ge(scanned, n + 1)
                dve.wait_ge(c_bc, n + 1)
                if not first:
                    dve.wait_ge(summed, n - 1)
                nc.vector.tensor_tensor(halves(hc[k][:]), halves(state[:]), pair[2], ALU.mult).then_inc(hc_ready, 1)

            for k in range(2):
                scan(k, k, True)
                dve.wait_ge(hc_ready, k + 1)
            with dve.Fori(1, STATES // 2) as i:
                for k in range(2):
                    scan(2 * i + k, k, False)
                    dve.wait_ge(hc_ready, 2 * i + k + 1)
            dve.wait_ge(summed, STATES)
            nc.vector.scalar_tensor_tensor(halves(y[:]), halves(u[:]), vecs[:, 1:2], pair[3], ALU.mult, ALU.add)\
                .then_inc(y_ready, 1)
            dve.wait_ge(yt_psum, 1)
            steps.step(nc.vector.tensor_tensor(rsd[:].rearrange("p (h t) c -> p h (t c)", h=2), g.x[:]
                                               .rearrange("p (h t) c -> p h (t c)", h=2), pair[0], ALU.add))
            norm_stats(nc, steps, nb, rsd)
            norm_scale(nc, dve, steps, nb, 1)
            norm_apply(nc, steps, nb, rsd, g.x)


HEADS, DK, MEM = 16, 64, 128
PAIRS = HEADS // 2
KEYS = SEQ + MEM
KT = KEYS // P
QT = SEQ // P
VW = DK + 1
UNITS = 2 * BATCH


def memory_attention(nc, g, a):
    with ExitStack() as ctx:
        r = Resources(nc, ctx, g.sems, "xattn")
        wv = r.sb("wv", [P, HEADS * DK])
        wo = r.sb("wo", [P, PAIRS, D])
        bv = r.sb("bv_all_rows", [P, HEADS * DK])
        bo = r.sb("bo_row", [1, D])
        bqk = r.sb("bq_bk_cols", [P, 2, PAIRS])
        wpair = r.sb("wq_wk_pair", [P, 2, P])
        mk = r.sb("mk_rows", [P, HEADS * DK])
        mkt_all = r.sb("mk_cols_all", [P, PAIRS, P])
        mkt = r.sb("mk_cols_pair", [P, P])
        q = r.sb("q_cols", [P, BATCH, SEQ])
        k = r.sb("k_cols", [P, BATCH, SEQ])
        v_rows = r.sb("value_rows", [P, 4, HEADS // 2, DK])
        mv = r.sb("mv_rows", [P, HEADS, DK])
        v_hi = r.sb("values_hi", [P, TILES + 1, HEADS, VW], F16)
        v_lo = r.sb("values_lo", [P, TILES + 1, HEADS, VW], F16)
        v_hi_flat = v_hi[:].rearrange("p t h w -> p (t h w)")
        v_lo_flat = v_lo[:].rearrange("p t h w -> p (t h w)")
        e = [r.sb(f"probs{i}", [P, QT, KEYS]) for i in range(2)]
        et_hi = [r.sb(f"probs_cols_hi{i}", [P, QT, KEYS], F16) for i in range(2)]
        et_lo = [r.sb(f"probs_cols_lo{i}", [P, QT, KEYS], F16) for i in range(2)]
        negmax = [r.sb(f"negmax{i}", [P, QT]) for i in range(2)]
        o = r.sb("out_raw", [P, TILES, HEADS, VW])
        o_heads = o[:].rearrange("p t h w -> p t (h w)")
        rsum = [r.sb(f"rsum{i}", [P, HEADS]) for i in range(2)]
        on = [r.sb(f"out_normal{i}", [P, HEADS, DK]) for i in range(2)]
        ont = [r.sb(f"out_cols{i}", [P, PAIRS, P]) for i in range(2)]
        rsd = r.sb("xattn_rows", [P, TILES, D])
        nb = NormBuffers(r, "xattn_norm")
        loaded, wpair_loaded, xt_psum, xt_ready, v_psum, v_ready = (r.sem(n) for n in (
            "loaded", "wpair_loaded", "xt_psum", "xt_ready", "v_psum", "v_ready"))
        v_ones, mk_psum, mk_ready, mkt_ready, projected, qk_ready = (r.sem(n) for n in (
            "v_ones", "mk_psum", "mk_ready", "mkt_ready", "projected", "qk_ready"))
        scored, max_ready, exp_ready, turned, et_hi_ready, et_lo_ready = (r.sem(n) for n in (
            "scored", "max_ready", "exp_ready", "turned", "et_hi_ready", "et_lo_ready"))
        pv_done, o_ready, on_ready, on_turned, ont_ready, y_psum = (r.sem(n) for n in (
            "pv_done", "o_ready", "on_ready", "on_turned", "ont_ready", "y_psum"))
        y_ready, dve_steps, v_rows_ready, v_hi_ready = (r.sem(n) for n in (
            "y_ready", "dve_steps", "v_rows_ready", "v_hi_ready"))
        bank = [g.psum[:, i, :] for i in range(8)]
        score_bank = [g.psum[:, 2 * i:2 * i + 2, 0:KEYS] for i in range(2)]
        turn_bank = [bank[4], bank[5]]
        proj_bank, o_bank = bank[6], bank[7]
        block = ctx.enter_context(nc.Block())

        @block.sync
        def _(sp):
            sp.dma_start(wv[:], a["L0_xattn_wv_w"]).then_inc(loaded, 16)
            sp.dma_start(bv[:], a["L0_xattn_wv_b"].rearrange("(o n) -> o n", o=1).broadcast_to([P, HEADS * DK]))\
                .then_inc(loaded, 16)
            sp.dma_start(mk[:], a["L0_xattn_mk"][0]).then_inc(loaded, 16)
            for j, b in enumerate((a["L0_xattn_wq_b"], a["L0_xattn_wk_b"])):
                sp.dma_start(bqk[:, j, :], b).then_inc(loaded, 16)
            sp.dma_start(mv[:], a["L0_xattn_mv"][0].rearrange("m (h d) -> m h d", h=HEADS))\
                .then_inc(loaded, 16)
            sp.dma_start(wo[:], a["L0_xattn_wo_w"].rearrange("(c p) n -> p c n", p=P)).then_inc(loaded, 16)
            sp.dma_start(bo[:], a["L0_xattn_wo_b"].rearrange("(o n) -> o n", o=1)).then_inc(loaded, 16)

            def load_pair(p):
                for j, w in enumerate((a["L0_xattn_wq_w"], a["L0_xattn_wk_w"])):
                    sp.dma_start(wpair[:, j, :], w[:, ds(p * P, P)]).then_inc(wpair_loaded, 16)

            load_pair(0)
            with sp.Fori(1, PAIRS) as p:
                sp.wait_ge(projected, BATCH * p)
                load_pair(p)

        @block.gpsimd
        def _(pool):
            nc.gpsimd.memset(v_hi[:, :, :, DK], 1.0).then_inc(v_ones, 1)
            nc.gpsimd.memset(v_lo[:, :, :, DK], 0.0).then_inc(v_ones, 1)
            for n in range(2 * TILES):
                t, h = n // 2, n % 2
                pool.wait_ge(v_hi_ready, n + 1)
                nc.gpsimd.tensor_tensor(v_lo[:, t, 8 * h:8 * h + 8, 0:DK], v_rows[:, n % 4],
                                        v_hi[:, t, 8 * h:8 * h + 8, 0:DK], ALU.subtract).then_inc(v_ready, 1)
            pool.wait_ge(v_hi_ready, 2 * TILES + 1)
            nc.gpsimd.tensor_tensor(v_lo[:, TILES, :, 0:DK], mv[:], v_hi[:, TILES, :, 0:DK], ALU.subtract)\
                .then_inc(v_ready, 1)

        @block.tensor
        def _(pe):
            transpose_rows(nc, pe, g.x, None, g.ident[:], bank[4:6], xt_psum)
            pe.wait_ge(loaded, 128)
            for c in range(PAIRS):
                if c == 4:
                    pe.wait_ge(mk_ready, 1)
                ins = nc.tensor.transpose(bank[6 + c // 4][:, (c % 4) * P:(c % 4 + 1) * P],
                                          mk[:, c * P:(c + 1) * P], g.ident[:])
                if c % 4 == 3:
                    ins.then_inc(mk_psum, 1)
            for t in range(TILES):
                for h in range(2):
                    n = 2 * t + h
                    if n >= 4:
                        pe.wait_ge(v_rows_ready, n - 3)
                    nc.tensor.matmul(bank[n % 4], g.ct[:, t * P:(t + 1) * P], wv[:, h * BANK:(h + 1) * BANK],
                                     start=True, stop=True).then_inc(v_psum, 1)
            pe.wait_ge(xt_ready, 2)
            pe.wait_ge(mk_ready, 2)

            def project(p, b, first=False):
                if not first:
                    pe.wait_ge(qk_ready, BATCH * p + b)
                pe.wait_ge(wpair_loaded, 32 * p + 32)
                for j, src in enumerate((g.xt, g.ct)):
                    ins = nc.tensor.matmul(proj_bank[:, j * SEQ:(j + 1) * SEQ], wpair[:, j, :],
                                           src[:, b * SEQ:(b + 1) * SEQ], start=True, stop=True)
                ins.then_inc(projected, 1)

            def scores(u, b, h, i, first):
                if not first:
                    pe.wait_ge(exp_ready, u - 1)
                rows = slice(h * DK, (h + 1) * DK)
                for qt in range(QT):
                    lhs = q[rows, b, qt * P:(qt + 1) * P]
                    nc.tensor.matmul(bank[2 * i + qt][:, 0:SEQ], lhs, k[rows, b, :], start=True, stop=True)
                    ins = nc.tensor.matmul(bank[2 * i + qt][:, SEQ:KEYS], lhs, mkt[rows, :], start=True, stop=True)
                ins.then_inc(scored, 1)

            def turn(u, i, first):
                pe.wait_ge(exp_ready, u + 1)
                if not first:
                    pe.wait_ge(et_lo_ready, QT * u)
                for qt in range(QT):
                    for kt in range(KT):
                        ins = nc.tensor.transpose(turn_bank[qt][:, kt * P:(kt + 1) * P],
                                                  e[i][:, qt, kt * P:(kt + 1) * P], g.ident[:])
                ins.then_inc(turned, 1)

            def values(u, p, b, h, i, first):
                pe.wait_ge(et_lo_ready, QT * u + QT)
                if not first:
                    pe.wait_ge(o_ready, u)
                for qt in range(QT):
                    for kt in range(KT):
                        tile = QT * b + kt if kt < QT else TILES
                        cols, head = slice(kt * P, (kt + 1) * P), ds((tile * HEADS + h) * VW + p * (2 * VW), VW)
                        for n, (probs, vals) in enumerate(((et_hi, v_hi_flat), (et_lo, v_hi_flat), (et_hi, v_lo_flat))):
                            ins = nc.tensor.matmul(o_bank[:, qt * VW:(qt + 1) * VW], probs[i][:, qt, cols],
                                                   vals[:, head], start=(kt == 0 and n == 0),
                                                   stop=(kt == KT - 1 and n == 2))
                ins.then_inc(pv_done, 1)

            def pair_steps(p, first, more):
                pe.wait_ge(mkt_ready, p + 1)
                for j in range(UNITS):
                    b, h = j // 2, j % 2
                    u = UNITS * p + j
                    pe.wait_ge(qk_ready, BATCH * p + b + 1)
                    scores(u, b, h, j % 2, first and j < 2)
                    if h == 1 and more:
                        project(p + 1, b)
                    if not (first and j < 1):
                        turn(u - 1, (j - 1) % 2, first and j == 1)
                    if not (first and j < 2):
                        jj = (j - 2) % UNITS
                        values(u - 2, p if j >= 2 else p - 1, jj // 2, jj % 2, j % 2, first and j == 2)

            for b in range(BATCH):
                project(0, b, b == 0)
            pe.wait_ge(v_ready, 2 * TILES + 1)
            pe.wait_ge(v_ones, 2)
            pair_steps(0, True, True)
            with pe.Fori(1, PAIRS - 1) as p:
                pair_steps(p, False, True)
            pair_steps(PAIRS - 1, False, False)
            last = PAIRS * UNITS
            turn(last - 1, 1, False)
            values(last - 2, PAIRS - 1, BATCH - 1, 0, 0, False)
            values(last - 1, PAIRS - 1, BATCH - 1, 1, 1, False)

            for t in range(TILES):
                i = t % 2
                pe.wait_ge(on_ready, t + 1)
                for c in range(PAIRS):
                    ins = nc.tensor.transpose(bank[2 * i + c // 4][:, (c % 4) * P:(c % 4 + 1) * P],
                                              on[i][:, 2 * c:2 * c + 2, :].rearrange("p h d -> p (h d)"), g.ident[:])
                ins.then_inc(on_turned, 1)
                if t:
                    output_product(nc, pe, ont_ready, y_ready, y_psum, t - 1, bank[4 + (t - 1) % 2],
                                   ont[(t - 1) % 2], wo, g.ones_row, bo)
            output_product(nc, pe, ont_ready, y_ready, y_psum, TILES - 1, bank[4 + 1], ont[1], wo, g.ones_row, bo)

        @block.scalar
        def _(act):
            act.wait_ge(xt_psum, 1)
            nc.scalar.copy(g.xt[:, 0:BANK], bank[4]).then_inc(xt_ready, 1)
            for h in range(2):
                act.wait_ge(mk_psum, h + 1)
                nc.scalar.copy(mkt_all[:, 4 * h:4 * h + 4, :].rearrange("p c m -> p (c m)"), bank[6 + h])\
                    .then_inc(mk_ready, 1)

            for n in range(2 * TILES):
                act.wait_ge(v_rows_ready, n + 1)
                nc.scalar.copy(v_hi[:, n // 2, 8 * (n % 2):8 * (n % 2) + 8, 0:DK], v_rows[:, n % 4])\
                    .then_inc(v_hi_ready, 1)
            nc.scalar.copy(v_hi[:, TILES, :, 0:DK], mv[:]).then_inc(v_hi_ready, 1)

            def exps(u, i, first):
                act.wait_ge(max_ready, u + 1)
                if not first:
                    act.wait_ge(turned, u - 1)
                for qt in range(QT):
                    ins = nc.scalar.activation(e[i][:, qt, :], score_bank[i][:, qt, :], ACT.Exp,
                                               bias=negmax[i][:, qt:qt + 1])
                ins.then_inc(exp_ready, 1)

            def split_high(u, i, first):
                act.wait_ge(turned, u + 1)
                if not first:
                    act.wait_ge(pv_done, u - 1)
                for qt in range(QT):
                    nc.scalar.copy(et_hi[i][:, qt, :], turn_bank[qt][:, 0:KEYS]).then_inc(et_hi_ready, 1)

            def pair_steps(p, first):
                for j in range(UNITS):
                    u = UNITS * p + j
                    if not (first and j < 1):
                        split_high(u - 1, (j - 1) % 2, first and j < 3)
                    exps(u, j % 2, first and j < 2)

            pair_steps(0, True)
            with act.Fori(1, PAIRS) as p:
                pair_steps(p, False)
            split_high(PAIRS * UNITS - 1, 1, False)
            for t in range(TILES):
                act.wait_ge(on_turned, t + 1)
                if t >= 2:
                    act.wait_ge(y_psum, t - 1)
                nc.scalar.copy(ont[t % 2][:].rearrange("p (h c) m -> p h (c m)", h=2),
                               g.psum[:, 2 * (t % 2):2 * (t % 2) + 2, :]).then_inc(ont_ready, 1)
            norm_root(nc, act, nb, 1)

        @block.vector
        def _(dve):
            steps = Tally(dve, dve_steps)
            dve.wait_ge(xt_psum, 2)
            nc.vector.tensor_copy(g.xt[:, BANK:], bank[5]).then_inc(xt_ready, 1)
            dve.wait_ge(loaded, 128)
            for t in range(TILES):
                for h in range(2):
                    n = 2 * t + h
                    dve.wait_ge(v_psum, n + 1)
                    if n >= 4:
                        dve.wait_ge(v_ready, n - 3)
                    nc.vector.tensor_tensor(v_rows[:, n % 4],
                                            bank[n % 4].rearrange("p (h d) -> p h d", h=8),
                                            bv[:, h * BANK:(h + 1) * BANK].rearrange("p (h d) -> p h d", h=8),
                                            ALU.add).then_inc(v_rows_ready, 1)

            def copy_projected(n, p, b):
                dve.wait_ge(projected, n + 1)
                nc.vector.tensor_scalar(q[:, b, :], proj_bank[:, 0:SEQ], bqk[:, 0, ds(p, 1)], DK ** -0.5,
                                        ALU.add, ALU.mult)
                nc.vector.tensor_scalar(k[:, b, :], proj_bank[:, SEQ:], bqk[:, 1, ds(p, 1)], None, ALU.add)\
                    .then_inc(qk_ready, 1)

            def copy_memory_keys(p):
                nc.vector.tensor_copy(mkt[:], mkt_all[:, ds(p, 1), :].rearrange("p o m -> p (o m)"))\
                    .then_inc(mkt_ready, 1)

            def maxima(u, i):
                dve.wait_ge(scored, u + 1)
                nc.vector.tensor_reduce(negmax[i][:], score_bank[i], AX.X, ALU.max, negate=True)\
                    .then_inc(max_ready, 1)

            def split_low(u, i):
                for qt in range(QT):
                    dve.wait_ge(et_hi_ready, QT * u + qt + 1)
                    nc.vector.tensor_tensor(et_lo[i][:, qt, :], turn_bank[qt][:, 0:KEYS], et_hi[i][:, qt, :],
                                            ALU.subtract).then_inc(et_lo_ready, 1)

            def copy_out(u, p, b, h):
                dve.wait_ge(pv_done, u + 1)
                nc.vector.tensor_copy(o_heads[:, QT * b:QT * b + QT, ds(h * VW + p * (2 * VW), VW)],
                                      o_bank[:, 0:QT * VW].rearrange("p (q w) -> p q w", q=QT))\
                    .then_inc(o_ready, 1)

            def pair_steps(p, first, more):
                for j in range(UNITS):
                    u = UNITS * p + j
                    maxima(u, j % 2)
                    if j % 2 == 1 and more:
                        copy_projected(BATCH * p + BATCH + j // 2, p + 1, j // 2)
                    if j == UNITS - 1 and more:
                        copy_memory_keys(p + 1)
                    if not (first and j < 1):
                        split_low(u - 1, (j - 1) % 2)
                    if not (first and j < 2):
                        jj = (j - 2) % UNITS
                        copy_out(u - 2, p if j >= 2 else p - 1, jj // 2, jj % 2)

            dve.wait_ge(mk_ready, 2)
            copy_memory_keys(0)
            for b in range(BATCH):
                copy_projected(b, 0, b)
            pair_steps(0, True, True)
            with dve.Fori(1, PAIRS - 1) as p:
                pair_steps(p, False, True)
            pair_steps(PAIRS - 1, False, False)
            last = PAIRS * UNITS
            split_low(last - 1, 1)
            copy_out(last - 2, PAIRS - 1, BATCH - 1, 0)
            copy_out(last - 1, PAIRS - 1, BATCH - 1, 1)
            dve.wait_ge(o_ready, last)
            for t in range(TILES):
                if t >= 2:
                    dve.wait_ge(on_turned, t - 1)
                steps.step(nc.vector.reciprocal(rsum[t % 2][:], o[:, t, :, DK]))
                nc.vector.tensor_tensor(on[t % 2][:], o[:, t, :, 0:DK],
                                        rsum[t % 2][:].unsqueeze(2).broadcast_to([P, HEADS, DK]), ALU.mult)\
                    .then_inc(on_ready, 1)
                if t:
                    add_residual(nc, dve, y_psum, y_ready, steps, t - 1, bank[4 + (t - 1) % 2], rsd, g.x)
            add_residual(nc, dve, y_psum, y_ready, steps, TILES - 1, bank[5], rsd, g.x)
            steps.settle()
            norm_stats(nc, steps, nb, rsd)
            norm_scale(nc, dve, steps, nb, 1)
            norm_apply(nc, steps, nb, rsd, g.x)


def output_product(nc, pe, ont_ready, y_ready, y_psum, t, y, cols, w, ones_row, bias_row):
    pe.wait_ge(ont_ready, t + 1)
    if t >= 2:
        pe.wait_ge(y_ready, t - 1)
    for c in range(w.shape[1]):
        nc.tensor.matmul(y[:, 0:D], cols[:, c, :], w[:, c, :], start=(c == 0), stop=False)
    nc.tensor.matmul(y[:, 0:D], ones_row[:], bias_row[:], start=False, stop=True).then_inc(y_psum, 1)


def add_residual(nc, dve, y_psum, y_ready, steps, t, y, rows, x):
    dve.wait_ge(y_psum, t + 1)
    nc.vector.tensor_tensor(rows[:, t, :], y[:, 0:D], x[:, t, :], ALU.add).then_inc(y_ready, 1)
    steps.engine.wait_ge(y_ready, t + 1)


FHEADS, FD = 16, 8
EXPERTS = 8
HALVES = TILES // BATCH


def expert_block(nc, g, a):
    with ExitStack() as ctx:
        r = Resources(nc, ctx, g.sems, "ffn")
        w_in = r.sb("w_qkv", [P, 3 * D])
        b_in = r.sb("b_qkv", [P, 3 * D])
        w_out = r.sb("w_out", [P, 1, D])
        b_out = r.sb("b_out", [1, D])
        gain = r.sb("norm_gains", [P, 4, D])
        w_route = r.sb("w_route", [P, EXPERTS])
        b_route = r.sb("b_route", [1, EXPERTS])
        w1 = [r.sb(f"w1_expert{i}", [P, D]) for i in range(2)]
        w2 = r.sb("w2_all", [P, EXPERTS, D])
        w2_flat = w2[:].rearrange("p e n -> p (e n)")
        b1 = r.sb("b1_cols", [P, EXPERTS])
        b2 = r.sb("b2_rows", [EXPERTS, D])
        number = r.sb("expert_number", [P, EXPERTS])
        pick = r.sb("pick_expert", [EXPERTS, EXPERTS, P], BF16)
        pick_flat = pick[:].rearrange("k e p -> k (e p)")
        qkv = r.sb("qkv", [P, TILES, 3 * D])
        prod = [r.sb(f"products{i}", [P, BATCH, D]) for i in range(2)]
        sc = r.sb("batch_scores", [P, HALVES, BATCH, BATCH, FHEADS])
        sc_rows = sc[:].rearrange("p a t s h -> p (a t) s h")
        peak = r.sb("batch_peak", [P, TILES, FHEADS])
        total = r.sb("batch_total", [P, TILES, FHEADS])
        mixed = r.sb("mixed", [P, TILES, D])
        mixed_cols = r.sb("mixed_cols", [P, TILES, 1, P])
        rsd = r.sb("ffn_rows", [P, TILES, D])
        h = r.sb("h_rows", [P, TILES, D])
        ht = r.sb("h_cols", [P, TOK])
        logit = r.sb("logits", [P, TILES, EXPERTS])
        lmax = r.sb("logit_max", [P, TILES])
        lsum = r.sb("logit_sum", [P, TILES])
        best = r.sb("best_probs", [P, TILES, 8])
        place = r.sb("best_places", [P, TILES, 8], U32)
        placef = r.sb("best_places_f", [P, TILES, 2])
        chosen = r.sb("chosen", [P, TILES])
        mask = r.sb("chosen_mask", [P, TILES, EXPERTS])
        maskt = r.sb("mask_cols", [EXPERTS, TOK])
        maskt_b = r.sb("mask_cols_b", [EXPERTS, TOK], BF16)
        he = [r.sb(f"hidden{i}", [P, TOK]) for i in range(2)]
        hem = [r.sb(f"hidden_masked{i}", [P, TOK]) for i in range(2)]
        nb = NormBuffers(r, "ffn_norm")
        loaded, const_done, xt_psum, xt_ready, qkv_psum, qkv_ready = (r.sem(n) for n in (
            "loaded", "const_done", "xt_psum", "xt_ready", "qkv_psum", "qkv_ready"))
        sub_ready, exp_ready, mixed_ready, mixed_psum, ont_ready, y_psum = (r.sem(n) for n in (
            "sub_ready", "exp_ready", "mixed_ready", "mixed_psum", "ont_ready", "y_psum"))
        y_ready, h_ready, ht_psum, ht_ready, logit_psum, lsub_ready = (r.sem(n) for n in (
            "y_ready", "h_ready", "ht_psum", "ht_ready", "logit_psum", "lsub_ready"))
        lexp_ready, mask_ready, maskt_psum, maskt_ready, he_psum, mask_bc = (r.sem(n) for n in (
            "lexp_ready", "mask_ready", "maskt_psum", "maskt_ready", "he_psum", "mask_bc"))
        he_ready, hem_ready, w2_done, dve_steps, pool_steps = (r.sem(n) for n in (
            "he_ready", "hem_ready", "w2_done", "dve_steps", "pool_steps"))
        expert_w1_loaded = [r.sem(f"expert_w1_loaded{i}") for i in range(2)]
        bank = [g.psum[:, i, :] for i in range(8)]
        pair = [g.psum[:, 2 * i:2 * i + 2, :] for i in range(4)]
        block = ctx.enter_context(nc.Block())

        @block.sync
        def _(sp):
            row = lambda v: v.rearrange("(o n) -> o n", o=1)
            every = lambda v, n: row(v).broadcast_to([P, n])
            for dst, src in ((w_in[:], a["L0_ffn_in_proj_w"]), (b_in[:], every(a["L0_ffn_in_proj_b"], 3 * D)),
                             (w_out[:, 0, :], a["L0_ffn_out_w"]), (b_out[:], row(a["L0_ffn_out_b"])),
                             (gain[:, 0, :], every(a["L0_ffn_ln1_g"], D)), (gain[:, 1, :], every(a["L0_ffn_ln1_b"], D)),
                             (gain[:, 2, :], every(a["L0_ffn_ln2_g"], D)), (gain[:, 3, :], every(a["L0_ffn_ln2_b"], D)),
                             (w_route[:], a["L0_ffn_router_w"]), (b_route[:], row(a["L0_ffn_router_b"])),
                             (w2[:], a["L0_ffn_w2"]), (b1[:], a["L0_ffn_b1"]), (b2[:], a["L0_ffn_b2"])):
                sp.dma_start(dst, src).then_inc(loaded, 16)

            def load_expert(e, k):
                sp.dma_start(w1[k][:], a["L0_ffn_w1"].rearrange("c e h -> c (e h)")[:, ds(e * D, D)])\
                    .then_inc(expert_w1_loaded[k], 16)

            for k in range(2):
                load_expert(k, k)
            with sp.Fori(1, EXPERTS // 2) as i:
                for k in range(2):
                    sp.wait_ge(he_psum, 2 * i + k - 1)
                    load_expert(2 * i + k, k)

        LOADS = 13 * 16

        @block.gpsimd
        def _(pool):
            steps = Tally(pool, pool_steps)
            for e in range(EXPERTS):
                nc.gpsimd.memset(number[:, e:e + 1], float(e))
            steps.step(nc.gpsimd.memset(pick[:], 0.0))
            nc.gpsimd.affine_select(out=pick[:], in_=pick[:], compare_op=ALU.not_equal, fill=1.0, base=0,
                                    pattern=[[-1, EXPERTS], [0, P]], channel_multiplier=1).then_inc(const_done, 1)

        @block.tensor
        def _(pe):
            transpose_rows(nc, pe, g.x, None, g.ident[:], bank[6:8], xt_psum)
            pe.wait_ge(loaded, LOADS)
            pe.wait_ge(xt_ready, 2)
            for t in range(TILES):
                if t >= 4:
                    pe.wait_ge(qkv_ready, t - 3)
                nc.tensor.matmul(bank[t % 4][:, 0:3 * D], g.xt[:, t * P:(t + 1) * P], w_in[:], start=True, stop=True)\
                    .then_inc(qkv_psum, 1)
            pe.wait_ge(qkv_ready, TILES)
            pe.wait_ge(mixed_ready, TILES)
            transpose_rows(nc, pe, mixed, None, g.ident[:], bank[4:6], mixed_psum)
            pe.wait_ge(ont_ready, 1)
            for t in range(TILES):
                y = bank[t // 4][:, (t % 4) * D:(t % 4 + 1) * D]
                nc.tensor.matmul(y, mixed_cols[:, t, 0, :], w_out[:, 0, :], start=True, stop=False)
                ins = nc.tensor.matmul(y, g.ones_row[:], b_out[:], start=False, stop=True)
            ins.then_inc(y_psum, 1)
            pe.wait_ge(h_ready, 1)
            transpose_rows(nc, pe, h, None, g.ident[:], bank[4:6], ht_psum)
            pe.wait_ge(ht_ready, 2)
            for t in range(TILES):
                y = bank[2][:, t * EXPERTS:(t + 1) * EXPERTS]
                nc.tensor.matmul(y, ht[:, t * P:(t + 1) * P], w_route[:], start=True, stop=False)
                ins = nc.tensor.matmul(y, g.ones_row[:], b_route[:], start=False, stop=True)
            ins.then_inc(logit_psum, 1)
            pe.wait_ge(mask_ready, 1)
            for t in range(TILES):
                ins = nc.tensor.transpose(bank[2 + t // 4][0:EXPERTS, (t % 4) * P:(t % 4 + 1) * P],
                                          mask[:, t, :], g.ident[:])
            ins.then_inc(maskt_psum, 1)
            pe.wait_ge(maskt_ready, 1)
            pe.wait_ge(const_done, 1)
            for t in range(TILES):
                nc.tensor.matmul(bank[6 + t // 4][:, (t % 4) * D:(t % 4 + 1) * D], maskt[:, t * P:(t + 1) * P], b2[:],
                                 start=(t % 4 == 0), stop=False, skip_group_check=True)

            def hidden(i, k, first):
                e = 2 * i + k
                pe.wait_ge(expert_w1_loaded[k], 16 * i + 16)
                if not first:
                    pe.wait_ge(he_ready, e - 1)
                for j in range(2):
                    ins = nc.tensor.matmul(bank[2 * k + j], w1[k][:], ht[:, j * BANK:(j + 1) * BANK],
                                           start=True, stop=True)
                ins.then_inc(he_psum, 1)

            def spread_mask(e, first):
                if not first:
                    pe.wait_ge(hem_ready, e)
                for j in range(2):
                    ins = nc.tensor.matmul(bank[4 + j], pick_flat[:, ds(e * P, P)],
                                           maskt_b[:, j * BANK:(j + 1) * BANK], start=True, stop=True)
                ins.then_inc(mask_bc, 1)

            def outputs(e, k, last=False):
                pe.wait_ge(hem_ready, e + 1)
                for t in range(TILES):
                    ins = nc.tensor.matmul(bank[6 + t // 4][:, (t % 4) * D:(t % 4 + 1) * D],
                                           hem[k][:, t * P:(t + 1) * P], w2_flat[:, ds(e * D, D)],
                                           start=False, stop=last, skip_group_check=True)
                ins.then_inc(w2_done, 1)

            hidden(0, 0, True)
            spread_mask(0, True)
            hidden(0, 1, True)
            outputs(0, 0)
            spread_mask(1, False)
            with pe.Fori(1, EXPERTS // 2) as i:
                for k in range(2):
                    e = 2 * i + k
                    hidden(i, k, False)
                    outputs(e - 1, 1 - k)
                    spread_mask(e, False)
            outputs(EXPERTS - 1, 1, True)

        @block.scalar
        def _(act):
            act.wait_ge(xt_psum, 1)
            nc.scalar.copy(g.xt[:, 0:BANK], bank[6]).then_inc(xt_ready, 1)
            act.wait_ge(sub_ready, 1)
            nc.scalar.activation(sc[:], sc[:], ACT.Exp, scale=FD ** -0.5).then_inc(exp_ready, 1)
            act.wait_ge(mixed_psum, 2)
            nc.scalar.copy(mixed_cols[:].rearrange("p (h t) o c -> p h (t o c)", h=2), pair[2])\
                .then_inc(ont_ready, 1)
            norm_root(nc, act, nb, 1)
            act.wait_ge(ht_psum, 1)
            nc.scalar.copy(ht[:, 0:BANK], bank[4]).then_inc(ht_ready, 1)
            act.wait_ge(lsub_ready, 1)
            nc.scalar.activation(logit[:], logit[:], ACT.Exp).then_inc(lexp_ready, 1)

            def gelus(e, k, first):
                act.wait_ge(he_psum, e + 1)
                if not first:
                    act.wait_ge(hem_ready, e - 1)
                nc.scalar.activation(halves(he[k][:]), pair[k], ACT.Gelu, bias=b1[:, ds(e, 1)]).then_inc(he_ready, 1)

            for k in range(2):
                gelus(k, k, True)
            with act.Fori(1, EXPERTS // 2) as i:
                for k in range(2):
                    gelus(2 * i + k, k, False)
            norm_root(nc, act, nb, 2)
            norm_root(nc, act, nb, 3)

        @block.vector
        def _(dve):
            steps = Tally(dve, dve_steps)
            dve.wait_ge(xt_psum, 2)
            nc.vector.tensor_copy(g.xt[:, BANK:], bank[7]).then_inc(xt_ready, 1)
            dve.wait_ge(loaded, LOADS)
            for t in range(TILES):
                dve.wait_ge(qkv_psum, t + 1)
                nc.vector.tensor_tensor(qkv[:, t, :], bank[t % 4][:, 0:3 * D], b_in[:], ALU.add).then_inc(qkv_ready, 1)
            dve.wait_ge(qkv_ready, TILES)
            for half in range(HALVES):
                for t in range(BATCH):
                    n = BATCH * half + t
                    p = prod[n % 2]
                    steps.step(nc.vector.tensor_tensor(
                        p[:], qkv[:, HALVES * t + half, 0:D].unsqueeze(1).broadcast_to([P, BATCH, D]),
                        qkv[:, half::HALVES, D:2 * D], ALU.mult))
                    steps.add(nc.vector.tensor_reduce(sc[:, half, t, :, :].rearrange("p s h -> p (s h)"),
                                                      p[:].rearrange("p s (h d) -> p (s h) d", d=FD), AX.X, ALU.add))
            steps.settle()
            steps.step(nc.vector.tensor_reduce(peak[:], sc_rows.rearrange("p a s h -> p a h s"), AX.X, ALU.max))
            bc = lambda z: z[:].unsqueeze(2).broadcast_to([P, TILES, BATCH, FHEADS])
            nc.vector.tensor_tensor(sc_rows, sc_rows, bc(peak), ALU.subtract).then_inc(sub_ready, 1)
            dve.wait_ge(exp_ready, 1)
            steps.step(nc.vector.tensor_reduce(total[:], sc_rows.rearrange("p a s h -> p a h s"), AX.X, ALU.add))
            steps.step(nc.vector.reciprocal(peak[:], total[:]))
            steps.step(nc.vector.tensor_tensor(sc_rows, sc_rows, bc(peak), ALU.mult))
            for half in range(HALVES):
                for t in range(BATCH):
                    n = BATCH * half + t
                    p = prod[n % 2]
                    steps.step(nc.vector.tensor_tensor(
                        p[:].rearrange("p s (h d) -> p s h d", d=FD),
                        sc[:, half, t, :, :].unsqueeze(3).broadcast_to([P, BATCH, FHEADS, FD]),
                        qkv[:, half::HALVES, 2 * D:3 * D].rearrange("p s (h d) -> p s h d", d=FD), ALU.mult))
                    nc.vector.tensor_reduce(mixed[:, HALVES * t + half, :], p[:].rearrange("p s c -> p c s"),
                                            AX.X, ALU.add).then_inc(mixed_ready, 1)
                    dve.wait_ge(mixed_ready, n + 1)
            dve.wait_ge(y_psum, 1)
            eights = lambda z: z.rearrange("p (h t) c -> p h (t c)", h=2)
            steps.step(nc.vector.tensor_tensor(eights(rsd[:]), eights(g.x[:]), pair[0], ALU.add))
            norm_stats(nc, steps, nb, rsd)
            norm_scale(nc, dve, steps, nb, 1)
            norm_apply(nc, steps, nb, rsd, h)
            all_rows = lambda j: gain[:, j, :].unsqueeze(1).broadcast_to([P, TILES, D])
            steps.step(nc.vector.tensor_tensor(h[:], h[:], all_rows(0), ALU.mult))
            nc.vector.tensor_tensor(h[:], h[:], all_rows(1), ALU.add).then_inc(h_ready, 1)
            dve.wait_ge(ht_psum, 2)
            nc.vector.tensor_copy(ht[:, BANK:], bank[5]).then_inc(ht_ready, 1)
            dve.wait_ge(logit_psum, 1)
            steps.step(nc.vector.tensor_copy(logit[:].rearrange("p t e -> p (t e)"), bank[2][:, 0:TILES * EXPERTS]))
            steps.step(nc.vector.tensor_reduce(lmax[:], logit[:], AX.X, ALU.max))
            bce = lambda z: z[:].unsqueeze(2).broadcast_to([P, TILES, EXPERTS])
            nc.vector.tensor_tensor(logit[:], logit[:], bce(lmax), ALU.subtract).then_inc(lsub_ready, 1)
            dve.wait_ge(lexp_ready, 1)
            steps.step(nc.vector.tensor_reduce(lsum[:], logit[:], AX.X, ALU.add))
            steps.step(nc.vector.reciprocal(lmax[:], lsum[:]))
            steps.step(nc.vector.tensor_tensor(logit[:], logit[:], bce(lmax), ALU.mult))
            for t in range(TILES):
                steps.add(nc.vector.max(best[:, t, :], logit[:, t, :]))
            steps.settle()
            for t in range(TILES):
                steps.add(nc.vector.max_index(place[:, t, :], best[:, t, :], logit[:, t, :]))
            steps.settle()
            steps.step(nc.vector.tensor_copy(placef[:], place[:, :, 0:2]))
            steps.step(nc.vector.tensor_tensor(chosen[:], placef[:, :, 0], placef[:, :, 1], ALU.max))
            dve.wait_ge(const_done, 1)
            nc.vector.tensor_tensor(mask[:], bce(chosen), number[:].unsqueeze(1).broadcast_to([P, TILES, EXPERTS]),
                                    ALU.is_equal).then_inc(mask_ready, 1)
            dve.wait_ge(maskt_psum, 1)
            steps.step(nc.vector.tensor_copy(halves(maskt[:]), pair[1][0:EXPERTS]))
            nc.vector.tensor_copy(maskt_b[:], maskt[:]).then_inc(maskt_ready, 1)

            def masked(e, k, first):
                dve.wait_ge(he_ready, e + 1)
                dve.wait_ge(mask_bc, e + 1)
                if not first:
                    dve.wait_ge(w2_done, e - 1)
                nc.vector.tensor_tensor(halves(hem[k][:]), halves(he[k][:]), pair[2], ALU.mult).then_inc(hem_ready, 1)

            for k in range(2):
                masked(k, k, True)
            with dve.Fori(1, EXPERTS // 2) as i:
                for k in range(2):
                    masked(2 * i + k, k, False)
            dve.wait_ge(w2_done, EXPERTS)
            steps.step(nc.vector.tensor_tensor(eights(rsd[:]), eights(h[:]), pair[3], ALU.add))
            norm_stats(nc, steps, nb, rsd)
            norm_scale(nc, dve, steps, nb, 2)
            norm_apply(nc, steps, nb, rsd, h)
            steps.step(nc.vector.tensor_tensor(h[:], h[:], all_rows(2), ALU.mult))
            steps.step(nc.vector.tensor_tensor(h[:], h[:], all_rows(3), ALU.add))
            steps.step(nc.vector.tensor_tensor(rsd[:], h[:], g.x[:], ALU.add))
            norm_stats(nc, steps, nb, rsd)
            norm_scale(nc, dve, steps, nb, 3)
            norm_apply(nc, steps, nb, rsd, g.x)


GHEADS, GK = 16, 64
GPAIRS = GHEADS // 2
GW = GK + 1
CK = P + 2 * P
MASKED = -1e30


def graph_attention(nc, g, a):
    with ExitStack() as ctx:
        r = Resources(nc, ctx, g.sems, "graph")
        w_qk = r.sb("g_wqk", [P, 2, GHEADS * GK])
        wv = r.sb("g_wv", [P, GHEADS * GK])
        wo = r.sb("g_wo", [P, GPAIRS, D])
        lin_wo = r.sb("g_lin_wo", [P, GPAIRS, D])
        lin_t = r.sb("lin_t_diag", [P, P])
        lin_b = r.sb("lin_b_col", [P, 1])
        w_g = [r.sb(f"graph_w_diag{l}", [P, P]) for l in range(2)]
        b_g = r.sb("graph_b", [P, 2, GK])
        gamma_in = r.sb("gamma_in", [P, 1])
        gamma_out = r.sb("gamma_out", [P, D])
        const_row = r.sb("lin_b_wo_row", [1, D])
        ident_b = r.sb("identity_b", [P, P], BF16)
        mask = r.sb("causal_mask", [P, P], BF16)
        head_sel = r.sb("head_select", [P, 2])
        xh = r.sb("xh_rows", [P, TILES, D])
        xnt = r.sb("xn_cols", [P, TOK])
        xb = r.sb("xn_cols_batch", [P, SEQ])
        q = r.sb("gq_cols", [P, GPAIRS, SEQ])
        k = r.sb("gk_cols", [P, GPAIRS, SEQ])
        qk = r.sb("gqk_products", [P, GPAIRS, SEQ])
        v = r.sb("g_values", [P, QT, GHEADS, GK])
        v_hi = r.sb("g_values_hi", [P, QT, GHEADS, GW], F16)
        v_lo = r.sb("g_values_lo", [P, QT, GHEADS, GW], F16)
        fb = r.sb("feats_plus_bias", [P, QT, GHEADS, GK])
        e = [r.sb(f"g_probs{i}", [P, 2, CK]) for i in range(2)]
        et_hi = r.sb("g_probs_cols_hi", [P, GHEADS, CK], F16)
        et_lo = r.sb("g_probs_cols_lo", [P, GHEADS, CK], F16)
        negmax = r.sb("g_negmax", [P, QT, GHEADS])
        sdiag = r.sb("diag_scores", [P, QT, GHEADS])
        o = r.sb("g_out_raw", [P, QT, GHEADS, GW])
        rs = r.sb("g_rsum", [P, QT, GHEADS])
        pd = r.sb("diag_probs", [P, QT, GHEADS])
        off = r.sb("one_minus_diag", [P, QT, GHEADS])
        rdeg = r.sb("inv_degree", [P, QT, GHEADS])
        keep, take = r.sb("keep_share", [P, QT, GHEADS]), r.sb("take_share", [P, QT, GHEADS])
        out_n = r.sb("g_out", [P, QT, GHEADS, GK])
        m = r.sb("propagated", [P, QT, GHEADS, GK])
        mt = r.sb("propagated_cols", [P, QT, GPAIRS, P])
        f1 = r.sb("feats1", [P, QT, GHEADS, GK])
        f1_hi = r.sb("feats1_hi", [P, QT, GHEADS, GK], F16)
        f1_lo = r.sb("feats1_lo", [P, QT, GHEADS, GK], F16)
        ot = r.sb("g_out_cols", [P, QT, GPAIRS, P])
        y = r.sb("g_y_rows", [P, TILES, D])
        nb = NormBuffers(r, "graph_norm")
        zeroed, loaded, const_done, lin_psum, lin_ready, xh_ready = (r.sem(n) for n in (
            "zeroed", "loaded", "const_done", "lin_psum", "lin_ready", "xh_ready"))
        xt_psum, xt_ready, xb_ready, v_psum, v_ready, v_ones = (r.sem(n) for n in (
            "xt_psum", "xt_ready", "xb_ready", "v_psum", "v_ready", "v_ones"))
        qk_psum, prod_ready, diag_psum, sdiag_ready = (r.sem(n) for n in (
            "qk_psum", "prod_ready", "diag_psum", "sdiag_ready"))
        scored, max_ready, exp_ready, turned, et_hi_ready, et_lo_ready = (r.sem(n) for n in (
            "scored", "max_ready", "exp_ready", "turned", "et_hi_ready", "et_lo_ready"))
        pv_done, o_ready, dsub_ready, dexp_ready, stats_ready, out_ready = (r.sem(n) for n in (
            "pv_done", "o_ready", "dsub_ready", "dexp_ready", "stats_ready", "out_ready"))
        fb_ready, kept, m_ready, m_turned, mt_ready, h_psum = (r.sem(n) for n in (
            "fb_ready", "kept", "m_ready", "m_turned", "mt_ready", "h_psum"))
        pre_ready, feat_ready, pv1_done, qk_ready, out_turned, ot_ready = (r.sem(n) for n in (
            "pre_ready", "feat_ready", "pv1_done", "qk_ready", "out_turned", "ot_ready"))
        f_turned, ft_ready, y_psum, y_ready, dve_steps = (r.sem(n) for n in (
            "f_turned", "ft_ready", "y_psum", "y_ready", "dve_steps"))
        end_steps, end_steps_v, v_hi_ready, v_lo_ready, f1_lo_ready, taken = (r.sem(n) for n in (
            "end_steps", "end_steps_v", "v_hi_ready", "v_lo_ready", "f1_lo_ready", "taken"))
        bank = [g.psum[:, i, :] for i in range(8)]
        pair = [g.psum[:, 2 * i:2 * i + 2, :] for i in range(4)]
        flat = lambda z, qt: z[:, qt].rearrange("p h d -> p (h d)")
        two = lambda z: z.rearrange("p (h n) -> p h n", h=2)
        spread = lambda z, qt: z[:, qt, :].unsqueeze(2).broadcast_to([P, GHEADS, GK])
        heads = lambda z: z.rearrange("p (h d) -> p h d", d=GK)
        block = ctx.enter_context(nc.Block())

        @block.sync
        def _(sp):
            every = lambda z, n: z.rearrange("(o n) -> o n", o=1).broadcast_to([P, n])
            sp.wait_ge(zeroed, 1)
            for dst, src in ((w_qk[:, 0, :], a["L1_attn_Wq"]), (w_qk[:, 1, :], a["L1_attn_Wk"]), (wv[:], a["L1_attn_Wv"]),
                             (wo[:], a["L1_attn_Wo"].rearrange("(c p) n -> p c n", p=P)),
                             (gamma_in[:], a["L1_attn_gamma_in"]), (gamma_out[:], every(a["L1_attn_gamma_out"], D)),
                             (b_g[:, 0, :], every(a["L1_attn_gnn_b"][0], GK)), (b_g[:, 1, :], every(a["L1_attn_gnn_b"][1], GK))):
                sp.dma_start(dst, src).then_inc(loaded, 16)
            for i in range(2):
                rows = slice(i * GK, (i + 1) * GK)
                sp.dma_start(lin_t[rows, rows], a["L1_attn_lin_w"]).then_inc(loaded, 16)
                sp.dma_start(lin_b[rows, :], a["L1_attn_lin_b"]).then_inc(loaded, 16)
                for l in range(2):
                    sp.dma_start(w_g[l][rows, rows], a["L1_attn_gnn_w"][l]).then_inc(loaded, 16)

        LOADS = 16 * 16
        @block.gpsimd
        def _(pool):
            steps = Tally(pool, end_steps)
            for z in (lin_t, w_g[0]):
                nc.gpsimd.memset(z[:], 0.0)
            nc.gpsimd.memset(w_g[1][:], 0.0).then_inc(zeroed, 1)
            nc.gpsimd.memset(v_hi[:, :, :, GK], 1.0).then_inc(v_ones, 1)
            nc.gpsimd.memset(v_lo[:, :, :, GK], 0.0).then_inc(v_ones, 1)
            steps.add(nc.gpsimd.memset(mask[:], 0.0))
            steps.add(nc.gpsimd.memset(ident_b[:], 0.0))
            steps.step(nc.gpsimd.memset(head_sel[:], 1.0))
            nc.gpsimd.affine_select(out=mask[:], in_=mask[:], compare_op=ALU.is_ge, fill=MASKED, base=0,
                                    pattern=[[-1, P]], channel_multiplier=1).then_inc(const_done, 1)
            nc.gpsimd.affine_select(out=ident_b[:], in_=ident_b[:], compare_op=ALU.not_equal, fill=1.0, base=0,
                                    pattern=[[-1, P]], channel_multiplier=1).then_inc(const_done, 1)
            steps.step(nc.gpsimd.affine_select(out=head_sel[:], in_=head_sel[:], compare_op=ALU.is_ge, fill=0.0,
                                               base=0, pattern=[[-GK, 2]], channel_multiplier=1))
            nc.gpsimd.affine_select(out=head_sel[:], in_=head_sel[:], compare_op=ALU.is_ge, fill=0.0, base=GK - 1,
                                    pattern=[[GK, 2]], channel_multiplier=-1).then_inc(const_done, 1)

            def copy_batch(b):
                nc.gpsimd.tensor_copy(xb[:], xnt[:, ds(b * SEQ, SEQ)]).then_inc(xb_ready, 1)

            def keep_share(f, qt):
                nc.gpsimd.tensor_tensor(m[:, qt], f[:, qt], spread(keep, qt), ALU.mult).then_inc(kept, 1)

            def batch(b, more):
                pool.wait_ge(qk_ready, GPAIRS * b + GPAIRS)
                nc.gpsimd.tensor_tensor(qk[:], q[:], k[:], ALU.mult).then_inc(prod_ready, 1)
                if more:
                    pool.wait_ge(v_psum, 4 * b + 4)
                    copy_batch(b + 1)
                for n in range(4):
                    qt, some = n // 2, slice(8 * (n % 2), 8 * (n % 2) + 8)
                    pool.wait_ge(v_hi_ready, 4 * b + n + 1)
                    nc.gpsimd.tensor_tensor(v_lo[:, qt, some, 0:GK], v[:, qt, some, :], v_hi[:, qt, some, 0:GK],
                                            ALU.subtract).then_inc(v_lo_ready, 1)
                b_all = lambda l: b_g[:, l, :].unsqueeze(1).broadcast_to([P, GHEADS, GK])
                for qt in range(QT):
                    nc.gpsimd.tensor_tensor(fb[:, qt], v[:, qt], b_all(0), ALU.add).then_inc(fb_ready, 1)
                pool.wait_ge(stats_ready, 2 * b + 1)
                for qt in range(QT):
                    keep_share(v, qt)
                for qt in range(QT):
                    pool.wait_ge(m_ready, 4 * b + qt + 1)
                    nc.gpsimd.tensor_tensor(out_n[:, qt], o[:, qt, :, 0:GK], spread(rs, qt), ALU.mult)\
                        .then_inc(out_ready, 1)
                for qt in range(QT):
                    pool.wait_ge(feat_ready, 6 * b + 2 * qt + 1)
                    pool.wait_ge(m_turned, 4 * b + qt + 1)
                    keep_share(f1, qt)
                for qt in range(QT):
                    pool.wait_ge(feat_ready, 6 * b + 2 * qt + 2)
                    nc.gpsimd.tensor_tensor(fb[:, qt], f1[:, qt], b_all(1), ALU.add).then_inc(fb_ready, 1)

            pool.wait_ge(xt_ready, 2)
            copy_batch(0)
            batch(0, True)
            with pool.Fori(1, BATCH - 1) as b:
                batch(b, True)
            batch(BATCH - 1, False)

        @block.tensor
        def _(pe):
            pe.wait_ge(loaded, LOADS)
            for c in range(GPAIRS):
                ins = nc.tensor.matmul(bank[c // 4][:, (c % 4) * D:(c % 4 + 1) * D], lin_t[:], wo[:, c, :],
                                       start=True, stop=True)
            for c in range(GPAIRS):
                ins = nc.tensor.matmul(bank[2][0:1, 0:D], lin_b[:], wo[:, c, :], start=(c == 0), stop=(c == GPAIRS - 1))
            ins.then_inc(lin_psum, 1)
            pe.wait_ge(xh_ready, 1)
            transpose_rows(nc, pe, xh, None, g.ident[:], bank[4:6], xt_psum)
            pe.wait_ge(const_done, 3)
            pe.wait_ge(v_ones, 2)

            def queries_keys(b):
                pe.wait_ge(xb_ready, b + 1)
                for c in range(GPAIRS):
                    if c >= 2:
                        pe.wait_ge(qk_ready, GPAIRS * b + c - 1)
                    for j in range(2):
                        ins = nc.tensor.matmul(bank[4 + c % 2][:, j * SEQ:(j + 1) * SEQ], w_qk[:, j, c * P:(c + 1) * P],
                                               xb[:], start=True, stop=True)
                    ins.then_inc(qk_psum, 1)

            def value_rows(b):
                for n in range(4):
                    qt, half = n // 2, n % 2
                    nc.tensor.matmul(bank[n], xb[:, qt * P:(qt + 1) * P], wv[:, half * BANK:(half + 1) * BANK],
                                     start=True, stop=True).then_inc(v_psum, 1)

            def scores(b, c):
                if c >= 2:
                    pe.wait_ge(exp_ready, GPAIRS * b + c - 1)
                for h in range(2):
                    rows = slice(h * GK, (h + 1) * GK)
                    sb = bank[2 * (c % 2) + h]
                    nc.tensor.matmul(sb[:, 0:P], q[rows, c, 0:P], k[rows, c, 0:P], start=True, stop=False)
                    nc.tensor.matmul(sb[:, 0:P], ident_b[:], mask[:], start=False, stop=True)
                    nc.tensor.matmul(sb[:, P:CK], q[rows, c, P:SEQ], k[rows, c, :], start=True, stop=False)
                    ins = nc.tensor.matmul(sb[:, 2 * P:CK], ident_b[:], mask[:], start=False, stop=True)
                ins.then_inc(scored, 1)

            def turn(b, c):
                pe.wait_ge(exp_ready, GPAIRS * b + c + 1)
                if c >= 1:
                    pe.wait_ge(et_lo_ready, 2 * GPAIRS * b + 2 * c)
                for h in range(2):
                    for j in range(3):
                        ins = nc.tensor.transpose(bank[4 + h][:, j * P:(j + 1) * P], e[c % 2][:, h, j * P:(j + 1) * P],
                                                  g.ident[:])
                ins.then_inc(turned, 1)

            def propagate(dst, head, qt, f_hi, f_lo):
                blocks = ((0, 0),) if qt == 0 else ((1, 0), (2, 1))
                for n, (block_at, kt) in enumerate(blocks):
                    cols = slice(block_at * P, (block_at + 1) * P)
                    for i, (probs, f) in enumerate(((et_hi, f_hi), (et_lo, f_hi), (et_hi, f_lo))):
                        ins = nc.tensor.matmul(dst, probs[:, head, cols], f(kt), start=(n == 0 and i == 0),
                                               stop=(n == len(blocks) - 1 and i == 2))
                return ins

            def values(b, c):
                pe.wait_ge(et_lo_ready, 2 * GPAIRS * b + 2 * c + 2)
                if c >= 1:
                    pe.wait_ge(o_ready, GPAIRS * b + c)
                for h in range(2):
                    head = 2 * c + h
                    for qt in range(QT):
                        ins = propagate(bank[6][:, (2 * qt + h) * GW:(2 * qt + h + 1) * GW], head, qt,
                                        lambda kt: v_hi[:, kt, head, :], lambda kt: v_lo[:, kt, head, :])
                ins.then_inc(pv_done, 1)

            def turn_wide(src, qt, where, done):
                for c in range(GPAIRS):
                    ins = nc.tensor.transpose(bank[2 * where + c // 4][:, (c % 4) * P:(c % 4 + 1) * P],
                                              src[:, qt, 2 * c:2 * c + 2, :].rearrange("p h d -> p (h d)"), g.ident[:])
                ins.then_inc(done, 1)

            def batch(b, first, more):
                if not first:
                    pe.wait_ge(y_ready, 2 * b)
                value_rows(b)
                pe.wait_ge(prod_ready, b + 1)
                for c in range(GPAIRS):
                    for qt in range(QT):
                        ins = nc.tensor.matmul(bank[7][:, (qt * GPAIRS + c) * 2:(qt * GPAIRS + c + 1) * 2],
                                               qk[:, c, qt * P:(qt + 1) * P], head_sel[:], start=True, stop=True)
                ins.then_inc(diag_psum, 1)
                pe.wait_ge(v_lo_ready, 4 * b + 4)
                for c in range(GPAIRS + 2):
                    if c < GPAIRS:
                        scores(b, c)
                    if 1 <= c <= GPAIRS:
                        turn(b, c - 1)
                    if c >= 2:
                        values(b, c - 2)
                if more:
                    queries_keys(b + 1)
                    pe.wait_ge(qk_ready, GPAIRS * b + 2 * GPAIRS)
                pe.wait_ge(o_ready, GPAIRS * b + GPAIRS)
                pe.wait_ge(sdiag_ready, b + 1)
                for l in range(2):
                    for qt in range(QT):
                        pe.wait_ge(m_ready, 4 * b + 2 * l + qt + 1)
                        turn_wide(m, qt, 2 * qt, m_turned)
                    for qt in range(QT):
                        pe.wait_ge(mt_ready, 4 * b + 2 * l + qt + 1)
                        where = 2 * qt + 1
                        for c in range(GPAIRS):
                            ins = nc.tensor.matmul(bank[2 * where + c // 4][:, (c % 4) * P:(c % 4 + 1) * P],
                                                   mt[:, qt, c, :], w_g[l][:], start=True, stop=True)
                        ins.then_inc(h_psum, 1)
                    if l == 0:
                        for qt in range(QT):
                            pe.wait_ge(out_ready, 2 * b + qt + 1)
                            turn_wide(out_n, qt, 2 * qt, out_turned)
                        for qt in range(QT):
                            pe.wait_ge(f1_lo_ready, 2 * b + qt + 1)
                            for head in range(GHEADS):
                                ins = propagate(bank[4 * qt + 2 + head // 8][:, (head % 8) * GK:(head % 8 + 1) * GK],
                                                head, qt, lambda kt: f1_hi[:, kt, head, :],
                                                lambda kt: f1_lo[:, kt, head, :])
                            ins.then_inc(pv1_done, 1)
                        for qt in range(QT):
                            pe.wait_ge(ot_ready, 2 * b + qt + 1)
                for qt in range(QT):
                    pe.wait_ge(pre_ready, 4 * b + 3 + qt)
                    for c in range(GPAIRS):
                        nc.tensor.matmul(bank[4 * qt + 2][:, 0:D], ot[:, qt, c, :], wo[:, c, :], start=(c == 0),
                                         stop=False)
                for qt in range(QT):
                    pe.wait_ge(feat_ready, 6 * b + 5 + qt)
                    turn_wide(m, qt, 2 * qt, f_turned)
                for qt in range(QT):
                    pe.wait_ge(ft_ready, 2 * b + qt + 1)
                    dst = bank[4 * qt + 2][:, 0:D]
                    for c in range(GPAIRS):
                        nc.tensor.matmul(dst, mt[:, qt, c, :], lin_wo[:, c, :], start=False, stop=False)
                    nc.tensor.matmul(dst, g.ones_row[:], const_row[:], start=False, stop=True).then_inc(y_psum, 1)

            pe.wait_ge(xt_ready, 2)
            pe.wait_ge(lin_ready, 1)
            queries_keys(0)
            batch(0, True, True)
            with pe.Fori(1, BATCH - 1) as b:
                batch(b, False, True)
            batch(BATCH - 1, False, False)

        @block.scalar
        def _(act):
            norm_root(nc, act, nb, 1)
            act.wait_ge(loaded, LOADS)
            act.wait_ge(xt_psum, 1)
            nc.scalar.activation(xnt[:, 0:BANK], bank[4], ACT.Copy, scale=gamma_in[:, 0:1]).then_inc(xt_ready, 1)

            def copy_queries_keys(b):
                for c in range(GPAIRS):
                    act.wait_ge(qk_psum, GPAIRS * b + c + 1)
                    nc.scalar.activation(q[:, c, :], bank[4 + c % 2][:, 0:SEQ], ACT.Copy, scale=GK ** -0.5)
                    nc.scalar.copy(k[:, c, :], bank[4 + c % 2][:, SEQ:]).then_inc(qk_ready, 1)

            def copy_cols(dst, qt, done):
                nc.scalar.copy(two(dst[:, qt].rearrange("p c n -> p (c n)")), pair[2 * qt]).then_inc(done, 1)

            def batch(b, more):
                for n in range(4):
                    qt, some = n // 2, slice(8 * (n % 2), 8 * (n % 2) + 8)
                    act.wait_ge(v_ready, 4 * b + n + 1)
                    nc.scalar.copy(v_hi[:, qt, some, 0:GK], v[:, qt, some, :]).then_inc(v_hi_ready, 1)
                for c in range(GPAIRS + 1):
                    if c >= 1:
                        act.wait_ge(turned, GPAIRS * b + c)
                        for h in range(2):
                            nc.scalar.copy(et_hi[:, 2 * c - 2 + h, :], bank[4 + h][:, 0:CK]).then_inc(et_hi_ready, 1)
                    if c < GPAIRS:
                        act.wait_ge(max_ready, GPAIRS * b + c + 1)
                        if c >= 2:
                            act.wait_ge(turned, GPAIRS * b + c - 1)
                        for h in range(2):
                            for lo, hi, qt in ((0, P, 0), (P, CK, 1)):
                                ins = nc.scalar.activation(e[c % 2][:, h, lo:hi], bank[2 * (c % 2) + h][:, lo:hi],
                                                           ACT.Exp, bias=negmax[:, qt, 2 * c + h:2 * c + h + 1])
                        ins.then_inc(exp_ready, 1)
                act.wait_ge(dsub_ready, b + 1)
                nc.scalar.activation(pd[:], pd[:], ACT.Exp).then_inc(dexp_ready, 1)
                if more:
                    copy_queries_keys(b + 1)
                for l in range(2):
                    for qt in range(QT):
                        act.wait_ge(m_turned, 4 * b + 2 * l + qt + 1)
                        copy_cols(mt, qt, mt_ready)
                    for qt in range(QT):
                        act.wait_ge(pre_ready, 4 * b + 2 * l + qt + 1)
                        for dst in ((f1, f1_hi) if l == 0 else (m, )):
                            nc.scalar.activation(dst[:, qt], fb[:, qt], ACT.Gelu).then_inc(feat_ready, 1)
                    if l == 0:
                        for qt in range(QT):
                            act.wait_ge(out_turned, 2 * b + qt + 1)
                            copy_cols(ot, qt, ot_ready)
                for qt in range(QT):
                    act.wait_ge(f_turned, 2 * b + qt + 1)
                    copy_cols(mt, qt, ft_ready)

            copy_queries_keys(0)
            batch(0, True)
            with act.Fori(1, BATCH - 1) as b:
                batch(b, True)
            batch(BATCH - 1, False)
            norm_root(nc, act, nb, 2)
            norm_root(nc, act, nb, 3)

        DVE_CHAIN = 5

        @block.vector
        def _(dve):
            ends = Tally(dve, end_steps_v)
            norm_stats(nc, ends, nb, g.x)
            norm_scale(nc, dve, ends, nb, 1)
            norm_apply(nc, ends, nb, g.x, xh)
            nc.vector.memset(pd[:], 0.0).then_inc(xh_ready, 1)
            dve.wait_ge(loaded, LOADS)
            dve.wait_ge(xt_psum, 2)
            nc.vector.tensor_scalar(xnt[:, BANK:], bank[5], gamma_in[:, 0:1], None, ALU.mult).then_inc(xt_ready, 1)
            dve.wait_ge(lin_psum, 1)
            nc.vector.tensor_copy(two(lin_wo[:].rearrange("p c n -> p (c n)")), pair[0])
            nc.vector.tensor_copy(const_row[:], bank[2][0:1, 0:D]).then_inc(lin_ready, 1)

            def batch(b, more):
                steps = Tally(dve, dve_steps, DVE_CHAIN * b)
                for n in range(4):
                    qt, half = n // 2, n % 2
                    dve.wait_ge(v_psum, 4 * b + n + 1)
                    nc.vector.tensor_copy(v[:, qt, 8 * half:8 * half + 8, :], heads(bank[n])).then_inc(v_ready, 1)
                dve.wait_ge(diag_psum, b + 1)
                nc.vector.tensor_copy(sdiag[:].rearrange("p q h -> p (q h)"), bank[7][:, 0:2 * GHEADS])\
                    .then_inc(sdiag_ready, 1)
                for c in range(GPAIRS + 2):
                    if c < GPAIRS:
                        dve.wait_ge(scored, GPAIRS * b + c + 1)
                        sb = g.psum[:, 2 * (c % 2):2 * (c % 2) + 2, :]
                        nc.vector.tensor_reduce(negmax[:, 0, 2 * c:2 * c + 2], sb[:, :, 0:P], AX.X, ALU.max, negate=True)
                        nc.vector.tensor_reduce(negmax[:, 1, 2 * c:2 * c + 2], sb[:, :, P:CK], AX.X, ALU.max,
                                                negate=True).then_inc(max_ready, 1)
                    if 1 <= c <= GPAIRS:
                        for h in range(2):
                            dve.wait_ge(et_hi_ready, 2 * GPAIRS * b + 2 * c - 1 + h)
                            nc.vector.tensor_tensor(et_lo[:, 2 * c - 2 + h, :], bank[4 + h][:, 0:CK],
                                                    et_hi[:, 2 * c - 2 + h, :], ALU.subtract).then_inc(et_lo_ready, 1)
                    if c >= 2:
                        dve.wait_ge(pv_done, GPAIRS * b + c - 1)
                        nc.vector.tensor_copy(
                            o[:, :, 2 * c - 4:2 * c - 2, :].rearrange("p q h w -> p q (h w)"),
                            bank[6][:, 0:4 * GW].rearrange("p (q n) -> p q n", q=QT)).then_inc(o_ready, 1)
                    if c == GPAIRS:
                        dve.wait_ge(max_ready, GPAIRS * b + GPAIRS)
                        dve.wait_ge(sdiag_ready, b + 1)
                        nc.vector.tensor_tensor(pd[:], sdiag[:], negmax[:], ALU.add).then_inc(dsub_ready, 1)
                dve.wait_ge(o_ready, GPAIRS * b + GPAIRS)
                steps.step(nc.vector.reciprocal(rs[:], o[:, :, :, GK]))
                dve.wait_ge(dexp_ready, b + 1)
                steps.step(nc.vector.tensor_tensor(pd[:], pd[:], rs[:], ALU.mult))
                steps.add(nc.vector.tensor_scalar(off[:], pd[:], -1.0, 1.0, ALU.mult, ALU.add))
                steps.step(nc.vector.tensor_scalar(rdeg[:], pd[:], -1.0, 2.0, ALU.mult, ALU.add))
                steps.step(nc.vector.reciprocal(rdeg[:], rdeg[:]))
                nc.vector.tensor_tensor(keep[:], off[:], rdeg[:], ALU.mult).then_inc(stats_ready, 1)
                nc.vector.tensor_tensor(take[:], rs[:], rdeg[:], ALU.mult).then_inc(stats_ready, 1)
                dve.wait_ge(stats_ready, 2 * b + 2)
                for l in range(2):
                    for qt in range(QT):
                        if l == 0:
                            dst, src, by = out_n[:, qt], o[:, qt, :, 0:GK], spread(take, qt)
                        else:
                            dve.wait_ge(out_turned, 2 * b + qt + 1)
                            dve.wait_ge(pv1_done, 2 * b + qt + 1)
                            by_bank = lambda z: z.rearrange("p (n h) d -> p n h d", n=2)
                            dst, by = by_bank(out_n[:, qt]), by_bank(spread(take, qt))
                            src = pair[2 * qt + 1].rearrange("p n (h d) -> p n h d", d=GK)
                        nc.vector.tensor_tensor(dst, src, by, ALU.mult).then_inc(taken, 1)
                    for qt in range(QT):
                        dve.wait_ge(taken, 4 * b + 2 * l + qt + 1)
                        dve.wait_ge(kept, 4 * b + 2 * l + qt + 1)
                        nc.vector.tensor_tensor(m[:, qt], m[:, qt], out_n[:, qt], ALU.add).then_inc(m_ready, 1)
                    for qt in range(QT):
                        dve.wait_ge(h_psum, 4 * b + 2 * l + qt + 1)
                        dve.wait_ge(fb_ready, 4 * b + 2 * l + qt + 1)
                        nc.vector.tensor_tensor(two(flat(fb, qt)), two(flat(fb, qt)), pair[2 * qt + 1], ALU.add)\
                            .then_inc(pre_ready, 1)
                    if l == 0:
                        for qt in range(QT):
                            dve.wait_ge(feat_ready, 6 * b + 2 * qt + 2)
                            nc.vector.tensor_tensor(f1_lo[:, qt], f1[:, qt], f1_hi[:, qt], ALU.subtract)\
                                .then_inc(f1_lo_ready, 1)
                for qt in range(QT):
                    dve.wait_ge(y_psum, 2 * b + qt + 1)
                    nc.vector.tensor_copy(y[:, ds(QT * b + qt, 1), :].rearrange("p o c -> p (o c)"),
                                          bank[4 * qt + 2][:, 0:D]).then_inc(y_ready, 1)

            batch(0, True)
            with dve.Fori(1, BATCH - 1) as b:
                batch(b, True)
            batch(BATCH - 1, False)
            dve.wait_ge(y_ready, 2 * BATCH)
            norm_stats(nc, ends, nb, y)
            norm_scale(nc, dve, ends, nb, 2)
            norm_apply(nc, ends, nb, y, xh)
            ends.step(nc.vector.tensor_tensor(xh[:], xh[:], gamma_out[:].unsqueeze(1).broadcast_to([P, TILES, D]),
                                              ALU.mult))
            ends.step(nc.vector.tensor_tensor(xh[:], xh[:], g.x[:], ALU.add))
            norm_stats(nc, ends, nb, xh)
            norm_scale(nc, dve, ends, nb, 3)
            norm_apply(nc, ends, nb, xh, g.x)


NHEADS, NK = 16, 8
NW = NK + 1


def narrow_attention(nc, g, a):
    with ExitStack() as ctx:
        r = Resources(nc, ctx, g.sems, "narrow")
        w = r.sb("n_w", [P, 4, D])
        bqk = r.sb("n_bqk", [P, 2])
        bv = r.sb("n_bv", [P, D])
        bo = r.sb("n_bo", [1, D])
        sel = r.sb("head_rows", [P, NHEADS])
        q = r.sb("nq_cols", [P, TOK])
        k = r.sb("nk_cols", [P, TOK])
        qm = [r.sb(f"nq_head{i}", [P, TOK]) for i in range(2)]
        v = r.sb("n_values", [P, TILES, NHEADS, NW])
        v_flat = v[:].rearrange("p t h w -> p (t h w)")
        e = [r.sb(f"n_probs{i}", [P, QT, SEQ]) for i in range(2)]
        et = [r.sb(f"n_probs_cols{i}", [P, QT, SEQ]) for i in range(2)]
        negmax = [r.sb(f"n_negmax{i}", [P, QT]) for i in range(2)]
        o = r.sb("n_out_raw", [P, TILES, NHEADS, NW])
        o_heads = o[:].rearrange("p t h w -> p t (h w)")
        rsum = r.sb("n_rsum", [P, TILES, NHEADS])
        on = r.sb("n_out", [P, TILES, D])
        ont = r.sb("n_out_cols", [P, TILES, P])
        rsd = r.sb("n_rows", [P, TILES, D])
        nb = NormBuffers(r, "narrow_norm")
        loaded, sel_ready, xt_psum, xt_ready, q_psum, q_ready = (r.sem(n) for n in (
            "loaded", "sel_ready", "xt_psum", "xt_ready", "q_psum", "q_ready"))
        k_ready, v_psum, v_ready, v_ones, qm_ready, scored = (r.sem(n) for n in (
            "k_ready", "v_psum", "v_ready", "v_ones", "qm_ready", "scored"))
        max_ready, exp_ready, turned, et0_ready, et1_ready, pv_done = (r.sem(n) for n in (
            "max_ready", "exp_ready", "turned", "et0_ready", "et1_ready", "pv_done"))
        o_ready, on_ready, on_turned, ont_ready, y_psum, dve_steps = (r.sem(n) for n in (
            "o_ready", "on_ready", "on_turned", "ont_ready", "y_psum", "dve_steps"))
        pool_steps = r.sem("pool_steps")
        bank = [g.psum[:, i, :] for i in range(8)]
        pair = [g.psum[:, 2 * i:2 * i + 2, :] for i in range(4)]
        HUNITS = 2 * BATCH
        block = ctx.enter_context(nc.Block())

        @block.sync
        def _(sp):
            for j, z in enumerate((a["L1_xattn_Wq"], a["L1_xattn_Wk"], a["L1_xattn_Wv"], a["L1_xattn_Wo"])):
                sp.dma_start(w[:, j, :], z).then_inc(loaded, 16)
            sp.dma_start(bqk[:, 0:1], a["L1_xattn_bq"]).then_inc(loaded, 16)
            sp.dma_start(bqk[:, 1:2], a["L1_xattn_bk"]).then_inc(loaded, 16)
            sp.dma_start(bv[:], a["L1_xattn_bv"].rearrange("(o n) -> o n", o=1).broadcast_to([P, D])).then_inc(loaded, 16)
            sp.dma_start(bo[:], a["L1_xattn_bo"].rearrange("(o n) -> o n", o=1)).then_inc(loaded, 16)

        LOADS = 8 * 16

        @block.gpsimd
        def _(pool):
            steps = Tally(pool, pool_steps)
            nc.gpsimd.memset(v[:, :, :, NK], 1.0).then_inc(v_ones, 1)
            steps.step(nc.gpsimd.memset(sel[:], 1.0))
            steps.step(nc.gpsimd.affine_select(out=sel[:], in_=sel[:], compare_op=ALU.is_ge, fill=0.0, base=0,
                                               pattern=[[-NK, NHEADS]], channel_multiplier=1))
            nc.gpsimd.affine_select(out=sel[:], in_=sel[:], compare_op=ALU.is_ge, fill=0.0, base=NK - 1,
                                    pattern=[[NK, NHEADS]], channel_multiplier=-1).then_inc(sel_ready, 1)

        @block.tensor
        def _(pe):
            transpose_rows(nc, pe, g.x, None, g.ident[:], bank[0:2], xt_psum)
            pe.wait_ge(loaded, LOADS)
            for j in range(2):
                nc.tensor.matmul(bank[4 + j], w[:, 1, :], g.ct[:, j * BANK:(j + 1) * BANK], start=True, stop=True)
            for t in range(TILES):
                ins = nc.tensor.matmul(bank[6 + t // 4][:, (t % 4) * D:(t % 4 + 1) * D], g.ct[:, t * P:(t + 1) * P],
                                       w[:, 2, :], start=True, stop=True)
            ins.then_inc(v_psum, 1)
            pe.wait_ge(xt_ready, 2)
            for j in range(2):
                ins = nc.tensor.matmul(bank[2 + j], w[:, 0, :], g.xt[:, j * BANK:(j + 1) * BANK], start=True, stop=True)
            ins.then_inc(q_psum, 1)
            pe.wait_ge(v_ready, 1)
            pe.wait_ge(v_ones, 1)
            pe.wait_ge(k_ready, 1)
            pe.wait_ge(q_ready, 1)

            def scores(u, b, h, i, first):
                if not first:
                    pe.wait_ge(exp_ready, u - 1)
                for qt in range(QT):
                    lo = b * SEQ + qt * P
                    ins = nc.tensor.matmul(bank[i][:, qt * SEQ:(qt + 1) * SEQ], qm[h][:, lo:lo + P],
                                           k[:, b * SEQ:(b + 1) * SEQ], start=True, stop=True)
                ins.then_inc(scored, 1)

            def turn(u, i, first):
                pe.wait_ge(exp_ready, u + 1)
                if not first:
                    pe.wait_ge(et0_ready, u - 1)
                    pe.wait_ge(et1_ready, u - 1)
                for qt in range(QT):
                    for kt in range(2):
                        ins = nc.tensor.transpose(bank[2 + 2 * i + qt][:, kt * P:(kt + 1) * P],
                                                  e[i][:, qt, kt * P:(kt + 1) * P], g.ident[:])
                ins.then_inc(turned, 1)

            def values(u, p, b, h, i, first):
                pe.wait_ge(et0_ready, u + 1)
                pe.wait_ge(et1_ready, u + 1)
                if not first:
                    pe.wait_ge(o_ready, u - 1)
                for qt in range(QT):
                    for kt in range(2):
                        ins = nc.tensor.matmul(bank[6 + i][:, qt * NW:(qt + 1) * NW], et[i][:, qt, kt * P:(kt + 1) * P],
                                               v_flat[:, ds(((QT * b + kt) * NHEADS + h) * NW + p * (2 * NW), NW)],
                                               start=(kt == 0), stop=(kt == 1))
                ins.then_inc(pv_done, 1)

            def pair_steps(p, first):
                for j in range(HUNITS):
                    h, b = j // BATCH, j % BATCH
                    u = HUNITS * p + j
                    if b == 0:
                        pe.wait_ge(qm_ready, 2 * p + h + 1)
                    scores(u, b, h, j % 2, first and j < 2)
                    if not (first and j < 1):
                        turn(u - 1, (j - 1) % 2, first and j < 3)
                    if not (first and j < 2):
                        jj = (j - 2) % HUNITS
                        values(u - 2, p if j >= 2 else p - 1, jj % BATCH, jj // BATCH, j % 2, first and j < 4)

            pair_steps(0, True)
            with pe.Fori(1, NHEADS // 2) as p:
                pair_steps(p, False)
            last = NHEADS // 2 * HUNITS
            turn(last - 1, 1, False)
            values(last - 2, NHEADS // 2 - 1, BATCH - 2, 1, 0, False)
            values(last - 1, NHEADS // 2 - 1, BATCH - 1, 1, 1, False)
            pe.wait_ge(on_ready, 1)
            transpose_rows(nc, pe, on, None, g.ident[:], bank[2:4], on_turned)
            pe.wait_ge(ont_ready, 2)
            for t in range(TILES):
                y = bank[t // 4][:, (t % 4) * D:(t % 4 + 1) * D]
                nc.tensor.matmul(y, ont[:, t, :], w[:, 3, :], start=True, stop=False)
                ins = nc.tensor.matmul(y, g.ones_row[:], bo[:], start=False, stop=True)
            ins.then_inc(y_psum, 1)

        @block.scalar
        def _(act):
            act.wait_ge(xt_psum, 1)
            nc.scalar.copy(g.xt[:, 0:BANK], bank[0]).then_inc(xt_ready, 1)
            act.wait_ge(loaded, LOADS)
            act.wait_ge(v_psum, 1)
            nc.scalar.activation(halves(k[:]), pair[2], ACT.Identity, bias=bqk[:, 1:2]).then_inc(k_ready, 1)

            def step(u, i, skip, first, et_first=False):
                act.wait_ge(max_ready, u + 1)
                if not first:
                    act.wait_ge(turned, u - 1)
                for qt in range(QT):
                    ins = nc.scalar.activation(e[i][:, qt, :], bank[i][:, qt * SEQ:(qt + 1) * SEQ], ACT.Exp,
                                               bias=negmax[i][:, qt:qt + 1])
                ins.then_inc(exp_ready, 1)
                if not skip:
                    copy_turned(u - 1, 1 - i, et_first)

            def copy_turned(u, i, first):
                act.wait_ge(turned, u + 1)
                if not first:
                    act.wait_ge(pv_done, u - 1)
                nc.scalar.copy(et[i][:, 0, :], bank[2 + 2 * i][:, 0:SEQ]).then_inc(et0_ready, 1)

            for j in range(HUNITS):
                step(j, j % 2, j == 0, j < 2, j < 3)
            with act.Fori(1, NHEADS // 2) as p:
                for j in range(HUNITS):
                    step(HUNITS * p + j, j % 2, False, False)
            copy_turned(NHEADS // 2 * HUNITS - 1, 1, False)
            act.wait_ge(on_turned, 1)
            nc.scalar.copy(ont[:, 0:4, :].rearrange("p t c -> p (t c)"), bank[2]).then_inc(ont_ready, 1)
            norm_root(nc, act, nb, 1)

        @block.vector
        def _(dve):
            steps = Tally(dve, dve_steps)
            dve.wait_ge(xt_psum, 2)
            nc.vector.tensor_copy(g.xt[:, BANK:], bank[1]).then_inc(xt_ready, 1)
            dve.wait_ge(loaded, LOADS)
            dve.wait_ge(v_psum, 1)
            for t in range(TILES):
                ins = nc.vector.tensor_tensor(v[:, t, :, 0:NK],
                                              bank[6 + t // 4][:, (t % 4) * D:(t % 4 + 1) * D]
                                              .rearrange("p (h d) -> p h d", d=NK),
                                              bv[:].rearrange("p (h d) -> p h d", d=NK), ALU.add)
            ins.then_inc(v_ready, 1)
            dve.wait_ge(q_psum, 1)
            nc.vector.tensor_scalar(halves(q[:]), pair[1], bqk[:, 0:1], NK ** -0.5, ALU.add, ALU.mult)\
                .then_inc(q_ready, 1)
            dve.wait_ge(q_ready, 1)
            dve.wait_ge(sel_ready, 1)

            def mask_queries(head, i):
                nc.vector.tensor_scalar(qm[i][:], q[:], sel[:, ds(head, 1)], None, ALU.mult).then_inc(qm_ready, 1)

            def maxima(u, i):
                dve.wait_ge(scored, u + 1)
                nc.vector.tensor_reduce(negmax[i][:], bank[i].rearrange("p (q n) -> p q n", q=QT), AX.X, ALU.max,
                                        negate=True).then_inc(max_ready, 1)

            def copy_turned(u, i):
                dve.wait_ge(turned, u + 1)
                nc.vector.tensor_copy(et[i][:, 1, :], bank[3 + 2 * i][:, 0:SEQ]).then_inc(et1_ready, 1)

            def copy_out(u, p, b, h, i):
                dve.wait_ge(pv_done, u + 1)
                nc.vector.tensor_copy(o_heads[:, QT * b:QT * b + QT, ds(h * NW + p * (2 * NW), NW)],
                                      bank[6 + i][:, 0:QT * NW].rearrange("p (q w) -> p q w", q=QT))\
                    .then_inc(o_ready, 1)

            def pair_steps(p, first, more):
                for j in range(HUNITS):
                    h, b = j // BATCH, j % BATCH
                    u = HUNITS * p + j
                    maxima(u, j % 2)
                    if b == BATCH - 1 and more:
                        mask_queries(2 * p + 2 + h, h)
                    if not (first and j < 1):
                        copy_turned(u - 1, (j - 1) % 2)
                    if not (first and j < 2):
                        jj = (j - 2) % HUNITS
                        copy_out(u - 2, p if j >= 2 else p - 1, jj % BATCH, jj // BATCH, j % 2)

            mask_queries(0, 0)
            mask_queries(1, 1)
            pair_steps(0, True, True)
            with dve.Fori(1, NHEADS // 2 - 1) as p:
                pair_steps(p, False, True)
            pair_steps(NHEADS // 2 - 1, False, False)
            last = NHEADS // 2 * HUNITS
            copy_turned(last - 1, 1)
            copy_out(last - 2, NHEADS // 2 - 1, BATCH - 2, 1, 0)
            copy_out(last - 1, NHEADS // 2 - 1, BATCH - 1, 1, 1)
            dve.wait_ge(o_ready, last)
            steps.step(nc.vector.reciprocal(rsum[:], o[:, :, :, NK]))
            nc.vector.tensor_tensor(on[:].rearrange("p t (h d) -> p (t h) d", d=NK),
                                    o[:, :, :, 0:NK].rearrange("p t h d -> p (t h) d"),
                                    rsum[:].rearrange("p t h -> p (t h)").unsqueeze(2)
                                    .broadcast_to([P, TILES * NHEADS, NK]), ALU.mult).then_inc(on_ready, 1)
            dve.wait_ge(on_turned, 2)
            nc.vector.tensor_copy(ont[:, 4:8, :].rearrange("p t c -> p (t c)"), bank[3]).then_inc(ont_ready, 1)
            dve.wait_ge(y_psum, 1)
            eights = lambda z: z.rearrange("p (h t) c -> p h (t c)", h=2)
            steps.step(nc.vector.tensor_tensor(eights(rsd[:]), eights(g.x[:]), pair[0], ALU.add))
            norm_stats(nc, steps, nb, rsd)
            norm_scale(nc, dve, steps, nb, 1)
            norm_apply(nc, steps, nb, rsd, g.x)


HID = 512
CHUNKS = HID // P
MAGIC = 1.5 * 2 ** 23
LEAST = 1e-5


def quantised_ffn(nc, g, a):
    with ExitStack() as ctx:
        r = Resources(nc, ctx, g.sems, "qffn")
        w1 = r.sb("w1_cols", [P, HID])
        w2 = r.sb("w2_cols", [P, HID])
        w2b = r.sb("w2_ternary", [P, HID], BF16)
        taps = r.sb("taps", [P, CHUNKS, 3])
        cb = r.sb("conv_bias", [P, CHUNKS])
        ones = r.sb("all_ones", [P, P])
        ident_b = r.sb("f_identity_b", [P, P], BF16)
        mag = r.sb("weight_magnitude", [P, 2])
        mean = r.sb("weight_mean", [P, 2])
        wscale = r.sb("weight_scale", [P, 2])
        wback = r.sb("weight_back", [P, 2])
        top = r.sb("row_top", [P, TILES])
        scale = r.sb("row_scale", [P, TILES])
        back = r.sb("row_back", [P, TILES])
        xq = r.sb("x_quant", [P, TILES, D])
        xqt = r.sb("x_quant_cols", [P, TOK])
        conv = [r.sb(f"conv{i}", [P, TOK]) for i in range(2)]
        act_cols = r.sb("silu_cols", [P, CHUNKS, TOK])
        top2 = r.sb("row_top2", [P, TILES])
        scale2 = r.sb("row_scale2", [P, TILES])
        back2 = r.sb("row_back2", [P, TILES])
        big = r.sb("rounded", [P, TILES, HID])
        hq = r.sb("hidden_int", [P, TILES, HID], BF16)
        hqt = r.sb("hidden_int_cols", [P, TILES, HID], BF16)
        rsd = r.sb("f_rows", [P, TILES, D])
        nb = NormBuffers(r, "f_norm")
        loaded, const_done, mag_ready, mag_psum, w_ready, xq_ready = (r.sem(n) for n in (
            "loaded", "const_done", "mag_ready", "mag_psum", "w_ready", "xq_ready"))
        xt_psum, xt_ready, h_psum, mid_ready, conv_ready, silu_ready = (r.sem(n) for n in (
            "xt_psum", "xt_ready", "h_psum", "mid_ready", "conv_ready", "silu_ready"))
        g_psum, rounded_ready, hq_ready, hq_psum, hqt_ready, y_psum = (r.sem(n) for n in (
            "g_psum", "rounded_ready", "hq_ready", "hq_psum", "hqt_ready", "y_psum"))
        dve_steps, pool_steps = (r.sem(n) for n in (
            "dve_steps", "pool_steps"))
        bank = [g.psum[:, i, :] for i in range(8)]
        pair = [g.psum[:, 2 * i:2 * i + 2, :] for i in range(4)]
        block = ctx.enter_context(nc.Block())

        @block.sync
        def _(sp):
            for dst, src in ((w1[:], a["L1_ffn_w1"]), (w2[:].rearrange("p (c n) -> p c n", c=CHUNKS), a["L1_ffn_w2"]),
                             (taps[:], a["L1_ffn_conv_w"]), (cb[:], a["L1_ffn_conv_b"])):
                sp.dma_start(dst, src).then_inc(loaded, 16)

        @block.gpsimd
        def _(pool):
            steps = Tally(pool, pool_steps)
            nc.gpsimd.memset(ones[:], 1.0).then_inc(const_done, 1)
            steps.step(nc.gpsimd.memset(ident_b[:], 0.0))
            nc.gpsimd.affine_select(out=ident_b[:], in_=ident_b[:], compare_op=ALU.not_equal, fill=1.0, base=0,
                                    pattern=[[-1, P]], channel_multiplier=1).then_inc(const_done, 1)

        @block.tensor
        def _(pe):
            pe.wait_ge(const_done, 2)
            pe.wait_ge(mag_ready, 1)
            nc.tensor.matmul(bank[7][:, 0:2], ones[:], mag[:], start=True, stop=True).then_inc(mag_psum, 1)
            pe.wait_ge(xq_ready, 1)
            transpose_rows(nc, pe, xq, None, g.ident[:], bank[4:6], xt_psum)
            pe.wait_ge(w_ready, 1)
            pe.wait_ge(xt_ready, 2)
            for c in range(CHUNKS):
                if c >= 2:
                    pe.wait_ge(conv_ready, c - 1)
                for j in range(2):
                    ins = nc.tensor.matmul(bank[2 * (c % 2) + j], w1[:, c * P:(c + 1) * P],
                                           xqt[:, j * BANK:(j + 1) * BANK], start=True, stop=True)
                ins.then_inc(h_psum, 1)
            for grp in range(2):
                if grp:
                    pe.wait_ge(rounded_ready, 1)
                for c in range(CHUNKS):
                    pe.wait_ge(silu_ready, c + 1)
                    if not grp and c == 0:
                        pe.wait_ge(conv_ready, CHUNKS)
                    for t in range(4):
                        lo = (4 * grp + t) * P
                        ins = nc.tensor.transpose(bank[t][:, c * P:(c + 1) * P], act_cols[:, c, lo:lo + P], g.ident[:])
                ins.then_inc(g_psum, 1)
            for grp in range(2):
                pe.wait_ge(hq_ready, grp + 1)
                if grp:
                    pe.wait_ge(hqt_ready, 2)
                for t in range(4):
                    for c in range(CHUNKS):
                        dst = bank[4 + t // 2].bitcast(BF16)[:, (t % 2) * HID + c * P:(t % 2) * HID + (c + 1) * P]
                        ins = nc.tensor.transpose(dst, hq[:, 4 * grp + t, c * P:(c + 1) * P], ident_b[:])
                    if t % 2:
                        ins.then_inc(hq_psum, 1)
            for t in range(TILES):
                pe.wait_ge(hqt_ready, t // 2 + 1)
                for c in range(CHUNKS):
                    ins = nc.tensor.matmul(bank[6 + t // 4][:, (t % 4) * D:(t % 4 + 1) * D],
                                           hqt[:, t, c * P:(c + 1) * P], w2b[:, c * P:(c + 1) * P],
                                           start=(c == 0), stop=(c == CHUNKS - 1))
                if t % 4 == 3:
                    ins.then_inc(y_psum, 1)

        @block.scalar
        def _(act):
            act.wait_ge(xt_psum, 1)
            nc.scalar.copy(xqt[:, 0:BANK], bank[4]).then_inc(xt_ready, 1)
            act.wait_ge(loaded, 64)
            for c in range(CHUNKS):
                act.wait_ge(h_psum, c + 1)
                if c >= 2:
                    act.wait_ge(silu_ready, c - 1)
                nc.scalar.activation(halves(conv[c % 2][:]), pair[c % 2], ACT.Identity, scale=taps[:, c, 1:2],
                                     bias=cb[:, c:c + 1]).then_inc(mid_ready, 1)
                if c >= 1:
                    act.wait_ge(conv_ready, c)
                    nc.scalar.activation(act_cols[:, c - 1, :], conv[(c - 1) % 2][:], ACT.Silu).then_inc(silu_ready, 1)
            act.wait_ge(conv_ready, CHUNKS)
            nc.scalar.activation(act_cols[:, CHUNKS - 1, :], conv[(CHUNKS - 1) % 2][:], ACT.Silu)\
                .then_inc(silu_ready, 1)
            for n in range(4):
                if n % 2 == 0:
                    act.wait_ge(hq_psum, n + 1)
                    nc.scalar.copy(hqt[:, 2 * n:2 * n + 2, :].rearrange("p t c -> p (t c)"), bank[4].bitcast(BF16))\
                        .then_inc(hqt_ready, 1)
                else:
                    act.wait_ge(hq_psum, n + 1)
                    nc.scalar.copy(hqt[:, 2 * n:2 * n + 2, :].rearrange("p t c -> p (t c)"), bank[5].bitcast(BF16))\
                        .then_inc(hqt_ready, 1)
            norm_root(nc, act, nb, 1)

        @block.vector
        def _(dve):
            steps = Tally(dve, dve_steps)
            dve.wait_ge(loaded, 64)
            steps.add(nc.vector.tensor_reduce(mag[:, 0:1], w1[:], AX.X, ALU.add, apply_absolute_value=True))
            nc.vector.tensor_reduce(mag[:, 1:2], w2[:], AX.X, ALU.add, apply_absolute_value=True)\
                .then_inc(mag_ready, 1)

            def quant_scales(top, scale, back, cols):
                steps.step(nc.vector.tensor_scalar(top[:, cols], top[:, cols], LEAST, None, ALU.max))
                steps.step(nc.vector.reciprocal(scale[:, cols], top[:, cols]))
                steps.step(nc.vector.tensor_scalar(scale[:, cols], scale[:, cols], 127.0, None, ALU.mult))
                steps.step(nc.vector.reciprocal(back[:, cols], scale[:, cols]))

            every = slice(0, TILES)
            steps.step(nc.vector.tensor_reduce(top[:], g.x[:], AX.X, ALU.max, apply_absolute_value=True))
            quant_scales(top, scale, back, every)
            for t in range(TILES):
                steps.add(nc.vector.tensor_scalar(xq[:, t, :], g.x[:, t, :], scale[:, t:t + 1], MAGIC,
                                                  ALU.mult, ALU.add))
            steps.settle()
            for t in range(TILES):
                ins = nc.vector.tensor_scalar(xq[:, t, :], xq[:, t, :], MAGIC, back[:, t:t + 1],
                                              ALU.subtract, ALU.mult)
            ins.then_inc(xq_ready, 1)
            dve.wait_ge(mag_psum, 1)
            steps.step(nc.vector.tensor_scalar(mean[:], bank[7][:, 0:2], 1.0 / (D * HID), LEAST, ALU.mult, ALU.max))
            steps.step(nc.vector.reciprocal(wscale[:], mean[:]))
            steps.step(nc.vector.reciprocal(wback[:], wscale[:]))
            for j, w in enumerate((w1, w2)):
                steps.step(nc.vector.tensor_scalar(w[:], w[:], wscale[:, j:j + 1], MAGIC, ALU.mult, ALU.add))
                steps.step(nc.vector.tensor_scalar(w[:], w[:], MAGIC, 1.0, ALU.subtract, ALU.min))
            steps.add(nc.vector.tensor_scalar(w2b[:], w2[:], -1.0, None, ALU.max))
            nc.vector.tensor_scalar(w1[:], w1[:], -1.0, wback[:, 0:1], ALU.max, ALU.mult).then_inc(w_ready, 1)
            dve.wait_ge(xt_psum, 2)
            nc.vector.tensor_copy(xqt[:, BANK:], bank[5]).then_inc(xt_ready, 1)
            seqs = lambda z: z.rearrange("p (b n) -> p b n", b=BATCH)
            for c in range(CHUNKS):
                h = seqs(pair[c % 2].rearrange("p j n -> p (j n)"))
                z = seqs(conv[c % 2][:])
                dve.wait_ge(mid_ready, c + 1)
                steps.step(nc.vector.scalar_tensor_tensor(z[:, :, 1:], h[:, :, :SEQ - 1], taps[:, c, 0:1], z[:, :, 1:],
                                                          ALU.mult, ALU.add))
                nc.vector.scalar_tensor_tensor(z[:, :, :SEQ - 1], h[:, :, 1:], taps[:, c, 2:3], z[:, :, :SEQ - 1],
                                               ALU.mult, ALU.add).then_inc(conv_ready, 1)
            for grp in range(2):
                cols = slice(4 * grp, 4 * grp + 4)
                dve.wait_ge(g_psum, grp + 1)
                steps.step(nc.vector.tensor_reduce(top2[:, cols], g.psum[:, 0:4, :], AX.X, ALU.max,
                                                   apply_absolute_value=True))
                quant_scales(top2, scale2, back2, cols)
                for t in range(4):
                    ins = nc.vector.tensor_scalar(big[:, 4 * grp + t, :], bank[t], scale2[:, 4 * grp + t:4 * grp + t + 1],
                                                  MAGIC, ALU.mult, ALU.add)
                ins.then_inc(rounded_ready, 1)
                dve.wait_ge(rounded_ready, grp + 1)
                nc.vector.tensor_scalar(hq[:, cols, :], big[:, cols, :], MAGIC, None, ALU.subtract)\
                    .then_inc(hq_ready, 1)
            steps.step(nc.vector.tensor_scalar(back2[:], back2[:], wback[:, 1:2], None, ALU.mult))
            for t in range(TILES):
                dve.wait_ge(y_psum, t // 4 + 1)
                steps.add(nc.vector.scalar_tensor_tensor(rsd[:, t, :], bank[6 + t // 4][:, (t % 4) * D:(t % 4 + 1) * D],
                                                         back2[:, t:t + 1], g.x[:, t, :], ALU.mult, ALU.add))
            steps.settle()
            norm_stats(nc, steps, nb, rsd)
            norm_scale(nc, dve, steps, nb, 1)
            norm_apply(nc, steps, nb, rsd, g.x)


def store(nc, g, out):
    stored = nc.alloc_semaphore(name="stored")
    with nc.Block() as block:
        @block.sync
        def _(sp):
            sp.dma_start(out.rearrange("b (h p) c -> p (b h) c", p=P), g.x[:]).then_inc(stored, 16)
            sp.wait_ge(stored, 16)




def decoder(nc, a, out):
    with ExitStack() as ctx:
        g = Shared(nc, ctx)
        for n, stage in enumerate((
                selective_scan, memory_attention, expert_block, graph_attention, narrow_attention, quantised_ffn)):
            if n == 3:
                nc.clear_and_free_semaphores(g.sems)
                g.sems.clear()
                nc.all_engine_barrier()
            stage(nc, g, a)
        store(nc, g, out)


_OUTS = [((4, 256, 128), 'float32')]


def kernel(**inputs):
    import numpy as _np
    import concourse.bacc as _bacc
    from concourse import mybir as _mybir
    from concourse.bass_utils import run_bass_kernel_spmd as _run

    nc = _bacc.Bacc("TRN2", target_bir_lowering=False, num_devices=1)
    def columns(v):
        return v.reshape(-1, 128).T

    given = {name: _np.asarray(v) for name, v in inputs.items()}
    for name in ("L0_xattn_wq_b", "L0_xattn_wk_b", "L0_ffn_b1", "L1_xattn_bq", "L1_xattn_bk", "L1_ffn_conv_b",
                 "L1_attn_gamma_in", "L0_attn_b_dt", "L0_attn_Dp"):
        given[name] = columns(given[name])
    given["L1_ffn_w1"] = given["L1_ffn_w1"].T
    given["L1_ffn_w2"] = given["L1_ffn_w2"].T.reshape(4, 128, 128).transpose(1, 0, 2)
    given["L1_attn_lin_b"] = given["L1_attn_lin_b"].reshape(64, 1)
    for name in ("L0_ffn_in_proj_w", "L0_ffn_out_w", "L0_ffn_router_w", "L1_attn_lin_w"):
        given[name] = given[name].T
    for name in ("L0_ffn_w1", "L0_ffn_w2"):
        given[name] = given[name].transpose(2, 0, 1)
    given["L1_ffn_conv_w"] = given["L1_ffn_conv_w"].reshape(4, 128, 3).transpose(1, 0, 2)
    arrays, args = {}, {}
    for name in given:
        a = _np.ascontiguousarray(given[name])
        arrays[f"in_{name}_dram"] = a
        args[name] = nc.dram_tensor(f"in_{name}_dram", a.shape, _mybir.dt.from_np(a.dtype), kind="ExternalInput").ap()
    shape, dtype = _OUTS[0]
    out = nc.dram_tensor("out_0_dram", shape, _mybir.dt.from_np(_np.dtype(dtype)), kind="ExternalOutput").ap()
    decoder(nc, args, out)
    r = _run(nc, [arrays], core_ids=[0])
    return r.results[0]["out_0_dram"]
```

```python
from contextlib import ExitStack

import concourse.bass as bass
from concourse import mybir

F32 = mybir.dt.float32
BF16 = mybir.dt.bfloat16
F16 = mybir.dt.float16
U32 = mybir.dt.uint32
ALU = mybir.AluOpType
ACT = mybir.ActivationFunctionType
AX = mybir.AxisListType
ds = bass.ds

P = 128
BATCH, SEQ, D = 4, 256, 128
TOK = BATCH * SEQ
TILES = TOK // P
BANK = 512
EPS = 1e-5


class Tally:

    def __init__(self, engine, sem, before=0):
        self.engine, self.sem, self.n, self.before = engine, sem, 0, before

    def add(self, instruction):
        instruction.then_inc(self.sem, 1)
        self.n += 1

    def settle(self):
        self.engine.wait_ge(self.sem, self.before + self.n)

    def step(self, instruction):
        self.add(instruction)
        self.settle()


class Resources:

    def __init__(self, nc, ctx, sems, tag):
        self.nc, self.ctx, self.sems, self.tag = nc, ctx, sems, tag

    def sb(self, name, shape, dt=F32):
        return self.ctx.enter_context(self.nc.sbuf_tensor(name, shape, dt))

    def sem(self, name):
        self.sems.append(self.nc.alloc_semaphore(name=f"{self.tag}_{name}"))
        return self.sems[-1]


class Weights:

    def __init__(self, nc, ctx, tag):
        self.nc, self.ctx, self.pairs = nc, ctx, []
        self.loaded = nc.alloc_semaphore(name=f"{tag}_weights_loaded")

    def sb(self, name, shape):
        return self.ctx.enter_context(self.nc.sbuf_tensor(name, shape, F32))

    def load(self, sp):
        for dst, src in self.pairs:
            sp.dma_start(dst, src).then_inc(self.loaded, 16)

    def wait(self, engine):
        engine.wait_ge(self.loaded, 16 * len(self.pairs))


def one_row(v):
    return v.rearrange("(o n) -> o n", o=1)


def every_row(v):
    return one_row(v).broadcast_to([P, v.shape[0]])


class Shared:

    def __init__(self, nc, ctx):
        r = Resources(nc, ctx, [], "kernel")
        self.sems = []
        self.x, self.xt = r.sb("x_rows", [P, TILES, D]), r.sb("x_cols", [P, TOK])
        self.ct = r.sb("ctx_cols", [P, TOK])
        self.ident, self.ones_row = r.sb("identity", [P, P]), r.sb("ones_row", [1, P])
        self.ones_row_b = r.sb("ones_row_b", [1, P], BF16)
        self.psum = ctx.enter_context(nc.psum_tensor("banks", [P, 8, BANK], F32))


def halves(ap):
    return ap.rearrange("p (h n) -> p h n", h=2)


def transpose_rows(nc, pe, src, src_ready, ident, banks, done):
    for t in range(TILES):
        if src_ready is not None:
            pe.wait_ge(src_ready[0], src_ready[1](t))
        ins = nc.tensor.transpose(banks[t // 4][:, (t % 4) * P:(t % 4 + 1) * P], src[:, t, :], ident)
        if t % 4 == 3:
            ins.then_inc(done, 1)


class NormBuffers:
    def __init__(self, r, tag):
        self.stats, self.mv = r.sb(f"{tag}_stats", [P, TILES, 6]), r.sb(f"{tag}_mean_var", [P, TILES, 2])
        self.ve, self.sd = r.sb(f"{tag}_var_eps", [P, TILES]), r.sb(f"{tag}_std", [P, TILES])
        self.rstd, self.shift = r.sb(f"{tag}_rstd", [P, TILES]), r.sb(f"{tag}_shift", [P, TILES])
        self.var_ready, self.sd_ready = r.sem(f"{tag}_var_ready"), r.sem(f"{tag}_sd_ready")


def norm_stats(nc, tally, b, rows):
    for t in range(TILES):
        tally.add(nc.vector.bn_stats(b.stats[:, t, :], rows[:, t, :]))
    tally.settle()
    for t in range(TILES):
        tally.add(nc.vector.bn_aggr(b.mv[:, t, :], b.stats[:, t, :]))
    tally.settle()
    nc.vector.tensor_scalar(b.ve[:], b.mv[:, :, 1], EPS, None, ALU.add).then_inc(b.var_ready, 1)


def norm_root(nc, act, b, k):
    act.wait_ge(b.var_ready, k)
    nc.scalar.activation(b.sd[:], b.ve[:], ACT.Sqrt).then_inc(b.sd_ready, 1)


def norm_scale(nc, dve, tally, b, k):
    dve.wait_ge(b.sd_ready, k)
    tally.step(nc.vector.reciprocal(b.rstd[:], b.sd[:]))
    tally.step(nc.vector.scalar_tensor_tensor(b.shift[:], b.mv[:, :, 0], -1.0, b.rstd[:], ALU.mult, ALU.mult))


def norm_apply(nc, tally, b, rows, out):
    for t in range(TILES):
        tally.add(nc.vector.tensor_scalar(out[:, t, :], rows[:, t, :], b.rstd[:, t:t + 1],
                                          b.shift[:, t:t + 1], ALU.mult, ALU.add))
    tally.settle()


DT_RANK, STATES = 64, 16
DT_MIN, DT_MAX = 0.001, 0.1


def selective_scan(nc, g, a):
    with ExitStack() as ctx:
        r = Resources(nc, ctx, g.sems, "ssm")
        w_in = r.sb("w_in", [P, D])
        w_x = r.sb("w_x", [P, DT_RANK + 2 * STATES])
        w_dt = r.sb("w_dt", [DT_RANK, D])
        vecs = r.sb("ssm_vecs", [P, 2])
        a_log = r.sb("a_log", [P, STATES])
        neg_a = r.sb("neg_a", [P, STATES])
        pick = r.sb("pick_state", [96, STATES, P], BF16)
        pick_rows = pick[:].rearrange("k n p -> k (n p)")
        parts = r.sb("row_parts", [96, 2, TOK], BF16)
        ctx_rows = r.sb("ctx_rows", [P, TILES, D])
        u = r.sb("u_cols", [P, TOK])
        low = r.sb("dt_low_cols", [DT_RANK, TOK])
        bm = r.sb("b_cols", [STATES, TOK])
        rows2 = r.sb("inp_c_cols", [STATES, 2, TOK])
        part = r.sb("rounded_part", [STATES, 2, TOK], BF16)
        absz = r.sb("abs_z", [P, TOK])
        soft = r.sb("soft_tail", [P, TOK])
        dt = r.sb("dt_cols", [P, TOK])
        dtu = r.sb("dtu_cols", [P, TOK])
        decay = [r.sb(f"decay{i}", [P, TOK]) for i in range(2)]
        zeros = r.sb("zeros", [P, BATCH])
        state = r.sb("state", [P, TOK])
        hc = [r.sb(f"state_c{i}", [P, TOK]) for i in range(2)]
        y = r.sb("ssm_y_cols", [P, TOK])
        rsd = r.sb("ssm_rows", [P, TILES, D])
        nb = NormBuffers(r, "ssm_norm")

        loaded = {k: r.sem(f"loaded_{k}") for k in ("x", "ctx", "w", "small")}
        const_done, xt_psum, xt_ready, ct_psum, ct_ready = (r.sem(n) for n in (
            "const_done", "xt_psum", "xt_ready", "ct_psum", "ct_ready"))
        u_psum, u_ready, low_psum, low_ready, bc_psum, z_psum = (r.sem(n) for n in (
            "u_psum", "u_ready", "low_psum", "low_ready", "bc_psum", "z_psum"))
        abs_ready, soft_ready, nega_exp, nega_ready, dt_ready, dtu_ready = (r.sem(n) for n in (
            "abs_ready", "soft_ready", "nega_exp", "nega_ready", "dt_ready", "dtu_ready"))
        s_psum, parts_ready, inp_bc, c_bc, decay_exp, decay_ready = (r.sem(n) for n in (
            "s_psum", "parts_ready", "inp_bc", "c_bc", "decay_exp", "decay_ready"))
        scanned, hc_ready, summed, y_ready, yt_psum = (r.sem(n) for n in (
            "scanned", "hc_ready", "summed", "y_ready", "yt_psum"))
        dve_steps, act_steps, pool_steps = r.sem("dve_steps"), r.sem("act_steps"), r.sem("pool_steps")
        bank = [g.psum[:, i, :] for i in range(8)]
        pair = [g.psum[:, 2 * i:2 * i + 2, :] for i in range(4)]
        block = ctx.enter_context(nc.Block())

        @block.sync
        def _(sp):
            sp.dma_start(g.x[:], a["x"].rearrange("b (h p) c -> p (b h) c", p=P)).then_inc(loaded["x"], 16)
            sp.dma_start(w_in[:], a["L0_attn_w_in"]).then_inc(loaded["w"], 16)
            sp.dma_start(w_x[:], a["L0_attn_w_x"]).then_inc(loaded["w"], 16)
            sp.dma_start(w_dt[:], a["L0_attn_w_dt"]).then_inc(loaded["w"], 16)
            sp.dma_start(ctx_rows[:], a["ctx_1024"].rearrange("b (h p) c -> p (b h) c", p=P)).then_inc(loaded["ctx"], 16)
            g.memory.load(sp)
            g.expert.load(sp)
            g.graph.load(sp)
            g.narrow.load(sp)

        @block.gpsimd
        def _(pool):
            steps = Tally(pool, pool_steps)
            steps.add(nc.gpsimd.memset(zeros[:], 0.0))
            steps.add(nc.gpsimd.memset(g.ident[:], 0.0))
            steps.add(nc.gpsimd.memset(g.ones_row[:], 1.0))
            steps.add(nc.gpsimd.memset(pick[:], 0.0))
            steps.settle()
            nc.gpsimd.affine_select(out=g.ident[:], in_=g.ident[:], compare_op=ALU.not_equal, fill=1.0,
                                    base=0, pattern=[[-1, P]], channel_multiplier=1).then_inc(const_done, 1)
            for j in range(3):
                steps.step(nc.gpsimd.affine_select(out=pick[:], in_=pick[:], compare_op=ALU.not_equal, fill=1.0,
                                                   base=-32 * j, pattern=[[-1, STATES], [0, P]],
                                                   channel_multiplier=1))
            steps.step(nc.gpsimd.memset(parts[:], 0.0))
            nc.gpsimd.memset(g.ones_row_b[:], 1.0).then_inc(const_done, 1)

            def clear_starts(n, k):
                pool.wait_ge(decay_exp, n + 1)
                nc.gpsimd.tensor_tensor(decay[k][:].rearrange("p (b s) -> p b s", b=BATCH)[:, :, 0],
                                        zeros[:], zeros[:], ALU.add)\
                    .then_inc(decay_ready, 1)

            with pool.Fori(0, STATES // 2) as i:
                for k in range(2):
                    clear_starts(2 * i + k, k)

        @block.scalar
        def _(act):
            act.dma_start(vecs[:, 0:1], a["L0_attn_b_dt"]).then_inc(loaded["small"], 16)
            act.dma_start(vecs[:, 1:2], a["L0_attn_Dp"]).then_inc(loaded["small"], 16)
            act.dma_start(a_log[:], a["L0_attn_A_log"]).then_inc(loaded["small"], 16)
            act.wait_ge(loaded["small"], 48)
            nc.scalar.activation(neg_a[:], a_log[:], ACT.Exp).then_inc(nega_exp, 1)
            act.wait_ge(xt_psum, 1)
            nc.scalar.copy(g.xt[:, 0:BANK], bank[0]).then_inc(xt_ready, 1)
            for h in range(2):
                act.wait_ge(u_psum, h + 1)
                nc.scalar.copy(u[:, h * BANK:(h + 1) * BANK], bank[2 + h]).then_inc(u_ready, 1)
            for h in range(2):
                act.wait_ge(low_psum, h + 1)
                nc.scalar.copy(low[:, h * BANK:(h + 1) * BANK], bank[4 + h][0:DT_RANK, :]).then_inc(low_ready, 1)
            act.wait_ge(z_psum, 2)
            steps = Tally(act, act_steps)
            steps.step(nc.scalar.activation(absz[:], g.psum[:, 6:8, :], ACT.Abs, bias=vecs[:, 0:1]))
            abs_sem = steps
            steps.step(nc.scalar.activation(absz[:], absz[:], ACT.Exp, scale=-1.0))
            nc.scalar.activation(soft[:], absz[:], ACT.Ln, bias=1.0).then_inc(soft_ready, 1)
            act.wait_ge(dt_ready, 1)
            act.wait_ge(nega_ready, 1)

            def decays(n, k, first):
                if not first:
                    act.wait_ge(scanned, n - 1)
                nc.scalar.activation(decay[k][:], dt[:], ACT.Exp, scale=neg_a[:, ds(n, 1)]).then_inc(decay_exp, 1)

            for k in range(2):
                decays(k, k, True)
            with act.Fori(1, STATES // 2) as i:
                for k in range(2):
                    decays(2 * i + k, k, False)
            norm_root(nc, act, nb, 1)

        @block.tensor
        def _(pe):
            pe.wait_ge(const_done, 1)
            pe.wait_ge(loaded["x"], 16)
            transpose_rows(nc, pe, g.x, None, g.ident[:], bank, xt_psum)
            pe.wait_ge(loaded["w"], 48)
            for h in range(2):
                pe.wait_ge(xt_ready, 2)
                nc.tensor.matmul(bank[2 + h], w_in[:], g.xt[:, h * BANK:(h + 1) * BANK], start=True, stop=True)\
                    .then_inc(u_psum, 1)
            for h in range(2):
                pe.wait_ge(u_ready, h + 1)
                nc.tensor.matmul(bank[4 + h][0:DT_RANK, :], w_x[:, 0:DT_RANK], u[:, h * BANK:(h + 1) * BANK],
                                 start=True, stop=True).then_inc(low_psum, 1)
            for h in range(2):
                pe.wait_ge(low_ready, h + 1)
                nc.tensor.matmul(bank[6 + h], w_dt[:], low[:, h * BANK:(h + 1) * BANK], start=True, stop=True)\
                    .then_inc(z_psum, 1)
            for h in range(2):
                for m in range(2):
                    lo = DT_RANK + m * STATES
                    ins = nc.tensor.matmul(bank[2 * m + h][0:STATES, :], w_x[:, lo:lo + STATES],
                                           u[:, h * BANK:(h + 1) * BANK], start=True, stop=True)
            ins.then_inc(bc_psum, 1)
            pe.wait_ge(loaded["ctx"], 16)
            pe.wait_ge(low_ready, 2)
            transpose_rows(nc, pe, ctx_rows, None, g.ident[:], bank[4:6], ct_psum)
            pe.wait_ge(dtu_ready, 1)
            pe.wait_ge(nega_ready, 1)
            for h in range(2):
                nc.tensor.matmul(bank[6 + h][0:STATES, :], neg_a[:], dtu[:, h * BANK:(h + 1) * BANK],
                                 start=True, stop=True).then_inc(s_psum, 1)
            pe.wait_ge(parts_ready, 1)
            pe.wait_ge(const_done, 2)
            pe.wait_ge(ct_ready, 2)

            def broadcasts(n, k, first):
                if not first:
                    pe.wait_ge(scanned, n - 1)
                for h in range(2):
                    ins = nc.tensor.matmul(bank[2 * k + h], pick_rows[:, ds(n * P, P)],
                                           parts[:, 0, h * BANK:(h + 1) * BANK], start=True, stop=True)
                ins.then_inc(inp_bc, 1)

            def outputs(n, k, zero, first, last):
                if not zero:
                    pe.wait_ge(hc_ready, n)
                for h in range(2):
                    ins = nc.tensor.matmul(bank[4 + h], pick_rows[:, ds(n * P, P)],
                                           parts[:, 1, h * BANK:(h + 1) * BANK], start=True, stop=True)
                ins.then_inc(c_bc, 1)
                if not zero:
                    gather(n - 1, 1 - k, last == "first", False)

            def gather(n, k, start, stop):
                pe.wait_ge(hc_ready, n + 1)
                for h in range(2):
                    ins = nc.tensor.matmul(bank[6 + h], g.ident[:], hc[k][:, h * BANK:(h + 1) * BANK],
                                           start=start, stop=stop)
                ins.then_inc(summed, 1)

            broadcasts(0, 0, True)
            broadcasts(1, 1, True)
            outputs(0, 0, True, True, "")
            outputs(1, 1, False, True, "first")
            with pe.Fori(1, STATES // 2) as i:
                for k in range(2):
                    broadcasts(2 * i + k, k, False)
                    outputs(2 * i + k, k, False, False, "")
            gather(STATES - 1, 1, False, True)
            pe.wait_ge(y_ready, 1)
            pe.wait_ge(scanned, STATES)
            for t in range(TILES):
                ins = nc.tensor.transpose(bank[t // 4][:, (t % 4) * P:(t % 4 + 1) * P],
                                          y[:, t * P:(t + 1) * P], g.ident[:])
            ins.then_inc(yt_psum, 1)

        @block.vector
        def _(dve):
            steps = Tally(dve, dve_steps)
            dve.wait_ge(xt_psum, 2)
            nc.vector.tensor_copy(g.xt[:, BANK:], bank[1]).then_inc(xt_ready, 1)
            dve.wait_ge(nega_exp, 1)
            steps.step(nc.vector.tensor_scalar(neg_a[:], neg_a[:], -1.0, None, ALU.mult))
            nc.vector.tensor_scalar(neg_a[:], neg_a[:], 1.0, None, ALU.mult).then_inc(nega_ready, 1)
            dve.wait_ge(bc_psum, 1)
            steps.add(nc.vector.tensor_copy(halves(bm[:]), pair[0][0:STATES]))
            steps.step(nc.vector.tensor_copy(halves(rows2[:, 1, :]), pair[1][0:STATES]))
            dve.wait_ge(ct_psum, 2)
            for h in range(2):
                nc.vector.tensor_copy(g.ct[:, h * BANK:(h + 1) * BANK], bank[4 + h]).then_inc(ct_ready, 1)
            dve.wait_ge(soft_ready, 1)
            dve.wait_ge(z_psum, 2)
            steps.step(nc.vector.tensor_scalar(halves(dt[:]), pair[3], vecs[:, 0:1], 0.0, ALU.add, ALU.max))
            steps.step(nc.vector.tensor_tensor(dt[:], dt[:], soft[:], ALU.add))
            steps.step(nc.vector.tensor_scalar(dtu[:], dt[:], DT_MAX - DT_MIN, DT_MIN, ALU.mult, ALU.add))
            nc.vector.tensor_copy(dt[:], dtu[:]).then_inc(dt_ready, 1)
            dve.wait_ge(dt_ready, 1)
            dve.wait_ge(u_ready, 2)
            nc.vector.tensor_tensor(dtu[:], dt[:], u[:], ALU.mult).then_inc(dtu_ready, 1)
            dve.wait_ge(s_psum, 2)
            steps.step(nc.vector.tensor_tensor(halves(rows2[:, 0, :]), halves(bm[:]), pair[3][0:STATES], ALU.mult))
            dve.wait_ge(const_done, 2)
            steps.step(nc.vector.tensor_copy(part[:], rows2[:]))
            steps.add(nc.vector.tensor_copy(parts[0:STATES], part[:]))
            steps.step(nc.vector.tensor_tensor(rows2[:], rows2[:], part[:], ALU.subtract))
            steps.step(nc.vector.tensor_copy(part[:], rows2[:]))
            steps.add(nc.vector.tensor_copy(parts[32:32 + STATES], part[:]))
            steps.step(nc.vector.tensor_tensor(rows2[:], rows2[:], part[:], ALU.subtract))
            nc.vector.tensor_copy(parts[64:64 + STATES], rows2[:]).then_inc(parts_ready, 1)

            def scan(n, k, first):
                dve.wait_ge(inp_bc, n + 1)
                dve.wait_ge(decay_ready, n + 1)
                nc.vector.tensor_tensor_scan(state[:], decay[k][:], g.psum[:, 2 * k:2 * k + 2, :]
                                             .rearrange("p h n -> p (h n)"), 0.0, ALU.mult, ALU.add)\
                    .then_inc(scanned, 1)
                dve.wait_ge(scanned, n + 1)
                dve.wait_ge(c_bc, n + 1)
                if not first:
                    dve.wait_ge(summed, n - 1)
                nc.vector.tensor_tensor(halves(hc[k][:]), halves(state[:]), pair[2], ALU.mult).then_inc(hc_ready, 1)

            for k in range(2):
                scan(k, k, True)
                dve.wait_ge(hc_ready, k + 1)
            with dve.Fori(1, STATES // 2) as i:
                for k in range(2):
                    scan(2 * i + k, k, False)
                    dve.wait_ge(hc_ready, 2 * i + k + 1)
            dve.wait_ge(summed, STATES)
            nc.vector.scalar_tensor_tensor(halves(y[:]), halves(u[:]), vecs[:, 1:2], pair[3], ALU.mult, ALU.add)\
                .then_inc(y_ready, 1)
            dve.wait_ge(yt_psum, 1)
            steps.step(nc.vector.tensor_tensor(rsd[:].rearrange("p (h t) c -> p h (t c)", h=2), g.x[:]
                                               .rearrange("p (h t) c -> p h (t c)", h=2), pair[0], ALU.add))
            norm_stats(nc, steps, nb, rsd)
            norm_scale(nc, dve, steps, nb, 1)
            norm_apply(nc, steps, nb, rsd, g.x)


HEADS, DK, MEM = 16, 64, 128
PAIRS = HEADS // 2
KEYS = SEQ + MEM
KT = KEYS // P
QT = SEQ // P
VW = DK + 1
UNITS = 2 * BATCH


class MemoryWeights(Weights):
    def __init__(self, nc, ctx, a):
        super().__init__(nc, ctx, "xattn")
        self.wv, self.wo = self.sb("wv", [P, HEADS * DK]), self.sb("wo", [P, PAIRS, D])
        self.bv, self.bo = self.sb("bv_all_rows", [P, HEADS * DK]), self.sb("bo_row", [1, D])
        self.bqk = self.sb("bq_bk_cols", [P, 2, PAIRS])
        self.mk, self.mv = self.sb("mk_rows", [P, HEADS * DK]), self.sb("mv_rows", [P, HEADS, DK])
        self.pairs = [
            (self.mk[:], a["L0_xattn_mk"][0]), (self.wv[:], a["L0_xattn_wv_w"]),
            (self.bv[:], every_row(a["L0_xattn_wv_b"])), (self.bqk[:, 0, :], a["L0_xattn_wq_b"]),
            (self.bqk[:, 1, :], a["L0_xattn_wk_b"]),
            (self.mv[:], a["L0_xattn_mv"][0].rearrange("m (h d) -> m h d", h=HEADS)),
            (self.wo[:], a["L0_xattn_wo_w"].rearrange("(c p) n -> p c n", p=P)), (self.bo[:], one_row(a["L0_xattn_wo_b"])),
        ]


def memory_attention(nc, g, a):
    with ExitStack() as ctx:
        r = Resources(nc, ctx, g.sems, "xattn")
        given = g.memory
        wv, wo, bv, bo, bqk, mk, mv = given.wv, given.wo, given.bv, given.bo, given.bqk, given.mk, given.mv
        wpair = r.sb("wq_wk_pair", [P, 2, P])
        mkt_all = r.sb("mk_cols_all", [P, PAIRS, P])
        mkt = r.sb("mk_cols_pair", [P, P])
        q = r.sb("q_cols", [P, BATCH, SEQ])
        k = r.sb("k_cols", [P, BATCH, SEQ])
        v_rows = r.sb("value_rows", [P, 4, HEADS // 2, DK])
        v_hi = r.sb("values_hi", [P, TILES + 1, HEADS, VW], F16)
        v_lo = r.sb("values_lo", [P, TILES + 1, HEADS, VW], F16)
        v_hi_flat = v_hi[:].rearrange("p t h w -> p (t h w)")
        v_lo_flat = v_lo[:].rearrange("p t h w -> p (t h w)")
        e = [r.sb(f"probs{i}", [P, QT, KEYS]) for i in range(2)]
        et_hi = [r.sb(f"probs_cols_hi{i}", [P, QT, KEYS], F16) for i in range(2)]
        et_lo = [r.sb(f"probs_cols_lo{i}", [P, QT, KEYS], F16) for i in range(2)]
        negmax = [r.sb(f"negmax{i}", [P, QT]) for i in range(2)]
        o = r.sb("out_raw", [P, TILES, HEADS, VW])
        o_heads = o[:].rearrange("p t h w -> p t (h w)")
        rsum = [r.sb(f"rsum{i}", [P, HEADS]) for i in range(2)]
        on = [r.sb(f"out_normal{i}", [P, HEADS, DK]) for i in range(2)]
        ont = [r.sb(f"out_cols{i}", [P, PAIRS, P]) for i in range(2)]
        rsd = r.sb("xattn_rows", [P, TILES, D])
        nb = NormBuffers(r, "xattn_norm")
        wpair_loaded, xt_psum, xt_ready, v_psum, v_ready = (r.sem(n) for n in (
            "wpair_loaded", "xt_psum", "xt_ready", "v_psum", "v_ready"))
        v_ones, mk_psum, mk_ready, mkt_ready, projected, qk_ready = (r.sem(n) for n in (
            "v_ones", "mk_psum", "mk_ready", "mkt_ready", "projected", "qk_ready"))
        scored, max_ready, exp_ready, turned, et_hi_ready, et_lo_ready = (r.sem(n) for n in (
            "scored", "max_ready", "exp_ready", "turned", "et_hi_ready", "et_lo_ready"))
        pv_done, o_ready, on_ready, on_turned, ont_ready, y_psum = (r.sem(n) for n in (
            "pv_done", "o_ready", "on_ready", "on_turned", "ont_ready", "y_psum"))
        y_ready, dve_steps, v_rows_ready, v_hi_ready = (r.sem(n) for n in (
            "y_ready", "dve_steps", "v_rows_ready", "v_hi_ready"))
        bank = [g.psum[:, i, :] for i in range(8)]
        score_bank = [g.psum[:, 2 * i:2 * i + 2, 0:KEYS] for i in range(2)]
        turn_bank = [bank[4], bank[5]]
        proj_bank, o_bank = bank[6], bank[7]
        block = ctx.enter_context(nc.Block())

        @block.sync
        def _(sp):
            def load_pair(p):
                for j, w in enumerate((a["L0_xattn_wq_w"], a["L0_xattn_wk_w"])):
                    sp.dma_start(wpair[:, j, :], w[:, ds(p * P, P)]).then_inc(wpair_loaded, 16)

            load_pair(0)
            with sp.Fori(1, PAIRS) as p:
                sp.wait_ge(projected, BATCH * p)
                load_pair(p)

        @block.gpsimd
        def _(pool):
            nc.gpsimd.memset(v_hi[:, :, :, DK], 1.0).then_inc(v_ones, 1)
            nc.gpsimd.memset(v_lo[:, :, :, DK], 0.0).then_inc(v_ones, 1)
            for n in range(2 * TILES):
                t, h = n // 2, n % 2
                pool.wait_ge(v_hi_ready, n + 1)
                nc.gpsimd.tensor_tensor(v_lo[:, t, 8 * h:8 * h + 8, 0:DK], v_rows[:, n % 4],
                                        v_hi[:, t, 8 * h:8 * h + 8, 0:DK], ALU.subtract).then_inc(v_ready, 1)
            pool.wait_ge(v_hi_ready, 2 * TILES + 1)
            nc.gpsimd.tensor_tensor(v_lo[:, TILES, :, 0:DK], mv[:], v_hi[:, TILES, :, 0:DK], ALU.subtract)\
                .then_inc(v_ready, 1)

        @block.tensor
        def _(pe):
            transpose_rows(nc, pe, g.x, None, g.ident[:], bank[4:6], xt_psum)
            given.wait(pe)
            for c in range(PAIRS):
                if c == 4:
                    pe.wait_ge(mk_ready, 1)
                ins = nc.tensor.transpose(bank[6 + c // 4][:, (c % 4) * P:(c % 4 + 1) * P],
                                          mk[:, c * P:(c + 1) * P], g.ident[:])
                if c % 4 == 3:
                    ins.then_inc(mk_psum, 1)
            for t in range(TILES):
                for h in range(2):
                    n = 2 * t + h
                    if n >= 4:
                        pe.wait_ge(v_rows_ready, n - 3)
                    nc.tensor.matmul(bank[n % 4], g.ct[:, t * P:(t + 1) * P], wv[:, h * BANK:(h + 1) * BANK],
                                     start=True, stop=True).then_inc(v_psum, 1)
            pe.wait_ge(xt_ready, 2)
            pe.wait_ge(mk_ready, 2)

            def project(p, b, first=False):
                if not first:
                    pe.wait_ge(qk_ready, BATCH * p + b)
                pe.wait_ge(wpair_loaded, 32 * p + 32)
                for j, src in enumerate((g.xt, g.ct)):
                    ins = nc.tensor.matmul(proj_bank[:, j * SEQ:(j + 1) * SEQ], wpair[:, j, :],
                                           src[:, b * SEQ:(b + 1) * SEQ], start=True, stop=True)
                ins.then_inc(projected, 1)

            def scores(u, b, h, i, first):
                if not first:
                    pe.wait_ge(exp_ready, u - 1)
                rows = slice(h * DK, (h + 1) * DK)
                for qt in range(QT):
                    lhs = q[rows, b, qt * P:(qt + 1) * P]
                    nc.tensor.matmul(bank[2 * i + qt][:, 0:SEQ], lhs, k[rows, b, :], start=True, stop=True)
                    ins = nc.tensor.matmul(bank[2 * i + qt][:, SEQ:KEYS], lhs, mkt[rows, :], start=True, stop=True)
                ins.then_inc(scored, 1)

            def turn(u, i, first):
                pe.wait_ge(exp_ready, u + 1)
                if not first:
                    pe.wait_ge(et_lo_ready, QT * u)
                for qt in range(QT):
                    for kt in range(KT):
                        ins = nc.tensor.transpose(turn_bank[qt][:, kt * P:(kt + 1) * P],
                                                  e[i][:, qt, kt * P:(kt + 1) * P], g.ident[:])
                ins.then_inc(turned, 1)

            def values(u, p, b, h, i, first):
                pe.wait_ge(et_lo_ready, QT * u + QT)
                if not first:
                    pe.wait_ge(o_ready, u)
                for qt in range(QT):
                    for kt in range(KT):
                        tile = QT * b + kt if kt < QT else TILES
                        cols, head = slice(kt * P, (kt + 1) * P), ds((tile * HEADS + h) * VW + p * (2 * VW), VW)
                        for n, (probs, vals) in enumerate(((et_hi, v_hi_flat), (et_lo, v_hi_flat), (et_hi, v_lo_flat))):
                            ins = nc.tensor.matmul(o_bank[:, qt * VW:(qt + 1) * VW], probs[i][:, qt, cols],
                                                   vals[:, head], start=(kt == 0 and n == 0),
                                                   stop=(kt == KT - 1 and n == 2))
                ins.then_inc(pv_done, 1)

            def pair_steps(p, first, more):
                pe.wait_ge(mkt_ready, p + 1)
                for j in range(UNITS):
                    b, h = j // 2, j % 2
                    u = UNITS * p + j
                    pe.wait_ge(qk_ready, BATCH * p + b + 1)
                    scores(u, b, h, j % 2, first and j < 2)
                    if h == 1 and more:
                        project(p + 1, b)
                    if not (first and j < 1):
                        turn(u - 1, (j - 1) % 2, first and j == 1)
                    if not (first and j < 2):
                        jj = (j - 2) % UNITS
                        values(u - 2, p if j >= 2 else p - 1, jj // 2, jj % 2, j % 2, first and j == 2)

            for b in range(BATCH):
                project(0, b, b == 0)
            pe.wait_ge(v_ready, 2 * TILES + 1)
            pe.wait_ge(v_ones, 2)
            pair_steps(0, True, True)
            with pe.Fori(1, PAIRS - 1) as p:
                pair_steps(p, False, True)
            pair_steps(PAIRS - 1, False, False)
            last = PAIRS * UNITS
            turn(last - 1, 1, False)
            values(last - 2, PAIRS - 1, BATCH - 1, 0, 0, False)
            values(last - 1, PAIRS - 1, BATCH - 1, 1, 1, False)

            for t in range(TILES):
                i = t % 2
                pe.wait_ge(on_ready, t + 1)
                for c in range(PAIRS):
                    ins = nc.tensor.transpose(bank[2 * i + c // 4][:, (c % 4) * P:(c % 4 + 1) * P],
                                              on[i][:, 2 * c:2 * c + 2, :].rearrange("p h d -> p (h d)"), g.ident[:])
                ins.then_inc(on_turned, 1)
                if t:
                    output_product(nc, pe, ont_ready, y_ready, y_psum, t - 1, bank[4 + (t - 1) % 2],
                                   ont[(t - 1) % 2], wo, g.ones_row, bo)
            output_product(nc, pe, ont_ready, y_ready, y_psum, TILES - 1, bank[4 + 1], ont[1], wo, g.ones_row, bo)

        @block.scalar
        def _(act):
            act.wait_ge(xt_psum, 1)
            nc.scalar.copy(g.xt[:, 0:BANK], bank[4]).then_inc(xt_ready, 1)
            for h in range(2):
                act.wait_ge(mk_psum, h + 1)
                nc.scalar.copy(mkt_all[:, 4 * h:4 * h + 4, :].rearrange("p c m -> p (c m)"), bank[6 + h])\
                    .then_inc(mk_ready, 1)

            for n in range(2 * TILES):
                act.wait_ge(v_rows_ready, n + 1)
                nc.scalar.copy(v_hi[:, n // 2, 8 * (n % 2):8 * (n % 2) + 8, 0:DK], v_rows[:, n % 4])\
                    .then_inc(v_hi_ready, 1)
            given.wait(act)
            nc.scalar.copy(v_hi[:, TILES, :, 0:DK], mv[:]).then_inc(v_hi_ready, 1)

            def exps(u, i, first):
                act.wait_ge(max_ready, u + 1)
                if not first:
                    act.wait_ge(turned, u - 1)
                for qt in range(QT):
                    ins = nc.scalar.activation(e[i][:, qt, :], score_bank[i][:, qt, :], ACT.Exp,
                                               bias=negmax[i][:, qt:qt + 1])
                ins.then_inc(exp_ready, 1)

            def split_high(u, i, first):
                act.wait_ge(turned, u + 1)
                if not first:
                    act.wait_ge(pv_done, u - 1)
                for qt in range(QT):
                    nc.scalar.copy(et_hi[i][:, qt, :], turn_bank[qt][:, 0:KEYS]).then_inc(et_hi_ready, 1)

            def pair_steps(p, first):
                for j in range(UNITS):
                    u = UNITS * p + j
                    if not (first and j < 1):
                        split_high(u - 1, (j - 1) % 2, first and j < 3)
                    exps(u, j % 2, first and j < 2)

            pair_steps(0, True)
            with act.Fori(1, PAIRS) as p:
                pair_steps(p, False)
            split_high(PAIRS * UNITS - 1, 1, False)
            for t in range(TILES):
                act.wait_ge(on_turned, t + 1)
                if t >= 2:
                    act.wait_ge(y_psum, t - 1)
                nc.scalar.copy(ont[t % 2][:].rearrange("p (h c) m -> p h (c m)", h=2),
                               g.psum[:, 2 * (t % 2):2 * (t % 2) + 2, :]).then_inc(ont_ready, 1)
            norm_root(nc, act, nb, 1)

        @block.vector
        def _(dve):
            steps = Tally(dve, dve_steps)
            dve.wait_ge(xt_psum, 2)
            nc.vector.tensor_copy(g.xt[:, BANK:], bank[5]).then_inc(xt_ready, 1)
            given.wait(dve)
            for t in range(TILES):
                for h in range(2):
                    n = 2 * t + h
                    dve.wait_ge(v_psum, n + 1)
                    if n >= 4:
                        dve.wait_ge(v_ready, n - 3)
                    nc.vector.tensor_tensor(v_rows[:, n % 4],
                                            bank[n % 4].rearrange("p (h d) -> p h d", h=8),
                                            bv[:, h * BANK:(h + 1) * BANK].rearrange("p (h d) -> p h d", h=8),
                                            ALU.add).then_inc(v_rows_ready, 1)

            def copy_projected(n, p, b):
                dve.wait_ge(projected, n + 1)
                nc.vector.tensor_scalar(q[:, b, :], proj_bank[:, 0:SEQ], bqk[:, 0, ds(p, 1)], DK ** -0.5,
                                        ALU.add, ALU.mult)
                nc.vector.tensor_scalar(k[:, b, :], proj_bank[:, SEQ:], bqk[:, 1, ds(p, 1)], None, ALU.add)\
                    .then_inc(qk_ready, 1)

            def copy_memory_keys(p):
                nc.vector.tensor_copy(mkt[:], mkt_all[:, ds(p, 1), :].rearrange("p o m -> p (o m)"))\
                    .then_inc(mkt_ready, 1)

            def maxima(u, i):
                dve.wait_ge(scored, u + 1)
                nc.vector.tensor_reduce(negmax[i][:], score_bank[i], AX.X, ALU.max, negate=True)\
                    .then_inc(max_ready, 1)

            def split_low(u, i):
                for qt in range(QT):
                    dve.wait_ge(et_hi_ready, QT * u + qt + 1)
                    nc.vector.tensor_tensor(et_lo[i][:, qt, :], turn_bank[qt][:, 0:KEYS], et_hi[i][:, qt, :],
                                            ALU.subtract).then_inc(et_lo_ready, 1)

            def copy_out(u, p, b, h):
                dve.wait_ge(pv_done, u + 1)
                nc.vector.tensor_copy(o_heads[:, QT * b:QT * b + QT, ds(h * VW + p * (2 * VW), VW)],
                                      o_bank[:, 0:QT * VW].rearrange("p (q w) -> p q w", q=QT))\
                    .then_inc(o_ready, 1)

            def pair_steps(p, first, more):
                for j in range(UNITS):
                    u = UNITS * p + j
                    maxima(u, j % 2)
                    if j % 2 == 1 and more:
                        copy_projected(BATCH * p + BATCH + j // 2, p + 1, j // 2)
                    if j == UNITS - 1 and more:
                        copy_memory_keys(p + 1)
                    if not (first and j < 1):
                        split_low(u - 1, (j - 1) % 2)
                    if not (first and j < 2):
                        jj = (j - 2) % UNITS
                        copy_out(u - 2, p if j >= 2 else p - 1, jj // 2, jj % 2)

            dve.wait_ge(mk_ready, 2)
            copy_memory_keys(0)
            for b in range(BATCH):
                copy_projected(b, 0, b)
            pair_steps(0, True, True)
            with dve.Fori(1, PAIRS - 1) as p:
                pair_steps(p, False, True)
            pair_steps(PAIRS - 1, False, False)
            last = PAIRS * UNITS
            split_low(last - 1, 1)
            copy_out(last - 2, PAIRS - 1, BATCH - 1, 0)
            copy_out(last - 1, PAIRS - 1, BATCH - 1, 1)
            dve.wait_ge(o_ready, last)
            for t in range(TILES):
                if t >= 2:
                    dve.wait_ge(on_turned, t - 1)
                steps.step(nc.vector.reciprocal(rsum[t % 2][:], o[:, t, :, DK]))
                nc.vector.tensor_tensor(on[t % 2][:], o[:, t, :, 0:DK],
                                        rsum[t % 2][:].unsqueeze(2).broadcast_to([P, HEADS, DK]), ALU.mult)\
                    .then_inc(on_ready, 1)
                if t:
                    add_residual(nc, dve, y_psum, y_ready, steps, t - 1, bank[4 + (t - 1) % 2], rsd, g.x)
            add_residual(nc, dve, y_psum, y_ready, steps, TILES - 1, bank[5], rsd, g.x)
            steps.settle()
            norm_stats(nc, steps, nb, rsd)
            norm_scale(nc, dve, steps, nb, 1)
            norm_apply(nc, steps, nb, rsd, g.x)


def output_product(nc, pe, ont_ready, y_ready, y_psum, t, y, cols, w, ones_row, bias_row):
    pe.wait_ge(ont_ready, t + 1)
    if t >= 2:
        pe.wait_ge(y_ready, t - 1)
    for c in range(w.shape[1]):
        nc.tensor.matmul(y[:, 0:D], cols[:, c, :], w[:, c, :], start=(c == 0), stop=False)
    nc.tensor.matmul(y[:, 0:D], ones_row[:], bias_row[:], start=False, stop=True).then_inc(y_psum, 1)


def add_residual(nc, dve, y_psum, y_ready, steps, t, y, rows, x):
    dve.wait_ge(y_psum, t + 1)
    nc.vector.tensor_tensor(rows[:, t, :], y[:, 0:D], x[:, t, :], ALU.add).then_inc(y_ready, 1)
    steps.engine.wait_ge(y_ready, t + 1)


FHEADS, FD = 16, 8
EXPERTS = 8
HALVES = TILES // BATCH


class ExpertWeights(Weights):
    def __init__(self, nc, ctx, a):
        super().__init__(nc, ctx, "ffn")
        self.w_in, self.b_in = self.sb("w_qkv", [P, 3 * D]), self.sb("b_qkv", [P, 3 * D])
        self.w_out, self.b_out = self.sb("w_out", [P, 1, D]), self.sb("b_out", [1, D])
        self.gain = self.sb("norm_gains", [P, 4, D])
        self.w_route, self.b_route = self.sb("w_route", [P, EXPERTS]), self.sb("b_route", [1, EXPERTS])
        self.w2, self.b1 = self.sb("w2_all", [P, EXPERTS, D]), self.sb("b1_cols", [P, EXPERTS])
        self.b2 = self.sb("b2_rows", [EXPERTS, D])
        self.pairs = [
            (self.w_in[:], a["L0_ffn_in_proj_w"]), (self.b_in[:], every_row(a["L0_ffn_in_proj_b"])),
            (self.w_out[:, 0, :], a["L0_ffn_out_w"]), (self.b_out[:], one_row(a["L0_ffn_out_b"])),
            (self.gain[:, 0, :], every_row(a["L0_ffn_ln1_g"])), (self.gain[:, 1, :], every_row(a["L0_ffn_ln1_b"])),
            (self.gain[:, 2, :], every_row(a["L0_ffn_ln2_g"])), (self.gain[:, 3, :], every_row(a["L0_ffn_ln2_b"])),
            (self.w_route[:], a["L0_ffn_router_w"]), (self.b_route[:], one_row(a["L0_ffn_router_b"])),
            (self.w2[:], a["L0_ffn_w2"]), (self.b1[:], a["L0_ffn_b1"]), (self.b2[:], a["L0_ffn_b2"]),
        ]


def expert_block(nc, g, a):
    with ExitStack() as ctx:
        r = Resources(nc, ctx, g.sems, "ffn")
        w1 = [r.sb(f"w1_expert{i}", [P, D]) for i in range(2)]
        given = g.expert
        w_in, b_in, w_out, b_out, gain = given.w_in, given.b_in, given.w_out, given.b_out, given.gain
        w_route, b_route, w2, b1, b2 = given.w_route, given.b_route, given.w2, given.b1, given.b2
        w2_flat = w2[:].rearrange("p e n -> p (e n)")
        number = r.sb("expert_number", [P, EXPERTS])
        pick = r.sb("pick_expert", [EXPERTS, EXPERTS, P], BF16)
        pick_flat = pick[:].rearrange("k e p -> k (e p)")
        qkv = r.sb("qkv", [P, TILES, 3 * D])
        prod = [r.sb(f"products{i}", [P, BATCH, D]) for i in range(2)]
        sc = r.sb("batch_scores", [P, HALVES, BATCH, BATCH, FHEADS])
        sc_rows = sc[:].rearrange("p a t s h -> p (a t) s h")
        peak = r.sb("batch_peak", [P, TILES, FHEADS])
        total = r.sb("batch_total", [P, TILES, FHEADS])
        mixed = r.sb("mixed", [P, TILES, D])
        mixed_cols = r.sb("mixed_cols", [P, TILES, 1, P])
        rsd = r.sb("ffn_rows", [P, TILES, D])
        h = r.sb("h_rows", [P, TILES, D])
        ht = r.sb("h_cols", [P, TOK])
        logit = r.sb("logits", [P, TILES, EXPERTS])
        lmax = r.sb("logit_max", [P, TILES])
        lsum = r.sb("logit_sum", [P, TILES])
        best = r.sb("best_probs", [P, TILES, 8])
        place = r.sb("best_places", [P, TILES, 8], U32)
        placef = r.sb("best_places_f", [P, TILES, 2])
        chosen = r.sb("chosen", [P, TILES])
        mask = r.sb("chosen_mask", [P, TILES, EXPERTS])
        maskt = r.sb("mask_cols", [EXPERTS, TOK])
        maskt_b = r.sb("mask_cols_b", [EXPERTS, TOK], BF16)
        he = [r.sb(f"hidden{i}", [P, TOK]) for i in range(2)]
        hem = [r.sb(f"hidden_masked{i}", [P, TOK]) for i in range(2)]
        nb = NormBuffers(r, "ffn_norm")
        const_done, xt_psum, xt_ready, qkv_psum, qkv_ready = (r.sem(n) for n in (
            "const_done", "xt_psum", "xt_ready", "qkv_psum", "qkv_ready"))
        sub_ready, exp_ready, mixed_ready, mixed_psum, ont_ready, y_psum = (r.sem(n) for n in (
            "sub_ready", "exp_ready", "mixed_ready", "mixed_psum", "ont_ready", "y_psum"))
        y_ready, h_ready, ht_psum, ht_ready, logit_psum, lsub_ready = (r.sem(n) for n in (
            "y_ready", "h_ready", "ht_psum", "ht_ready", "logit_psum", "lsub_ready"))
        lexp_ready, mask_ready, maskt_psum, maskt_ready, he_psum, mask_bc = (r.sem(n) for n in (
            "lexp_ready", "mask_ready", "maskt_psum", "maskt_ready", "he_psum", "mask_bc"))
        he_ready, hem_ready, w2_done, dve_steps, pool_steps = (r.sem(n) for n in (
            "he_ready", "hem_ready", "w2_done", "dve_steps", "pool_steps"))
        expert_w1_loaded = [r.sem(f"expert_w1_loaded{i}") for i in range(2)]
        bank = [g.psum[:, i, :] for i in range(8)]
        pair = [g.psum[:, 2 * i:2 * i + 2, :] for i in range(4)]
        block = ctx.enter_context(nc.Block())

        @block.sync
        def _(sp):
            def load_expert(e, k):
                sp.dma_start(w1[k][:], a["L0_ffn_w1"].rearrange("c e h -> c (e h)")[:, ds(e * D, D)])\
                    .then_inc(expert_w1_loaded[k], 16)

            for k in range(2):
                load_expert(k, k)
            with sp.Fori(1, EXPERTS // 2) as i:
                for k in range(2):
                    sp.wait_ge(he_psum, 2 * i + k - 1)
                    load_expert(2 * i + k, k)

        @block.gpsimd
        def _(pool):
            steps = Tally(pool, pool_steps)
            for e in range(EXPERTS):
                nc.gpsimd.memset(number[:, e:e + 1], float(e))
            steps.step(nc.gpsimd.memset(pick[:], 0.0))
            nc.gpsimd.affine_select(out=pick[:], in_=pick[:], compare_op=ALU.not_equal, fill=1.0, base=0,
                                    pattern=[[-1, EXPERTS], [0, P]], channel_multiplier=1).then_inc(const_done, 1)

        @block.tensor
        def _(pe):
            transpose_rows(nc, pe, g.x, None, g.ident[:], bank[6:8], xt_psum)
            given.wait(pe)
            pe.wait_ge(xt_ready, 2)
            for t in range(TILES):
                if t >= 4:
                    pe.wait_ge(qkv_ready, t - 3)
                nc.tensor.matmul(bank[t % 4][:, 0:3 * D], g.xt[:, t * P:(t + 1) * P], w_in[:], start=True, stop=True)\
                    .then_inc(qkv_psum, 1)
            pe.wait_ge(qkv_ready, TILES)
            pe.wait_ge(mixed_ready, TILES)
            transpose_rows(nc, pe, mixed, None, g.ident[:], bank[4:6], mixed_psum)
            pe.wait_ge(ont_ready, 1)
            for t in range(TILES):
                y = bank[t // 4][:, (t % 4) * D:(t % 4 + 1) * D]
                nc.tensor.matmul(y, mixed_cols[:, t, 0, :], w_out[:, 0, :], start=True, stop=False)
                ins = nc.tensor.matmul(y, g.ones_row[:], b_out[:], start=False, stop=True)
            ins.then_inc(y_psum, 1)
            pe.wait_ge(h_ready, 1)
            transpose_rows(nc, pe, h, None, g.ident[:], bank[4:6], ht_psum)
            pe.wait_ge(ht_ready, 2)
            for t in range(TILES):
                y = bank[2][:, t * EXPERTS:(t + 1) * EXPERTS]
                nc.tensor.matmul(y, ht[:, t * P:(t + 1) * P], w_route[:], start=True, stop=False)
                ins = nc.tensor.matmul(y, g.ones_row[:], b_route[:], start=False, stop=True)
            ins.then_inc(logit_psum, 1)
            pe.wait_ge(mask_ready, 1)
            for t in range(TILES):
                ins = nc.tensor.transpose(bank[2 + t // 4][0:EXPERTS, (t % 4) * P:(t % 4 + 1) * P],
                                          mask[:, t, :], g.ident[:])
            ins.then_inc(maskt_psum, 1)
            pe.wait_ge(maskt_ready, 1)
            pe.wait_ge(const_done, 1)
            for t in range(TILES):
                nc.tensor.matmul(bank[6 + t // 4][:, (t % 4) * D:(t % 4 + 1) * D], maskt[:, t * P:(t + 1) * P], b2[:],
                                 start=(t % 4 == 0), stop=False, skip_group_check=True)

            def hidden(i, k, first):
                e = 2 * i + k
                pe.wait_ge(expert_w1_loaded[k], 16 * i + 16)
                if not first:
                    pe.wait_ge(he_ready, e - 1)
                for j in range(2):
                    ins = nc.tensor.matmul(bank[2 * k + j], w1[k][:], ht[:, j * BANK:(j + 1) * BANK],
                                           start=True, stop=True)
                ins.then_inc(he_psum, 1)

            def spread_mask(e, first):
                if not first:
                    pe.wait_ge(hem_ready, e)
                for j in range(2):
                    ins = nc.tensor.matmul(bank[4 + j], pick_flat[:, ds(e * P, P)],
                                           maskt_b[:, j * BANK:(j + 1) * BANK], start=True, stop=True)
                ins.then_inc(mask_bc, 1)

            def outputs(e, k, last=False):
                pe.wait_ge(hem_ready, e + 1)
                for t in range(TILES):
                    ins = nc.tensor.matmul(bank[6 + t // 4][:, (t % 4) * D:(t % 4 + 1) * D],
                                           hem[k][:, t * P:(t + 1) * P], w2_flat[:, ds(e * D, D)],
                                           start=False, stop=last, skip_group_check=True)
                ins.then_inc(w2_done, 1)

            hidden(0, 0, True)
            spread_mask(0, True)
            hidden(0, 1, True)
            outputs(0, 0)
            spread_mask(1, False)
            with pe.Fori(1, EXPERTS // 2) as i:
                for k in range(2):
                    e = 2 * i + k
                    hidden(i, k, False)
                    outputs(e - 1, 1 - k)
                    spread_mask(e, False)
            outputs(EXPERTS - 1, 1, True)

        @block.scalar
        def _(act):
            act.wait_ge(xt_psum, 1)
            nc.scalar.copy(g.xt[:, 0:BANK], bank[6]).then_inc(xt_ready, 1)
            act.wait_ge(sub_ready, 1)
            nc.scalar.activation(sc[:], sc[:], ACT.Exp, scale=FD ** -0.5).then_inc(exp_ready, 1)
            act.wait_ge(mixed_psum, 2)
            nc.scalar.copy(mixed_cols[:].rearrange("p (h t) o c -> p h (t o c)", h=2), pair[2])\
                .then_inc(ont_ready, 1)
            norm_root(nc, act, nb, 1)
            act.wait_ge(ht_psum, 1)
            nc.scalar.copy(ht[:, 0:BANK], bank[4]).then_inc(ht_ready, 1)
            act.wait_ge(lsub_ready, 1)
            nc.scalar.activation(logit[:], logit[:], ACT.Exp).then_inc(lexp_ready, 1)

            def gelus(e, k, first):
                act.wait_ge(he_psum, e + 1)
                if not first:
                    act.wait_ge(hem_ready, e - 1)
                nc.scalar.activation(halves(he[k][:]), pair[k], ACT.Gelu, bias=b1[:, ds(e, 1)]).then_inc(he_ready, 1)

            for k in range(2):
                gelus(k, k, True)
            with act.Fori(1, EXPERTS // 2) as i:
                for k in range(2):
                    gelus(2 * i + k, k, False)
            norm_root(nc, act, nb, 2)
            norm_root(nc, act, nb, 3)

        @block.vector
        def _(dve):
            steps = Tally(dve, dve_steps)
            dve.wait_ge(xt_psum, 2)
            nc.vector.tensor_copy(g.xt[:, BANK:], bank[7]).then_inc(xt_ready, 1)
            given.wait(dve)
            for t in range(TILES):
                dve.wait_ge(qkv_psum, t + 1)
                nc.vector.tensor_tensor(qkv[:, t, :], bank[t % 4][:, 0:3 * D], b_in[:], ALU.add).then_inc(qkv_ready, 1)
            dve.wait_ge(qkv_ready, TILES)
            for half in range(HALVES):
                for t in range(BATCH):
                    n = BATCH * half + t
                    p = prod[n % 2]
                    steps.step(nc.vector.tensor_tensor(
                        p[:], qkv[:, HALVES * t + half, 0:D].unsqueeze(1).broadcast_to([P, BATCH, D]),
                        qkv[:, half::HALVES, D:2 * D], ALU.mult))
                    steps.add(nc.vector.tensor_reduce(sc[:, half, t, :, :].rearrange("p s h -> p (s h)"),
                                                      p[:].rearrange("p s (h d) -> p (s h) d", d=FD), AX.X, ALU.add))
            steps.settle()
            steps.step(nc.vector.tensor_reduce(peak[:], sc_rows.rearrange("p a s h -> p a h s"), AX.X, ALU.max))
            bc = lambda z: z[:].unsqueeze(2).broadcast_to([P, TILES, BATCH, FHEADS])
            nc.vector.tensor_tensor(sc_rows, sc_rows, bc(peak), ALU.subtract).then_inc(sub_ready, 1)
            dve.wait_ge(exp_ready, 1)
            steps.step(nc.vector.tensor_reduce(total[:], sc_rows.rearrange("p a s h -> p a h s"), AX.X, ALU.add))
            steps.step(nc.vector.reciprocal(peak[:], total[:]))
            steps.step(nc.vector.tensor_tensor(sc_rows, sc_rows, bc(peak), ALU.mult))
            for half in range(HALVES):
                for t in range(BATCH):
                    n = BATCH * half + t
                    p = prod[n % 2]
                    steps.step(nc.vector.tensor_tensor(
                        p[:].rearrange("p s (h d) -> p s h d", d=FD),
                        sc[:, half, t, :, :].unsqueeze(3).broadcast_to([P, BATCH, FHEADS, FD]),
                        qkv[:, half::HALVES, 2 * D:3 * D].rearrange("p s (h d) -> p s h d", d=FD), ALU.mult))
                    nc.vector.tensor_reduce(mixed[:, HALVES * t + half, :], p[:].rearrange("p s c -> p c s"),
                                            AX.X, ALU.add).then_inc(mixed_ready, 1)
                    dve.wait_ge(mixed_ready, n + 1)
            dve.wait_ge(y_psum, 1)
            eights = lambda z: z.rearrange("p (h t) c -> p h (t c)", h=2)
            steps.step(nc.vector.tensor_tensor(eights(rsd[:]), eights(g.x[:]), pair[0], ALU.add))
            norm_stats(nc, steps, nb, rsd)
            norm_scale(nc, dve, steps, nb, 1)
            norm_apply(nc, steps, nb, rsd, h)
            all_rows = lambda j: gain[:, j, :].unsqueeze(1).broadcast_to([P, TILES, D])
            steps.step(nc.vector.tensor_tensor(h[:], h[:], all_rows(0), ALU.mult))
            nc.vector.tensor_tensor(h[:], h[:], all_rows(1), ALU.add).then_inc(h_ready, 1)
            dve.wait_ge(ht_psum, 2)
            nc.vector.tensor_copy(ht[:, BANK:], bank[5]).then_inc(ht_ready, 1)
            dve.wait_ge(logit_psum, 1)
            steps.step(nc.vector.tensor_copy(logit[:].rearrange("p t e -> p (t e)"), bank[2][:, 0:TILES * EXPERTS]))
            steps.step(nc.vector.tensor_reduce(lmax[:], logit[:], AX.X, ALU.max))
            bce = lambda z: z[:].unsqueeze(2).broadcast_to([P, TILES, EXPERTS])
            nc.vector.tensor_tensor(logit[:], logit[:], bce(lmax), ALU.subtract).then_inc(lsub_ready, 1)
            dve.wait_ge(lexp_ready, 1)
            steps.step(nc.vector.tensor_reduce(lsum[:], logit[:], AX.X, ALU.add))
            steps.step(nc.vector.reciprocal(lmax[:], lsum[:]))
            steps.step(nc.vector.tensor_tensor(logit[:], logit[:], bce(lmax), ALU.mult))
            for t in range(TILES):
                steps.add(nc.vector.max(best[:, t, :], logit[:, t, :]))
            steps.settle()
            for t in range(TILES):
                steps.add(nc.vector.max_index(place[:, t, :], best[:, t, :], logit[:, t, :]))
            steps.settle()
            steps.step(nc.vector.tensor_copy(placef[:], place[:, :, 0:2]))
            steps.step(nc.vector.tensor_tensor(chosen[:], placef[:, :, 0], placef[:, :, 1], ALU.max))
            dve.wait_ge(const_done, 1)
            nc.vector.tensor_tensor(mask[:], bce(chosen), number[:].unsqueeze(1).broadcast_to([P, TILES, EXPERTS]),
                                    ALU.is_equal).then_inc(mask_ready, 1)
            dve.wait_ge(maskt_psum, 1)
            steps.step(nc.vector.tensor_copy(halves(maskt[:]), pair[1][0:EXPERTS]))
            nc.vector.tensor_copy(maskt_b[:], maskt[:]).then_inc(maskt_ready, 1)

            def masked(e, k, first):
                dve.wait_ge(he_ready, e + 1)
                dve.wait_ge(mask_bc, e + 1)
                if not first:
                    dve.wait_ge(w2_done, e - 1)
                nc.vector.tensor_tensor(halves(hem[k][:]), halves(he[k][:]), pair[2], ALU.mult).then_inc(hem_ready, 1)

            for k in range(2):
                masked(k, k, True)
            with dve.Fori(1, EXPERTS // 2) as i:
                for k in range(2):
                    masked(2 * i + k, k, False)
            dve.wait_ge(w2_done, EXPERTS)
            steps.step(nc.vector.tensor_tensor(eights(rsd[:]), eights(h[:]), pair[3], ALU.add))
            norm_stats(nc, steps, nb, rsd)
            norm_scale(nc, dve, steps, nb, 2)
            norm_apply(nc, steps, nb, rsd, h)
            steps.step(nc.vector.tensor_tensor(h[:], h[:], all_rows(2), ALU.mult))
            steps.step(nc.vector.tensor_tensor(h[:], h[:], all_rows(3), ALU.add))
            steps.step(nc.vector.tensor_tensor(rsd[:], h[:], g.x[:], ALU.add))
            norm_stats(nc, steps, nb, rsd)
            norm_scale(nc, dve, steps, nb, 3)
            norm_apply(nc, steps, nb, rsd, g.x)


GHEADS, GK = 16, 64
GPAIRS = GHEADS // 2
GW = GK + 1
CK = P + 2 * P
MASKED = -1e30


class GraphWeights(Weights):
    def __init__(self, nc, ctx, a):
        super().__init__(nc, ctx, "graph")
        self.w_qk, self.wv = self.sb("g_wqk", [P, 2, GHEADS * GK]), self.sb("g_wv", [P, GHEADS * GK])
        self.wo = self.sb("g_wo", [P, GPAIRS, D])
        self.gamma_in, self.gamma_out = self.sb("gamma_in", [P, 1]), self.sb("gamma_out", [P, D])
        self.b_g = self.sb("graph_b", [P, 2, GK])
        self.pairs = [
            (self.w_qk[:, 0, :], a["L1_attn_Wq"]), (self.w_qk[:, 1, :], a["L1_attn_Wk"]), (self.wv[:], a["L1_attn_Wv"]),
            (self.wo[:], a["L1_attn_Wo"].rearrange("(c p) n -> p c n", p=P)), (self.gamma_in[:], a["L1_attn_gamma_in"]),
            (self.gamma_out[:], every_row(a["L1_attn_gamma_out"])), (self.b_g[:, 0, :], every_row(a["L1_attn_gnn_b"][0])),
            (self.b_g[:, 1, :], every_row(a["L1_attn_gnn_b"][1])),
        ]


def graph_attention(nc, g, a):
    with ExitStack() as ctx:
        r = Resources(nc, ctx, g.sems, "graph")
        given = g.graph
        w_qk, wv, wo, b_g = given.w_qk, given.wv, given.wo, given.b_g
        gamma_in, gamma_out = given.gamma_in, given.gamma_out
        lin_wo = r.sb("g_lin_wo", [P, GPAIRS, D])
        lin_t = r.sb("lin_t_diag", [P, P])
        lin_b = r.sb("lin_b_col", [P, 1])
        w_g = [r.sb(f"graph_w_diag{l}", [P, P]) for l in range(2)]
        const_row = r.sb("lin_b_wo_row", [1, D])
        ident_b = r.sb("identity_b", [P, P], BF16)
        mask = r.sb("causal_mask", [P, P], BF16)
        head_sel = r.sb("head_select", [P, 2])
        xh = r.sb("xh_rows", [P, TILES, D])
        xnt = r.sb("xn_cols", [P, TOK])
        xb = r.sb("xn_cols_batch", [P, SEQ])
        q = r.sb("gq_cols", [P, GPAIRS, SEQ])
        k = r.sb("gk_cols", [P, GPAIRS, SEQ])
        qk = r.sb("gqk_products", [P, GPAIRS, SEQ])
        v = r.sb("g_values", [P, QT, GHEADS, GK])
        v_hi = r.sb("g_values_hi", [P, QT, GHEADS, GW], F16)
        v_lo = r.sb("g_values_lo", [P, QT, GHEADS, GW], F16)
        fb = r.sb("feats_plus_bias", [P, QT, GHEADS, GK])
        e = [r.sb(f"g_probs{i}", [P, 2, CK]) for i in range(2)]
        et_hi = r.sb("g_probs_cols_hi", [P, GHEADS, CK], F16)
        et_lo = r.sb("g_probs_cols_lo", [P, GHEADS, CK], F16)
        negmax = r.sb("g_negmax", [P, QT, GHEADS])
        sdiag = r.sb("diag_scores", [P, QT, GHEADS])
        o = r.sb("g_out_raw", [P, QT, GHEADS, GW])
        rs = r.sb("g_rsum", [P, QT, GHEADS])
        pd = r.sb("diag_probs", [P, QT, GHEADS])
        off = r.sb("one_minus_diag", [P, QT, GHEADS])
        rdeg = r.sb("inv_degree", [P, QT, GHEADS])
        keep, take = r.sb("keep_share", [P, QT, GHEADS]), r.sb("take_share", [P, QT, GHEADS])
        out_n = r.sb("g_out", [P, QT, GHEADS, GK])
        m = r.sb("propagated", [P, QT, GHEADS, GK])
        mt = r.sb("propagated_cols", [P, QT, GPAIRS, P])
        f1 = r.sb("feats1", [P, QT, GHEADS, GK])
        f1_hi = r.sb("feats1_hi", [P, QT, GHEADS, GK], F16)
        f1_lo = r.sb("feats1_lo", [P, QT, GHEADS, GK], F16)
        ot = r.sb("g_out_cols", [P, QT, GPAIRS, P])
        y = r.sb("g_y_rows", [P, TILES, D])
        nb = NormBuffers(r, "graph_norm")
        zeroed, loaded, const_done, lin_psum, lin_ready, xh_ready = (r.sem(n) for n in (
            "zeroed", "loaded", "const_done", "lin_psum", "lin_ready", "xh_ready"))
        xt_psum, xt_ready, xb_ready, v_psum, v_ready, v_ones = (r.sem(n) for n in (
            "xt_psum", "xt_ready", "xb_ready", "v_psum", "v_ready", "v_ones"))
        qk_psum, prod_ready, diag_psum, sdiag_ready = (r.sem(n) for n in (
            "qk_psum", "prod_ready", "diag_psum", "sdiag_ready"))
        scored, max_ready, exp_ready, turned, et_hi_ready, et_lo_ready = (r.sem(n) for n in (
            "scored", "max_ready", "exp_ready", "turned", "et_hi_ready", "et_lo_ready"))
        pv_done, o_ready, dsub_ready, dexp_ready, stats_ready, out_ready = (r.sem(n) for n in (
            "pv_done", "o_ready", "dsub_ready", "dexp_ready", "stats_ready", "out_ready"))
        fb_ready, kept, m_ready, m_turned, mt_ready, h_psum = (r.sem(n) for n in (
            "fb_ready", "kept", "m_ready", "m_turned", "mt_ready", "h_psum"))
        pre_ready, feat_ready, pv1_done, qk_ready, out_turned, ot_ready = (r.sem(n) for n in (
            "pre_ready", "feat_ready", "pv1_done", "qk_ready", "out_turned", "ot_ready"))
        f_turned, ft_ready, y_psum, y_ready, dve_steps = (r.sem(n) for n in (
            "f_turned", "ft_ready", "y_psum", "y_ready", "dve_steps"))
        end_steps, end_steps_v, v_hi_ready, v_lo_ready, f1_lo_ready, taken = (r.sem(n) for n in (
            "end_steps", "end_steps_v", "v_hi_ready", "v_lo_ready", "f1_lo_ready", "taken"))
        bank = [g.psum[:, i, :] for i in range(8)]
        pair = [g.psum[:, 2 * i:2 * i + 2, :] for i in range(4)]
        flat = lambda z, qt: z[:, qt].rearrange("p h d -> p (h d)")
        two = lambda z: z.rearrange("p (h n) -> p h n", h=2)
        spread = lambda z, qt: z[:, qt, :].unsqueeze(2).broadcast_to([P, GHEADS, GK])
        heads = lambda z: z.rearrange("p (h d) -> p h d", d=GK)
        block = ctx.enter_context(nc.Block())

        @block.sync
        def _(sp):
            sp.wait_ge(zeroed, 1)
            for i in range(2):
                rows = slice(i * GK, (i + 1) * GK)
                sp.dma_start(lin_t[rows, rows], a["L1_attn_lin_w"]).then_inc(loaded, 16)
                sp.dma_start(lin_b[rows, :], a["L1_attn_lin_b"]).then_inc(loaded, 16)
                for l in range(2):
                    sp.dma_start(w_g[l][rows, rows], a["L1_attn_gnn_w"][l]).then_inc(loaded, 16)

        LOADS = 8 * 16
        @block.gpsimd
        def _(pool):
            steps = Tally(pool, end_steps)
            for z in (lin_t, w_g[0]):
                nc.gpsimd.memset(z[:], 0.0)
            nc.gpsimd.memset(w_g[1][:], 0.0).then_inc(zeroed, 1)
            nc.gpsimd.memset(v_hi[:, :, :, GK], 1.0).then_inc(v_ones, 1)
            nc.gpsimd.memset(v_lo[:, :, :, GK], 0.0).then_inc(v_ones, 1)
            steps.add(nc.gpsimd.memset(mask[:], 0.0))
            steps.add(nc.gpsimd.memset(ident_b[:], 0.0))
            steps.step(nc.gpsimd.memset(head_sel[:], 1.0))
            nc.gpsimd.affine_select(out=mask[:], in_=mask[:], compare_op=ALU.is_ge, fill=MASKED, base=0,
                                    pattern=[[-1, P]], channel_multiplier=1).then_inc(const_done, 1)
            nc.gpsimd.affine_select(out=ident_b[:], in_=ident_b[:], compare_op=ALU.not_equal, fill=1.0, base=0,
                                    pattern=[[-1, P]], channel_multiplier=1).then_inc(const_done, 1)
            steps.step(nc.gpsimd.affine_select(out=head_sel[:], in_=head_sel[:], compare_op=ALU.is_ge, fill=0.0,
                                               base=0, pattern=[[-GK, 2]], channel_multiplier=1))
            nc.gpsimd.affine_select(out=head_sel[:], in_=head_sel[:], compare_op=ALU.is_ge, fill=0.0, base=GK - 1,
                                    pattern=[[GK, 2]], channel_multiplier=-1).then_inc(const_done, 1)

            def copy_batch(b):
                nc.gpsimd.tensor_copy(xb[:], xnt[:, ds(b * SEQ, SEQ)]).then_inc(xb_ready, 1)

            def keep_share(f, qt):
                nc.gpsimd.tensor_tensor(m[:, qt], f[:, qt], spread(keep, qt), ALU.mult).then_inc(kept, 1)

            given.wait(pool)
            b_all = lambda l: b_g[:, l, :].unsqueeze(1).broadcast_to([P, GHEADS, GK])

            def diagonal_products(b):
                pool.wait_ge(qk_ready, GPAIRS * b + GPAIRS)
                nc.gpsimd.tensor_tensor(qk[:], q[:], k[:], ALU.mult).then_inc(prod_ready, 1)

            def values_low(b):
                for n in range(4):
                    qt, some = n // 2, slice(8 * (n % 2), 8 * (n % 2) + 8)
                    pool.wait_ge(v_hi_ready, 4 * b + n + 1)
                    nc.gpsimd.tensor_tensor(v_lo[:, qt, some, 0:GK], v[:, qt, some, :], v_hi[:, qt, some, 0:GK],
                                            ALU.subtract).then_inc(v_lo_ready, 1)

            def batch(b, more, next_more):
                for qt in range(QT):
                    nc.gpsimd.tensor_tensor(fb[:, qt], v[:, qt], b_all(0), ALU.add).then_inc(fb_ready, 1)
                pool.wait_ge(stats_ready, 2 * b + 1)
                for qt in range(QT):
                    keep_share(v, qt)
                for qt in range(QT):
                    pool.wait_ge(m_ready, 4 * b + qt + 1)
                    nc.gpsimd.tensor_tensor(out_n[:, qt], o[:, qt, :, 0:GK], spread(rs, qt), ALU.mult)\
                        .then_inc(out_ready, 1)
                if more:
                    diagonal_products(b + 1)
                for qt in range(QT):
                    pool.wait_ge(feat_ready, 6 * b + 2 * qt + 1)
                    pool.wait_ge(m_turned, 4 * b + qt + 1)
                    keep_share(f1, qt)
                for qt in range(QT):
                    pool.wait_ge(feat_ready, 6 * b + 2 * qt + 2)
                    nc.gpsimd.tensor_tensor(fb[:, qt], f1[:, qt], b_all(1), ALU.add).then_inc(fb_ready, 1)
                if next_more:
                    pool.wait_ge(v_psum, 4 * b + 8)
                    copy_batch(b + 2)
                if more:
                    values_low(b + 1)

            pool.wait_ge(xt_ready, 2)
            copy_batch(0)
            diagonal_products(0)
            pool.wait_ge(v_psum, 4)
            copy_batch(1)
            values_low(0)
            batch(0, True, True)
            with pool.Fori(1, BATCH - 2) as b:
                batch(b, True, True)
            batch(BATCH - 2, True, False)
            batch(BATCH - 1, False, False)

        @block.tensor
        def _(pe):
            pe.wait_ge(xh_ready, 1)
            transpose_rows(nc, pe, xh, None, g.ident[:], bank[4:6], xt_psum)
            pe.wait_ge(const_done, 3)
            pe.wait_ge(v_ones, 2)

            def queries_keys(b, pairs):
                for c in pairs:
                    if c >= 2:
                        pe.wait_ge(qk_ready, GPAIRS * b + c - 1)
                    for j in range(2):
                        ins = nc.tensor.matmul(bank[4 + c % 2][:, j * SEQ:(j + 1) * SEQ], w_qk[:, j, c * P:(c + 1) * P],
                                               xb[:], start=True, stop=True)
                    ins.then_inc(qk_psum, 1)

            def value_rows(b):
                for n in range(4):
                    qt, half = n // 2, n % 2
                    nc.tensor.matmul(bank[4 * qt + half], xb[:, qt * P:(qt + 1) * P],
                                     wv[:, half * BANK:(half + 1) * BANK], start=True, stop=True).then_inc(v_psum, 1)

            def diagonal_scores(b):
                pe.wait_ge(prod_ready, b + 1)
                for c in range(GPAIRS):
                    for qt in range(QT):
                        ins = nc.tensor.matmul(bank[7][:, (qt * GPAIRS + c) * 2:(qt * GPAIRS + c + 1) * 2],
                                               qk[:, c, qt * P:(qt + 1) * P], head_sel[:], start=True, stop=True)
                ins.then_inc(diag_psum, 1)

            def scores(b, c):
                if c >= 2:
                    pe.wait_ge(exp_ready, GPAIRS * b + c - 1)
                for h in range(2):
                    rows = slice(h * GK, (h + 1) * GK)
                    sb = bank[2 * (c % 2) + h]
                    nc.tensor.matmul(sb[:, 0:P], q[rows, c, 0:P], k[rows, c, 0:P], start=True, stop=False)
                    nc.tensor.matmul(sb[:, 0:P], ident_b[:], mask[:], start=False, stop=True)
                    nc.tensor.matmul(sb[:, P:CK], q[rows, c, P:SEQ], k[rows, c, :], start=True, stop=False)
                    ins = nc.tensor.matmul(sb[:, 2 * P:CK], ident_b[:], mask[:], start=False, stop=True)
                ins.then_inc(scored, 1)

            def turn(b, c):
                pe.wait_ge(exp_ready, GPAIRS * b + c + 1)
                if c >= 1:
                    pe.wait_ge(et_lo_ready, 2 * GPAIRS * b + 2 * c)
                for h in range(2):
                    for j in range(3):
                        ins = nc.tensor.transpose(bank[4 + h][:, j * P:(j + 1) * P], e[c % 2][:, h, j * P:(j + 1) * P],
                                                  g.ident[:])
                ins.then_inc(turned, 1)

            def propagate(dst, head, qt, f_hi, f_lo):
                blocks = ((0, 0),) if qt == 0 else ((1, 0), (2, 1))
                for n, (block_at, kt) in enumerate(blocks):
                    cols = slice(block_at * P, (block_at + 1) * P)
                    for i, (probs, f) in enumerate(((et_hi, f_hi), (et_lo, f_hi), (et_hi, f_lo))):
                        ins = nc.tensor.matmul(dst, probs[:, head, cols], f(kt), start=(n == 0 and i == 0),
                                               stop=(n == len(blocks) - 1 and i == 2))
                return ins

            def values(b, c):
                pe.wait_ge(et_lo_ready, 2 * GPAIRS * b + 2 * c + 2)
                if c >= 1:
                    pe.wait_ge(o_ready, GPAIRS * b + c)
                for h in range(2):
                    head = 2 * c + h
                    for qt in range(QT):
                        ins = propagate(bank[6][:, (2 * qt + h) * GW:(2 * qt + h + 1) * GW], head, qt,
                                        lambda kt: v_hi[:, kt, head, :], lambda kt: v_lo[:, kt, head, :])
                ins.then_inc(pv_done, 1)

            def turn_wide(src, qt, where, done):
                for c in range(GPAIRS):
                    ins = nc.tensor.transpose(bank[2 * where + c // 4][:, (c % 4) * P:(c % 4 + 1) * P],
                                              src[:, qt, 2 * c:2 * c + 2, :].rearrange("p h d -> p (h d)"), g.ident[:])
                ins.then_inc(done, 1)

            def graph_product(b, l, qt):
                pe.wait_ge(mt_ready, 4 * b + 2 * l + qt + 1)
                for c in range(GPAIRS):
                    ins = nc.tensor.matmul(bank[4 * qt + 2 + c // 4][:, (c % 4) * P:(c % 4 + 1) * P],
                                           mt[:, qt, c, :], w_g[l][:], start=True, stop=True)
                ins.then_inc(h_psum, 1)

            def turn_propagated(b, l, qt):
                pe.wait_ge(m_ready, 4 * b + 2 * l + qt + 1)
                turn_wide(m, qt, 2 * qt, m_turned)

            def batch(b, first, more):
                for c in range(GPAIRS + 2):
                    if c == 1 and not first:
                        pe.wait_ge(y_ready, 2 * b)
                    if c == 2:
                        pe.wait_ge(v_lo_ready, 4 * b + 4)
                    if c < GPAIRS:
                        scores(b, c)
                    if 1 <= c <= GPAIRS:
                        turn(b, c - 1)
                    if c >= 2:
                        values(b, c - 2)
                if more:
                    pe.wait_ge(xb_ready, b + 2)
                    queries_keys(b + 1, range(GPAIRS - 2))
                pe.wait_ge(o_ready, GPAIRS * b + GPAIRS)
                pe.wait_ge(sdiag_ready, b + 1)
                turn_propagated(b, 0, 0)
                if more:
                    queries_keys(b + 1, range(GPAIRS - 2, GPAIRS))
                graph_product(b, 0, 0)
                if more:
                    pe.wait_ge(qk_ready, GPAIRS * b + 2 * GPAIRS)
                turn_propagated(b, 0, 1)
                graph_product(b, 0, 1)
                for l in range(2):
                    if l == 1:
                        for qt in range(QT):
                            turn_propagated(b, 1, qt)
                        for qt in range(QT):
                            graph_product(b, 1, qt)
                    else:
                        for qt in range(QT):
                            pe.wait_ge(out_ready, 2 * b + qt + 1)
                            turn_wide(out_n, qt, 2 * qt, out_turned)
                        if more:
                            pe.wait_ge(pre_ready, 4 * b + 2)
                            diagonal_scores(b + 1)
                        for qt in range(QT):
                            if qt == 1 and more:
                                pe.wait_ge(sdiag_ready, b + 2)
                            pe.wait_ge(f1_lo_ready, 2 * b + qt + 1)
                            for head in range(GHEADS):
                                ins = propagate(bank[4 * qt + 2 + head // 8][:, (head % 8) * GK:(head % 8 + 1) * GK],
                                                head, qt, lambda kt: f1_hi[:, kt, head, :],
                                                lambda kt: f1_lo[:, kt, head, :])
                            ins.then_inc(pv1_done, 1)
                        for qt in range(QT):
                            pe.wait_ge(ot_ready, 2 * b + qt + 1)
                if more:
                    value_rows(b + 1)
                for qt in range(QT):
                    pe.wait_ge(pre_ready, 4 * b + 3 + qt)
                    for c in range(GPAIRS):
                        nc.tensor.matmul(bank[4 * qt + 2][:, 0:D], ot[:, qt, c, :], wo[:, c, :], start=(c == 0),
                                         stop=False)
                for qt in range(QT):
                    pe.wait_ge(feat_ready, 6 * b + 5 + qt)
                    if more:
                        pe.wait_ge(v_ready, 4 * b + 6 + 2 * qt)
                    turn_wide(m, qt, 2 * qt, f_turned)
                for qt in range(QT):
                    pe.wait_ge(ft_ready, 2 * b + qt + 1)
                    dst = bank[4 * qt + 2][:, 0:D]
                    for c in range(GPAIRS):
                        nc.tensor.matmul(dst, mt[:, qt, c, :], lin_wo[:, c, :], start=False, stop=False)
                    nc.tensor.matmul(dst, g.ones_row[:], const_row[:], start=False, stop=True).then_inc(y_psum, 1)

            pe.wait_ge(xt_ready, 2)
            given.wait(pe)
            pe.wait_ge(xb_ready, 1)
            queries_keys(0, range(GPAIRS))
            pe.wait_ge(qk_ready, GPAIRS)
            value_rows(0)
            pe.wait_ge(v_ready, 4)
            pe.wait_ge(loaded, LOADS)
            for c in range(GPAIRS):
                ins = nc.tensor.matmul(bank[c // 4][:, (c % 4) * D:(c % 4 + 1) * D], lin_t[:], wo[:, c, :],
                                       start=True, stop=True)
            for c in range(GPAIRS):
                ins = nc.tensor.matmul(bank[2][0:1, 0:D], lin_b[:], wo[:, c, :], start=(c == 0), stop=(c == GPAIRS - 1))
            ins.then_inc(lin_psum, 1)
            diagonal_scores(0)
            pe.wait_ge(sdiag_ready, 1)
            pe.wait_ge(lin_ready, 1)
            batch(0, True, True)
            with pe.Fori(1, BATCH - 1) as b:
                batch(b, False, True)
            batch(BATCH - 1, False, False)

        @block.scalar
        def _(act):
            norm_root(nc, act, nb, 1)
            given.wait(act)
            act.wait_ge(xt_psum, 1)
            nc.scalar.activation(xnt[:, 0:BANK], bank[4], ACT.Copy, scale=gamma_in[:, 0:1]).then_inc(xt_ready, 1)

            def copy_queries_keys(b, pairs):
                for c in pairs:
                    act.wait_ge(qk_psum, GPAIRS * b + c + 1)
                    nc.scalar.activation(q[:, c, :], bank[4 + c % 2][:, 0:SEQ], ACT.Copy, scale=GK ** -0.5)
                    nc.scalar.copy(k[:, c, :], bank[4 + c % 2][:, SEQ:]).then_inc(qk_ready, 1)

            def copy_cols(dst, qt, done):
                nc.scalar.copy(two(dst[:, qt].rearrange("p c n -> p (c n)")), pair[2 * qt]).then_inc(done, 1)

            def values_high(b):
                for n in range(4):
                    qt, some = n // 2, slice(8 * (n % 2), 8 * (n % 2) + 8)
                    act.wait_ge(v_ready, 4 * b + n + 1)
                    nc.scalar.copy(v_hi[:, qt, some, 0:GK], v[:, qt, some, :]).then_inc(v_hi_ready, 1)

            def copy_propagated(b, l, qt):
                act.wait_ge(m_turned, 4 * b + 2 * l + qt + 1)
                copy_cols(mt, qt, mt_ready)

            def batch(b, more):
                for c in range(GPAIRS + 1):
                    if c >= 1:
                        act.wait_ge(turned, GPAIRS * b + c)
                        for h in range(2):
                            nc.scalar.copy(et_hi[:, 2 * c - 2 + h, :], bank[4 + h][:, 0:CK]).then_inc(et_hi_ready, 1)
                    if c < GPAIRS:
                        act.wait_ge(max_ready, GPAIRS * b + c + 1)
                        if c >= 2:
                            act.wait_ge(turned, GPAIRS * b + c - 1)
                        for h in range(2):
                            for lo, hi, qt in ((0, P, 0), (P, CK, 1)):
                                ins = nc.scalar.activation(e[c % 2][:, h, lo:hi], bank[2 * (c % 2) + h][:, lo:hi],
                                                           ACT.Exp, bias=negmax[:, qt, 2 * c + h:2 * c + h + 1])
                        ins.then_inc(exp_ready, 1)
                act.wait_ge(dsub_ready, b + 1)
                nc.scalar.activation(pd[:], pd[:], ACT.Exp).then_inc(dexp_ready, 1)
                if more:
                    copy_queries_keys(b + 1, range(GPAIRS - 2))
                copy_propagated(b, 0, 0)
                if more:
                    copy_queries_keys(b + 1, range(GPAIRS - 2, GPAIRS))
                copy_propagated(b, 0, 1)
                for l in range(2):
                    if l == 1:
                        for qt in range(QT):
                            copy_propagated(b, 1, qt)
                    for qt in range(QT):
                        act.wait_ge(pre_ready, 4 * b + 2 * l + qt + 1)
                        for dst in ((f1, f1_hi) if l == 0 else (m, )):
                            nc.scalar.activation(dst[:, qt], fb[:, qt], ACT.Gelu).then_inc(feat_ready, 1)
                    if l == 0:
                        for qt in range(QT):
                            act.wait_ge(out_turned, 2 * b + qt + 1)
                            copy_cols(ot, qt, ot_ready)
                if more:
                    values_high(b + 1)
                for qt in range(QT):
                    act.wait_ge(f_turned, 2 * b + qt + 1)
                    copy_cols(mt, qt, ft_ready)

            copy_queries_keys(0, range(GPAIRS))
            values_high(0)
            batch(0, True)
            with act.Fori(1, BATCH - 1) as b:
                batch(b, True)
            batch(BATCH - 1, False)
            norm_root(nc, act, nb, 2)
            norm_root(nc, act, nb, 3)

        DVE_CHAIN = 5

        @block.vector
        def _(dve):
            ends = Tally(dve, end_steps_v)
            norm_stats(nc, ends, nb, g.x)
            norm_scale(nc, dve, ends, nb, 1)
            norm_apply(nc, ends, nb, g.x, xh)
            nc.vector.memset(pd[:], 0.0).then_inc(xh_ready, 1)
            given.wait(dve)
            dve.wait_ge(xt_psum, 2)
            nc.vector.tensor_scalar(xnt[:, BANK:], bank[5], gamma_in[:, 0:1], None, ALU.mult).then_inc(xt_ready, 1)

            def copy_values(b):
                for n in range(4):
                    qt, half = n // 2, n % 2
                    dve.wait_ge(v_psum, 4 * b + n + 1)
                    nc.vector.tensor_copy(v[:, qt, 8 * half:8 * half + 8, :], heads(bank[4 * qt + half]))\
                        .then_inc(v_ready, 1)

            def copy_diagonal(b):
                dve.wait_ge(diag_psum, b + 1)
                nc.vector.tensor_copy(sdiag[:].rearrange("p q h -> p (q h)"), bank[7][:, 0:2 * GHEADS])\
                    .then_inc(sdiag_ready, 1)

            def take_share(b, l, qt):
                if l == 0:
                    dst, src, by = out_n[:, qt], o[:, qt, :, 0:GK], spread(take, qt)
                else:
                    dve.wait_ge(out_turned, 2 * b + qt + 1)
                    dve.wait_ge(pv1_done, 2 * b + qt + 1)
                    by_bank = lambda z: z.rearrange("p (n h) d -> p n h d", n=2)
                    dst, by = by_bank(out_n[:, qt]), by_bank(spread(take, qt))
                    src = pair[2 * qt + 1].rearrange("p n (h d) -> p n h d", d=GK)
                nc.vector.tensor_tensor(dst, src, by, ALU.mult).then_inc(taken, 1)

            def add_shares(b, l, qt):
                dve.wait_ge(taken, 4 * b + 2 * l + qt + 1)
                dve.wait_ge(kept, 4 * b + 2 * l + qt + 1)
                nc.vector.tensor_tensor(m[:, qt], m[:, qt], out_n[:, qt], ALU.add).then_inc(m_ready, 1)

            def batch(b, more):
                steps = Tally(dve, dve_steps, DVE_CHAIN * b)
                for c in range(GPAIRS + 2):
                    if c < GPAIRS:
                        dve.wait_ge(scored, GPAIRS * b + c + 1)
                        sb = g.psum[:, 2 * (c % 2):2 * (c % 2) + 2, :]
                        nc.vector.tensor_reduce(negmax[:, 0, 2 * c:2 * c + 2], sb[:, :, 0:P], AX.X, ALU.max, negate=True)
                        nc.vector.tensor_reduce(negmax[:, 1, 2 * c:2 * c + 2], sb[:, :, P:CK], AX.X, ALU.max,
                                                negate=True).then_inc(max_ready, 1)
                    if 1 <= c <= GPAIRS:
                        for h in range(2):
                            dve.wait_ge(et_hi_ready, 2 * GPAIRS * b + 2 * c - 1 + h)
                            nc.vector.tensor_tensor(et_lo[:, 2 * c - 2 + h, :], bank[4 + h][:, 0:CK],
                                                    et_hi[:, 2 * c - 2 + h, :], ALU.subtract).then_inc(et_lo_ready, 1)
                    if c >= 2:
                        dve.wait_ge(pv_done, GPAIRS * b + c - 1)
                        nc.vector.tensor_copy(
                            o[:, :, 2 * c - 4:2 * c - 2, :].rearrange("p q h w -> p q (h w)"),
                            bank[6][:, 0:4 * GW].rearrange("p (q n) -> p q n", q=QT)).then_inc(o_ready, 1)
                    if c == GPAIRS:
                        dve.wait_ge(max_ready, GPAIRS * b + GPAIRS)
                        dve.wait_ge(sdiag_ready, b + 1)
                        nc.vector.tensor_tensor(pd[:], sdiag[:], negmax[:], ALU.add).then_inc(dsub_ready, 1)
                dve.wait_ge(o_ready, GPAIRS * b + GPAIRS)
                steps.step(nc.vector.reciprocal(rs[:], o[:, :, :, GK]))
                dve.wait_ge(dexp_ready, b + 1)
                steps.step(nc.vector.tensor_tensor(pd[:], pd[:], rs[:], ALU.mult))
                steps.add(nc.vector.tensor_scalar(off[:], pd[:], -1.0, 1.0, ALU.mult, ALU.add))
                steps.step(nc.vector.tensor_scalar(rdeg[:], pd[:], -1.0, 2.0, ALU.mult, ALU.add))
                steps.step(nc.vector.reciprocal(rdeg[:], rdeg[:]))
                nc.vector.tensor_tensor(keep[:], off[:], rdeg[:], ALU.mult).then_inc(stats_ready, 1)
                nc.vector.tensor_tensor(take[:], rs[:], rdeg[:], ALU.mult).then_inc(stats_ready, 1)
                dve.wait_ge(stats_ready, 2 * b + 2)
                for l in range(2):
                    if l == 0:
                        take_share(b, 0, 0)
                        take_share(b, 0, 1)
                        add_shares(b, 0, 0)
                        add_shares(b, 0, 1)
                    else:
                        for qt in range(QT):
                            take_share(b, 1, qt)
                            add_shares(b, 1, qt)
                    for qt in range(QT):
                        dve.wait_ge(h_psum, 4 * b + 2 * l + qt + 1)
                        dve.wait_ge(fb_ready, 4 * b + 2 * l + qt + 1)
                        nc.vector.tensor_tensor(two(flat(fb, qt)), two(flat(fb, qt)), pair[2 * qt + 1], ALU.add)\
                            .then_inc(pre_ready, 1)
                    if l == 1 and more:
                        copy_values(b + 1)
                    if l == 0:
                        if more:
                            copy_diagonal(b + 1)
                        for qt in range(QT):
                            dve.wait_ge(feat_ready, 6 * b + 2 * qt + 2)
                            nc.vector.tensor_tensor(f1_lo[:, qt], f1[:, qt], f1_hi[:, qt], ALU.subtract)\
                                .then_inc(f1_lo_ready, 1)
                for qt in range(QT):
                    dve.wait_ge(y_psum, 2 * b + qt + 1)
                    nc.vector.tensor_copy(y[:, ds(QT * b + qt, 1), :].rearrange("p o c -> p (o c)"),
                                          bank[4 * qt + 2][:, 0:D]).then_inc(y_ready, 1)

            copy_values(0)
            dve.wait_ge(lin_psum, 1)
            nc.vector.tensor_copy(two(lin_wo[:].rearrange("p c n -> p (c n)")), pair[0])
            nc.vector.tensor_copy(const_row[:], bank[2][0:1, 0:D]).then_inc(lin_ready, 1)
            copy_diagonal(0)
            batch(0, True)
            with dve.Fori(1, BATCH - 1) as b:
                batch(b, True)
            batch(BATCH - 1, False)
            dve.wait_ge(y_ready, 2 * BATCH)
            norm_stats(nc, ends, nb, y)
            norm_scale(nc, dve, ends, nb, 2)
            norm_apply(nc, ends, nb, y, xh)
            ends.step(nc.vector.tensor_tensor(xh[:], xh[:], gamma_out[:].unsqueeze(1).broadcast_to([P, TILES, D]),
                                              ALU.mult))
            ends.step(nc.vector.tensor_tensor(xh[:], xh[:], g.x[:], ALU.add))
            norm_stats(nc, ends, nb, xh)
            norm_scale(nc, dve, ends, nb, 3)
            norm_apply(nc, ends, nb, xh, g.x)


NHEADS, NK = 16, 8
NW = NK + 1


class NarrowWeights(Weights):
    def __init__(self, nc, ctx, a):
        super().__init__(nc, ctx, "narrow")
        self.w, self.bqk = self.sb("n_w", [P, 4, D]), self.sb("n_bqk", [P, 2])
        self.bv, self.bo = self.sb("n_bv", [P, D]), self.sb("n_bo", [1, D])
        self.pairs = [(self.w[:, j, :], a[f"L1_xattn_W{name}"]) for j, name in enumerate("qkvo")] + [
            (self.bqk[:, 0:1], a["L1_xattn_bq"]), (self.bqk[:, 1:2], a["L1_xattn_bk"]),
            (self.bv[:], every_row(a["L1_xattn_bv"])), (self.bo[:], one_row(a["L1_xattn_bo"])),
        ]


def narrow_attention(nc, g, a):
    with ExitStack() as ctx:
        r = Resources(nc, ctx, g.sems, "narrow")
        given = g.narrow
        w, bqk, bv, bo = given.w, given.bqk, given.bv, given.bo
        sel = r.sb("head_rows", [P, NHEADS])
        q, k = r.sb("nq_cols", [P, TOK]), r.sb("nk_cols", [P, TOK])
        q_parts = [r.sb(f"nq_part{i}", [P, TOK], F16) for i in range(2)]
        k_parts = [r.sb(f"nk_part{i}", [P, TOK], F16) for i in range(2)]
        qm = [[r.sb(f"nq_head{i}_part{j}", [P, TOK], F16) for j in range(2)] for i in range(2)]
        v = r.sb("n_value_rows", [P, TILES, NHEADS, NK])
        v_parts = [r.sb(f"n_values_part{i}", [P, TILES, NHEADS, NW], F16) for i in range(2)]
        v_flat = [z[:].rearrange("p t h w -> p (t h w)") for z in v_parts]
        e = [r.sb(f"n_probs{i}", [P, QT, SEQ]) for i in range(2)]
        et = [[r.sb(f"n_probs_cols{i}_part{j}", [P, QT, SEQ], F16) for j in range(2)] for i in range(2)]
        negmax = [r.sb(f"n_negmax{i}", [P, QT]) for i in range(4)]
        o = r.sb("n_out_raw", [P, TILES, NHEADS, NW])
        o_heads = o[:].rearrange("p t h w -> p t (h w)")
        rsum = r.sb("n_rsum", [P, TILES, NHEADS])
        on = r.sb("n_out", [P, TILES, D])
        ont = r.sb("n_out_cols", [P, TILES, P])
        rsd = r.sb("n_rows", [P, TILES, D])
        nb = NormBuffers(r, "narrow_norm")
        sel_ready, xt_psum, xt_ready, q_psum, q_ready = (r.sem(n) for n in (
            "sel_ready", "xt_psum", "xt_ready", "q_psum", "q_ready"))
        k_ready, v_psum, v_ready, v_ones, qm_ready, scored = (r.sem(n) for n in (
            "k_ready", "v_psum", "v_ready", "v_ones", "qm_ready", "scored"))
        max_ready, exp_ready, turned, et_hi_ready, et_lo_ready, pv_done = (r.sem(n) for n in (
            "max_ready", "exp_ready", "turned", "et_hi_ready", "et_lo_ready", "pv_done"))
        o_ready, on_ready, on_turned, ont_ready, y_psum, dve_steps = (r.sem(n) for n in (
            "o_ready", "on_ready", "on_turned", "ont_ready", "y_psum", "dve_steps"))
        pool_steps, q_hi_ready, k_hi_ready, v_hi_ready, lo_ready = (r.sem(n) for n in (
            "pool_steps", "q_hi_ready", "k_hi_ready", "v_hi_ready", "lo_ready"))
        PARTS = ((0, 0), (1, 0), (0, 1))
        bank = [g.psum[:, i, :] for i in range(8)]
        pair = [g.psum[:, 2 * i:2 * i + 2, :] for i in range(4)]
        score_bank = [bank[0], bank[1], bank[4], bank[5]]
        HUNITS = 2 * BATCH
        block = ctx.enter_context(nc.Block())

        @block.sync
        def _(sp):
            g.quantised.load(sp)

        @block.gpsimd
        def _(pool):
            steps = Tally(pool, pool_steps)
            nc.gpsimd.memset(v_parts[0][:, :, :, NK], 1.0).then_inc(v_ones, 1)
            nc.gpsimd.memset(v_parts[1][:, :, :, NK], 0.0).then_inc(v_ones, 1)
            steps.step(nc.gpsimd.memset(sel[:], 1.0))
            steps.step(nc.gpsimd.affine_select(out=sel[:], in_=sel[:], compare_op=ALU.is_ge, fill=0.0, base=0,
                                               pattern=[[-NK, NHEADS]], channel_multiplier=1))
            nc.gpsimd.affine_select(out=sel[:], in_=sel[:], compare_op=ALU.is_ge, fill=0.0, base=NK - 1,
                                    pattern=[[NK, NHEADS]], channel_multiplier=-1).then_inc(sel_ready, 1)
            pool.wait_ge(v_hi_ready, 1)
            nc.gpsimd.tensor_tensor(v_parts[1][:, :, :, 0:NK], v[:], v_parts[0][:, :, :, 0:NK], ALU.subtract)\
                .then_inc(lo_ready, 1)

        @block.tensor
        def _(pe):
            transpose_rows(nc, pe, g.x, None, g.ident[:], bank[0:2], xt_psum)
            given.wait(pe)
            for j in range(2):
                nc.tensor.matmul(bank[4 + j], w[:, 1, :], g.ct[:, j * BANK:(j + 1) * BANK], start=True, stop=True)
            for t in range(TILES):
                ins = nc.tensor.matmul(bank[6 + t // 4][:, (t % 4) * D:(t % 4 + 1) * D], g.ct[:, t * P:(t + 1) * P],
                                       w[:, 2, :], start=True, stop=True)
            ins.then_inc(v_psum, 1)
            pe.wait_ge(xt_ready, 2)
            for j in range(2):
                ins = nc.tensor.matmul(bank[2 + j], w[:, 0, :], g.xt[:, j * BANK:(j + 1) * BANK], start=True, stop=True)
            ins.then_inc(q_psum, 1)
            pe.wait_ge(v_ready, 1)
            pe.wait_ge(v_ones, 2)
            pe.wait_ge(lo_ready, 3)

            def scores(u, b, h, i, first):
                if not first:
                    pe.wait_ge(exp_ready, u - 3)
                for qt in range(QT):
                    at = b * SEQ + qt * P
                    for n, (x, y) in enumerate(PARTS):
                        ins = nc.tensor.matmul(score_bank[i][:, qt * SEQ:(qt + 1) * SEQ], qm[h][x][:, at:at + P],
                                               k_parts[y][:, b * SEQ:(b + 1) * SEQ], start=(n == 0), stop=(n == 2))
                ins.then_inc(scored, 1)

            def turn(u, i, first):
                pe.wait_ge(exp_ready, u + 1)
                if not first:
                    pe.wait_ge(et_lo_ready, u - 1)
                for qt in range(QT):
                    for kt in range(2):
                        ins = nc.tensor.transpose(bank[2 + i][:, (2 * qt + kt) * P:(2 * qt + kt + 1) * P],
                                                  e[i][:, qt, kt * P:(kt + 1) * P], g.ident[:])
                ins.then_inc(turned, 1)

            def values(u, p, b, h, i, first):
                pe.wait_ge(et_lo_ready, u + 1)
                if not first:
                    pe.wait_ge(o_ready, u - 1)
                for qt in range(QT):
                    for kt in range(2):
                        head = ds(((QT * b + kt) * NHEADS + h) * NW + p * (2 * NW), NW)
                        for n, (x, y) in enumerate(PARTS):
                            ins = nc.tensor.matmul(bank[6 + i][:, qt * NW:(qt + 1) * NW],
                                                   et[i][x][:, qt, kt * P:(kt + 1) * P], v_flat[y][:, head],
                                                   start=(kt == 0 and n == 0), stop=(kt == 1 and n == 2))
                ins.then_inc(pv_done, 1)

            def pair_steps(p, first, more):
                for j in range(HUNITS):
                    u, n = HUNITS * p + j, (j + 1) % HUNITS
                    h, b = n // BATCH, n % BATCH
                    if j + 1 < HUNITS or more:
                        if b == 0:
                            pe.wait_ge(qm_ready, 4 * (p if n else p + 1) + 2 * h + 2)
                        scores(u + 1, b, h, n % 4, first and j < 3)
                    if not (first and j < 1):
                        turn(u - 1, (j - 1) % 2, first and j < 3)
                    if not (first and j < 2):
                        jj = (j - 2) % HUNITS
                        values(u - 2, p if j >= 2 else p - 1, jj % BATCH, jj // BATCH, j % 2, first and j < 4)

            pe.wait_ge(qm_ready, 2)
            scores(0, 0, 0, 0, True)
            pair_steps(0, True, True)
            with pe.Fori(1, NHEADS // 2 - 1) as p:
                pair_steps(p, False, True)
            pair_steps(NHEADS // 2 - 1, False, False)
            last = NHEADS // 2 * HUNITS
            turn(last - 1, 1, False)
            values(last - 2, NHEADS // 2 - 1, BATCH - 2, 1, 0, False)
            values(last - 1, NHEADS // 2 - 1, BATCH - 1, 1, 1, False)
            pe.wait_ge(on_ready, 1)
            transpose_rows(nc, pe, on, None, g.ident[:], bank[2:4], on_turned)
            pe.wait_ge(ont_ready, 2)
            for t in range(TILES):
                y = bank[t // 4][:, (t % 4) * D:(t % 4 + 1) * D]
                nc.tensor.matmul(y, ont[:, t, :], w[:, 3, :], start=True, stop=False)
                ins = nc.tensor.matmul(y, g.ones_row[:], bo[:], start=False, stop=True)
            ins.then_inc(y_psum, 1)

        @block.scalar
        def _(act):
            act.wait_ge(xt_psum, 1)
            nc.scalar.copy(g.xt[:, 0:BANK], bank[0]).then_inc(xt_ready, 1)
            given.wait(act)
            act.wait_ge(v_psum, 1)
            nc.scalar.activation(halves(k[:]), pair[2], ACT.Identity, bias=bqk[:, 1:2]).then_inc(k_ready, 1)

            nc.scalar.activation(halves(k_parts[0][:]), pair[2], ACT.Identity, bias=bqk[:, 1:2]).then_inc(k_hi_ready, 1)
            act.wait_ge(v_ready, 1)
            nc.scalar.copy(v_parts[0][:, :, :, 0:NK], v[:]).then_inc(v_hi_ready, 1)
            act.wait_ge(q_ready, 1)
            nc.scalar.copy(q_parts[0][:], q[:]).then_inc(q_hi_ready, 1)

            def exps(u, i, k, first):
                act.wait_ge(max_ready, u + 1)
                if not first:
                    act.wait_ge(turned, u - 1)
                for qt in range(QT):
                    ins = nc.scalar.activation(e[i][:, qt, :], score_bank[k][:, qt * SEQ:(qt + 1) * SEQ], ACT.Exp,
                                               bias=negmax[k][:, qt:qt + 1])
                ins.then_inc(exp_ready, 1)

            def split_high(u, i, first):
                act.wait_ge(turned, u + 1)
                if not first:
                    act.wait_ge(pv_done, u - 1)
                nc.scalar.copy(et[i][0][:].rearrange("p q n -> p (q n)"), bank[2 + i]).then_inc(et_hi_ready, 1)

            def pair_steps(p, first):
                for j in range(HUNITS):
                    u = HUNITS * p + j
                    exps(u, j % 2, j % 4, first and j < 2)
                    if not (first and j < 1):
                        split_high(u - 1, (j - 1) % 2, first and j < 3)

            pair_steps(0, True)
            with act.Fori(1, NHEADS // 2) as p:
                pair_steps(p, False)
            split_high(NHEADS // 2 * HUNITS - 1, 1, False)
            act.wait_ge(on_turned, 1)
            nc.scalar.copy(ont[:, 0:4, :].rearrange("p t c -> p (t c)"), bank[2]).then_inc(ont_ready, 1)
            norm_root(nc, act, nb, 1)

        @block.vector
        def _(dve):
            steps = Tally(dve, dve_steps)
            dve.wait_ge(xt_psum, 2)
            nc.vector.tensor_copy(g.xt[:, BANK:], bank[1]).then_inc(xt_ready, 1)
            given.wait(dve)
            dve.wait_ge(v_psum, 1)
            for t in range(TILES):
                ins = nc.vector.tensor_tensor(v[:, t].rearrange("p h d -> p (h d)"),
                                              bank[6 + t // 4][:, (t % 4) * D:(t % 4 + 1) * D], bv[:], ALU.add)
            ins.then_inc(v_ready, 1)
            dve.wait_ge(q_psum, 1)
            nc.vector.tensor_scalar(halves(q[:]), pair[1], bqk[:, 0:1], NK ** -0.5, ALU.add, ALU.mult)\
                .then_inc(q_ready, 1)
            dve.wait_ge(k_ready, 1)
            dve.wait_ge(k_hi_ready, 1)
            nc.vector.tensor_tensor(k_parts[1][:], k[:], k_parts[0][:], ALU.subtract).then_inc(lo_ready, 1)
            dve.wait_ge(q_ready, 1)
            dve.wait_ge(q_hi_ready, 1)
            nc.vector.tensor_tensor(q_parts[1][:], q[:], q_parts[0][:], ALU.subtract).then_inc(lo_ready, 1)
            dve.wait_ge(lo_ready, 3)
            dve.wait_ge(sel_ready, 1)

            def mask_queries(head, i):
                for part in range(2):
                    nc.vector.tensor_scalar(qm[i][part][:], q_parts[part][:], sel[:, ds(head, 1)], None, ALU.mult)\
                        .then_inc(qm_ready, 1)

            def maxima(u, i):
                dve.wait_ge(scored, u + 1)
                nc.vector.tensor_reduce(negmax[i][:], score_bank[i].rearrange("p (q n) -> p q n", q=QT), AX.X, ALU.max,
                                        negate=True).then_inc(max_ready, 1)

            def split_low(u, i):
                dve.wait_ge(et_hi_ready, u + 1)
                nc.vector.tensor_tensor(et[i][1][:].rearrange("p q n -> p (q n)"), bank[2 + i],
                                        et[i][0][:].rearrange("p q n -> p (q n)"), ALU.subtract)\
                    .then_inc(et_lo_ready, 1)

            def copy_out(u, p, b, h, i):
                dve.wait_ge(pv_done, u + 1)
                nc.vector.tensor_copy(o_heads[:, QT * b:QT * b + QT, ds(h * NW + p * (2 * NW), NW)],
                                      bank[6 + i][:, 0:QT * NW].rearrange("p (q w) -> p q w", q=QT))\
                    .then_inc(o_ready, 1)

            def pair_steps(p, first, more):
                for j in range(HUNITS):
                    u, n = HUNITS * p + j, (j + 1) % HUNITS
                    if j + 1 < HUNITS or more:
                        maxima(u + 1, n % 4)
                    if n % BATCH == BATCH - 1 and more:
                        mask_queries(2 * p + 2 + n // BATCH, n // BATCH)
                    if not (first and j < 1):
                        split_low(u - 1, (j - 1) % 2)
                    if not (first and j < 2):
                        jj = (j - 2) % HUNITS
                        copy_out(u - 2, p if j >= 2 else p - 1, jj % BATCH, jj // BATCH, j % 2)

            mask_queries(0, 0)
            mask_queries(1, 1)
            maxima(0, 0)
            pair_steps(0, True, True)
            with dve.Fori(1, NHEADS // 2 - 1) as p:
                pair_steps(p, False, True)
            pair_steps(NHEADS // 2 - 1, False, False)
            last = NHEADS // 2 * HUNITS
            split_low(last - 1, 1)
            copy_out(last - 2, NHEADS // 2 - 1, BATCH - 2, 1, 0)
            copy_out(last - 1, NHEADS // 2 - 1, BATCH - 1, 1, 1)
            dve.wait_ge(o_ready, last)
            steps.step(nc.vector.reciprocal(rsum[:], o[:, :, :, NK]))
            nc.vector.tensor_tensor(on[:].rearrange("p t (h d) -> p (t h) d", d=NK),
                                    o[:, :, :, 0:NK].rearrange("p t h d -> p (t h) d"),
                                    rsum[:].rearrange("p t h -> p (t h)").unsqueeze(2)
                                    .broadcast_to([P, TILES * NHEADS, NK]), ALU.mult).then_inc(on_ready, 1)
            dve.wait_ge(on_turned, 2)
            nc.vector.tensor_copy(ont[:, 4:8, :].rearrange("p t c -> p (t c)"), bank[3]).then_inc(ont_ready, 1)
            dve.wait_ge(y_psum, 1)
            eights = lambda z: z.rearrange("p (h t) c -> p h (t c)", h=2)
            steps.step(nc.vector.tensor_tensor(eights(rsd[:]), eights(g.x[:]), pair[0], ALU.add))
            norm_stats(nc, steps, nb, rsd)
            norm_scale(nc, dve, steps, nb, 1)
            norm_apply(nc, steps, nb, rsd, g.x)


HID = 512
CHUNKS = HID // P
MAGIC = 1.5 * 2 ** 23
LEAST = 1e-5


class QuantisedWeights(Weights):
    def __init__(self, nc, ctx, a):
        super().__init__(nc, ctx, "qffn")
        self.w1, self.w2 = self.sb("w1_cols", [P, HID]), self.sb("w2_cols", [P, HID])
        self.taps, self.cb = self.sb("taps", [P, CHUNKS, 3]), self.sb("conv_bias", [P, CHUNKS])
        self.pairs = [
            (self.w1[:], a["L1_ffn_w1"]), (self.w2[:].rearrange("p (c n) -> p c n", c=CHUNKS), a["L1_ffn_w2"]),
            (self.taps[:], a["L1_ffn_conv_w"]), (self.cb[:], a["L1_ffn_conv_b"]),
        ]


def quantised_ffn(nc, g, a):
    with ExitStack() as ctx:
        r = Resources(nc, ctx, g.sems, "qffn")
        given = g.quantised
        w1, w2, taps, cb = given.w1, given.w2, given.taps, given.cb
        w2b = r.sb("w2_ternary", [P, HID], BF16)
        ones = r.sb("all_ones", [P, P])
        ident_b = r.sb("f_identity_b", [P, P], BF16)
        mag = r.sb("weight_magnitude", [P, 2])
        mean = r.sb("weight_mean", [P, 2])
        wscale = r.sb("weight_scale", [P, 2])
        wback = r.sb("weight_back", [P, 2])
        top = r.sb("row_top", [P, TILES])
        scale = r.sb("row_scale", [P, TILES])
        back = r.sb("row_back", [P, TILES])
        xq = r.sb("x_quant", [P, TILES, D])
        xqt = r.sb("x_quant_cols", [P, TOK])
        conv = [r.sb(f"conv{i}", [P, TOK]) for i in range(2)]
        act_cols = r.sb("silu_cols", [P, CHUNKS, TOK])
        top2 = r.sb("row_top2", [P, TILES])
        scale2 = r.sb("row_scale2", [P, TILES])
        back2 = r.sb("row_back2", [P, TILES])
        big = r.sb("rounded", [P, TILES, HID])
        hq = r.sb("hidden_int", [P, TILES, HID], BF16)
        hqt = r.sb("hidden_int_cols", [P, TILES, HID], BF16)
        rsd = r.sb("f_rows", [P, TILES, D])
        nb = NormBuffers(r, "f_norm")
        const_done, mag_ready, mag_psum, w_ready, xq_ready = (r.sem(n) for n in (
            "const_done", "mag_ready", "mag_psum", "w_ready", "xq_ready"))
        xt_psum, xt_ready, h_psum, mid_ready, conv_ready, silu_ready = (r.sem(n) for n in (
            "xt_psum", "xt_ready", "h_psum", "mid_ready", "conv_ready", "silu_ready"))
        g_psum, rounded_ready, hq_ready, hq_psum, hqt_ready, y_psum = (r.sem(n) for n in (
            "g_psum", "rounded_ready", "hq_ready", "hq_psum", "hqt_ready", "y_psum"))
        dve_steps, pool_steps = (r.sem(n) for n in (
            "dve_steps", "pool_steps"))
        bank = [g.psum[:, i, :] for i in range(8)]
        pair = [g.psum[:, 2 * i:2 * i + 2, :] for i in range(4)]
        block = ctx.enter_context(nc.Block())

        @block.gpsimd
        def _(pool):
            steps = Tally(pool, pool_steps)
            nc.gpsimd.memset(ones[:], 1.0).then_inc(const_done, 1)
            steps.step(nc.gpsimd.memset(ident_b[:], 0.0))
            nc.gpsimd.affine_select(out=ident_b[:], in_=ident_b[:], compare_op=ALU.not_equal, fill=1.0, base=0,
                                    pattern=[[-1, P]], channel_multiplier=1).then_inc(const_done, 1)

        @block.tensor
        def _(pe):
            pe.wait_ge(const_done, 2)
            pe.wait_ge(mag_ready, 1)
            nc.tensor.matmul(bank[7][:, 0:2], ones[:], mag[:], start=True, stop=True).then_inc(mag_psum, 1)
            pe.wait_ge(xq_ready, 1)
            transpose_rows(nc, pe, xq, None, g.ident[:], bank[4:6], xt_psum)
            pe.wait_ge(w_ready, 1)
            pe.wait_ge(xt_ready, 2)
            for c in range(CHUNKS):
                if c >= 2:
                    pe.wait_ge(conv_ready, c - 1)
                for j in range(2):
                    ins = nc.tensor.matmul(bank[2 * (c % 2) + j], w1[:, c * P:(c + 1) * P],
                                           xqt[:, j * BANK:(j + 1) * BANK], start=True, stop=True)
                ins.then_inc(h_psum, 1)
            for grp in range(2):
                if grp:
                    pe.wait_ge(rounded_ready, 1)
                for c in range(CHUNKS):
                    pe.wait_ge(silu_ready, c + 1)
                    if not grp and c == 0:
                        pe.wait_ge(conv_ready, CHUNKS)
                    for t in range(4):
                        lo = (4 * grp + t) * P
                        ins = nc.tensor.transpose(bank[t][:, c * P:(c + 1) * P], act_cols[:, c, lo:lo + P], g.ident[:])
                ins.then_inc(g_psum, 1)
            for grp in range(2):
                pe.wait_ge(hq_ready, grp + 1)
                if grp:
                    pe.wait_ge(hqt_ready, 2)
                for t in range(4):
                    for c in range(CHUNKS):
                        dst = bank[4 + t // 2].bitcast(BF16)[:, (t % 2) * HID + c * P:(t % 2) * HID + (c + 1) * P]
                        ins = nc.tensor.transpose(dst, hq[:, 4 * grp + t, c * P:(c + 1) * P], ident_b[:])
                    if t % 2:
                        ins.then_inc(hq_psum, 1)
            for t in range(TILES):
                pe.wait_ge(hqt_ready, t // 2 + 1)
                for c in range(CHUNKS):
                    ins = nc.tensor.matmul(bank[6 + t // 4][:, (t % 4) * D:(t % 4 + 1) * D],
                                           hqt[:, t, c * P:(c + 1) * P], w2b[:, c * P:(c + 1) * P],
                                           start=(c == 0), stop=(c == CHUNKS - 1))
                if t % 4 == 3:
                    ins.then_inc(y_psum, 1)

        @block.scalar
        def _(act):
            act.wait_ge(xt_psum, 1)
            nc.scalar.copy(xqt[:, 0:BANK], bank[4]).then_inc(xt_ready, 1)
            given.wait(act)
            for c in range(CHUNKS):
                act.wait_ge(h_psum, c + 1)
                if c >= 2:
                    act.wait_ge(silu_ready, c - 1)
                nc.scalar.activation(halves(conv[c % 2][:]), pair[c % 2], ACT.Identity, scale=taps[:, c, 1:2],
                                     bias=cb[:, c:c + 1]).then_inc(mid_ready, 1)
                if c >= 1:
                    act.wait_ge(conv_ready, c)
                    nc.scalar.activation(act_cols[:, c - 1, :], conv[(c - 1) % 2][:], ACT.Silu).then_inc(silu_ready, 1)
            act.wait_ge(conv_ready, CHUNKS)
            nc.scalar.activation(act_cols[:, CHUNKS - 1, :], conv[(CHUNKS - 1) % 2][:], ACT.Silu)\
                .then_inc(silu_ready, 1)
            for n in range(4):
                if n % 2 == 0:
                    act.wait_ge(hq_psum, n + 1)
                    nc.scalar.copy(hqt[:, 2 * n:2 * n + 2, :].rearrange("p t c -> p (t c)"), bank[4].bitcast(BF16))\
                        .then_inc(hqt_ready, 1)
                else:
                    act.wait_ge(hq_psum, n + 1)
                    nc.scalar.copy(hqt[:, 2 * n:2 * n + 2, :].rearrange("p t c -> p (t c)"), bank[5].bitcast(BF16))\
                        .then_inc(hqt_ready, 1)
            norm_root(nc, act, nb, 1)

        @block.vector
        def _(dve):
            steps = Tally(dve, dve_steps)
            given.wait(dve)
            steps.add(nc.vector.tensor_reduce(mag[:, 0:1], w1[:], AX.X, ALU.add, apply_absolute_value=True))
            nc.vector.tensor_reduce(mag[:, 1:2], w2[:], AX.X, ALU.add, apply_absolute_value=True)\
                .then_inc(mag_ready, 1)

            def quant_scales(top, scale, back, cols):
                steps.step(nc.vector.tensor_scalar(top[:, cols], top[:, cols], LEAST, None, ALU.max))
                steps.step(nc.vector.reciprocal(scale[:, cols], top[:, cols]))
                steps.step(nc.vector.tensor_scalar(scale[:, cols], scale[:, cols], 127.0, None, ALU.mult))
                steps.step(nc.vector.reciprocal(back[:, cols], scale[:, cols]))

            every = slice(0, TILES)
            steps.step(nc.vector.tensor_reduce(top[:], g.x[:], AX.X, ALU.max, apply_absolute_value=True))
            quant_scales(top, scale, back, every)
            for t in range(TILES):
                steps.add(nc.vector.tensor_scalar(xq[:, t, :], g.x[:, t, :], scale[:, t:t + 1], MAGIC,
                                                  ALU.mult, ALU.add))
            steps.settle()
            for t in range(TILES):
                ins = nc.vector.tensor_scalar(xq[:, t, :], xq[:, t, :], MAGIC, back[:, t:t + 1],
                                              ALU.subtract, ALU.mult)
            ins.then_inc(xq_ready, 1)
            dve.wait_ge(mag_psum, 1)
            steps.step(nc.vector.tensor_scalar(mean[:], bank[7][:, 0:2], 1.0 / (D * HID), LEAST, ALU.mult, ALU.max))
            steps.step(nc.vector.reciprocal(wscale[:], mean[:]))
            steps.step(nc.vector.reciprocal(wback[:], wscale[:]))
            for j, w in enumerate((w1, w2)):
                steps.step(nc.vector.tensor_scalar(w[:], w[:], wscale[:, j:j + 1], MAGIC, ALU.mult, ALU.add))
                steps.step(nc.vector.tensor_scalar(w[:], w[:], MAGIC, 1.0, ALU.subtract, ALU.min))
            steps.add(nc.vector.tensor_scalar(w2b[:], w2[:], -1.0, None, ALU.max))
            nc.vector.tensor_scalar(w1[:], w1[:], -1.0, wback[:, 0:1], ALU.max, ALU.mult).then_inc(w_ready, 1)
            dve.wait_ge(xt_psum, 2)
            nc.vector.tensor_copy(xqt[:, BANK:], bank[5]).then_inc(xt_ready, 1)
            seqs = lambda z: z.rearrange("p (b n) -> p b n", b=BATCH)
            for c in range(CHUNKS):
                h = seqs(pair[c % 2].rearrange("p j n -> p (j n)"))
                z = seqs(conv[c % 2][:])
                dve.wait_ge(mid_ready, c + 1)
                steps.step(nc.vector.scalar_tensor_tensor(z[:, :, 1:], h[:, :, :SEQ - 1], taps[:, c, 0:1], z[:, :, 1:],
                                                          ALU.mult, ALU.add))
                nc.vector.scalar_tensor_tensor(z[:, :, :SEQ - 1], h[:, :, 1:], taps[:, c, 2:3], z[:, :, :SEQ - 1],
                                               ALU.mult, ALU.add).then_inc(conv_ready, 1)
            for grp in range(2):
                cols = slice(4 * grp, 4 * grp + 4)
                dve.wait_ge(g_psum, grp + 1)
                steps.step(nc.vector.tensor_reduce(top2[:, cols], g.psum[:, 0:4, :], AX.X, ALU.max,
                                                   apply_absolute_value=True))
                quant_scales(top2, scale2, back2, cols)
                for t in range(4):
                    ins = nc.vector.tensor_scalar(big[:, 4 * grp + t, :], bank[t], scale2[:, 4 * grp + t:4 * grp + t + 1],
                                                  MAGIC, ALU.mult, ALU.add)
                ins.then_inc(rounded_ready, 1)
                dve.wait_ge(rounded_ready, grp + 1)
                nc.vector.tensor_scalar(hq[:, cols, :], big[:, cols, :], MAGIC, None, ALU.subtract)\
                    .then_inc(hq_ready, 1)
            steps.step(nc.vector.tensor_scalar(back2[:], back2[:], wback[:, 1:2], None, ALU.mult))
            for t in range(TILES):
                dve.wait_ge(y_psum, t // 4 + 1)
                steps.add(nc.vector.scalar_tensor_tensor(rsd[:, t, :], bank[6 + t // 4][:, (t % 4) * D:(t % 4 + 1) * D],
                                                         back2[:, t:t + 1], g.x[:, t, :], ALU.mult, ALU.add))
            steps.settle()
            norm_stats(nc, steps, nb, rsd)
            norm_scale(nc, dve, steps, nb, 1)
            norm_apply(nc, steps, nb, rsd, g.x)


def store(nc, g, out):
    stored = nc.alloc_semaphore(name="stored")
    with nc.Block() as block:
        @block.sync
        def _(sp):
            sp.dma_start(out.rearrange("b (h p) c -> p (b h) c", p=P), g.x[:]).then_inc(stored, 16)
            sp.wait_ge(stored, 16)




def decoder(nc, a, out):
    with ExitStack() as ctx:
        g = Shared(nc, ctx)
        g.narrow = NarrowWeights(nc, ctx, a)
        with ExitStack() as layers:
            g.graph = GraphWeights(nc, layers, a)
            with ExitStack() as layer0:
                g.expert = ExpertWeights(nc, layer0, a)
                with ExitStack() as mixers:
                    g.memory = MemoryWeights(nc, mixers, a)
                    selective_scan(nc, g, a)
                    memory_attention(nc, g, a)
                expert_block(nc, g, a)
            nc.clear_and_free_semaphores(g.sems)
            g.sems.clear()
            nc.all_engine_barrier()
            graph_attention(nc, g, a)
        with ExitStack() as last:
            g.quantised = QuantisedWeights(nc, last, a)
            narrow_attention(nc, g, a)
            quantised_ffn(nc, g, a)
        store(nc, g, out)


_OUTS = [((4, 256, 128), 'float32')]


def kernel(**inputs):
    import numpy as _np
    import concourse.bacc as _bacc
    from concourse import mybir as _mybir
    from concourse.bass_utils import run_bass_kernel_spmd as _run

    nc = _bacc.Bacc("TRN2", target_bir_lowering=False, num_devices=1)
    def columns(v):
        return v.reshape(-1, 128).T

    given = {name: _np.asarray(v) for name, v in inputs.items()}
    for name in ("L0_xattn_wq_b", "L0_xattn_wk_b", "L0_ffn_b1", "L1_xattn_bq", "L1_xattn_bk", "L1_ffn_conv_b",
                 "L1_attn_gamma_in", "L0_attn_b_dt", "L0_attn_Dp"):
        given[name] = columns(given[name])
    given["L1_ffn_w1"] = given["L1_ffn_w1"].T
    given["L1_ffn_w2"] = given["L1_ffn_w2"].T.reshape(4, 128, 128).transpose(1, 0, 2)
    given["L1_attn_lin_b"] = given["L1_attn_lin_b"].reshape(64, 1)
    for name in ("L0_ffn_in_proj_w", "L0_ffn_out_w", "L0_ffn_router_w", "L1_attn_lin_w"):
        given[name] = given[name].T
    for name in ("L0_ffn_w1", "L0_ffn_w2"):
        given[name] = given[name].transpose(2, 0, 1)
    given["L1_ffn_conv_w"] = given["L1_ffn_conv_w"].reshape(4, 128, 3).transpose(1, 0, 2)
    arrays, args = {}, {}
    for name in given:
        a = _np.ascontiguousarray(given[name])
        arrays[f"in_{name}_dram"] = a
        args[name] = nc.dram_tensor(f"in_{name}_dram", a.shape, _mybir.dt.from_np(a.dtype), kind="ExternalInput").ap()
    shape, dtype = _OUTS[0]
    out = nc.dram_tensor("out_0_dram", shape, _mybir.dt.from_np(_np.dtype(dtype)), kind="ExternalOutput").ap()
    decoder(nc, args, out)
    r = _run(nc, [arrays], core_ids=[0])
    return r.results[0]["out_0_dram"]
```

```python
from contextlib import ExitStack

import concourse.bass as bass
from concourse import mybir

F32 = mybir.dt.float32
BF16 = mybir.dt.bfloat16
F16 = mybir.dt.float16
U32 = mybir.dt.uint32
ALU = mybir.AluOpType
ACT = mybir.ActivationFunctionType
AX = mybir.AxisListType
ds = bass.ds

P = 128
BATCH, SEQ, D = 4, 256, 128
TOK = BATCH * SEQ
TILES = TOK // P
BANK = 512
EPS = 1e-5


class Tally:

    def __init__(self, engine, sem, before=0):
        self.engine, self.sem, self.n, self.before = engine, sem, 0, before

    def add(self, instruction):
        instruction.then_inc(self.sem, 1)
        self.n += 1

    def settle(self):
        self.engine.wait_ge(self.sem, self.before + self.n)

    def step(self, instruction):
        self.add(instruction)
        self.settle()


class Resources:

    def __init__(self, nc, ctx, sems, tag):
        self.nc, self.ctx, self.sems, self.tag = nc, ctx, sems, tag

    def sb(self, name, shape, dt=F32):
        return self.ctx.enter_context(self.nc.sbuf_tensor(name, shape, dt))

    def sem(self, name):
        self.sems.append(self.nc.alloc_semaphore(name=f"{self.tag}_{name}"))
        return self.sems[-1]


class Weights:

    def __init__(self, nc, ctx, tag):
        self.nc, self.ctx, self.pairs = nc, ctx, []
        self.loaded = nc.alloc_semaphore(name=f"{tag}_weights_loaded")

    def sb(self, name, shape):
        return self.ctx.enter_context(self.nc.sbuf_tensor(name, shape, F32))

    def load(self, sp):
        for dst, src in self.pairs:
            sp.dma_start(dst, src).then_inc(self.loaded, 16)

    def wait(self, engine):
        engine.wait_ge(self.loaded, 16 * len(self.pairs))


def one_row(v):
    return v.rearrange("(o n) -> o n", o=1)


def every_row(v):
    return one_row(v).broadcast_to([P, v.shape[0]])


class Shared:

    def __init__(self, nc, ctx):
        r = Resources(nc, ctx, [], "kernel")
        self.sems = []
        self.x, self.xt = r.sb("x_rows", [P, TILES, D]), r.sb("x_cols", [P, TOK])
        self.ct = r.sb("ctx_cols", [P, TOK])
        self.ident, self.ones_row = r.sb("identity", [P, P]), r.sb("ones_row", [1, P])
        self.psum = ctx.enter_context(nc.psum_tensor("banks", [P, 8, BANK], F32))


def halves(ap):
    return ap.rearrange("p (h n) -> p h n", h=2)


def transpose_rows(nc, pe, src, src_ready, ident, banks, done):
    for t in range(TILES):
        if src_ready is not None:
            pe.wait_ge(src_ready[0], src_ready[1](t))
        ins = nc.tensor.transpose(banks[t // 4][:, (t % 4) * P:(t % 4 + 1) * P], src[:, t, :], ident)
        if t % 4 == 3:
            ins.then_inc(done, 1)


class NormBuffers:
    def __init__(self, r, tag):
        self.stats, self.mv = r.sb(f"{tag}_stats", [P, TILES, 6]), r.sb(f"{tag}_mean_var", [P, TILES, 2])
        self.ve, self.sd = r.sb(f"{tag}_var_eps", [P, TILES]), r.sb(f"{tag}_std", [P, TILES])
        self.rstd, self.shift = r.sb(f"{tag}_rstd", [P, TILES]), r.sb(f"{tag}_shift", [P, TILES])
        self.var_ready, self.sd_ready = r.sem(f"{tag}_var_ready"), r.sem(f"{tag}_sd_ready")
        self.scale_ready = r.sem(f"{tag}_scale_ready")


def norm_stats(nc, tally, b, rows):
    for t in range(TILES):
        tally.add(nc.vector.bn_stats(b.stats[:, t, :], rows[:, t, :]))
    tally.settle()
    for t in range(TILES):
        tally.add(nc.vector.bn_aggr(b.mv[:, t, :], b.stats[:, t, :]))
    tally.settle()
    nc.vector.tensor_scalar(b.ve[:], b.mv[:, :, 1], EPS, None, ALU.add).then_inc(b.var_ready, 1)


def norm_root(nc, act, b, k):
    act.wait_ge(b.var_ready, k)
    nc.scalar.activation(b.sd[:], b.ve[:], ACT.Sqrt).then_inc(b.sd_ready, 1)


def norm_scale(nc, dve, tally, b, k):
    dve.wait_ge(b.sd_ready, k)
    tally.step(nc.vector.reciprocal(b.rstd[:], b.sd[:]))
    nc.vector.scalar_tensor_tensor(b.shift[:], b.mv[:, :, 0], -1.0, b.rstd[:], ALU.mult, ALU.mult)\
        .then_inc(b.scale_ready, 1)
    dve.wait_ge(b.scale_ready, k)


def norm_apply(nc, tally, b, rows, out, tiles=range(TILES)):
    for t in tiles:
        tally.add(nc.vector.tensor_scalar(out[:, t, :], rows[:, t, :], b.rstd[:, t:t + 1],
                                          b.shift[:, t:t + 1], ALU.mult, ALU.add))
    tally.settle()


VECTOR_TILES, SCALAR_TILES = range(5), range(5, TILES)


def norm_finish(nc, act, b, k, rows, out):
    norm_root(nc, act, b, k)
    act.wait_ge(b.scale_ready, k)
    for t in SCALAR_TILES:
        nc.scalar.activation(out[:, t, :], rows[:, t, :], ACT.Identity, bias=b.shift[:, t:t + 1],
                             scale=b.rstd[:, t:t + 1])


DT_RANK, STATES = 64, 16
DT_MIN, DT_MAX = 0.001, 0.1


def selective_scan(nc, g, a):
    with ExitStack() as ctx:
        r = Resources(nc, ctx, g.sems, "ssm")
        w_in = r.sb("w_in", [P, D])
        w_x = r.sb("w_x", [P, DT_RANK + 2 * STATES])
        w_dt = r.sb("w_dt", [DT_RANK, D])
        vecs = r.sb("ssm_vecs", [P, 2])
        a_log = r.sb("a_log", [P, STATES])
        neg_a = r.sb("neg_a", [P, STATES])
        pick = r.sb("pick_state", [96, STATES, P], BF16)
        pick_rows = pick[:].rearrange("k n p -> k (n p)")
        parts = r.sb("row_parts", [96, 2, TOK], BF16)
        ctx_rows = r.sb("ctx_rows", [P, TILES, D])
        u = r.sb("u_cols", [P, TOK])
        low = r.sb("dt_low_cols", [DT_RANK, TOK])
        bm = r.sb("b_cols", [STATES, TOK])
        inp, c_rows = r.sb("inp_cols", [STATES, TOK]), r.sb("c_cols", [STATES, TOK])
        inp_mid, c_mid = r.sb("inp_middle_part", [STATES, TOK], BF16), r.sb("c_middle_part", [STATES, TOK], BF16)
        absz = r.sb("abs_z", [P, TOK])
        soft = r.sb("soft_tail", [P, TOK])
        dt = r.sb("dt_cols", [P, TOK])
        dtu = r.sb("dtu_cols", [P, TOK])
        decay = [r.sb(f"decay{i}", [P, TOK]) for i in range(2)]
        zeros = r.sb("zeros", [P, BATCH])
        state = r.sb("state", [P, TOK])
        hc = [r.sb(f"state_c{i}", [P, TOK]) for i in range(2)]
        y = r.sb("ssm_y_cols", [P, TOK])
        rsd = r.sb("ssm_rows", [P, TILES, D])
        nb = NormBuffers(r, "ssm_norm")

        loaded = {k: r.sem(f"loaded_{k}") for k in ("x", "ctx", "w", "small")}
        const_done, xt_psum, xt_ready, ct_psum, ct_ready = (r.sem(n) for n in (
            "const_done", "xt_psum", "xt_ready", "ct_psum", "ct_ready"))
        u_psum, u_ready, low_psum, low_ready, bc_psum, z_psum = (r.sem(n) for n in (
            "u_psum", "u_ready", "low_psum", "low_ready", "bc_psum", "z_psum"))
        soft_ready, nega_exp, nega_ready, dt_ready, dtu_ready = (r.sem(n) for n in (
            "soft_ready", "nega_exp", "nega_ready", "dt_ready", "dtu_ready"))
        s_psum, parts_ready, inp_bc, c_bc, decay_exp, decay_ready = (r.sem(n) for n in (
            "s_psum", "parts_ready", "inp_bc", "c_bc", "decay_exp", "decay_ready"))
        scanned, hc_ready, summed, y_ready, yt_psum = (r.sem(n) for n in (
            "scanned", "hc_ready", "summed", "y_ready", "yt_psum"))
        dve_steps, act_steps, pool_steps = r.sem("dve_steps"), r.sem("act_steps"), r.sem("pool_steps")
        c_rows_ready, c_rounded, c_left, c_parts_ready = (r.sem(n) for n in (
            "c_rows_ready", "c_rounded", "c_left", "c_parts_ready"))
        bank = [g.psum[:, i, :] for i in range(8)]
        pair = [g.psum[:, 2 * i:2 * i + 2, :] for i in range(4)]
        block = ctx.enter_context(nc.Block())

        @block.sync
        def _(sp):
            sp.dma_start(g.x[:], a["x"].rearrange("b (h p) c -> p (b h) c", p=P)).then_inc(loaded["x"], 16)
            sp.dma_start(w_in[:], a["L0_attn_w_in"]).then_inc(loaded["w"], 16)
            sp.dma_start(w_x[:], a["L0_attn_w_x"]).then_inc(loaded["w"], 16)
            sp.dma_start(w_dt[:], a["L0_attn_w_dt"]).then_inc(loaded["w"], 16)
            sp.dma_start(ctx_rows[:], a["ctx_1024"].rearrange("b (h p) c -> p (b h) c", p=P)).then_inc(loaded["ctx"], 16)
            g.memory.load(sp)
            g.expert.load(sp)
            g.graph.load(sp)
            g.narrow.load(sp)

        @block.gpsimd
        def _(pool):
            steps = Tally(pool, pool_steps)
            steps.add(nc.gpsimd.memset(zeros[:], 0.0))
            steps.add(nc.gpsimd.memset(g.ident[:], 0.0))
            steps.add(nc.gpsimd.memset(g.ones_row[:], 1.0))
            steps.add(nc.gpsimd.memset(pick[:], 0.0))
            steps.settle()
            nc.gpsimd.affine_select(out=g.ident[:], in_=g.ident[:], compare_op=ALU.not_equal, fill=1.0,
                                    base=0, pattern=[[-1, P]], channel_multiplier=1).then_inc(const_done, 1)
            for j in range(3):
                steps.step(nc.gpsimd.affine_select(out=pick[:], in_=pick[:], compare_op=ALU.not_equal, fill=1.0,
                                                   base=-32 * j, pattern=[[-1, STATES], [0, P]],
                                                   channel_multiplier=1))
            nc.gpsimd.memset(parts[:], 0.0).then_inc(const_done, 1)


            pool.wait_ge(c_rounded, 1)
            nc.gpsimd.tensor_tensor(c_rows[:], c_rows[:], parts[0:STATES, 1, :], ALU.subtract).then_inc(c_left, 1)
            pool.wait_ge(c_rounded, 2)
            nc.gpsimd.tensor_tensor(c_rows[:], c_rows[:], c_mid[:], ALU.subtract).then_inc(c_left, 1)
            pool.wait_ge(c_left, 2)

            def clear_starts(n, k):
                pool.wait_ge(decay_exp, n + 1)
                nc.gpsimd.tensor_tensor(decay[k][:].rearrange("p (b s) -> p b s", b=BATCH)[:, :, 0],
                                        zeros[:], zeros[:], ALU.add)\
                    .then_inc(decay_ready, 1)

            with pool.Fori(0, STATES // 2) as i:
                for k in range(2):
                    clear_starts(2 * i + k, k)

        @block.scalar
        def _(act):
            act.dma_start(vecs[:, 0:1], a["L0_attn_b_dt"]).then_inc(loaded["small"], 16)
            act.dma_start(vecs[:, 1:2], a["L0_attn_Dp"]).then_inc(loaded["small"], 16)
            act.dma_start(a_log[:], a["L0_attn_A_log"]).then_inc(loaded["small"], 16)
            act.wait_ge(loaded["small"], 48)
            nc.scalar.activation(neg_a[:], a_log[:], ACT.Exp).then_inc(nega_exp, 1)
            act.wait_ge(xt_psum, 1)
            nc.scalar.copy(g.xt[:, 0:BANK], bank[0]).then_inc(xt_ready, 1)
            for h in range(2):
                act.wait_ge(u_psum, h + 1)
                nc.scalar.copy(u[:, h * BANK:(h + 1) * BANK], bank[2 + h]).then_inc(u_ready, 1)
            for h in range(2):
                act.wait_ge(low_psum, h + 1)
                nc.scalar.copy(low[:, h * BANK:(h + 1) * BANK], bank[4 + h][0:DT_RANK, :]).then_inc(low_ready, 1)
            act.wait_ge(z_psum, 2)
            steps = Tally(act, act_steps)
            steps.step(nc.scalar.activation(absz[:], g.psum[:, 6:8, :], ACT.Abs, bias=vecs[:, 0:1]))
            steps.step(nc.scalar.activation(absz[:], absz[:], ACT.Exp, scale=-1.0))
            nc.scalar.activation(soft[:], absz[:], ACT.Ln, bias=1.0).then_inc(soft_ready, 1)
            act.wait_ge(const_done, 2)
            act.wait_ge(c_rows_ready, 1)
            nc.scalar.copy(parts[0:STATES, 1, :], c_rows[:]).then_inc(c_rounded, 1)
            act.wait_ge(c_left, 1)
            nc.scalar.copy(c_mid[:], c_rows[:]).then_inc(c_rounded, 1)
            act.wait_ge(c_rounded, 2)
            nc.scalar.copy(parts[32:32 + STATES, 1, :], c_mid[:]).then_inc(c_parts_ready, 1)
            act.wait_ge(c_left, 2)
            nc.scalar.copy(parts[64:64 + STATES, 1, :], c_rows[:]).then_inc(c_parts_ready, 1)
            act.wait_ge(dt_ready, 1)
            act.wait_ge(nega_ready, 1)

            def decays(n, k, first):
                if not first:
                    act.wait_ge(scanned, n - 1)
                nc.scalar.activation(decay[k][:], dt[:], ACT.Exp, scale=neg_a[:, ds(n, 1)]).then_inc(decay_exp, 1)

            for k in range(2):
                decays(k, k, True)
            with act.Fori(1, STATES // 2) as i:
                for k in range(2):
                    decays(2 * i + k, k, False)
            norm_finish(nc, act, nb, 1, rsd, g.x)

        @block.tensor
        def _(pe):
            pe.wait_ge(const_done, 1)
            pe.wait_ge(loaded["x"], 16)
            transpose_rows(nc, pe, g.x, None, g.ident[:], bank, xt_psum)
            pe.wait_ge(loaded["w"], 48)
            for h in range(2):
                pe.wait_ge(xt_ready, 2)
                nc.tensor.matmul(bank[2 + h], w_in[:], g.xt[:, h * BANK:(h + 1) * BANK], start=True, stop=True)\
                    .then_inc(u_psum, 1)
            for h in range(2):
                pe.wait_ge(u_ready, h + 1)
                nc.tensor.matmul(bank[4 + h][0:DT_RANK, :], w_x[:, 0:DT_RANK], u[:, h * BANK:(h + 1) * BANK],
                                 start=True, stop=True).then_inc(low_psum, 1)
            for h in range(2):
                pe.wait_ge(low_ready, h + 1)
                nc.tensor.matmul(bank[6 + h], w_dt[:], low[:, h * BANK:(h + 1) * BANK], start=True, stop=True)\
                    .then_inc(z_psum, 1)
            for h in range(2):
                for m in range(2):
                    lo = DT_RANK + m * STATES
                    ins = nc.tensor.matmul(bank[2 * m + h][0:STATES, :], w_x[:, lo:lo + STATES],
                                           u[:, h * BANK:(h + 1) * BANK], start=True, stop=True)
            ins.then_inc(bc_psum, 1)
            pe.wait_ge(loaded["ctx"], 16)
            pe.wait_ge(low_ready, 2)
            transpose_rows(nc, pe, ctx_rows, None, g.ident[:], bank[4:6], ct_psum)
            pe.wait_ge(dtu_ready, 1)
            pe.wait_ge(nega_ready, 1)
            for h in range(2):
                nc.tensor.matmul(bank[6 + h][0:STATES, :], neg_a[:], dtu[:, h * BANK:(h + 1) * BANK],
                                 start=True, stop=True).then_inc(s_psum, 1)
            pe.wait_ge(parts_ready, 1)
            pe.wait_ge(c_parts_ready, 2)
            pe.wait_ge(const_done, 2)
            pe.wait_ge(ct_ready, 2)

            def broadcasts(n, k, first):
                if not first:
                    pe.wait_ge(scanned, n - 1)
                for h in range(2):
                    ins = nc.tensor.matmul(bank[2 * k + h], pick_rows[:, ds(n * P, P)],
                                           parts[:, 0, h * BANK:(h + 1) * BANK], start=True, stop=True)
                ins.then_inc(inp_bc, 1)

            def outputs(n, k, zero, first, last):
                if not zero:
                    pe.wait_ge(hc_ready, n)
                for h in range(2):
                    ins = nc.tensor.matmul(bank[4 + h], pick_rows[:, ds(n * P, P)],
                                           parts[:, 1, h * BANK:(h + 1) * BANK], start=True, stop=True)
                ins.then_inc(c_bc, 1)
                if not zero:
                    gather(n - 1, 1 - k, last == "first", False)

            def gather(n, k, start, stop):
                pe.wait_ge(hc_ready, n + 1)
                for h in range(2):
                    ins = nc.tensor.matmul(bank[6 + h], g.ident[:], hc[k][:, h * BANK:(h + 1) * BANK],
                                           start=start, stop=stop)
                ins.then_inc(summed, 1)

            broadcasts(0, 0, True)
            broadcasts(1, 1, True)
            outputs(0, 0, True, True, "")
            outputs(1, 1, False, True, "first")
            with pe.Fori(1, STATES // 2) as i:
                for k in range(2):
                    broadcasts(2 * i + k, k, False)
                    outputs(2 * i + k, k, False, False, "")
            gather(STATES - 1, 1, False, True)
            pe.wait_ge(y_ready, 1)
            pe.wait_ge(scanned, STATES)
            for t in range(TILES):
                ins = nc.tensor.transpose(bank[t // 4][:, (t % 4) * P:(t % 4 + 1) * P],
                                          y[:, t * P:(t + 1) * P], g.ident[:])
            ins.then_inc(yt_psum, 1)

        @block.vector
        def _(dve):
            steps = Tally(dve, dve_steps)
            dve.wait_ge(xt_psum, 2)
            nc.vector.tensor_copy(g.xt[:, BANK:], bank[1]).then_inc(xt_ready, 1)
            dve.wait_ge(nega_exp, 1)
            steps.step(nc.vector.tensor_scalar(neg_a[:], neg_a[:], -1.0, None, ALU.mult))
            nc.vector.tensor_scalar(neg_a[:], neg_a[:], 1.0, None, ALU.mult).then_inc(nega_ready, 1)
            dve.wait_ge(bc_psum, 1)
            steps.add(nc.vector.tensor_copy(halves(bm[:]), pair[0][0:STATES]))
            nc.vector.tensor_copy(halves(c_rows[:]), pair[1][0:STATES]).then_inc(c_rows_ready, 1)
            steps.settle()
            dve.wait_ge(ct_psum, 2)
            for h in range(2):
                nc.vector.tensor_copy(g.ct[:, h * BANK:(h + 1) * BANK], bank[4 + h]).then_inc(ct_ready, 1)
            dve.wait_ge(soft_ready, 1)
            dve.wait_ge(z_psum, 2)
            steps.step(nc.vector.tensor_scalar(halves(dt[:]), pair[3], vecs[:, 0:1], 0.0, ALU.add, ALU.max))
            steps.step(nc.vector.tensor_tensor(dt[:], dt[:], soft[:], ALU.add))
            steps.step(nc.vector.tensor_scalar(dtu[:], dt[:], DT_MAX - DT_MIN, DT_MIN, ALU.mult, ALU.add))
            nc.vector.tensor_copy(dt[:], dtu[:]).then_inc(dt_ready, 1)
            dve.wait_ge(dt_ready, 1)
            dve.wait_ge(u_ready, 2)
            nc.vector.tensor_tensor(dtu[:], dt[:], u[:], ALU.mult).then_inc(dtu_ready, 1)
            dve.wait_ge(s_psum, 2)
            steps.step(nc.vector.tensor_tensor(halves(inp[:]), halves(bm[:]), pair[3][0:STATES], ALU.mult))
            dve.wait_ge(const_done, 2)
            steps.step(nc.vector.tensor_copy(parts[0:STATES, 0, :], inp[:]))
            steps.step(nc.vector.tensor_tensor(inp[:], inp[:], parts[0:STATES, 0, :], ALU.subtract))
            steps.step(nc.vector.tensor_copy(inp_mid[:], inp[:]))
            steps.add(nc.vector.tensor_copy(parts[32:32 + STATES, 0, :], inp_mid[:]))
            steps.step(nc.vector.tensor_tensor(inp[:], inp[:], inp_mid[:], ALU.subtract))
            nc.vector.tensor_copy(parts[64:64 + STATES, 0, :], inp[:]).then_inc(parts_ready, 1)

            def scan(n, k, first):
                dve.wait_ge(inp_bc, n + 1)
                dve.wait_ge(decay_ready, n + 1)
                nc.vector.tensor_tensor_scan(state[:], decay[k][:], g.psum[:, 2 * k:2 * k + 2, :]
                                             .rearrange("p h n -> p (h n)"), 0.0, ALU.mult, ALU.add)\
                    .then_inc(scanned, 1)
                dve.wait_ge(scanned, n + 1)
                dve.wait_ge(c_bc, n + 1)
                if not first:
                    dve.wait_ge(summed, n - 1)
                nc.vector.tensor_tensor(halves(hc[k][:]), halves(state[:]), pair[2], ALU.mult).then_inc(hc_ready, 1)

            for k in range(2):
                scan(k, k, True)
                dve.wait_ge(hc_ready, k + 1)
            with dve.Fori(1, STATES // 2) as i:
                for k in range(2):
                    scan(2 * i + k, k, False)
                    dve.wait_ge(hc_ready, 2 * i + k + 1)
            dve.wait_ge(summed, STATES)
            nc.vector.scalar_tensor_tensor(halves(y[:]), halves(u[:]), vecs[:, 1:2], pair[3], ALU.mult, ALU.add)\
                .then_inc(y_ready, 1)
            dve.wait_ge(yt_psum, 1)
            steps.step(nc.vector.tensor_tensor(rsd[:].rearrange("p (h t) c -> p h (t c)", h=2), g.x[:]
                                               .rearrange("p (h t) c -> p h (t c)", h=2), pair[0], ALU.add))
            norm_stats(nc, steps, nb, rsd)
            norm_scale(nc, dve, steps, nb, 1)
            norm_apply(nc, steps, nb, rsd, g.x, VECTOR_TILES)


HEADS, DK, MEM = 16, 64, 128
PAIRS = HEADS // 2
KEYS = SEQ + MEM
KT = KEYS // P
QT = SEQ // P
VW = DK + 1
UNITS = 2 * BATCH


class MemoryWeights(Weights):
    def __init__(self, nc, ctx, a):
        super().__init__(nc, ctx, "xattn")
        self.wv, self.wo = self.sb("wv", [P, HEADS * DK]), self.sb("wo", [P, PAIRS, D])
        self.bv, self.bo = self.sb("bv_all_rows", [P, HEADS * DK]), self.sb("bo_all_rows", [P, D])
        self.bqk = self.sb("bq_bk_cols", [P, 2, PAIRS])
        self.mk, self.mv = self.sb("mk_rows", [P, HEADS * DK]), self.sb("mv_rows", [P, HEADS, DK])
        self.pairs = [
            (self.mk[:], a["L0_xattn_mk"][0]), (self.wv[:], a["L0_xattn_wv_w"]),
            (self.bv[:], every_row(a["L0_xattn_wv_b"])), (self.bqk[:, 0, :], a["L0_xattn_wq_b"]),
            (self.bqk[:, 1, :], a["L0_xattn_wk_b"]),
            (self.mv[:], a["L0_xattn_mv"][0].rearrange("m (h d) -> m h d", h=HEADS)),
            (self.wo[:], a["L0_xattn_wo_w"].rearrange("(c p) n -> p c n", p=P)), (self.bo[:], every_row(a["L0_xattn_wo_b"])),
        ]


def memory_attention(nc, g, a):
    with ExitStack() as ctx:
        r = Resources(nc, ctx, g.sems, "xattn")
        given = g.memory
        wv, wo, bv, bo, bqk, mk, mv = given.wv, given.wo, given.bv, given.bo, given.bqk, given.mk, given.mv
        wpair = r.sb("wq_wk_pair", [P, 2, P])
        mkt_all = r.sb("mk_cols_all", [P, PAIRS, 2, P], F16)
        mkt = r.sb("mk_cols_pair", [P, 2, P], F16)
        qk_whole = [r.sb(f"qk_cols{i}", [P, 2, SEQ]) for i in range(2)]
        qk = [r.sb(f"qk_cols_part{i}", [P, 2, BATCH, SEQ], F16) for i in range(2)]
        v_rows = r.sb("value_rows", [P, 4, HEADS // 2, DK])
        v_hi = r.sb("values_hi", [P, TILES + 1, HEADS, VW], F16)
        v_lo = r.sb("values_lo", [P, TILES + 1, HEADS, VW], F16)
        v_hi_flat = v_hi[:].rearrange("p t h w -> p (t h w)")
        v_lo_flat = v_lo[:].rearrange("p t h w -> p (t h w)")
        e = [r.sb(f"probs{i}", [P, QT, KEYS]) for i in range(2)]
        et_hi = [r.sb(f"probs_cols_hi{i}", [P, QT, KEYS], F16) for i in range(2)]
        et_lo = [r.sb(f"probs_cols_lo{i}", [P, QT, KEYS], F16) for i in range(2)]
        negmax = [r.sb(f"negmax{i}", [P, QT]) for i in range(2)]
        o = r.sb("out_raw", [P, TILES, HEADS, VW])
        o_heads = o[:].rearrange("p t h w -> p t (h w)")
        rsum = [r.sb(f"rsum{i}", [P, HEADS]) for i in range(2)]
        on = [r.sb(f"out_normal{i}", [P, HEADS, DK]) for i in range(2)]
        ont = [r.sb(f"out_cols{i}", [P, PAIRS, P]) for i in range(2)]
        rsd = r.sb("xattn_rows", [P, TILES, D])
        mkt_whole = rsd
        nb = NormBuffers(r, "xattn_norm")
        x_biased, wpair_loaded, xt_psum, xt_ready, v_psum, v_even_ready = (r.sem(n) for n in (
            "x_biased", "wpair_loaded", "xt_psum", "xt_ready", "v_psum", "v_even_ready"))
        v_ones, mk_psum, mk_ready, mkt_ready, projected, qk_ready = (r.sem(n) for n in (
            "v_ones", "mk_psum", "mk_ready", "mkt_ready", "projected", "qk_ready"))
        scored, max_ready, exp_ready, turned, et_hi_ready, et_lo_ready = (r.sem(n) for n in (
            "scored", "max_ready", "exp_ready", "turned", "et_hi_ready", "et_lo_ready"))
        pv_done, o_ready, on_ready, on_turned, ont_ready, y_psum = (r.sem(n) for n in (
            "pv_done", "o_ready", "on_ready", "on_turned", "ont_ready", "y_psum"))
        y_ready, dve_steps, v_rows_ready, v_hi_ready = (r.sem(n) for n in (
            "y_ready", "dve_steps", "v_rows_ready", "v_hi_ready"))
        mk_split, qk_copied, qk_hi_ready, v_odd_ready = (r.sem(n) for n in (
            "mk_split", "qk_copied", "qk_hi_ready", "v_odd_ready"))
        bank = [g.psum[:, i, :] for i in range(8)]
        score_bank = [g.psum[:, 2 * i:2 * i + 2, 0:KEYS] for i in range(2)]
        turn_bank = [bank[4], bank[5]]
        proj_bank, o_bank = bank[6], bank[7]
        block = ctx.enter_context(nc.Block())

        @block.sync
        def _(sp):
            def load_pair(p):
                for j, w in enumerate((a["L0_xattn_wq_w"], a["L0_xattn_wk_w"])):
                    sp.dma_start(wpair[:, j, :], w[:, ds(p * P, P)]).then_inc(wpair_loaded, 16)

            load_pair(0)
            with sp.Fori(1, PAIRS) as p:
                sp.wait_ge(projected, 2 * BATCH * p)
                load_pair(p)

        @block.gpsimd
        def _(pool):
            nc.gpsimd.memset(v_hi[:, :, :, DK], 1.0).then_inc(v_ones, 1)
            nc.gpsimd.memset(v_lo[:, :, :, DK], 0.0).then_inc(v_ones, 1)
            pool.wait_ge(mk_split, 1)
            nc.gpsimd.tensor_tensor(mkt_all[:, :, 1, :], mkt_whole[:], mkt_all[:, :, 0, :], ALU.subtract)\
                .then_inc(mk_split, 1)

            def project_low(n, b):
                pool.wait_ge(qk_hi_ready, n + 1)
                nc.gpsimd.tensor_tensor(qk[1][:, :, b, :], qk_whole[b % 2][:], qk[0][:, :, b, :], ALU.subtract)\
                    .then_inc(qk_ready, 1)

            for n in range(0, 2 * TILES, 2):
                pool.wait_ge(v_hi_ready, n + 1)
                nc.gpsimd.tensor_tensor(v_lo[:, n // 2, 0:8, 0:DK], v_rows[:, n % 4], v_hi[:, n // 2, 0:8, 0:DK],
                                        ALU.subtract).then_inc(v_even_ready, 1)
                if n % 4 == 2:
                    project_low(n // 4, n // 4)
            pool.wait_ge(v_hi_ready, 2 * TILES + 1)
            nc.gpsimd.tensor_tensor(v_lo[:, TILES, :, 0:DK], mv[:], v_hi[:, TILES, :, 0:DK], ALU.subtract)\
                .then_inc(v_even_ready, 1)
            given.wait(pool)
            pool.wait_ge(xt_psum, 2)
            add_bias(nc, g.x, bo).then_inc(x_biased, 1)
            with pool.Fori(1, PAIRS) as p:
                for b in range(BATCH):
                    project_low(BATCH * p + b, b)

        @block.tensor
        def _(pe):
            transpose_rows(nc, pe, g.x, None, g.ident[:], bank[4:6], xt_psum)
            given.wait(pe)
            for c in range(PAIRS):
                if c == 4:
                    pe.wait_ge(mk_ready, 1)
                ins = nc.tensor.transpose(bank[6 + c // 4][:, (c % 4) * P:(c % 4 + 1) * P],
                                          mk[:, c * P:(c + 1) * P], g.ident[:])
                if c % 4 == 3:
                    ins.then_inc(mk_psum, 1)
            pe.wait_ge(xt_ready, 2)
            pe.wait_ge(mk_ready, 2)

            def project(p, b, j, first=False):
                if not first:
                    pe.wait_ge(qk_copied, 2 * (BATCH * p + b) + j)
                pe.wait_ge(wpair_loaded, 32 * p + 32)
                nc.tensor.matmul(proj_bank[:, j * SEQ:(j + 1) * SEQ], wpair[:, j, :],
                                 (g.xt, g.ct)[j][:, b * SEQ:(b + 1) * SEQ], start=True, stop=True).then_inc(projected, 1)

            def scores(u, b, h, i, first):
                if not first:
                    pe.wait_ge(exp_ready, u - 1)
                rows = slice(h * DK, (h + 1) * DK)
                for qt in range(QT):
                    for dst, keys in ((slice(0, SEQ), lambda y: qk[y][rows, 1, b, :]),
                                      (slice(SEQ, KEYS), lambda y: mkt[rows, y, :])):
                        for n, (x, y) in enumerate(((0, 0), (1, 0), (0, 1))):
                            ins = nc.tensor.matmul(bank[2 * i + qt][:, dst], qk[x][rows, 0, b, qt * P:(qt + 1) * P],
                                                   keys(y), start=(n == 0), stop=(n == 2))
                ins.then_inc(scored, 1)

            def turn(u, i, first):
                pe.wait_ge(exp_ready, u + 1)
                if not first:
                    pe.wait_ge(et_lo_ready, QT * u)
                for qt in range(QT):
                    for kt in range(KT):
                        ins = nc.tensor.transpose(turn_bank[qt][:, kt * P:(kt + 1) * P],
                                                  e[i][:, qt, kt * P:(kt + 1) * P], g.ident[:])
                ins.then_inc(turned, 1)

            def values(u, p, b, h, i, first):
                pe.wait_ge(et_lo_ready, QT * u + QT)
                if not first:
                    pe.wait_ge(o_ready, u)
                for qt in range(QT):
                    for kt in range(KT):
                        tile = QT * b + kt if kt < QT else TILES
                        cols, head = slice(kt * P, (kt + 1) * P), ds((tile * HEADS + h) * VW + p * (2 * VW), VW)
                        for n, (probs, vals) in enumerate(((et_hi, v_hi_flat), (et_lo, v_hi_flat), (et_hi, v_lo_flat))):
                            ins = nc.tensor.matmul(o_bank[:, qt * VW:(qt + 1) * VW], probs[i][:, qt, cols],
                                                   vals[:, head], start=(kt == 0 and n == 0),
                                                   stop=(kt == KT - 1 and n == 2))
                ins.then_inc(pv_done, 1)

            def pair_steps(p, first, more):
                for j in range(UNITS):
                    u, n = UNITS * p + j, (j + 1) % UNITS
                    b, h = n // 2, n % 2
                    if n or more:
                        at = p if n else p + 1
                        pe.wait_ge(mkt_ready, at + 1)
                        pe.wait_ge(qk_ready, BATCH * at + b + 1)
                        scores(u + 1, b, h, n % 2, first and j < 1)
                    if more:
                        project(p + 1, j // 2, j % 2)
                    if not (first and j < 1):
                        turn(u - 1, (j - 1) % 2, first and j == 1)
                    if not (first and j < 2):
                        jj = (j - 2) % UNITS
                        values(u - 2, p if j >= 2 else p - 1, jj // 2, jj % 2, j % 2, first and j == 2)

            for n in range(2 * TILES):
                if n >= 4:
                    pe.wait_ge(v_rows_ready, n - 3)
                nc.tensor.matmul(bank[n % 4], g.ct[:, n // 2 * P:(n // 2 + 1) * P],
                                 wv[:, (n % 2) * BANK:(n % 2 + 1) * BANK], start=True, stop=True).then_inc(v_psum, 1)
                if n % 2:
                    project(0, n // 4, n // 2 % 2, n == 1)
            pe.wait_ge(v_rows_ready, 2 * TILES)
            pe.wait_ge(mkt_ready, 1)
            pe.wait_ge(qk_ready, 1)
            scores(0, 0, 0, 0, True)
            pe.wait_ge(v_even_ready, TILES + 1)
            pe.wait_ge(v_odd_ready, TILES)
            pe.wait_ge(v_ones, 2)
            pair_steps(0, True, True)
            with pe.Fori(1, PAIRS - 1) as p:
                pair_steps(p, False, True)
            pair_steps(PAIRS - 1, False, False)
            last = PAIRS * UNITS
            turn(last - 1, 1, False)
            values(last - 2, PAIRS - 1, BATCH - 1, 0, 0, False)
            values(last - 1, PAIRS - 1, BATCH - 1, 1, 1, False)

            for t in range(TILES):
                i = t % 2
                pe.wait_ge(on_ready, t + 1)
                for c in range(PAIRS):
                    ins = nc.tensor.transpose(bank[2 * i + c // 4][:, (c % 4) * P:(c % 4 + 1) * P],
                                              on[i][:, 2 * c:2 * c + 2, :].rearrange("p h d -> p (h d)"), g.ident[:])
                ins.then_inc(on_turned, 1)
                if t:
                    output_product(nc, pe, ont_ready, y_ready, y_psum, t - 1, bank[4 + (t - 1) % 2],
                                   ont[(t - 1) % 2], wo)
            output_product(nc, pe, ont_ready, y_ready, y_psum, TILES - 1, bank[4 + 1], ont[1], wo)

        @block.scalar
        def _(act):
            act.wait_ge(xt_psum, 1)
            nc.scalar.copy(g.xt[:, 0:BANK], bank[4]).then_inc(xt_ready, 1)
            for h in range(2):
                act.wait_ge(mk_psum, h + 1)
                nc.scalar.copy(mkt_whole[:, 4 * h:4 * h + 4, :].rearrange("p c m -> p (c m)"), bank[6 + h])\
                    .then_inc(mk_ready, 1)
            act.wait_ge(mk_ready, 2)
            nc.scalar.copy(mkt_all[:, :, 0, :], mkt_whole[:]).then_inc(mk_split, 1)

            def project_high(n, b):
                act.wait_ge(qk_copied, 2 * n + 2)
                nc.scalar.copy(qk[0][:, :, b, :], qk_whole[b % 2][:]).then_inc(qk_hi_ready, 1)

            for n in range(2 * TILES):
                act.wait_ge(v_rows_ready, n + 1)
                nc.scalar.copy(v_hi[:, n // 2, 8 * (n % 2):8 * (n % 2) + 8, 0:DK], v_rows[:, n % 4])\
                    .then_inc(v_hi_ready, 1)
                if n % 4 == 3:
                    project_high(n // 4, n // 4)
            given.wait(act)
            nc.scalar.copy(v_hi[:, TILES, :, 0:DK], mv[:]).then_inc(v_hi_ready, 1)

            def exps(u, i, first):
                act.wait_ge(max_ready, u + 1)
                if not first:
                    act.wait_ge(turned, u - 1)
                for qt in range(QT):
                    ins = nc.scalar.activation(e[i][:, qt, :], score_bank[i][:, qt, :], ACT.Exp,
                                               bias=negmax[i][:, qt:qt + 1])
                ins.then_inc(exp_ready, 1)

            def split_high(u, i, first):
                act.wait_ge(turned, u + 1)
                if not first:
                    act.wait_ge(pv_done, u - 1)
                for qt in range(QT):
                    nc.scalar.copy(et_hi[i][:, qt, :], turn_bank[qt][:, 0:KEYS]).then_inc(et_hi_ready, 1)

            def pair_steps(p, first, more):
                for j in range(UNITS):
                    u = UNITS * p + j
                    exps(u, j % 2, first and j < 2)
                    if not (first and j < 1):
                        split_high(u - 1, (j - 1) % 2, first and j < 3)
                    if j % 2 == 1 and more:
                        project_high(BATCH * p + BATCH + j // 2, j // 2)

            pair_steps(0, True, True)
            with act.Fori(1, PAIRS - 1) as p:
                pair_steps(p, False, True)
            pair_steps(PAIRS - 1, False, False)
            split_high(PAIRS * UNITS - 1, 1, False)
            for t in range(TILES):
                act.wait_ge(on_turned, t + 1)
                if t >= 2:
                    act.wait_ge(y_psum, t - 1)
                nc.scalar.copy(ont[t % 2][:].rearrange("p (h c) m -> p h (c m)", h=2),
                               g.psum[:, 2 * (t % 2):2 * (t % 2) + 2, :]).then_inc(ont_ready, 1)
            norm_finish(nc, act, nb, 1, rsd, g.x)

        @block.vector
        def _(dve):
            steps = Tally(dve, dve_steps)
            dve.wait_ge(xt_psum, 2)
            nc.vector.tensor_copy(g.xt[:, BANK:], bank[5]).then_inc(xt_ready, 1)
            given.wait(dve)

            def value_rows(n):
                dve.wait_ge(v_psum, n + 1)
                if n >= 4:
                    dve.wait_ge(v_odd_ready if n % 2 else v_even_ready, n // 2 - 1)
                nc.vector.tensor_tensor(v_rows[:, n % 4], bank[n % 4].rearrange("p (h d) -> p h d", h=8),
                                        bv[:, (n % 2) * BANK:(n % 2 + 1) * BANK].rearrange("p (h d) -> p h d", h=8),
                                        ALU.add).then_inc(v_rows_ready, 1)

            def values_low(n):
                dve.wait_ge(v_hi_ready, n + 1)
                nc.vector.tensor_tensor(v_lo[:, n // 2, 8:16, 0:DK], v_rows[:, n % 4], v_hi[:, n // 2, 8:16, 0:DK],
                                        ALU.subtract).then_inc(v_odd_ready, 1)

            def copy_queries(n, p, b, first=False):
                dve.wait_ge(projected, 2 * n + 1)
                if not first:
                    dve.wait_ge(qk_ready, n - 1)
                nc.vector.tensor_scalar(qk_whole[b % 2][:, 0, :], proj_bank[:, 0:SEQ], bqk[:, 0, ds(p, 1)], DK ** -0.5,
                                        ALU.add, ALU.mult).then_inc(qk_copied, 1)

            def copy_keys(n, p, b):
                dve.wait_ge(projected, 2 * n + 2)
                nc.vector.tensor_scalar(qk_whole[b % 2][:, 1, :], proj_bank[:, SEQ:], bqk[:, 1, ds(p, 1)], None,
                                        ALU.add).then_inc(qk_copied, 1)

            def copy_memory_keys(p):
                nc.vector.tensor_copy(mkt[:], mkt_all[:, ds(p, 1), :, :].rearrange("p o y m -> p (o y) m"))\
                    .then_inc(mkt_ready, 1)

            def maxima(u, i):
                dve.wait_ge(scored, u + 1)
                nc.vector.tensor_reduce(negmax[i][:], score_bank[i], AX.X, ALU.max, negate=True)\
                    .then_inc(max_ready, 1)

            def split_low(u, i):
                for qt in range(QT):
                    dve.wait_ge(et_hi_ready, QT * u + qt + 1)
                    nc.vector.tensor_tensor(et_lo[i][:, qt, :], turn_bank[qt][:, 0:KEYS], et_hi[i][:, qt, :],
                                            ALU.subtract).then_inc(et_lo_ready, 1)

            def copy_out(u, p, b, h):
                dve.wait_ge(pv_done, u + 1)
                nc.vector.tensor_copy(o_heads[:, QT * b:QT * b + QT, ds(h * VW + p * (2 * VW), VW)],
                                      o_bank[:, 0:QT * VW].rearrange("p (q w) -> p q w", q=QT))\
                    .then_inc(o_ready, 1)

            def pair_steps(p, first, more):
                for j in range(UNITS):
                    u = UNITS * p + j
                    if j + 1 < UNITS or more:
                        maxima(u + 1, (j + 1) % 2)
                    if more:
                        (copy_queries, copy_keys)[j % 2](BATCH * p + BATCH + j // 2, p + 1, j // 2)
                    if j == UNITS - 2 and more:
                        copy_memory_keys(p + 1)
                    if not (first and j < 1):
                        split_low(u - 1, (j - 1) % 2)
                    if not (first and j < 2):
                        jj = (j - 2) % UNITS
                        copy_out(u - 2, p if j >= 2 else p - 1, jj // 2, jj % 2)

            dve.wait_ge(mk_split, 2)
            copy_memory_keys(0)
            for n in range(2 * TILES):
                value_rows(n)
                if n % 2 and n >= 3:
                    values_low(n - 2)
                if n % 4 == 1:
                    copy_queries(n // 4, 0, n // 4, n < 8)
                if n % 4 == 3:
                    copy_keys(n // 4, 0, n // 4)
            values_low(2 * TILES - 1)
            maxima(0, 0)
            pair_steps(0, True, True)
            with dve.Fori(1, PAIRS - 1) as p:
                pair_steps(p, False, True)
            pair_steps(PAIRS - 1, False, False)
            last = PAIRS * UNITS
            split_low(last - 1, 1)
            copy_out(last - 2, PAIRS - 1, BATCH - 1, 0)
            copy_out(last - 1, PAIRS - 1, BATCH - 1, 1)
            dve.wait_ge(o_ready, last)
            dve.wait_ge(x_biased, 1)
            for t in range(TILES):
                if t >= 2:
                    dve.wait_ge(on_turned, t - 1)
                steps.step(nc.vector.reciprocal(rsum[t % 2][:], o[:, t, :, DK]))
                nc.vector.tensor_tensor(on[t % 2][:], o[:, t, :, 0:DK],
                                        rsum[t % 2][:].unsqueeze(2).broadcast_to([P, HEADS, DK]), ALU.mult)\
                    .then_inc(on_ready, 1)
                if t:
                    add_residual(nc, dve, y_psum, y_ready, steps, t - 1, bank[4 + (t - 1) % 2], rsd, g.x)
            add_residual(nc, dve, y_psum, y_ready, steps, TILES - 1, bank[5], rsd, g.x)
            steps.settle()
            norm_stats(nc, steps, nb, rsd)
            norm_scale(nc, dve, steps, nb, 1)
            norm_apply(nc, steps, nb, rsd, g.x, VECTOR_TILES)


def add_bias(nc, x, bias):
    return nc.gpsimd.tensor_tensor(x[:], x[:], bias[:].unsqueeze(1).broadcast_to([P, TILES, D]), ALU.add)


def output_product(nc, pe, ont_ready, y_ready, y_psum, t, y, cols, w):
    pe.wait_ge(ont_ready, t + 1)
    if t >= 2:
        pe.wait_ge(y_ready, t - 1)
    for c in range(w.shape[1]):
        ins = nc.tensor.matmul(y[:, 0:D], cols[:, c, :], w[:, c, :], start=(c == 0), stop=(c == w.shape[1] - 1))
    ins.then_inc(y_psum, 1)


def add_residual(nc, dve, y_psum, y_ready, steps, t, y, rows, x):
    dve.wait_ge(y_psum, t + 1)
    nc.vector.tensor_tensor(rows[:, t, :], y[:, 0:D], x[:, t, :], ALU.add).then_inc(y_ready, 1)
    steps.engine.wait_ge(y_ready, t + 1)


FHEADS, FD = 16, 8
EXPERTS = 8
HALVES = TILES // BATCH


class ExpertWeights(Weights):
    def __init__(self, nc, ctx, a):
        super().__init__(nc, ctx, "ffn")
        self.w_in, self.b_in = self.sb("w_qkv", [P, 3 * D]), self.sb("b_qkv", [P, 3 * D])
        self.w_out, self.b_out = self.sb("w_out", [P, 1, D]), self.sb("b_out", [P, D])
        self.gain = self.sb("norm_gains", [P, 4, D])
        self.w_route, self.b_route = self.sb("w_route", [P, EXPERTS]), self.sb("b_route", [P, EXPERTS])
        self.w2, self.b1 = self.sb("w2_all", [P, EXPERTS, D]), self.sb("b1_cols", [P, EXPERTS])
        self.b2 = self.sb("b2_rows", [EXPERTS, D])
        self.pairs = [
            (self.w_in[:], a["L0_ffn_in_proj_w"]), (self.b_in[:], every_row(a["L0_ffn_in_proj_b"])),
            (self.w_out[:, 0, :], a["L0_ffn_out_w"]), (self.b_out[:], every_row(a["L0_ffn_out_b"])),
            (self.gain[:, 0, :], every_row(a["L0_ffn_ln1_g"])), (self.gain[:, 1, :], every_row(a["L0_ffn_ln1_b"])),
            (self.gain[:, 2, :], every_row(a["L0_ffn_ln2_g"])), (self.gain[:, 3, :], every_row(a["L0_ffn_ln2_b"])),
            (self.w_route[:], a["L0_ffn_router_w"]), (self.b_route[:], every_row(a["L0_ffn_router_b"])),
            (self.w2[:], a["L0_ffn_w2"]), (self.b1[:], a["L0_ffn_b1"]), (self.b2[:], a["L0_ffn_b2"]),
        ]


def expert_block(nc, g, a):
    with ExitStack() as ctx:
        r = Resources(nc, ctx, g.sems, "ffn")
        w1 = [r.sb(f"w1_expert{i}", [P, D]) for i in range(2)]
        given = g.expert
        w_in, b_in, w_out, b_out, gain = given.w_in, given.b_in, given.w_out, given.b_out, given.gain
        w_route, b_route, w2, b1, b2 = given.w_route, given.b_route, given.w2, given.b1, given.b2
        w2_flat = w2[:].rearrange("p e n -> p (e n)")
        number = r.sb("expert_number", [P, EXPERTS])
        pick = r.sb("pick_expert", [EXPERTS, EXPERTS, P], BF16)
        pick_flat = pick[:].rearrange("k e p -> k (e p)")
        qkv = r.sb("qkv", [P, TILES, 3 * D])
        prod = [r.sb(f"products{i}", [P, BATCH, D]) for i in range(4)]
        sc = r.sb("batch_scores", [P, HALVES, BATCH, BATCH, FHEADS])
        sc_rows = sc[:].rearrange("p a t s h -> p (a t) s h")
        peak = r.sb("batch_peak", [P, TILES, FHEADS])
        total = r.sb("batch_total", [P, TILES, FHEADS])
        mixed = r.sb("mixed", [P, TILES, D])
        mixed_cols = r.sb("mixed_cols", [P, TILES, 1, P])
        rsd = r.sb("ffn_rows", [P, TILES, D])
        x_out = r.sb("x_plus_b_out", [P, TILES, D])
        h = r.sb("h_rows", [P, TILES, D])
        ht = r.sb("h_cols", [P, TOK])
        logit = r.sb("logits", [P, TILES, EXPERTS])
        lmax = r.sb("logit_max", [P, TILES])
        lsum = r.sb("logit_sum", [P, TILES])
        best = r.sb("best_probs", [P, TILES, 8])
        place = r.sb("best_places", [P, TILES, 8], U32)
        placef = r.sb("best_places_f", [P, TILES, 2])
        chosen = r.sb("chosen", [P, TILES])
        mask = r.sb("chosen_mask", [P, TILES, EXPERTS])
        maskt = r.sb("mask_cols", [EXPERTS, TOK])
        maskt_b = r.sb("mask_cols_b", [EXPERTS, TOK], BF16)
        he = [r.sb(f"hidden{i}", [P, TOK]) for i in range(2)]
        hem = [r.sb(f"hidden_masked{i}", [P, TOK]) for i in range(2)]
        nb = NormBuffers(r, "ffn_norm")
        x_biased, const_done, xt_psum, xt_ready, qkv_psum, qkv_ready = (r.sem(n) for n in (
            "x_biased", "const_done", "xt_psum", "xt_ready", "qkv_psum", "qkv_ready"))
        sub_ready, exp_ready, mixed_ready, mixed_psum, ont_ready, y_psum = (r.sem(n) for n in (
            "sub_ready", "exp_ready", "mixed_ready", "mixed_psum", "ont_ready", "y_psum"))
        y_ready, h_ready, ht_psum, ht_ready, logit_psum, lsub_ready = (r.sem(n) for n in (
            "y_ready", "h_ready", "ht_psum", "ht_ready", "logit_psum", "lsub_ready"))
        lexp_ready, mask_ready, maskt_psum, maskt_ready, he_psum, mask_bc = (r.sem(n) for n in (
            "lexp_ready", "mask_ready", "maskt_psum", "maskt_ready", "he_psum", "mask_bc"))
        he_ready, hem_ready, w2_done, dve_steps, pool_steps = (r.sem(n) for n in (
            "he_ready", "hem_ready", "w2_done", "dve_steps", "pool_steps"))
        expert_w1_loaded = [r.sem(f"expert_w1_loaded{i}") for i in range(2)]
        pool_products, reduced, weights_ready = (r.sem(n) for n in ("pool_products", "reduced", "weights_ready"))
        bank = [g.psum[:, i, :] for i in range(8)]

        def score_products(engine, n):
            half, t = n // BATCH, n % BATCH
            return engine.tensor_tensor(
                prod[n % 4][:], qkv[:, HALVES * t + half, 0:D].unsqueeze(1).broadcast_to([P, BATCH, D]),
                qkv[:, half::HALVES, D:2 * D], ALU.mult)

        def value_products(engine, n):
            half, t = n // BATCH, n % BATCH
            return engine.tensor_tensor(
                prod[n % 4][:].rearrange("p s (h d) -> p s h d", d=FD),
                sc[:, half, t, :, :].unsqueeze(3).broadcast_to([P, BATCH, FHEADS, FD]),
                qkv[:, half::HALVES, 2 * D:3 * D].rearrange("p s (h d) -> p s h d", d=FD), ALU.mult)

        pair = [g.psum[:, 2 * i:2 * i + 2, :] for i in range(4)]
        block = ctx.enter_context(nc.Block())

        @block.sync
        def _(sp):
            def load_expert(e, k):
                sp.dma_start(w1[k][:], a["L0_ffn_w1"].rearrange("c e h -> c (e h)")[:, ds(e * D, D)])\
                    .then_inc(expert_w1_loaded[k], 16)

            for k in range(2):
                load_expert(k, k)
            with sp.Fori(1, EXPERTS // 2) as i:
                for k in range(2):
                    sp.wait_ge(he_psum, 2 * i + k - 1)
                    load_expert(2 * i + k, k)

        @block.gpsimd
        def _(pool):
            steps = Tally(pool, pool_steps)
            for e in range(EXPERTS):
                nc.gpsimd.memset(number[:, e:e + 1], float(e))
            steps.step(nc.gpsimd.memset(pick[:], 0.0))
            nc.gpsimd.affine_select(out=pick[:], in_=pick[:], compare_op=ALU.not_equal, fill=1.0, base=0,
                                    pattern=[[-1, EXPERTS], [0, P]], channel_multiplier=1).then_inc(const_done, 1)

            given.wait(pool)
            pool.wait_ge(xt_psum, 2)
            nc.gpsimd.tensor_tensor(x_out[:], g.x[:], b_out[:].unsqueeze(1).broadcast_to([P, TILES, D]), ALU.add)\
                .then_inc(x_biased, 1)
            pool.wait_ge(x_biased, 1)
            nc.gpsimd.tensor_tensor(g.x[:], g.x[:], gain[:, 3, :].unsqueeze(1).broadcast_to([P, TILES, D]), ALU.add)\
                .then_inc(x_biased, 1)
            pool.wait_ge(qkv_ready, TILES)
            for n in range(1, TILES, 2):
                if n > 4:
                    pool.wait_ge(reduced, n - 3)
                score_products(nc.gpsimd, n).then_inc(pool_products, 1)
            pool.wait_ge(weights_ready, 1)
            for n in range(1, TILES, 2):
                if n > 4:
                    pool.wait_ge(mixed_ready, n - 3)
                value_products(nc.gpsimd, n).then_inc(pool_products, 1)

        @block.tensor
        def _(pe):
            transpose_rows(nc, pe, g.x, None, g.ident[:], bank[6:8], xt_psum)
            given.wait(pe)
            pe.wait_ge(xt_ready, 2)
            for t in range(TILES):
                if t >= 4:
                    pe.wait_ge(qkv_ready, t - 3)
                nc.tensor.matmul(bank[t % 4][:, 0:3 * D], g.xt[:, t * P:(t + 1) * P], w_in[:], start=True, stop=True)\
                    .then_inc(qkv_psum, 1)
            pe.wait_ge(qkv_ready, TILES)
            pe.wait_ge(mixed_ready, TILES)
            transpose_rows(nc, pe, mixed, None, g.ident[:], bank[4:6], mixed_psum)
            pe.wait_ge(ont_ready, 1)
            for t in range(TILES):
                y = bank[t // 4][:, (t % 4) * D:(t % 4 + 1) * D]
                ins = nc.tensor.matmul(y, mixed_cols[:, t, 0, :], w_out[:, 0, :], start=True, stop=True)
            ins.then_inc(y_psum, 1)
            pe.wait_ge(h_ready, 1)
            transpose_rows(nc, pe, h, None, g.ident[:], bank[4:6], ht_psum)
            pe.wait_ge(ht_ready, 2)
            for t in range(TILES):
                y = bank[2][:, t * EXPERTS:(t + 1) * EXPERTS]
                ins = nc.tensor.matmul(y, ht[:, t * P:(t + 1) * P], w_route[:], start=True, stop=True)
            ins.then_inc(logit_psum, 1)
            def hidden(i, k, first):
                e = 2 * i + k
                pe.wait_ge(expert_w1_loaded[k], 16 * i + 16)
                if not first:
                    pe.wait_ge(he_ready, e - 1)
                for j in range(2):
                    ins = nc.tensor.matmul(bank[2 * k + j], w1[k][:], ht[:, j * BANK:(j + 1) * BANK],
                                           start=True, stop=True)
                ins.then_inc(he_psum, 1)

            hidden(0, 0, True)
            pe.wait_ge(mask_ready, 1)
            for t in range(TILES):
                ins = nc.tensor.transpose(bank[2 + t // 4][0:EXPERTS, (t % 4) * P:(t % 4 + 1) * P],
                                          mask[:, t, :], g.ident[:])
            ins.then_inc(maskt_psum, 1)
            pe.wait_ge(maskt_ready, 1)
            pe.wait_ge(const_done, 1)
            for t in range(TILES):
                nc.tensor.matmul(bank[6 + t // 4][:, (t % 4) * D:(t % 4 + 1) * D], maskt[:, t * P:(t + 1) * P], b2[:],
                                 start=(t % 4 == 0), stop=False, skip_group_check=True)

            def spread_mask(e, first):
                if not first:
                    pe.wait_ge(hem_ready, e)
                for j in range(2):
                    ins = nc.tensor.matmul(bank[4 + j], pick_flat[:, ds(e * P, P)],
                                           maskt_b[:, j * BANK:(j + 1) * BANK], start=True, stop=True)
                ins.then_inc(mask_bc, 1)

            def outputs(e, k, last=False):
                pe.wait_ge(hem_ready, e + 1)
                for t in range(TILES):
                    ins = nc.tensor.matmul(bank[6 + t // 4][:, (t % 4) * D:(t % 4 + 1) * D],
                                           hem[k][:, t * P:(t + 1) * P], w2_flat[:, ds(e * D, D)],
                                           start=False, stop=last, skip_group_check=True)
                ins.then_inc(w2_done, 1)

            spread_mask(0, True)
            hidden(0, 1, True)
            outputs(0, 0)
            spread_mask(1, False)
            with pe.Fori(1, EXPERTS // 2) as i:
                for k in range(2):
                    e = 2 * i + k
                    hidden(i, k, False)
                    outputs(e - 1, 1 - k)
                    spread_mask(e, False)
            outputs(EXPERTS - 1, 1, True)

        @block.scalar
        def _(act):
            act.wait_ge(xt_psum, 1)
            nc.scalar.copy(g.xt[:, 0:BANK], bank[6]).then_inc(xt_ready, 1)
            act.wait_ge(sub_ready, 1)
            nc.scalar.activation(sc[:], sc[:], ACT.Exp, scale=FD ** -0.5).then_inc(exp_ready, 1)
            act.wait_ge(mixed_psum, 2)
            nc.scalar.copy(mixed_cols[:].rearrange("p (h t) o c -> p h (t o c)", h=2), pair[2])\
                .then_inc(ont_ready, 1)
            norm_root(nc, act, nb, 1)
            act.wait_ge(ht_psum, 1)
            nc.scalar.copy(ht[:, 0:BANK], bank[4]).then_inc(ht_ready, 1)
            act.wait_ge(lsub_ready, 1)
            nc.scalar.activation(logit[:], logit[:], ACT.Exp).then_inc(lexp_ready, 1)

            def gelus(e, k, first):
                act.wait_ge(he_psum, e + 1)
                if not first:
                    act.wait_ge(hem_ready, e - 1)
                nc.scalar.activation(halves(he[k][:]), pair[k], ACT.Gelu, bias=b1[:, ds(e, 1)]).then_inc(he_ready, 1)

            for k in range(2):
                gelus(k, k, True)
            with act.Fori(1, EXPERTS // 2) as i:
                for k in range(2):
                    gelus(2 * i + k, k, False)
            norm_root(nc, act, nb, 2)
            norm_finish(nc, act, nb, 3, rsd, g.x)

        @block.vector
        def _(dve):
            steps = Tally(dve, dve_steps)
            dve.wait_ge(xt_psum, 2)
            nc.vector.tensor_copy(g.xt[:, BANK:], bank[7]).then_inc(xt_ready, 1)
            given.wait(dve)
            for t in range(TILES):
                dve.wait_ge(qkv_psum, t + 1)
                nc.vector.tensor_tensor(qkv[:, t, :], bank[t % 4][:, 0:3 * D], b_in[:], ALU.add).then_inc(qkv_ready, 1)
            dve.wait_ge(qkv_ready, TILES)
            for n in range(TILES):
                if n % 2:
                    dve.wait_ge(pool_products, n // 2 + 1)
                else:
                    steps.step(score_products(nc.vector, n))
                nc.vector.tensor_reduce(sc[:, n // BATCH, n % BATCH, :, :].rearrange("p s h -> p (s h)"),
                                        prod[n % 4][:].rearrange("p s (h d) -> p (s h) d", d=FD), AX.X, ALU.add)\
                    .then_inc(reduced, 1)
            dve.wait_ge(reduced, TILES)
            steps.step(nc.vector.tensor_reduce(peak[:], sc_rows.rearrange("p a s h -> p a h s"), AX.X, ALU.max))
            bc = lambda z: z[:].unsqueeze(2).broadcast_to([P, TILES, BATCH, FHEADS])
            nc.vector.tensor_tensor(sc_rows, sc_rows, bc(peak), ALU.subtract).then_inc(sub_ready, 1)
            dve.wait_ge(exp_ready, 1)
            steps.step(nc.vector.tensor_reduce(total[:], sc_rows.rearrange("p a s h -> p a h s"), AX.X, ALU.add))
            steps.step(nc.vector.reciprocal(peak[:], total[:]))
            nc.vector.tensor_tensor(sc_rows, sc_rows, bc(peak), ALU.mult).then_inc(weights_ready, 1)
            dve.wait_ge(weights_ready, 1)
            for n in range(TILES):
                half, t = n // BATCH, n % BATCH
                if n % 2:
                    dve.wait_ge(pool_products, TILES // 2 + n // 2 + 1)
                else:
                    steps.step(value_products(nc.vector, n))
                nc.vector.tensor_reduce(mixed[:, HALVES * t + half, :], prod[n % 4][:].rearrange("p s c -> p c s"),
                                        AX.X, ALU.add).then_inc(mixed_ready, 1)
            dve.wait_ge(mixed_ready, TILES)
            dve.wait_ge(y_psum, 1)
            dve.wait_ge(x_biased, 2)
            eights = lambda z: z.rearrange("p (h t) c -> p h (t c)", h=2)
            steps.step(nc.vector.tensor_tensor(eights(rsd[:]), eights(x_out[:]), pair[0], ALU.add))
            norm_stats(nc, steps, nb, rsd)
            norm_scale(nc, dve, steps, nb, 1)
            norm_apply(nc, steps, nb, rsd, h)
            all_rows = lambda j: gain[:, j, :].unsqueeze(1).broadcast_to([P, TILES, D])
            steps.step(nc.vector.tensor_tensor(h[:], h[:], all_rows(0), ALU.mult))
            nc.vector.tensor_tensor(h[:], h[:], all_rows(1), ALU.add).then_inc(h_ready, 1)
            dve.wait_ge(ht_psum, 2)
            nc.vector.tensor_copy(ht[:, BANK:], bank[5]).then_inc(ht_ready, 1)
            dve.wait_ge(logit_psum, 1)
            steps.step(nc.vector.tensor_tensor(
                logit[:], bank[2][:, 0:TILES * EXPERTS].rearrange("p (t e) -> p t e", e=EXPERTS),
                b_route[:].unsqueeze(1).broadcast_to([P, TILES, EXPERTS]), ALU.add))
            steps.step(nc.vector.tensor_reduce(lmax[:], logit[:], AX.X, ALU.max))
            bce = lambda z: z[:].unsqueeze(2).broadcast_to([P, TILES, EXPERTS])
            nc.vector.tensor_tensor(logit[:], logit[:], bce(lmax), ALU.subtract).then_inc(lsub_ready, 1)
            dve.wait_ge(lexp_ready, 1)
            steps.step(nc.vector.tensor_reduce(lsum[:], logit[:], AX.X, ALU.add))
            steps.step(nc.vector.reciprocal(lmax[:], lsum[:]))
            steps.step(nc.vector.tensor_tensor(logit[:], logit[:], bce(lmax), ALU.mult))
            for t in range(TILES):
                steps.add(nc.vector.max(best[:, t, :], logit[:, t, :]))
            steps.settle()
            for t in range(TILES):
                steps.add(nc.vector.max_index(place[:, t, :], best[:, t, :], logit[:, t, :]))
            steps.settle()
            steps.step(nc.vector.tensor_copy(placef[:], place[:, :, 0:2]))
            steps.step(nc.vector.tensor_tensor(chosen[:], placef[:, :, 0], placef[:, :, 1], ALU.max))
            dve.wait_ge(const_done, 1)
            nc.vector.tensor_tensor(mask[:], bce(chosen), number[:].unsqueeze(1).broadcast_to([P, TILES, EXPERTS]),
                                    ALU.is_equal).then_inc(mask_ready, 1)
            dve.wait_ge(maskt_psum, 1)
            steps.step(nc.vector.tensor_copy(halves(maskt[:]), pair[1][0:EXPERTS]))
            nc.vector.tensor_copy(maskt_b[:], maskt[:]).then_inc(maskt_ready, 1)

            def masked(e, k, first):
                dve.wait_ge(he_ready, e + 1)
                dve.wait_ge(mask_bc, e + 1)
                if not first:
                    dve.wait_ge(w2_done, e - 1)
                nc.vector.tensor_tensor(halves(hem[k][:]), halves(he[k][:]), pair[2], ALU.mult).then_inc(hem_ready, 1)

            for k in range(2):
                masked(k, k, True)
            with dve.Fori(1, EXPERTS // 2) as i:
                for k in range(2):
                    masked(2 * i + k, k, False)
            dve.wait_ge(w2_done, EXPERTS)
            steps.step(nc.vector.tensor_tensor(eights(rsd[:]), eights(h[:]), pair[3], ALU.add))
            norm_stats(nc, steps, nb, rsd)
            norm_scale(nc, dve, steps, nb, 2)
            norm_apply(nc, steps, nb, rsd, h)
            steps.step(nc.vector.tensor_tensor(h[:], h[:], all_rows(2), ALU.mult))
            steps.step(nc.vector.tensor_tensor(rsd[:], h[:], g.x[:], ALU.add))
            norm_stats(nc, steps, nb, rsd)
            norm_scale(nc, dve, steps, nb, 3)
            norm_apply(nc, steps, nb, rsd, g.x, VECTOR_TILES)


GHEADS, GK = 16, 64
GPAIRS = GHEADS // 2
GW = GK + 1
CK = P + 2 * P
MASKED = -1e30


class GraphWeights(Weights):
    def __init__(self, nc, ctx, a):
        super().__init__(nc, ctx, "graph")
        self.w_qk, self.wv = self.sb("g_wqk", [P, 2, GHEADS * GK]), self.sb("g_wv", [P, GHEADS * GK])
        self.wo = self.sb("g_wo", [P, GPAIRS, D])
        self.gamma_in, self.gamma_out = self.sb("gamma_in", [P, 1]), self.sb("gamma_out", [P, D])
        self.b_g = self.sb("graph_b", [P, 2, GK])
        self.pairs = [
            (self.w_qk[:, 0, :], a["L1_attn_Wq"]), (self.w_qk[:, 1, :], a["L1_attn_Wk"]), (self.wv[:], a["L1_attn_Wv"]),
            (self.wo[:], a["L1_attn_Wo"].rearrange("(c p) n -> p c n", p=P)), (self.gamma_in[:], a["L1_attn_gamma_in"]),
            (self.gamma_out[:], every_row(a["L1_attn_gamma_out"])), (self.b_g[:, 0, :], every_row(a["L1_attn_gnn_b"][0])),
            (self.b_g[:, 1, :], every_row(a["L1_attn_gnn_b"][1])),
        ]


def graph_attention(nc, g, a):
    with ExitStack() as ctx:
        r = Resources(nc, ctx, g.sems, "graph")
        given = g.graph
        w_qk, wv, wo, b_g = given.w_qk, given.wv, given.wo, given.b_g
        gamma_in, gamma_out = given.gamma_in, given.gamma_out
        lin_wo = r.sb("g_lin_wo", [P, GPAIRS, D])
        lin_t = r.sb("lin_t_diag", [P, P])
        lin_b = r.sb("lin_b_col", [P, 1])
        w_g = [r.sb(f"graph_w_diag{l}", [P, P]) for l in range(2)]
        const_row = r.sb("lin_b_wo_row", [1, D])
        ident_b = r.sb("identity_b", [P, P], BF16)
        mask = r.sb("causal_mask", [P, P], BF16)
        head_sel = r.sb("head_select", [P, 2])
        xh = r.sb("xh_rows", [P, TILES, D])
        xnt = r.sb("xn_cols", [P, TOK])
        xb = r.sb("xn_cols_batch", [P, SEQ])
        q = r.sb("gq_cols", [P, GPAIRS, SEQ])
        k = r.sb("gk_cols", [P, GPAIRS, SEQ])
        qk = r.sb("gqk_products", [P, GPAIRS, SEQ])
        v = r.sb("g_values", [P, QT, GHEADS, GK])
        v_hi = r.sb("g_values_hi", [P, QT, GHEADS, GW], F16)
        v_lo = r.sb("g_values_lo", [P, QT, GHEADS, GW], F16)
        fb = r.sb("feats_plus_bias", [P, QT, GHEADS, GK])
        e = [r.sb(f"g_probs{i}", [P, 2, CK]) for i in range(2)]
        et_hi = r.sb("g_probs_cols_hi", [P, GHEADS, CK], F16)
        et_lo = r.sb("g_probs_cols_lo", [P, GHEADS, CK], F16)
        negmax = r.sb("g_negmax", [P, QT, GHEADS])
        sdiag = r.sb("diag_scores", [P, QT, GHEADS])
        o = r.sb("g_out_raw", [P, QT, GHEADS, GW])
        rs = r.sb("g_rsum", [P, QT, GHEADS])
        pd = r.sb("diag_probs", [P, QT, GHEADS])
        off = r.sb("one_minus_diag", [P, QT, GHEADS])
        rdeg = r.sb("inv_degree", [P, QT, GHEADS])
        keep, take = r.sb("keep_share", [P, QT, GHEADS]), r.sb("take_share", [P, QT, GHEADS])
        out_n = r.sb("g_out", [P, QT, GHEADS, GK])
        m = r.sb("propagated", [P, QT, GHEADS, GK])
        mt = r.sb("propagated_cols", [P, QT, GPAIRS, P])
        f1 = r.sb("feats1", [P, QT, GHEADS, GK])
        f1_hi = r.sb("feats1_hi", [P, QT, GHEADS, GK], F16)
        f1_lo = r.sb("feats1_lo", [P, QT, GHEADS, GK], F16)
        ot = r.sb("g_out_cols", [P, QT, GPAIRS, P])
        y = r.sb("g_y_rows", [P, TILES, D])
        nb = NormBuffers(r, "graph_norm")
        zeroed, loaded, const_done, lin_psum, lin_ready, xh_ready = (r.sem(n) for n in (
            "zeroed", "loaded", "const_done", "lin_psum", "lin_ready", "xh_ready"))
        xt_psum, xt_ready, xb_ready, v_psum, v_ready, v_ones = (r.sem(n) for n in (
            "xt_psum", "xt_ready", "xb_ready", "v_psum", "v_ready", "v_ones"))
        qk_psum, prod_ready, diag_psum, sdiag_ready = (r.sem(n) for n in (
            "qk_psum", "prod_ready", "diag_psum", "sdiag_ready"))
        scored, max_ready, exp_ready, turned, et_hi_ready, et_lo_ready = (r.sem(n) for n in (
            "scored", "max_ready", "exp_ready", "turned", "et_hi_ready", "et_lo_ready"))
        pv_done, o_ready, dsub_ready, dexp_ready, stats_ready, out_ready = (r.sem(n) for n in (
            "pv_done", "o_ready", "dsub_ready", "dexp_ready", "stats_ready", "out_ready"))
        fb_ready, kept, m_ready, m_turned, mt_ready, h_psum = (r.sem(n) for n in (
            "fb_ready", "kept", "m_ready", "m_turned", "mt_ready", "h_psum"))
        pre_ready, feat_ready, pv1_done, qk_ready, out_turned, ot_ready = (r.sem(n) for n in (
            "pre_ready", "feat_ready", "pv1_done", "qk_ready", "out_turned", "ot_ready"))
        f_turned, ft_ready, y_psum, y_ready, dve_steps = (r.sem(n) for n in (
            "f_turned", "ft_ready", "y_psum", "y_ready", "dve_steps"))
        end_steps, end_steps_v, v_hi_ready, v_lo_ready, f1_lo_ready, taken = (r.sem(n) for n in (
            "end_steps", "end_steps_v", "v_hi_ready", "v_lo_ready", "f1_lo_ready", "taken"))
        bank = [g.psum[:, i, :] for i in range(8)]
        pair = [g.psum[:, 2 * i:2 * i + 2, :] for i in range(4)]
        flat = lambda z, qt: z[:, qt].rearrange("p h d -> p (h d)")
        two = lambda z: z.rearrange("p (h n) -> p h n", h=2)
        spread = lambda z, qt: z[:, qt, :].unsqueeze(2).broadcast_to([P, GHEADS, GK])
        heads = lambda z: z.rearrange("p (h d) -> p h d", d=GK)
        block = ctx.enter_context(nc.Block())

        @block.sync
        def _(sp):
            sp.wait_ge(zeroed, 1)
            for i in range(2):
                rows = slice(i * GK, (i + 1) * GK)
                sp.dma_start(lin_t[rows, rows], a["L1_attn_lin_w"]).then_inc(loaded, 16)
                sp.dma_start(lin_b[rows, :], a["L1_attn_lin_b"]).then_inc(loaded, 16)
                for l in range(2):
                    sp.dma_start(w_g[l][rows, rows], a["L1_attn_gnn_w"][l]).then_inc(loaded, 16)

        LOADS = 8 * 16
        @block.gpsimd
        def _(pool):
            steps = Tally(pool, end_steps)
            for z in (lin_t, w_g[0]):
                nc.gpsimd.memset(z[:], 0.0)
            nc.gpsimd.memset(w_g[1][:], 0.0).then_inc(zeroed, 1)
            nc.gpsimd.memset(v_hi[:, :, :, GK], 1.0).then_inc(v_ones, 1)
            nc.gpsimd.memset(v_lo[:, :, :, GK], 0.0).then_inc(v_ones, 1)
            steps.add(nc.gpsimd.memset(mask[:], 0.0))
            steps.add(nc.gpsimd.memset(ident_b[:], 0.0))
            steps.step(nc.gpsimd.memset(head_sel[:], 1.0))
            nc.gpsimd.affine_select(out=mask[:], in_=mask[:], compare_op=ALU.is_ge, fill=MASKED, base=0,
                                    pattern=[[-1, P]], channel_multiplier=1).then_inc(const_done, 1)
            nc.gpsimd.affine_select(out=ident_b[:], in_=ident_b[:], compare_op=ALU.not_equal, fill=1.0, base=0,
                                    pattern=[[-1, P]], channel_multiplier=1).then_inc(const_done, 1)
            steps.step(nc.gpsimd.affine_select(out=head_sel[:], in_=head_sel[:], compare_op=ALU.is_ge, fill=0.0,
                                               base=0, pattern=[[-GK, 2]], channel_multiplier=1))
            nc.gpsimd.affine_select(out=head_sel[:], in_=head_sel[:], compare_op=ALU.is_ge, fill=0.0, base=GK - 1,
                                    pattern=[[GK, 2]], channel_multiplier=-1).then_inc(const_done, 1)

            def copy_batch(b):
                nc.gpsimd.tensor_copy(xb[:], xnt[:, ds(b * SEQ, SEQ)]).then_inc(xb_ready, 1)

            def keep_share(f, qt):
                nc.gpsimd.tensor_tensor(m[:, qt], f[:, qt], spread(keep, qt), ALU.mult).then_inc(kept, 1)

            given.wait(pool)
            b_all = lambda l: b_g[:, l, :].unsqueeze(1).broadcast_to([P, GHEADS, GK])

            def diagonal_products(b):
                pool.wait_ge(qk_ready, GPAIRS * b + GPAIRS)
                nc.gpsimd.tensor_tensor(qk[:], q[:], k[:], ALU.mult).then_inc(prod_ready, 1)

            def values_low(b):
                for n in range(4):
                    qt, some = n // 2, slice(8 * (n % 2), 8 * (n % 2) + 8)
                    pool.wait_ge(v_hi_ready, 4 * b + n + 1)
                    nc.gpsimd.tensor_tensor(v_lo[:, qt, some, 0:GK], v[:, qt, some, :], v_hi[:, qt, some, 0:GK],
                                            ALU.subtract).then_inc(v_lo_ready, 1)

            def batch(b, more, next_more):
                for qt in range(QT):
                    nc.gpsimd.tensor_tensor(fb[:, qt], v[:, qt], b_all(0), ALU.add).then_inc(fb_ready, 1)
                pool.wait_ge(stats_ready, 2 * b + 1)
                for qt in range(QT):
                    keep_share(v, qt)
                for qt in range(QT):
                    pool.wait_ge(m_ready, 4 * b + qt + 1)
                    nc.gpsimd.tensor_tensor(out_n[:, qt], o[:, qt, :, 0:GK], spread(rs, qt), ALU.mult)\
                        .then_inc(out_ready, 1)
                if more:
                    diagonal_products(b + 1)
                for qt in range(QT):
                    pool.wait_ge(feat_ready, 6 * b + 2 * qt + 1)
                    pool.wait_ge(m_turned, 4 * b + qt + 1)
                    keep_share(f1, qt)
                for qt in range(QT):
                    pool.wait_ge(feat_ready, 6 * b + 2 * qt + 2)
                    nc.gpsimd.tensor_tensor(fb[:, qt], f1[:, qt], b_all(1), ALU.add).then_inc(fb_ready, 1)
                if next_more:
                    pool.wait_ge(v_psum, 4 * b + 8)
                    copy_batch(b + 2)
                if more:
                    values_low(b + 1)

            pool.wait_ge(xt_ready, 2)
            copy_batch(0)
            diagonal_products(0)
            pool.wait_ge(v_psum, 4)
            copy_batch(1)
            values_low(0)
            batch(0, True, True)
            with pool.Fori(1, BATCH - 2) as b:
                batch(b, True, True)
            batch(BATCH - 2, True, False)
            batch(BATCH - 1, False, False)

        @block.tensor
        def _(pe):
            pe.wait_ge(xh_ready, 1)
            transpose_rows(nc, pe, xh, None, g.ident[:], bank[4:6], xt_psum)
            pe.wait_ge(const_done, 3)
            pe.wait_ge(v_ones, 2)

            def queries_keys(b, pairs):
                for c in pairs:
                    if c >= 2:
                        pe.wait_ge(qk_ready, GPAIRS * b + c - 1)
                    for j in range(2):
                        ins = nc.tensor.matmul(bank[4 + c % 2][:, j * SEQ:(j + 1) * SEQ], w_qk[:, j, c * P:(c + 1) * P],
                                               xb[:], start=True, stop=True)
                    ins.then_inc(qk_psum, 1)

            def value_rows(b):
                for n in range(4):
                    qt, half = n // 2, n % 2
                    nc.tensor.matmul(bank[4 * qt + half], xb[:, qt * P:(qt + 1) * P],
                                     wv[:, half * BANK:(half + 1) * BANK], start=True, stop=True).then_inc(v_psum, 1)

            def diagonal_scores(b):
                pe.wait_ge(prod_ready, b + 1)
                for c in range(GPAIRS):
                    for qt in range(QT):
                        ins = nc.tensor.matmul(bank[7][:, (qt * GPAIRS + c) * 2:(qt * GPAIRS + c + 1) * 2],
                                               qk[:, c, qt * P:(qt + 1) * P], head_sel[:], start=True, stop=True)
                ins.then_inc(diag_psum, 1)

            def scores(b, c):
                if c >= 2:
                    pe.wait_ge(exp_ready, GPAIRS * b + c - 1)
                for h in range(2):
                    rows = slice(h * GK, (h + 1) * GK)
                    sb = bank[2 * (c % 2) + h]
                    nc.tensor.matmul(sb[:, 0:P], q[rows, c, 0:P], k[rows, c, 0:P], start=True, stop=False)
                    nc.tensor.matmul(sb[:, 0:P], ident_b[:], mask[:], start=False, stop=True)
                    nc.tensor.matmul(sb[:, P:CK], q[rows, c, P:SEQ], k[rows, c, :], start=True, stop=False)
                    ins = nc.tensor.matmul(sb[:, 2 * P:CK], ident_b[:], mask[:], start=False, stop=True)
                ins.then_inc(scored, 1)

            def turn(b, c):
                pe.wait_ge(exp_ready, GPAIRS * b + c + 1)
                if c >= 1:
                    pe.wait_ge(et_lo_ready, 2 * GPAIRS * b + 2 * c)
                for h in range(2):
                    for j in range(3):
                        ins = nc.tensor.transpose(bank[4 + h][:, j * P:(j + 1) * P], e[c % 2][:, h, j * P:(j + 1) * P],
                                                  g.ident[:])
                ins.then_inc(turned, 1)

            def propagate(dst, head, qt, f_hi, f_lo):
                blocks = ((0, 0),) if qt == 0 else ((1, 0), (2, 1))
                for n, (block_at, kt) in enumerate(blocks):
                    cols = slice(block_at * P, (block_at + 1) * P)
                    for i, (probs, f) in enumerate(((et_hi, f_hi), (et_lo, f_hi), (et_hi, f_lo))):
                        ins = nc.tensor.matmul(dst, probs[:, head, cols], f(kt), start=(n == 0 and i == 0),
                                               stop=(n == len(blocks) - 1 and i == 2))
                return ins

            def values(b, c):
                pe.wait_ge(et_lo_ready, 2 * GPAIRS * b + 2 * c + 2)
                if c >= 1:
                    pe.wait_ge(o_ready, GPAIRS * b + c)
                for h in range(2):
                    head = 2 * c + h
                    for qt in range(QT):
                        ins = propagate(bank[6][:, (2 * qt + h) * GW:(2 * qt + h + 1) * GW], head, qt,
                                        lambda kt: v_hi[:, kt, head, :], lambda kt: v_lo[:, kt, head, :])
                ins.then_inc(pv_done, 1)

            def turn_wide(src, qt, where, done):
                for c in range(GPAIRS):
                    ins = nc.tensor.transpose(bank[2 * where + c // 4][:, (c % 4) * P:(c % 4 + 1) * P],
                                              src[:, qt, 2 * c:2 * c + 2, :].rearrange("p h d -> p (h d)"), g.ident[:])
                ins.then_inc(done, 1)

            def graph_product(b, l, qt):
                pe.wait_ge(mt_ready, 4 * b + 2 * l + qt + 1)
                for c in range(GPAIRS):
                    ins = nc.tensor.matmul(bank[4 * qt + 2 + c // 4][:, (c % 4) * P:(c % 4 + 1) * P],
                                           mt[:, qt, c, :], w_g[l][:], start=True, stop=True)
                ins.then_inc(h_psum, 1)

            def turn_propagated(b, l, qt):
                pe.wait_ge(m_ready, 4 * b + 2 * l + qt + 1)
                turn_wide(m, qt, 2 * qt, m_turned)

            def batch(b, first, more):
                for c in range(GPAIRS + 2):
                    if c == 1 and not first:
                        pe.wait_ge(y_ready, 2 * b)
                    if c == 2:
                        pe.wait_ge(v_lo_ready, 4 * b + 4)
                    if c < GPAIRS:
                        scores(b, c)
                    if 1 <= c <= GPAIRS:
                        turn(b, c - 1)
                    if c >= 2:
                        values(b, c - 2)
                if more:
                    pe.wait_ge(xb_ready, b + 2)
                    queries_keys(b + 1, range(GPAIRS - 2))
                pe.wait_ge(o_ready, GPAIRS * b + GPAIRS)
                pe.wait_ge(sdiag_ready, b + 1)
                turn_propagated(b, 0, 0)
                if more:
                    queries_keys(b + 1, range(GPAIRS - 2, GPAIRS))
                graph_product(b, 0, 0)
                if more:
                    pe.wait_ge(qk_ready, GPAIRS * b + 2 * GPAIRS)
                turn_propagated(b, 0, 1)
                graph_product(b, 0, 1)
                for l in range(2):
                    if l == 1:
                        for qt in range(QT):
                            turn_propagated(b, 1, qt)
                        for qt in range(QT):
                            graph_product(b, 1, qt)
                    else:
                        for qt in range(QT):
                            pe.wait_ge(out_ready, 2 * b + qt + 1)
                            turn_wide(out_n, qt, 2 * qt, out_turned)
                        if more:
                            pe.wait_ge(pre_ready, 4 * b + 2)
                            diagonal_scores(b + 1)
                        for qt in range(QT):
                            if qt == 1 and more:
                                pe.wait_ge(sdiag_ready, b + 2)
                            pe.wait_ge(f1_lo_ready, 2 * b + qt + 1)
                            for head in range(GHEADS):
                                ins = propagate(bank[4 * qt + 2 + head // 8][:, (head % 8) * GK:(head % 8 + 1) * GK],
                                                head, qt, lambda kt: f1_hi[:, kt, head, :],
                                                lambda kt: f1_lo[:, kt, head, :])
                            ins.then_inc(pv1_done, 1)
                        for qt in range(QT):
                            pe.wait_ge(ot_ready, 2 * b + qt + 1)
                if more:
                    value_rows(b + 1)
                for qt in range(QT):
                    pe.wait_ge(pre_ready, 4 * b + 3 + qt)
                    for c in range(GPAIRS):
                        nc.tensor.matmul(bank[4 * qt + 2][:, 0:D], ot[:, qt, c, :], wo[:, c, :], start=(c == 0),
                                         stop=False)
                for qt in range(QT):
                    pe.wait_ge(feat_ready, 6 * b + 5 + qt)
                    if more:
                        pe.wait_ge(v_ready, 4 * b + 6 + 2 * qt)
                    turn_wide(m, qt, 2 * qt, f_turned)
                for qt in range(QT):
                    pe.wait_ge(ft_ready, 2 * b + qt + 1)
                    dst = bank[4 * qt + 2][:, 0:D]
                    for c in range(GPAIRS):
                        nc.tensor.matmul(dst, mt[:, qt, c, :], lin_wo[:, c, :], start=False, stop=False)
                    nc.tensor.matmul(dst, g.ones_row[:], const_row[:], start=False, stop=True).then_inc(y_psum, 1)

            pe.wait_ge(xt_ready, 2)
            given.wait(pe)
            pe.wait_ge(xb_ready, 1)
            queries_keys(0, range(GPAIRS))
            pe.wait_ge(qk_ready, GPAIRS)
            value_rows(0)
            pe.wait_ge(v_ready, 4)
            pe.wait_ge(loaded, LOADS)
            for c in range(GPAIRS):
                ins = nc.tensor.matmul(bank[c // 4][:, (c % 4) * D:(c % 4 + 1) * D], lin_t[:], wo[:, c, :],
                                       start=True, stop=True)
            for c in range(GPAIRS):
                ins = nc.tensor.matmul(bank[2][0:1, 0:D], lin_b[:], wo[:, c, :], start=(c == 0), stop=(c == GPAIRS - 1))
            ins.then_inc(lin_psum, 1)
            diagonal_scores(0)
            pe.wait_ge(sdiag_ready, 1)
            pe.wait_ge(lin_ready, 1)
            batch(0, True, True)
            with pe.Fori(1, BATCH - 1) as b:
                batch(b, False, True)
            batch(BATCH - 1, False, False)

        @block.scalar
        def _(act):
            norm_root(nc, act, nb, 1)
            given.wait(act)
            act.wait_ge(xt_psum, 1)
            nc.scalar.activation(xnt[:, 0:BANK], bank[4], ACT.Copy, scale=gamma_in[:, 0:1]).then_inc(xt_ready, 1)

            def copy_queries_keys(b, pairs):
                for c in pairs:
                    act.wait_ge(qk_psum, GPAIRS * b + c + 1)
                    nc.scalar.activation(q[:, c, :], bank[4 + c % 2][:, 0:SEQ], ACT.Copy, scale=GK ** -0.5)
                    nc.scalar.copy(k[:, c, :], bank[4 + c % 2][:, SEQ:]).then_inc(qk_ready, 1)

            def copy_cols(dst, qt, done):
                nc.scalar.copy(two(dst[:, qt].rearrange("p c n -> p (c n)")), pair[2 * qt]).then_inc(done, 1)

            def values_high(b):
                for n in range(4):
                    qt, some = n // 2, slice(8 * (n % 2), 8 * (n % 2) + 8)
                    act.wait_ge(v_ready, 4 * b + n + 1)
                    nc.scalar.copy(v_hi[:, qt, some, 0:GK], v[:, qt, some, :]).then_inc(v_hi_ready, 1)

            def copy_propagated(b, l, qt):
                act.wait_ge(m_turned, 4 * b + 2 * l + qt + 1)
                copy_cols(mt, qt, mt_ready)

            def batch(b, more):
                for c in range(GPAIRS + 1):
                    if c >= 1:
                        act.wait_ge(turned, GPAIRS * b + c)
                        for h in range(2):
                            nc.scalar.copy(et_hi[:, 2 * c - 2 + h, :], bank[4 + h][:, 0:CK]).then_inc(et_hi_ready, 1)
                    if c < GPAIRS:
                        act.wait_ge(max_ready, GPAIRS * b + c + 1)
                        if c >= 2:
                            act.wait_ge(turned, GPAIRS * b + c - 1)
                        for h in range(2):
                            for lo, hi, qt in ((0, P, 0), (P, CK, 1)):
                                ins = nc.scalar.activation(e[c % 2][:, h, lo:hi], bank[2 * (c % 2) + h][:, lo:hi],
                                                           ACT.Exp, bias=negmax[:, qt, 2 * c + h:2 * c + h + 1])
                        ins.then_inc(exp_ready, 1)
                act.wait_ge(dsub_ready, b + 1)
                nc.scalar.activation(pd[:], pd[:], ACT.Exp).then_inc(dexp_ready, 1)
                if more:
                    copy_queries_keys(b + 1, range(GPAIRS - 2))
                copy_propagated(b, 0, 0)
                if more:
                    copy_queries_keys(b + 1, range(GPAIRS - 2, GPAIRS))
                copy_propagated(b, 0, 1)
                for l in range(2):
                    if l == 1:
                        for qt in range(QT):
                            copy_propagated(b, 1, qt)
                    for qt in range(QT):
                        act.wait_ge(pre_ready, 4 * b + 2 * l + qt + 1)
                        for dst in ((f1, f1_hi) if l == 0 else (m, )):
                            nc.scalar.activation(dst[:, qt], fb[:, qt], ACT.Gelu).then_inc(feat_ready, 1)
                    if l == 0:
                        for qt in range(QT):
                            act.wait_ge(out_turned, 2 * b + qt + 1)
                            copy_cols(ot, qt, ot_ready)
                if more:
                    values_high(b + 1)
                for qt in range(QT):
                    act.wait_ge(f_turned, 2 * b + qt + 1)
                    copy_cols(mt, qt, ft_ready)

            copy_queries_keys(0, range(GPAIRS))
            values_high(0)
            batch(0, True)
            with act.Fori(1, BATCH - 1) as b:
                batch(b, True)
            batch(BATCH - 1, False)
            norm_root(nc, act, nb, 2)
            norm_finish(nc, act, nb, 3, xh, g.x)

        DVE_CHAIN = 5

        @block.vector
        def _(dve):
            ends = Tally(dve, end_steps_v)
            norm_stats(nc, ends, nb, g.x)
            norm_scale(nc, dve, ends, nb, 1)
            norm_apply(nc, ends, nb, g.x, xh)
            nc.vector.memset(pd[:], 0.0).then_inc(xh_ready, 1)
            given.wait(dve)
            dve.wait_ge(xt_psum, 2)
            nc.vector.tensor_scalar(xnt[:, BANK:], bank[5], gamma_in[:, 0:1], None, ALU.mult).then_inc(xt_ready, 1)

            def copy_values(b):
                for n in range(4):
                    qt, half = n // 2, n % 2
                    dve.wait_ge(v_psum, 4 * b + n + 1)
                    nc.vector.tensor_copy(v[:, qt, 8 * half:8 * half + 8, :], heads(bank[4 * qt + half]))\
                        .then_inc(v_ready, 1)

            def copy_diagonal(b):
                dve.wait_ge(diag_psum, b + 1)
                nc.vector.tensor_copy(sdiag[:].rearrange("p q h -> p (q h)"), bank[7][:, 0:2 * GHEADS])\
                    .then_inc(sdiag_ready, 1)

            def take_share(b, l, qt):
                if l == 0:
                    dst, src, by = out_n[:, qt], o[:, qt, :, 0:GK], spread(take, qt)
                else:
                    dve.wait_ge(out_turned, 2 * b + qt + 1)
                    dve.wait_ge(pv1_done, 2 * b + qt + 1)
                    by_bank = lambda z: z.rearrange("p (n h) d -> p n h d", n=2)
                    dst, by = by_bank(out_n[:, qt]), by_bank(spread(take, qt))
                    src = pair[2 * qt + 1].rearrange("p n (h d) -> p n h d", d=GK)
                nc.vector.tensor_tensor(dst, src, by, ALU.mult).then_inc(taken, 1)

            def add_shares(b, l, qt):
                dve.wait_ge(taken, 4 * b + 2 * l + qt + 1)
                dve.wait_ge(kept, 4 * b + 2 * l + qt + 1)
                nc.vector.tensor_tensor(m[:, qt], m[:, qt], out_n[:, qt], ALU.add).then_inc(m_ready, 1)

            def batch(b, more):
                steps = Tally(dve, dve_steps, DVE_CHAIN * b)
                for c in range(GPAIRS + 2):
                    if c < GPAIRS:
                        dve.wait_ge(scored, GPAIRS * b + c + 1)
                        sb = g.psum[:, 2 * (c % 2):2 * (c % 2) + 2, :]
                        nc.vector.tensor_reduce(negmax[:, 0, 2 * c:2 * c + 2], sb[:, :, 0:P], AX.X, ALU.max, negate=True)
                        nc.vector.tensor_reduce(negmax[:, 1, 2 * c:2 * c + 2], sb[:, :, P:CK], AX.X, ALU.max,
                                                negate=True).then_inc(max_ready, 1)
                    if 1 <= c <= GPAIRS:
                        for h in range(2):
                            dve.wait_ge(et_hi_ready, 2 * GPAIRS * b + 2 * c - 1 + h)
                            nc.vector.tensor_tensor(et_lo[:, 2 * c - 2 + h, :], bank[4 + h][:, 0:CK],
                                                    et_hi[:, 2 * c - 2 + h, :], ALU.subtract).then_inc(et_lo_ready, 1)
                    if c >= 2:
                        dve.wait_ge(pv_done, GPAIRS * b + c - 1)
                        nc.vector.tensor_copy(
                            o[:, :, 2 * c - 4:2 * c - 2, :].rearrange("p q h w -> p q (h w)"),
                            bank[6][:, 0:4 * GW].rearrange("p (q n) -> p q n", q=QT)).then_inc(o_ready, 1)
                    if c == GPAIRS:
                        dve.wait_ge(max_ready, GPAIRS * b + GPAIRS)
                        dve.wait_ge(sdiag_ready, b + 1)
                        nc.vector.tensor_tensor(pd[:], sdiag[:], negmax[:], ALU.add).then_inc(dsub_ready, 1)
                dve.wait_ge(o_ready, GPAIRS * b + GPAIRS)
                steps.step(nc.vector.reciprocal(rs[:], o[:, :, :, GK]))
                dve.wait_ge(dexp_ready, b + 1)
                steps.step(nc.vector.tensor_tensor(pd[:], pd[:], rs[:], ALU.mult))
                steps.add(nc.vector.tensor_scalar(off[:], pd[:], -1.0, 1.0, ALU.mult, ALU.add))
                steps.step(nc.vector.tensor_scalar(rdeg[:], pd[:], -1.0, 2.0, ALU.mult, ALU.add))
                steps.step(nc.vector.reciprocal(rdeg[:], rdeg[:]))
                nc.vector.tensor_tensor(keep[:], off[:], rdeg[:], ALU.mult).then_inc(stats_ready, 1)
                nc.vector.tensor_tensor(take[:], rs[:], rdeg[:], ALU.mult).then_inc(stats_ready, 1)
                dve.wait_ge(stats_ready, 2 * b + 2)
                for l in range(2):
                    if l == 0:
                        take_share(b, 0, 0)
                        take_share(b, 0, 1)
                        add_shares(b, 0, 0)
                        add_shares(b, 0, 1)
                    else:
                        for qt in range(QT):
                            take_share(b, 1, qt)
                            add_shares(b, 1, qt)
                    for qt in range(QT):
                        dve.wait_ge(h_psum, 4 * b + 2 * l + qt + 1)
                        dve.wait_ge(fb_ready, 4 * b + 2 * l + qt + 1)
                        nc.vector.tensor_tensor(two(flat(fb, qt)), two(flat(fb, qt)), pair[2 * qt + 1], ALU.add)\
                            .then_inc(pre_ready, 1)
                    if l == 1 and more:
                        copy_values(b + 1)
                    if l == 0:
                        if more:
                            copy_diagonal(b + 1)
                        for qt in range(QT):
                            dve.wait_ge(feat_ready, 6 * b + 2 * qt + 2)
                            nc.vector.tensor_tensor(f1_lo[:, qt], f1[:, qt], f1_hi[:, qt], ALU.subtract)\
                                .then_inc(f1_lo_ready, 1)
                for qt in range(QT):
                    dve.wait_ge(y_psum, 2 * b + qt + 1)
                    nc.vector.tensor_copy(y[:, ds(QT * b + qt, 1), :].rearrange("p o c -> p (o c)"),
                                          bank[4 * qt + 2][:, 0:D]).then_inc(y_ready, 1)

            copy_values(0)
            dve.wait_ge(lin_psum, 1)
            nc.vector.tensor_copy(two(lin_wo[:].rearrange("p c n -> p (c n)")), pair[0])
            nc.vector.tensor_copy(const_row[:], bank[2][0:1, 0:D]).then_inc(lin_ready, 1)
            copy_diagonal(0)
            batch(0, True)
            with dve.Fori(1, BATCH - 1) as b:
                batch(b, True)
            batch(BATCH - 1, False)
            dve.wait_ge(y_ready, 2 * BATCH)
            norm_stats(nc, ends, nb, y)
            norm_scale(nc, dve, ends, nb, 2)
            norm_apply(nc, ends, nb, y, xh)
            ends.step(nc.vector.tensor_tensor(xh[:], xh[:], gamma_out[:].unsqueeze(1).broadcast_to([P, TILES, D]),
                                              ALU.mult))
            ends.step(nc.vector.tensor_tensor(xh[:], xh[:], g.x[:], ALU.add))
            norm_stats(nc, ends, nb, xh)
            norm_scale(nc, dve, ends, nb, 3)
            norm_apply(nc, ends, nb, xh, g.x, VECTOR_TILES)


NHEADS, NK = 16, 8
NW = NK + 1


class NarrowWeights(Weights):
    def __init__(self, nc, ctx, a):
        super().__init__(nc, ctx, "narrow")
        self.w, self.bqk = self.sb("n_w", [P, 4, D]), self.sb("n_bqk", [P, 2])
        self.bv, self.bo = self.sb("n_bv", [P, D]), self.sb("n_bo", [P, D])
        self.pairs = [(self.w[:, j, :], a[f"L1_xattn_W{name}"]) for j, name in enumerate("qkvo")] + [
            (self.bqk[:, 0:1], a["L1_xattn_bq"]), (self.bqk[:, 1:2], a["L1_xattn_bk"]),
            (self.bv[:], every_row(a["L1_xattn_bv"])), (self.bo[:], every_row(a["L1_xattn_bo"])),
        ]


def narrow_attention(nc, g, a):
    with ExitStack() as ctx:
        r = Resources(nc, ctx, g.sems, "narrow")
        given = g.narrow
        w, bqk, bv, bo = given.w, given.bqk, given.bv, given.bo
        sel = r.sb("head_rows", [P, NHEADS])
        q, k = r.sb("nq_cols", [P, TOK]), r.sb("nk_cols", [P, TOK])
        q_parts = [r.sb(f"nq_part{i}", [P, TOK], F16) for i in range(2)]
        k_parts = [r.sb(f"nk_part{i}", [P, TOK], F16) for i in range(2)]
        qm = [[r.sb(f"nq_head{i}_part{j}", [P, TOK], F16) for j in range(2)] for i in range(2)]
        v = r.sb("n_value_rows", [P, TILES, NHEADS, NK])
        v_both = r.sb("n_values_parts", [P, TILES, NHEADS, 2, NW], F16)
        v_flat = v_both[:].rearrange("p t h y w -> p (t h y w)")
        v_parts = [v_both[:, :, :, y, :] for y in range(2)]
        e = [r.sb(f"n_probs{i}", [P, QT, SEQ]) for i in range(2)]
        et = [[r.sb(f"n_probs_cols{i}_part{j}", [P, QT, SEQ], F16) for j in range(2)] for i in range(2)]
        negmax = [r.sb(f"n_negmax{i}", [P, QT]) for i in range(4)]
        o_both = r.sb("n_out_raw", [P, TILES, NHEADS, 2, NW])
        o_heads = o_both[:].rearrange("p t h y w -> p t (h y w)")
        o = r.sb("n_out_sum", [P, TILES * NHEADS, NW])
        rsum = r.sb("n_rsum", [P, TILES, NHEADS])
        on = r.sb("n_out", [P, TILES, D])
        ont = r.sb("n_out_cols", [P, TILES, P])
        rsd = r.sb("n_rows", [P, TILES, D])
        nb = NormBuffers(r, "narrow_norm")
        x_biased, sel_ready, xt_psum, xt_ready, q_psum, q_ready = (r.sem(n) for n in (
            "x_biased", "sel_ready", "xt_psum", "xt_ready", "q_psum", "q_ready"))
        k_ready, v_psum, v_ready, v_ones, qm_ready, scored = (r.sem(n) for n in (
            "k_ready", "v_psum", "v_ready", "v_ones", "qm_ready", "scored"))
        max_ready, exp_ready, turned, et_hi_ready, et_lo_ready, pv_done = (r.sem(n) for n in (
            "max_ready", "exp_ready", "turned", "et_hi_ready", "et_lo_ready", "pv_done"))
        o_ready, on_ready, on_turned, ont_ready, y_psum, dve_steps = (r.sem(n) for n in (
            "o_ready", "on_ready", "on_turned", "ont_ready", "y_psum", "dve_steps"))
        pool_steps, q_hi_ready, k_hi_ready, v_hi_ready, lo_ready = (r.sem(n) for n in (
            "pool_steps", "q_hi_ready", "k_hi_ready", "v_hi_ready", "lo_ready"))
        PARTS = ((0, 0), (1, 0), (0, 1))
        bank = [g.psum[:, i, :] for i in range(8)]
        pair = [g.psum[:, 2 * i:2 * i + 2, :] for i in range(4)]
        score_bank = [bank[0], bank[1], bank[4], bank[5]]
        HUNITS = 2 * BATCH
        block = ctx.enter_context(nc.Block())

        @block.sync
        def _(sp):
            g.quantised.load(sp)

        @block.gpsimd
        def _(pool):
            steps = Tally(pool, pool_steps)
            nc.gpsimd.memset(v_parts[0][:, :, :, NK], 1.0).then_inc(v_ones, 1)
            nc.gpsimd.memset(v_parts[1][:, :, :, NK], 0.0).then_inc(v_ones, 1)
            steps.step(nc.gpsimd.memset(sel[:], 1.0))
            steps.step(nc.gpsimd.affine_select(out=sel[:], in_=sel[:], compare_op=ALU.is_ge, fill=0.0, base=0,
                                               pattern=[[-NK, NHEADS]], channel_multiplier=1))
            nc.gpsimd.affine_select(out=sel[:], in_=sel[:], compare_op=ALU.is_ge, fill=0.0, base=NK - 1,
                                    pattern=[[NK, NHEADS]], channel_multiplier=-1).then_inc(sel_ready, 1)
            pool.wait_ge(v_hi_ready, 1)
            nc.gpsimd.tensor_tensor(v_parts[1][:, :, :, 0:NK], v[:], v_parts[0][:, :, :, 0:NK], ALU.subtract)\
                .then_inc(lo_ready, 1)
            pool.wait_ge(lo_ready, 3)
            pool.wait_ge(sel_ready, 1)

            def mask_queries(head, i):
                for part in range(2):
                    nc.gpsimd.tensor_tensor(qm[i][part][:], q_parts[part][:],
                                            sel[:, ds(head, 1)].broadcast_to([P, TOK]), ALU.mult).then_inc(qm_ready, 1)

            mask_queries(0, 0)
            mask_queries(1, 1)
            given.wait(pool)
            pool.wait_ge(xt_psum, 2)
            add_bias(nc, g.x, bo).then_inc(x_biased, 1)
            with pool.Fori(0, NHEADS // 2 - 1) as p:
                for h in range(2):
                    pool.wait_ge(scored, HUNITS * p + BATCH * (h + 1))
                    mask_queries(2 * p + 2 + h, h)

        @block.tensor
        def _(pe):
            transpose_rows(nc, pe, g.x, None, g.ident[:], bank[0:2], xt_psum)
            given.wait(pe)
            for j in range(2):
                nc.tensor.matmul(bank[4 + j], w[:, 1, :], g.ct[:, j * BANK:(j + 1) * BANK], start=True, stop=True)
            for t in range(TILES):
                ins = nc.tensor.matmul(bank[6 + t // 4][:, (t % 4) * D:(t % 4 + 1) * D], g.ct[:, t * P:(t + 1) * P],
                                       w[:, 2, :], start=True, stop=True)
            ins.then_inc(v_psum, 1)
            pe.wait_ge(xt_ready, 2)
            for j in range(2):
                ins = nc.tensor.matmul(bank[2 + j], w[:, 0, :], g.xt[:, j * BANK:(j + 1) * BANK], start=True, stop=True)
            ins.then_inc(q_psum, 1)
            pe.wait_ge(v_ready, 1)
            pe.wait_ge(v_ones, 2)
            pe.wait_ge(lo_ready, 3)

            def scores(b, h, i):
                for qt in range(QT):
                    at = b * SEQ + qt * P
                    for n, (x, y) in enumerate(PARTS):
                        ins = nc.tensor.matmul(score_bank[i][:, qt * SEQ:(qt + 1) * SEQ], qm[h][x][:, at:at + P],
                                               k_parts[y][:, b * SEQ:(b + 1) * SEQ], start=(n == 0), stop=(n == 2))
                ins.then_inc(scored, 1)

            def turn(u, i):
                pe.wait_ge(exp_ready, u + 1)
                for qt in range(QT):
                    for kt in range(2):
                        ins = nc.tensor.transpose(bank[2 + i][:, (2 * qt + kt) * P:(2 * qt + kt + 1) * P],
                                                  e[i][:, qt, kt * P:(kt + 1) * P], g.ident[:])
                ins.then_inc(turned, 1)

            def values(u, p, b, h, i):
                pe.wait_ge(et_lo_ready, u + 1)
                for qt in range(QT):
                    for kt in range(2):
                        head = ds(((QT * b + kt) * NHEADS + h) * 2 * NW + p * (4 * NW), 2 * NW)
                        for x in range(2):
                            ins = nc.tensor.matmul(bank[6 + i][:, qt * 2 * NW:(qt + 1) * 2 * NW],
                                                   et[i][x][:, qt, kt * P:(kt + 1) * P], v_flat[:, head],
                                                   start=(kt == 0 and x == 0), stop=(kt == 1 and x == 1))
                ins.then_inc(pv_done, 1)

            def pair_steps(p, first, more):
                for j in range(HUNITS):
                    u, n = HUNITS * p + j, (j + 1) % HUNITS
                    h, b = n // BATCH, n % BATCH
                    if j + 1 < HUNITS or more:
                        if b == 0:
                            pe.wait_ge(qm_ready, 4 * (p if n else p + 1) + 2 * h + 2)
                        scores(b, h, n % 4)
                    if not (first and j < 1):
                        turn(u - 1, (j - 1) % 2)
                    if not (first and j < 2):
                        jj = (j - 2) % HUNITS
                        values(u - 2, p if j >= 2 else p - 1, jj % BATCH, jj // BATCH, j % 2)

            pe.wait_ge(qm_ready, 2)
            scores(0, 0, 0)
            pair_steps(0, True, True)
            with pe.Fori(1, NHEADS // 2 - 1) as p:
                pair_steps(p, False, True)
            pair_steps(NHEADS // 2 - 1, False, False)
            last = NHEADS // 2 * HUNITS
            turn(last - 1, 1)
            values(last - 2, NHEADS // 2 - 1, BATCH - 2, 1, 0)
            values(last - 1, NHEADS // 2 - 1, BATCH - 1, 1, 1)
            pe.wait_ge(on_ready, 1)
            transpose_rows(nc, pe, on, None, g.ident[:], bank[2:4], on_turned)
            pe.wait_ge(ont_ready, 2)
            for t in range(TILES):
                y = bank[t // 4][:, (t % 4) * D:(t % 4 + 1) * D]
                ins = nc.tensor.matmul(y, ont[:, t, :], w[:, 3, :], start=True, stop=True)
            ins.then_inc(y_psum, 1)

        @block.scalar
        def _(act):
            act.wait_ge(xt_psum, 1)
            nc.scalar.copy(g.xt[:, 0:BANK], bank[0]).then_inc(xt_ready, 1)
            given.wait(act)
            act.wait_ge(v_psum, 1)
            nc.scalar.activation(halves(k[:]), pair[2], ACT.Identity, bias=bqk[:, 1:2]).then_inc(k_ready, 1)

            nc.scalar.activation(halves(k_parts[0][:]), pair[2], ACT.Identity, bias=bqk[:, 1:2]).then_inc(k_hi_ready, 1)
            act.wait_ge(v_ready, 1)
            nc.scalar.copy(v_parts[0][:, :, :, 0:NK], v[:]).then_inc(v_hi_ready, 1)
            act.wait_ge(q_ready, 1)
            nc.scalar.copy(q_parts[0][:], q[:]).then_inc(q_hi_ready, 1)

            def exps(u, i, k, first):
                act.wait_ge(max_ready, u + 1)
                if not first:
                    act.wait_ge(turned, u - 1)
                for qt in range(QT):
                    ins = nc.scalar.activation(e[i][:, qt, :], score_bank[k][:, qt * SEQ:(qt + 1) * SEQ], ACT.Exp,
                                               bias=negmax[k][:, qt:qt + 1])
                ins.then_inc(exp_ready, 1)

            def split_high(u, i, first):
                act.wait_ge(turned, u + 1)
                if not first:
                    act.wait_ge(pv_done, u - 1)
                nc.scalar.copy(et[i][0][:].rearrange("p q n -> p (q n)"), bank[2 + i]).then_inc(et_hi_ready, 1)

            def pair_steps(p, first):
                for j in range(HUNITS):
                    u = HUNITS * p + j
                    exps(u, j % 2, j % 4, first and j < 2)
                    if not (first and j < 1):
                        split_high(u - 1, (j - 1) % 2, first and j < 3)

            pair_steps(0, True)
            with act.Fori(1, NHEADS // 2) as p:
                pair_steps(p, False)
            split_high(NHEADS // 2 * HUNITS - 1, 1, False)
            act.wait_ge(on_turned, 1)
            nc.scalar.copy(ont[:, 0:4, :].rearrange("p t c -> p (t c)"), bank[2]).then_inc(ont_ready, 1)
            norm_finish(nc, act, nb, 1, rsd, g.x)

        @block.vector
        def _(dve):
            steps = Tally(dve, dve_steps)
            dve.wait_ge(xt_psum, 2)
            nc.vector.tensor_copy(g.xt[:, BANK:], bank[1]).then_inc(xt_ready, 1)
            given.wait(dve)
            dve.wait_ge(v_psum, 1)
            for t in range(TILES):
                ins = nc.vector.tensor_tensor(v[:, t].rearrange("p h d -> p (h d)"),
                                              bank[6 + t // 4][:, (t % 4) * D:(t % 4 + 1) * D], bv[:], ALU.add)
            ins.then_inc(v_ready, 1)
            dve.wait_ge(q_psum, 1)
            nc.vector.tensor_scalar(halves(q[:]), pair[1], bqk[:, 0:1], NK ** -0.5, ALU.add, ALU.mult)\
                .then_inc(q_ready, 1)
            dve.wait_ge(k_ready, 1)
            dve.wait_ge(k_hi_ready, 1)
            nc.vector.tensor_tensor(k_parts[1][:], k[:], k_parts[0][:], ALU.subtract).then_inc(lo_ready, 1)
            dve.wait_ge(q_ready, 1)
            dve.wait_ge(q_hi_ready, 1)
            nc.vector.tensor_tensor(q_parts[1][:], q[:], q_parts[0][:], ALU.subtract).then_inc(lo_ready, 1)

            def maxima(u, i):
                dve.wait_ge(scored, u + 1)
                nc.vector.tensor_reduce(negmax[i][:], score_bank[i].rearrange("p (q n) -> p q n", q=QT), AX.X, ALU.max,
                                        negate=True).then_inc(max_ready, 1)

            def split_low(u, i):
                dve.wait_ge(et_hi_ready, u + 1)
                nc.vector.tensor_tensor(et[i][1][:].rearrange("p q n -> p (q n)"), bank[2 + i],
                                        et[i][0][:].rearrange("p q n -> p (q n)"), ALU.subtract)\
                    .then_inc(et_lo_ready, 1)

            def copy_out(u, p, b, h, i):
                dve.wait_ge(pv_done, u + 1)
                nc.vector.tensor_copy(o_heads[:, QT * b:QT * b + QT, ds(h * 2 * NW + p * (4 * NW), 2 * NW)],
                                      bank[6 + i][:, 0:QT * 2 * NW].rearrange("p (q w) -> p q w", q=QT))\
                    .then_inc(o_ready, 1)

            def pair_steps(p, first, more):
                for j in range(HUNITS):
                    u, n = HUNITS * p + j, (j + 1) % HUNITS
                    if j + 1 < HUNITS or more:
                        maxima(u + 1, n % 4)
                    if not (first and j < 1):
                        split_low(u - 1, (j - 1) % 2)
                    if not (first and j < 2):
                        jj = (j - 2) % HUNITS
                        copy_out(u - 2, p if j >= 2 else p - 1, jj % BATCH, jj // BATCH, j % 2)

            maxima(0, 0)
            pair_steps(0, True, True)
            with dve.Fori(1, NHEADS // 2 - 1) as p:
                pair_steps(p, False, True)
            pair_steps(NHEADS // 2 - 1, False, False)
            last = NHEADS // 2 * HUNITS
            split_low(last - 1, 1)
            copy_out(last - 2, NHEADS // 2 - 1, BATCH - 2, 1, 0)
            copy_out(last - 1, NHEADS // 2 - 1, BATCH - 1, 1, 1)
            dve.wait_ge(o_ready, last)
            both = o_both[:].rearrange("p t h y w -> p (t h) y w")
            steps.step(nc.vector.tensor_tensor(o[:], both[:, :, 0, :], both[:, :, 1, :], ALU.add))
            steps.step(nc.vector.reciprocal(rsum[:].rearrange("p t h -> p (t h)"), o[:, :, NK]))
            nc.vector.tensor_tensor(on[:].rearrange("p t (h d) -> p (t h) d", d=NK), o[:, :, 0:NK],
                                    rsum[:].rearrange("p t h -> p (t h)").unsqueeze(2)
                                    .broadcast_to([P, TILES * NHEADS, NK]), ALU.mult).then_inc(on_ready, 1)
            dve.wait_ge(on_turned, 2)
            nc.vector.tensor_copy(ont[:, 4:8, :].rearrange("p t c -> p (t c)"), bank[3]).then_inc(ont_ready, 1)
            dve.wait_ge(y_psum, 1)
            dve.wait_ge(x_biased, 1)
            eights = lambda z: z.rearrange("p (h t) c -> p h (t c)", h=2)
            steps.step(nc.vector.tensor_tensor(eights(rsd[:]), eights(g.x[:]), pair[0], ALU.add))
            norm_stats(nc, steps, nb, rsd)
            norm_scale(nc, dve, steps, nb, 1)
            norm_apply(nc, steps, nb, rsd, g.x, VECTOR_TILES)


HID = 512
CHUNKS = HID // P
MAGIC = 1.5 * 2 ** 23
LEAST = 1e-5


class QuantisedWeights(Weights):
    def __init__(self, nc, ctx, a):
        super().__init__(nc, ctx, "qffn")
        self.w1, self.w2 = self.sb("w1_cols", [P, HID]), self.sb("w2_cols", [P, HID])
        self.taps, self.cb = self.sb("taps", [P, CHUNKS, 3]), self.sb("conv_bias", [P, CHUNKS])
        self.pairs = [
            (self.w1[:], a["L1_ffn_w1"]), (self.w2[:].rearrange("p (c n) -> p c n", c=CHUNKS), a["L1_ffn_w2"]),
            (self.taps[:], a["L1_ffn_conv_w"]), (self.cb[:], a["L1_ffn_conv_b"]),
        ]


def quantised_ffn(nc, g, a):
    with ExitStack() as ctx:
        r = Resources(nc, ctx, g.sems, "qffn")
        given = g.quantised
        w1, w2, taps, cb = given.w1, given.w2, given.taps, given.cb
        w2b = r.sb("w2_ternary", [P, HID], BF16)
        ones = r.sb("all_ones", [P, P])
        ident_b = r.sb("f_identity_b", [P, P], BF16)
        mag = r.sb("weight_magnitude", [P, 2])
        mean = r.sb("weight_mean", [P, 2])
        wscale = r.sb("weight_scale", [P, 2])
        wback = r.sb("weight_back", [P, 2])
        top = r.sb("row_top", [P, TILES])
        scale = r.sb("row_scale", [P, TILES])
        back = r.sb("row_back", [P, TILES])
        xq = r.sb("x_quant", [P, TILES, D])
        xqt = r.sb("x_quant_cols", [P, TOK])
        conv = [r.sb(f"conv{i}", [P, TOK]) for i in range(2)]
        act_cols = r.sb("silu_cols", [P, CHUNKS, TOK])
        top2 = r.sb("row_top2", [P, TILES])
        scale2 = r.sb("row_scale2", [P, TILES])
        back2 = r.sb("row_back2", [P, TILES])
        big = r.sb("rounded", [P, TILES, HID])
        hq = r.sb("hidden_int", [P, TILES, HID], BF16)
        hqt = r.sb("hidden_int_cols", [P, TILES, HID], BF16)
        rsd = r.sb("f_rows", [P, TILES, D])
        nb = NormBuffers(r, "f_norm")
        const_done, mag_ready, mag_psum, w_ready, xq_ready = (r.sem(n) for n in (
            "const_done", "mag_ready", "mag_psum", "w_ready", "xq_ready"))
        xt_psum, xt_ready, h_psum, mid_ready, conv_ready, silu_ready = (r.sem(n) for n in (
            "xt_psum", "xt_ready", "h_psum", "mid_ready", "conv_ready", "silu_ready"))
        g_psum, rounded_ready, hq_ready, hq_psum, hqt_ready, y_psum = (r.sem(n) for n in (
            "g_psum", "rounded_ready", "hq_ready", "hq_psum", "hqt_ready", "y_psum"))
        dve_steps, pool_steps = (r.sem(n) for n in (
            "dve_steps", "pool_steps"))
        bank = [g.psum[:, i, :] for i in range(8)]
        pair = [g.psum[:, 2 * i:2 * i + 2, :] for i in range(4)]
        block = ctx.enter_context(nc.Block())

        @block.gpsimd
        def _(pool):
            steps = Tally(pool, pool_steps)
            nc.gpsimd.memset(ones[:], 1.0).then_inc(const_done, 1)
            steps.step(nc.gpsimd.memset(ident_b[:], 0.0))
            nc.gpsimd.affine_select(out=ident_b[:], in_=ident_b[:], compare_op=ALU.not_equal, fill=1.0, base=0,
                                    pattern=[[-1, P]], channel_multiplier=1).then_inc(const_done, 1)

        @block.tensor
        def _(pe):
            pe.wait_ge(const_done, 2)
            pe.wait_ge(mag_ready, 1)
            nc.tensor.matmul(bank[7][:, 0:2], ones[:], mag[:], start=True, stop=True).then_inc(mag_psum, 1)
            pe.wait_ge(xq_ready, 1)
            transpose_rows(nc, pe, xq, None, g.ident[:], bank[4:6], xt_psum)
            pe.wait_ge(w_ready, 1)
            pe.wait_ge(xt_ready, 2)
            for c in range(CHUNKS):
                if c >= 2:
                    pe.wait_ge(conv_ready, c - 1)
                for j in range(2):
                    ins = nc.tensor.matmul(bank[2 * (c % 2) + j], w1[:, c * P:(c + 1) * P],
                                           xqt[:, j * BANK:(j + 1) * BANK], start=True, stop=True)
                ins.then_inc(h_psum, 1)
            for grp in range(2):
                for c in range(CHUNKS):
                    pe.wait_ge(silu_ready, c + 1)
                    if not grp and c == 0:
                        pe.wait_ge(conv_ready, CHUNKS)
                    for t in range(4):
                        lo = (4 * grp + t) * P
                        ins = nc.tensor.transpose(bank[4 * grp + t][:, c * P:(c + 1) * P], act_cols[:, c, lo:lo + P], g.ident[:])
                ins.then_inc(g_psum, 1)
            for grp in range(2):
                pe.wait_ge(hq_ready, grp + 1)
                for t in range(4):
                    for c in range(CHUNKS):
                        dst = bank[2 * grp + t // 2].bitcast(BF16)[:, (t % 2) * HID + c * P:(t % 2) * HID + (c + 1) * P]
                        ins = nc.tensor.transpose(dst, hq[:, 4 * grp + t, c * P:(c + 1) * P], ident_b[:])
                    if t % 2:
                        ins.then_inc(hq_psum, 1)
            for t in range(TILES):
                pe.wait_ge(hqt_ready, t // 2 + 1)
                for c in range(CHUNKS):
                    ins = nc.tensor.matmul(bank[6 + t // 4][:, (t % 4) * D:(t % 4 + 1) * D],
                                           hqt[:, t, c * P:(c + 1) * P], w2b[:, c * P:(c + 1) * P],
                                           start=(c == 0), stop=(c == CHUNKS - 1))
                if t % 4 == 3:
                    ins.then_inc(y_psum, 1)

        @block.scalar
        def _(act):
            act.wait_ge(xt_psum, 1)
            nc.scalar.copy(xqt[:, 0:BANK], bank[4]).then_inc(xt_ready, 1)
            given.wait(act)
            for c in range(CHUNKS):
                act.wait_ge(h_psum, c + 1)
                if c >= 2:
                    act.wait_ge(silu_ready, c - 1)
                nc.scalar.activation(halves(conv[c % 2][:]), pair[c % 2], ACT.Identity, scale=taps[:, c, 1:2],
                                     bias=cb[:, c:c + 1]).then_inc(mid_ready, 1)
                if c >= 1:
                    act.wait_ge(conv_ready, c)
                    nc.scalar.activation(act_cols[:, c - 1, :], conv[(c - 1) % 2][:], ACT.Silu).then_inc(silu_ready, 1)
            act.wait_ge(conv_ready, CHUNKS)
            nc.scalar.activation(act_cols[:, CHUNKS - 1, :], conv[(CHUNKS - 1) % 2][:], ACT.Silu)\
                .then_inc(silu_ready, 1)
            for n in range(4):
                act.wait_ge(hq_psum, n + 1)
                nc.scalar.copy(hqt[:, 2 * n:2 * n + 2, :].rearrange("p t c -> p (t c)"), bank[n].bitcast(BF16))\
                    .then_inc(hqt_ready, 1)
            norm_finish(nc, act, nb, 1, rsd, g.x)

        @block.vector
        def _(dve):
            steps = Tally(dve, dve_steps)
            given.wait(dve)
            steps.add(nc.vector.tensor_reduce(mag[:, 0:1], w1[:], AX.X, ALU.add, apply_absolute_value=True))
            nc.vector.tensor_reduce(mag[:, 1:2], w2[:], AX.X, ALU.add, apply_absolute_value=True)\
                .then_inc(mag_ready, 1)

            def quant_scales(top, scale, back, cols):
                steps.step(nc.vector.tensor_scalar(top[:, cols], top[:, cols], LEAST, None, ALU.max))
                steps.step(nc.vector.reciprocal(scale[:, cols], top[:, cols]))
                steps.step(nc.vector.tensor_scalar(scale[:, cols], scale[:, cols], 127.0, None, ALU.mult))
                steps.step(nc.vector.reciprocal(back[:, cols], scale[:, cols]))

            every = slice(0, TILES)
            steps.step(nc.vector.tensor_reduce(top[:], g.x[:], AX.X, ALU.max, apply_absolute_value=True))
            quant_scales(top, scale, back, every)
            for t in range(TILES):
                steps.add(nc.vector.tensor_scalar(xq[:, t, :], g.x[:, t, :], scale[:, t:t + 1], MAGIC,
                                                  ALU.mult, ALU.add))
            steps.settle()
            for t in range(TILES):
                ins = nc.vector.tensor_scalar(xq[:, t, :], xq[:, t, :], MAGIC, back[:, t:t + 1],
                                              ALU.subtract, ALU.mult)
            ins.then_inc(xq_ready, 1)
            dve.wait_ge(mag_psum, 1)
            steps.step(nc.vector.tensor_scalar(mean[:], bank[7][:, 0:2], 1.0 / (D * HID), LEAST, ALU.mult, ALU.max))
            steps.step(nc.vector.reciprocal(wscale[:], mean[:]))
            steps.step(nc.vector.reciprocal(wback[:], wscale[:]))
            for j, w in enumerate((w1, w2)):
                steps.step(nc.vector.tensor_scalar(w[:], w[:], wscale[:, j:j + 1], MAGIC, ALU.mult, ALU.add))
                steps.step(nc.vector.tensor_scalar(w[:], w[:], MAGIC, 1.0, ALU.subtract, ALU.min))
            steps.add(nc.vector.tensor_scalar(w2b[:], w2[:], -1.0, None, ALU.max))
            nc.vector.tensor_scalar(w1[:], w1[:], -1.0, wback[:, 0:1], ALU.max, ALU.mult).then_inc(w_ready, 1)
            dve.wait_ge(xt_psum, 2)
            nc.vector.tensor_copy(xqt[:, BANK:], bank[5]).then_inc(xt_ready, 1)
            seqs = lambda z: z.rearrange("p (b n) -> p b n", b=BATCH)
            for c in range(CHUNKS):
                h = seqs(pair[c % 2].rearrange("p j n -> p (j n)"))
                z = seqs(conv[c % 2][:])
                dve.wait_ge(mid_ready, c + 1)
                steps.step(nc.vector.scalar_tensor_tensor(z[:, :, 1:], h[:, :, :SEQ - 1], taps[:, c, 0:1], z[:, :, 1:],
                                                          ALU.mult, ALU.add))
                nc.vector.scalar_tensor_tensor(z[:, :, :SEQ - 1], h[:, :, 1:], taps[:, c, 2:3], z[:, :, :SEQ - 1],
                                               ALU.mult, ALU.add).then_inc(conv_ready, 1)
            for grp in range(2):
                cols = slice(4 * grp, 4 * grp + 4)
                dve.wait_ge(g_psum, grp + 1)
                steps.step(nc.vector.tensor_reduce(top2[:, cols], g.psum[:, 4 * grp:4 * grp + 4, :], AX.X, ALU.max,
                                                   apply_absolute_value=True))
                quant_scales(top2, scale2, back2, cols)
                for t in range(4):
                    n = 4 * grp + t
                    ins = nc.vector.tensor_scalar(big[:, n, :], bank[n], scale2[:, n:n + 1], MAGIC, ALU.mult, ALU.add)
                ins.then_inc(rounded_ready, 1)
                dve.wait_ge(rounded_ready, grp + 1)
                nc.vector.tensor_scalar(hq[:, cols, :], big[:, cols, :], MAGIC, None, ALU.subtract)\
                    .then_inc(hq_ready, 1)
            steps.step(nc.vector.tensor_scalar(back2[:], back2[:], wback[:, 1:2], None, ALU.mult))
            for t in range(TILES):
                dve.wait_ge(y_psum, t // 4 + 1)
                steps.add(nc.vector.scalar_tensor_tensor(rsd[:, t, :], bank[6 + t // 4][:, (t % 4) * D:(t % 4 + 1) * D],
                                                         back2[:, t:t + 1], g.x[:, t, :], ALU.mult, ALU.add))
            steps.settle()
            norm_stats(nc, steps, nb, rsd)
            norm_scale(nc, dve, steps, nb, 1)
            norm_apply(nc, steps, nb, rsd, g.x, VECTOR_TILES)


def store(nc, g, out):
    stored = nc.alloc_semaphore(name="stored")
    with nc.Block() as block:
        @block.sync
        def _(sp):
            sp.dma_start(out.rearrange("b (h p) c -> p (b h) c", p=P), g.x[:]).then_inc(stored, 16)
            sp.wait_ge(stored, 16)




def decoder(nc, a, out):
    with ExitStack() as ctx:
        g = Shared(nc, ctx)
        g.narrow = NarrowWeights(nc, ctx, a)
        with ExitStack() as layers:
            g.graph = GraphWeights(nc, layers, a)
            with ExitStack() as layer0:
                g.expert = ExpertWeights(nc, layer0, a)
                with ExitStack() as mixers:
                    g.memory = MemoryWeights(nc, mixers, a)
                    selective_scan(nc, g, a)
                    memory_attention(nc, g, a)
                expert_block(nc, g, a)
            nc.clear_and_free_semaphores(g.sems)
            g.sems.clear()
            nc.all_engine_barrier()
            graph_attention(nc, g, a)
        with ExitStack() as last:
            g.quantised = QuantisedWeights(nc, last, a)
            narrow_attention(nc, g, a)
            quantised_ffn(nc, g, a)
        store(nc, g, out)


_OUTS = [((4, 256, 128), 'float32')]


def kernel(**inputs):
    import numpy as _np
    import concourse.bacc as _bacc
    from concourse import mybir as _mybir
    from concourse.bass_utils import run_bass_kernel_spmd as _run

    nc = _bacc.Bacc("TRN2", target_bir_lowering=False, num_devices=1)
    def columns(v):
        return v.reshape(-1, 128).T

    given = {name: _np.asarray(v) for name, v in inputs.items()}
    for name in ("L0_xattn_wq_b", "L0_xattn_wk_b", "L0_ffn_b1", "L1_xattn_bq", "L1_xattn_bk", "L1_ffn_conv_b",
                 "L1_attn_gamma_in", "L0_attn_b_dt", "L0_attn_Dp"):
        given[name] = columns(given[name])
    given["L1_ffn_w1"] = given["L1_ffn_w1"].T
    given["L1_ffn_w2"] = given["L1_ffn_w2"].T.reshape(4, 128, 128).transpose(1, 0, 2)
    given["L1_attn_lin_b"] = given["L1_attn_lin_b"].reshape(64, 1)
    for name in ("L0_ffn_in_proj_w", "L0_ffn_out_w", "L0_ffn_router_w", "L1_attn_lin_w"):
        given[name] = given[name].T
    for name in ("L0_ffn_w1", "L0_ffn_w2"):
        given[name] = given[name].transpose(2, 0, 1)
    given["L1_ffn_conv_w"] = given["L1_ffn_conv_w"].reshape(4, 128, 3).transpose(1, 0, 2)
    arrays, args = {}, {}
    for name in given:
        a = _np.ascontiguousarray(given[name])
        arrays[f"in_{name}_dram"] = a
        args[name] = nc.dram_tensor(f"in_{name}_dram", a.shape, _mybir.dt.from_np(a.dtype), kind="ExternalInput").ap()
    shape, dtype = _OUTS[0]
    out = nc.dram_tensor("out_0_dram", shape, _mybir.dt.from_np(_np.dtype(dtype)), kind="ExternalOutput").ap()
    decoder(nc, args, out)
    r = _run(nc, [arrays], core_ids=[0])
    return r.results[0]["out_0_dram"]
```
